# Optimizing a Trainium2 kernel written in Bass

```python
import numpy as np
import jax
import jax.numpy as jnp

def _softmax(x, axis=-1):
    return jax.nn.softmax(x, axis=axis)

def _gelu(x):
    return jax.nn.gelu(x, approximate=True)

def _silu(x):
    return jax.nn.silu(x)

def _sigmoid(x):
    return jax.nn.sigmoid(x)

def _layernorm(x, axis=-1, eps=1e-05):
    m = jnp.mean(x, axis=axis, keepdims=True)
    v = jnp.var(x, axis=axis, keepdims=True)
    return (x - m) / jnp.sqrt(v + eps)

def _scatter_add(tgt, idx, src, axis=0):
    return tgt.at[idx].add(src)

def _segment_sum(src, seg, n):
    return jax.ops.segment_sum(src, seg, n)
kernel_name = 'mk_lm_tower_d4_tok_ids1024_r4_d367ae'

def setup_inputs(seed: int=0):
    np.random.seed(seed)
    _w = jnp.asarray

    def _rec_inputs():
        import jax
        import jax.numpy as jnp
        _rk = jax.random.key(seed)
        x = jax.random.randint(jax.random.fold_in(_rk, 1), (16, 128), 0, 200, jnp.int32)
        return x
    x = _rec_inputs()

    def _L0_tok_setup():
        import jax, jax.numpy as jnp
        import numpy as np
        NUM_LEVELS = 32
        SCALE = 0.15
        OPEN_TOKENS = jnp.array([40, 91, 123], dtype=jnp.int32)
        CLOSE_TOKENS = jnp.array([41, 93, 125], dtype=jnp.int32)

        def _compute_levels(token_ids, num_levels):
            is_open = (token_ids[..., None] == OPEN_TOKENS).any(-1)
            is_close = (token_ids[..., None] == CLOSE_TOKENS).any(-1)
            delta = is_open.astype(jnp.int32) - is_close.astype(jnp.int32)

            def step(lvl, d):
                lvl = jnp.clip(lvl + d, 0, num_levels - 1)
                return (lvl, lvl)
            init = jnp.zeros(token_ids.shape[0], dtype=jnp.int32)
            _, levels = jax.lax.scan(step, init, delta.T)
            return levels.T
        key = jax.random.key(seed)
        k1, k2 = jax.random.split(key)
        token_ids = jax.random.randint(k1, (8, 2048), 0, 200, dtype=jnp.int32)
        level_emb = jax.random.normal(k2, (NUM_LEVELS, 256), dtype=jnp.float32)
        return {'token_ids': token_ids, 'level_emb': level_emb}
    _L0_tok_all = _L0_tok_setup()
    _L0_tok_in = {k: v for k, v in _L0_tok_all.items() if k in ('level_emb',)}
    del _L0_tok_all

    def _L0_attn_setup():
        import jax, jax.numpy as jnp
        import numpy as np
        B, T, C = (2, 512, 256)
        H, DK, OUT = (16, 64, 256)
        key = jax.random.key(seed)
        k1, k2, k3, k4, k5 = jax.random.split(key, 5)
        glorot_qkv = (2.0 / (C + H * DK)) ** 0.5
        glorot_o = (2.0 / (H * DK + OUT)) ** 0.5
        return {'x': jax.random.normal(k1, (B, T, C), dtype=jnp.float32), 'query_mat': jax.random.normal(k2, (C, H, DK), dtype=jnp.float32) * glorot_qkv, 'key_mat': jax.random.normal(k3, (C, H, DK), dtype=jnp.float32) * glorot_qkv, 'value_mat': jax.random.normal(k4, (C, H, DK), dtype=jnp.float32) * glorot_qkv, 'linear_m1': jax.random.normal(k5, (H * DK, OUT), dtype=jnp.float32) * glorot_o}
    _L0_attn_all = _L0_attn_setup()
    _L0_attn_in = {k: v for k, v in _L0_attn_all.items() if k in ('query_mat', 'key_mat', 'value_mat', 'linear_m1')}
    del _L0_attn_all

    def _L0_ffn_setup():
        import jax, jax.numpy as jnp
        import numpy as np
        D_MODEL = 256
        N_HEADS = 16
        N_KV = 4
        NUM_REP = N_HEADS // N_KV
        HEAD_DIM = D_MODEL // N_HEADS
        N_EXPERTS = 8
        TOP_K = 2
        CAP_FACTOR = 1.25
        EPS_NORM = 1e-06

        def _rmsnorm(x, w):
            var = jnp.mean(x * x, axis=-1, keepdims=True)
            return w * (x * jax.lax.rsqrt(var + EPS_NORM))

        def _gqa(x, qw, qb, kw, kb, vw, vb, ow, ob):
            B, S, D = x.shape
            q = (x @ qw + qb).reshape(B, S, N_HEADS, HEAD_DIM).transpose(0, 2, 1, 3)
            k = (x @ kw + kb).reshape(B, S, N_KV, HEAD_DIM).transpose(0, 2, 1, 3)
            v = (x @ vw + vb).reshape(B, S, N_KV, HEAD_DIM).transpose(0, 2, 1, 3)
            k = jnp.repeat(k, NUM_REP, axis=1)
            v = jnp.repeat(v, NUM_REP, axis=1)
            scores = jnp.einsum('bhqd,bhkd->bhqk', q, k) / np.sqrt(HEAD_DIM).astype(np.float32)
            attn = jax.nn.softmax(scores, axis=-1)
            out = jnp.einsum('bhqk,bhkd->bhqd', attn, v)
            out = out.transpose(0, 2, 1, 3).reshape(B, S, D)
            return out @ ow + ob

        def _moe(x, gate_w, w1, w2):
            B, S, D = x.shape
            T = B * S
            x_flat = x.reshape(T, D)
            capacity = int(CAP_FACTOR * T * TOP_K / N_EXPERTS)
            logits = x_flat @ gate_w
            probs = jax.nn.sigmoid(logits)
            _, sel = jax.lax.top_k(probs, TOP_K)
            w_topk = jnp.take_along_axis(probs, sel, axis=1)
            w_topk = w_topk / (jnp.sum(w_topk, axis=-1, keepdims=True) + 1e-06)
            flat_sel = sel.reshape(-1)
            em = jax.nn.one_hot(flat_sel, N_EXPERTS, dtype=jnp.int32)
            ranks = jnp.take_along_axis(jnp.cumsum(em, axis=0), flat_sel[:, None], axis=1)[:, 0] - 1
            valid = ranks < capacity
            slot = flat_sel * capacity + ranks
            scatter_idx = jnp.where(valid, slot, N_EXPERTS * capacity)
            x_rep = jnp.repeat(x_flat, TOP_K, axis=0)
            padded = jnp.zeros((N_EXPERTS * capacity + 1, D), x.dtype).at[scatter_idx].set(x_rep)
            padded_x = padded[:N_EXPERTS * capacity].reshape(N_EXPERTS, capacity, D)
            h = jax.nn.gelu(jnp.einsum('ecd,edf->ecf', padded_x, w1), approximate=False)
            out_padded = jnp.einsum('ecf,efd->ecd', h, w2).reshape(N_EXPERTS * capacity, D)
            gather_idx = jnp.where(valid, slot, 0)
            out_rep = jnp.where(valid[:, None], out_padded[gather_idx], 0.0)
            out_w = out_rep * w_topk.reshape(-1)[:, None]
            return out_w.reshape(T, TOP_K, D).sum(axis=1).reshape(B, S, D)
        key = jax.random.key(seed)
        ks = jax.random.split(key, 12)
        s = 0.02
        return {'x': jax.random.normal(ks[0], (4, 256, D_MODEL), jnp.float32), 'qw': jax.random.normal(ks[1], (D_MODEL, D_MODEL), jnp.float32) * s, 'qb': jnp.zeros((D_MODEL,), jnp.float32), 'kw': jax.random.normal(ks[2], (D_MODEL, N_KV * HEAD_DIM), jnp.float32) * s, 'kb': jnp.zeros((N_KV * HEAD_DIM,), jnp.float32), 'vw': jax.random.normal(ks[3], (D_MODEL, N_KV * HEAD_DIM), jnp.float32) * s, 'vb': jnp.zeros((N_KV * HEAD_DIM,), jnp.float32), 'ow': jax.random.normal(ks[4], (D_MODEL, D_MODEL), jnp.float32) * s, 'ob': jnp.zeros((D_MODEL,), jnp.float32), 'gate_w': jax.random.normal(ks[5], (D_MODEL, N_EXPERTS), jnp.float32) * s, 'w1': jax.random.normal(ks[6], (N_EXPERTS, D_MODEL, 512), jnp.float32) * s, 'w2': jax.random.normal(ks[7], (N_EXPERTS, 512, D_MODEL), jnp.float32) * s, 'norm1_w': jnp.ones((D_MODEL,), jnp.float32), 'norm2_w': jnp.ones((D_MODEL,), jnp.float32)}
    _L0_ffn_all = _L0_ffn_setup()
    _L0_ffn_in = {k: v for k, v in _L0_ffn_all.items() if k in ('qw', 'qb', 'kw', 'kb', 'vw', 'vb', 'ow', 'ob', 'gate_w', 'w1', 'w2', 'norm1_w', 'norm2_w')}
    del _L0_ffn_all

    def _L1_attn_setup():
        import jax, jax.numpy as jnp
        import numpy as np
        D_MODEL = 256
        NUM_HEADS = 16
        HEAD_DIM = D_MODEL // NUM_HEADS
        D_FF = 1024
        EPS = 1e-05

        def layer_norm(x, gamma, beta):
            mu = jnp.mean(x, axis=-1, keepdims=True)
            var = jnp.mean((x - mu) ** 2, axis=-1, keepdims=True)
            return (x - mu) * jax.lax.rsqrt(var + EPS) * gamma + beta

        def apply_rope(t):
            S, d = (t.shape[-2], t.shape[-1])
            inv_freq = 1.0 / 10000.0 ** (jnp.arange(0, d, 2, dtype=jnp.float32) / d)
            angles = jnp.arange(S, dtype=jnp.float32)[:, None] * inv_freq[None, :]
            sin, cos = (jnp.sin(angles), jnp.cos(angles))
            tp = t.reshape(*t.shape[:-1], d // 2, 2)
            t0, t1 = (tp[..., 0], tp[..., 1])
            rot = jnp.stack([t0 * cos - t1 * sin, t0 * sin + t1 * cos], axis=-1)
            return rot.reshape(t.shape)
        key = jax.random.key(seed)
        ks = jax.random.split(key, 18)
        s = 0.02
        d, f = (D_MODEL, D_FF)
        return {'x': jax.random.normal(ks[0], (2, 512, d), dtype=jnp.float32), 'Wq': jax.random.normal(ks[1], (d, d), dtype=jnp.float32) * s, 'bq': jnp.zeros((d,), jnp.float32), 'Wk': jax.random.normal(ks[2], (d, d), dtype=jnp.float32) * s, 'bk': jnp.zeros((d,), jnp.float32), 'Wv': jax.random.normal(ks[3], (d, d), dtype=jnp.float32) * s, 'bv': jnp.zeros((d,), jnp.float32), 'Wo': jax.random.normal(ks[4], (d, d), dtype=jnp.float32) * s, 'bo': jnp.zeros((d,), jnp.float32), 'W1': jax.random.normal(ks[5], (d, f), dtype=jnp.float32) * s, 'b1': jnp.zeros((f,), jnp.float32), 'W2': jax.random.normal(ks[6], (f, d), dtype=jnp.float32) * s, 'b2': jnp.zeros((d,), jnp.float32), 'g1': jnp.ones((d,), jnp.float32), 'beta1': jnp.zeros((d,), jnp.float32), 'g2': jnp.ones((d,), jnp.float32), 'beta2': jnp.zeros((d,), jnp.float32)}
    _L1_attn_all = _L1_attn_setup()
    _L1_attn_in = {k: v for k, v in _L1_attn_all.items() if k in ('Wq', 'bq', 'Wk', 'bk', 'Wv', 'bv', 'Wo', 'bo', 'W1', 'b1', 'W2', 'b2', 'g1', 'beta1', 'g2', 'beta2')}
    del _L1_attn_all

    def _L1_ffn_setup():
        import jax, jax.numpy as jnp
        import numpy as np
        B, S, D_MODEL, D_HIDDEN = (4, 512, 256, 1024)

        def act_quant(x):
            scale = 127.0 / jnp.clip(jnp.max(jnp.abs(x), axis=-1, keepdims=True), 1e-05)
            return jnp.clip(jnp.round(x * scale), -128, 127) / scale

        def weight_quant(w):
            scale = 1.0 / jnp.clip(jnp.mean(jnp.abs(w)), 1e-05)
            return jnp.clip(jnp.round(w * scale), -1, 1) / scale

        def bit_linear(x, w):
            xq = x + jax.lax.stop_gradient(act_quant(x) - x)
            wq = w + jax.lax.stop_gradient(weight_quant(w) - w)
            return jnp.einsum('bsd,hd->bsh', xq, wq)

        def depthwise_conv1d(x_bcl, w, b):
            y = jax.lax.conv_general_dilated(x_bcl, w, window_strides=(1,), padding=[(1, 1)], dimension_numbers=('NCH', 'OIH', 'NCH'), feature_group_count=x_bcl.shape[1])
            return y + b[None, :, None]
        key = jax.random.key(seed)
        ks = jax.random.split(key, 5)
        lim1 = 1.0 / np.sqrt(D_MODEL)
        lim2 = 1.0 / np.sqrt(D_HIDDEN)
        limc = 1.0 / np.sqrt(3.0)
        return {'x': jax.random.normal(ks[0], (B, S, D_MODEL), dtype=jnp.float32), 'w1': jax.random.uniform(ks[1], (D_HIDDEN, D_MODEL), jnp.float32, -lim1, lim1), 'conv_w': jax.random.uniform(ks[2], (D_HIDDEN, 1, 3), jnp.float32, -limc, limc), 'conv_b': jax.random.uniform(ks[3], (D_HIDDEN,), jnp.float32, -limc, limc), 'w2': jax.random.uniform(ks[4], (D_MODEL, D_HIDDEN), jnp.float32, -lim2, lim2)}
    _L1_ffn_all = _L1_ffn_setup()
    _L1_ffn_in = {k: v for k, v in _L1_ffn_all.items() if k in ('w1', 'conv_w', 'conv_b', 'w2')}
    del _L1_ffn_all

    def _L2_attn_setup():
        import jax, jax.numpy as jnp
        import numpy as np
        H = 16
        EPS = 1e-06
        key = jax.random.key(seed)
        ks = jax.random.split(key, 5)
        B, N, D = (4, 1024, 256)
        x = jax.random.normal(ks[0], (B, N, D), dtype=jnp.float32)
        q = jax.random.normal(ks[1], (D,), dtype=jnp.float32)
        k = jax.random.normal(ks[2], (D,), dtype=jnp.float32)
        log_decay = jax.random.normal(ks[3], (H,), dtype=jnp.float32)
        norm_weight = jnp.ones((D,), dtype=jnp.float32)
        o_w = jax.random.normal(ks[4], (D, D), dtype=jnp.float32) * 0.02
        return {'x': x, 'q': q, 'k': k, 'log_decay': log_decay, 'norm_weight': norm_weight, 'o_w': o_w}
    _L2_attn_all = _L2_attn_setup()
    _L2_attn_in = {k: v for k, v in _L2_attn_all.items() if k in ('q', 'k', 'log_decay', 'norm_weight', 'o_w')}
    del _L2_attn_all

    def _L2_ffn_setup():
        import jax, jax.numpy as jnp
        import numpy as np
        D = 256
        I = 128
        E = 32
        K = 4
        T = 2 * 512
        C = 2 * T * K // E
        key = jax.random.key(seed)
        ks = jax.random.split(key, 9)
        bf = jnp.bfloat16
        std = 0.02
        x = jax.random.normal(ks[0], (2, 512, D), dtype=jnp.float32).astype(bf)
        gate_w = (std * jax.random.normal(ks[1], (E, D), dtype=jnp.float32)).astype(bf)
        bias = jnp.zeros((E,), jnp.float32)
        W1 = (std * jax.random.normal(ks[2], (E, D, I), dtype=jnp.float32)).astype(bf)
        W3 = (std * jax.random.normal(ks[3], (E, D, I), dtype=jnp.float32)).astype(bf)
        W2 = (std * jax.random.normal(ks[4], (E, I, D), dtype=jnp.float32)).astype(bf)
        sw1 = (std * jax.random.normal(ks[5], (I, D), dtype=jnp.float32)).astype(bf)
        sw3 = (std * jax.random.normal(ks[6], (I, D), dtype=jnp.float32)).astype(bf)
        sw2 = (std * jax.random.normal(ks[7], (D, I), dtype=jnp.float32)).astype(bf)
        return {'x': x, 'gate_w': gate_w, 'bias': bias, 'W1': W1, 'W3': W3, 'W2': W2, 'sw1': sw1, 'sw3': sw3, 'sw2': sw2}
    _L2_ffn_all = _L2_ffn_setup()
    _L2_ffn_in = {k: v for k, v in _L2_ffn_all.items() if k in ('gate_w', 'bias', 'W1', 'W3', 'W2', 'sw1', 'sw3', 'sw2')}
    del _L2_ffn_all

    def _L3_attn_setup():
        import jax, jax.numpy as jnp
        import numpy as np
        from jax import lax
        D_MODEL = 256
        SEQ_LEN = 2048
        ORDER = 2
        BATCH = 2

        def _hyena_fwd(x, in_proj_w, in_proj_b, short_w, short_b, fw1, fb1, fw2, fb2, fw3, fb3, out_w, out_b):
            B, L, C = x.shape
            proj = (x @ in_proj_w + in_proj_b).reshape(B, L, C, ORDER + 1)
            v = proj[..., 0]
            x_branches = [proj[..., i] for i in range(1, ORDER + 1)]
            vc = v.transpose(0, 2, 1)
            vc = lax.conv_general_dilated(vc, short_w, window_strides=(1,), padding=((1, 1),), feature_group_count=C, dimension_numbers=('NCH', 'OIH', 'NCH'))
            v = (vc + short_b[None, :, None]).transpose(0, 2, 1)
            pos = jnp.linspace(0.0, 1.0, L, dtype=x.dtype)[:, None]
            h = jax.nn.gelu(pos @ fw1 + fb1, approximate=False)
            h = jax.nn.gelu(h @ fw2 + fb2, approximate=False)
            coefs = (h @ fw3 + fb3).reshape(L, C, ORDER)
            n = 2 * L
            v_fft = jnp.fft.rfft(v, n=n, axis=1)
            output = v
            for i in range(ORDER):
                h_fft = jnp.fft.rfft(coefs[:, :, i], n=n, axis=0)
                conv = jnp.fft.irfft(v_fft * h_fft[None], n=n, axis=1)[:, :L, :]
                output = x_branches[i] * conv
            return output @ out_w + out_b
        key = jax.random.key(seed)
        ks = jax.random.split(key, 16)
        s = 0.02
        return {'x': jax.random.normal(ks[0], (BATCH, SEQ_LEN, D_MODEL), jnp.float32), 'in_proj_w': jax.random.normal(ks[1], (D_MODEL, D_MODEL * (ORDER + 1)), jnp.float32) * s, 'in_proj_b': jax.random.normal(ks[2], (D_MODEL * (ORDER + 1),), jnp.float32) * s, 'short_w': jax.random.normal(ks[3], (D_MODEL, 1, 3), jnp.float32) * 0.5, 'short_b': jax.random.normal(ks[4], (D_MODEL,), jnp.float32) * s, 'fw1': jax.random.normal(ks[5], (1, 64), jnp.float32) * 0.5, 'fb1': jax.random.normal(ks[6], (64,), jnp.float32) * s, 'fw2': jax.random.normal(ks[7], (64, 128), jnp.float32) * 0.1, 'fb2': jax.random.normal(ks[8], (128,), jnp.float32) * s, 'fw3': jax.random.normal(ks[9], (128, D_MODEL * ORDER), jnp.float32) * 0.05, 'fb3': jax.random.normal(ks[10], (D_MODEL * ORDER,), jnp.float32) * s, 'out_w': jax.random.normal(ks[11], (D_MODEL, D_MODEL), jnp.float32) * s, 'out_b': jax.random.normal(ks[12], (D_MODEL,), jnp.float32) * s}
    _L3_attn_all = _L3_attn_setup()
    _L3_attn_in = {k: v for k, v in _L3_attn_all.items() if k in ('in_proj_w', 'in_proj_b', 'short_w', 'short_b', 'fw1', 'fb1', 'fw2', 'fb2', 'fw3', 'fb3', 'out_w', 'out_b')}
    del _L3_attn_all

    def _L3_ffn_setup():
        import jax, jax.numpy as jnp
        import numpy as np
        THRESHOLD = 0.1
        key = jax.random.key(seed)
        k1, k2, k3 = jax.random.split(key, 3)
        B, S, D, E = (4, 1024, 256, 8)
        inputs = jax.random.normal(k1, (B, S, D), dtype=jnp.float32)
        gate_w = jax.random.normal(k2, (D, E), dtype=jnp.float32) * 0.02
        gate_b = jnp.zeros((E,), dtype=jnp.float32)
        expert_w = jax.random.normal(k3, (E, D, D), dtype=jnp.float32) * 0.02
        expert_b = jnp.zeros((E, D), dtype=jnp.float32)
        return {'inputs': inputs, 'gate_w': gate_w, 'gate_b': gate_b, 'expert_w': expert_w, 'expert_b': expert_b}
    _L3_ffn_all = _L3_ffn_setup()
    _L3_ffn_in = {k: v for k, v in _L3_ffn_all.items() if k in ('gate_w', 'gate_b', 'expert_w', 'expert_b')}
    del _L3_ffn_all
    return {'x': x, 'L0_tok_level_emb': _L0_tok_in['level_emb'], 'L0_attn_query_mat': _L0_attn_in['query_mat'], 'L0_attn_key_mat': _L0_attn_in['key_mat'], 'L0_attn_value_mat': _L0_attn_in['value_mat'], 'L0_attn_linear_m1': _L0_attn_in['linear_m1'], 'L0_ffn_qw': _L0_ffn_in['qw'], 'L0_ffn_qb': _L0_ffn_in['qb'], 'L0_ffn_kw': _L0_ffn_in['kw'], 'L0_ffn_kb': _L0_ffn_in['kb'], 'L0_ffn_vw': _L0_ffn_in['vw'], 'L0_ffn_vb': _L0_ffn_in['vb'], 'L0_ffn_ow': _L0_ffn_in['ow'], 'L0_ffn_ob': _L0_ffn_in['ob'], 'L0_ffn_gate_w': _L0_ffn_in['gate_w'], 'L0_ffn_w1': _L0_ffn_in['w1'], 'L0_ffn_w2': _L0_ffn_in['w2'], 'L0_ffn_norm1_w': _L0_ffn_in['norm1_w'], 'L0_ffn_norm2_w': _L0_ffn_in['norm2_w'], 'L1_attn_Wq': _L1_attn_in['Wq'], 'L1_attn_bq': _L1_attn_in['bq'], 'L1_attn_Wk': _L1_attn_in['Wk'], 'L1_attn_bk': _L1_attn_in['bk'], 'L1_attn_Wv': _L1_attn_in['Wv'], 'L1_attn_bv': _L1_attn_in['bv'], 'L1_attn_Wo': _L1_attn_in['Wo'], 'L1_attn_bo': _L1_attn_in['bo'], 'L1_attn_W1': _L1_attn_in['W1'], 'L1_attn_b1': _L1_attn_in['b1'], 'L1_attn_W2': _L1_attn_in['W2'], 'L1_attn_b2': _L1_attn_in['b2'], 'L1_attn_g1': _L1_attn_in['g1'], 'L1_attn_beta1': _L1_attn_in['beta1'], 'L1_attn_g2': _L1_attn_in['g2'], 'L1_attn_beta2': _L1_attn_in['beta2'], 'L1_ffn_w1': _L1_ffn_in['w1'], 'L1_ffn_conv_w': _L1_ffn_in['conv_w'], 'L1_ffn_conv_b': _L1_ffn_in['conv_b'], 'L1_ffn_w2': _L1_ffn_in['w2'], 'L2_attn_q': _L2_attn_in['q'], 'L2_attn_k': _L2_attn_in['k'], 'L2_attn_log_decay': _L2_attn_in['log_decay'], 'L2_attn_norm_weight': _L2_attn_in['norm_weight'], 'L2_attn_o_w': _L2_attn_in['o_w'], 'L2_ffn_gate_w': _L2_ffn_in['gate_w'], 'L2_ffn_bias': _L2_ffn_in['bias'], 'L2_ffn_W1': _L2_ffn_in['W1'], 'L2_ffn_W3': _L2_ffn_in['W3'], 'L2_ffn_W2': _L2_ffn_in['W2'], 'L2_ffn_sw1': _L2_ffn_in['sw1'], 'L2_ffn_sw3': _L2_ffn_in['sw3'], 'L2_ffn_sw2': _L2_ffn_in['sw2'], 'L3_attn_in_proj_w': _L3_attn_in['in_proj_w'], 'L3_attn_in_proj_b': _L3_attn_in['in_proj_b'], 'L3_attn_short_w': _L3_attn_in['short_w'], 'L3_attn_short_b': _L3_attn_in['short_b'], 'L3_attn_fw1': _L3_attn_in['fw1'], 'L3_attn_fb1': _L3_attn_in['fb1'], 'L3_attn_fw2': _L3_attn_in['fw2'], 'L3_attn_fb2': _L3_attn_in['fb2'], 'L3_attn_fw3': _L3_attn_in['fw3'], 'L3_attn_fb3': _L3_attn_in['fb3'], 'L3_attn_out_w': _L3_attn_in['out_w'], 'L3_attn_out_b': _L3_attn_in['out_b'], 'L3_ffn_gate_w': _L3_ffn_in['gate_w'], 'L3_ffn_gate_b': _L3_ffn_in['gate_b'], 'L3_ffn_expert_w': _L3_ffn_in['expert_w'], 'L3_ffn_expert_b': _L3_ffn_in['expert_b']}

def reference(x, L0_tok_level_emb, L0_attn_query_mat, L0_attn_key_mat, L0_attn_value_mat, L0_attn_linear_m1, L0_ffn_qw, L0_ffn_qb, L0_ffn_kw, L0_ffn_kb, L0_ffn_vw, L0_ffn_vb, L0_ffn_ow, L0_ffn_ob, L0_ffn_gate_w, L0_ffn_w1, L0_ffn_w2, L0_ffn_norm1_w, L0_ffn_norm2_w, L1_attn_Wq, L1_attn_bq, L1_attn_Wk, L1_attn_bk, L1_attn_Wv, L1_attn_bv, L1_attn_Wo, L1_attn_bo, L1_attn_W1, L1_attn_b1, L1_attn_W2, L1_attn_b2, L1_attn_g1, L1_attn_beta1, L1_attn_g2, L1_attn_beta2, L1_ffn_w1, L1_ffn_conv_w, L1_ffn_conv_b, L1_ffn_w2, L2_attn_q, L2_attn_k, L2_attn_log_decay, L2_attn_norm_weight, L2_attn_o_w, L2_ffn_gate_w, L2_ffn_bias, L2_ffn_W1, L2_ffn_W3, L2_ffn_W2, L2_ffn_sw1, L2_ffn_sw3, L2_ffn_sw2, L3_attn_in_proj_w, L3_attn_in_proj_b, L3_attn_short_w, L3_attn_short_b, L3_attn_fw1, L3_attn_fb1, L3_attn_fw2, L3_attn_fb2, L3_attn_fw3, L3_attn_fb3, L3_attn_out_w, L3_attn_out_b, L3_ffn_gate_w, L3_ffn_gate_b, L3_ffn_expert_w, L3_ffn_expert_b):
    import jax
    import jax.numpy as jnp

    def _L0_tok_ref(token_ids, level_emb):
        import jax, jax.numpy as jnp
        import numpy as np
        NUM_LEVELS = 32
        SCALE = 0.15
        OPEN_TOKENS = jnp.array([40, 91, 123], dtype=jnp.int32)
        CLOSE_TOKENS = jnp.array([41, 93, 125], dtype=jnp.int32)

        def _compute_levels(token_ids, num_levels):
            is_open = (token_ids[..., None] == OPEN_TOKENS).any(-1)
            is_close = (token_ids[..., None] == CLOSE_TOKENS).any(-1)
            delta = is_open.astype(jnp.int32) - is_close.astype(jnp.int32)

            def step(lvl, d):
                lvl = jnp.clip(lvl + d, 0, num_levels - 1)
                return (lvl, lvl)
            init = jnp.zeros(token_ids.shape[0], dtype=jnp.int32)
            _, levels = jax.lax.scan(step, init, delta.T)
            return levels.T
        levels = _compute_levels(token_ids, NUM_LEVELS)
        hierarchy_pos = level_emb[levels]
        return hierarchy_pos * SCALE

    def _L0_attn_ref(x, query_mat, key_mat, value_mat, linear_m1):
        import jax, jax.numpy as jnp
        import numpy as np
        B, T, C = (2, 512, 256)
        H, DK, OUT = (16, 64, 256)
        q = jnp.einsum('btc,chd->bhtd', x, query_mat)
        k = jnp.einsum('btc,chd->bhtd', x, key_mat)
        v = jnp.einsum('btc,chd->bhtd', x, value_mat)
        d_k = query_mat.shape[-1]
        w = jnp.einsum('bhtd,bhzd->bhtz', q, k) * d_k ** 0.5
        t = w.shape[-1]
        causal = jnp.tril(jnp.ones((t, t), dtype=bool))
        w = jnp.where(causal, w, -jnp.inf)
        w = jax.nn.softmax(w, axis=-1)
        o = jnp.einsum('bhtz,bhzd->bhtd', w, v)
        o = o.transpose(0, 2, 1, 3).reshape(o.shape[0], o.shape[2], -1)
        return jnp.einsum('btc,cz->btz', o, linear_m1)

    def _L0_ffn_ref(x, qw, qb, kw, kb, vw, vb, ow, ob, gate_w, w1, w2, norm1_w, norm2_w):
        import jax, jax.numpy as jnp
        import numpy as np
        D_MODEL = 256
        N_HEADS = 16
        N_KV = 4
        NUM_REP = N_HEADS // N_KV
        HEAD_DIM = D_MODEL // N_HEADS
        N_EXPERTS = 8
        TOP_K = 2
        CAP_FACTOR = 1.25
        EPS_NORM = 1e-06

        def _rmsnorm(x, w):
            var = jnp.mean(x * x, axis=-1, keepdims=True)
            return w * (x * jax.lax.rsqrt(var + EPS_NORM))

        def _gqa(x, qw, qb, kw, kb, vw, vb, ow, ob):
            B, S, D = x.shape
            q = (x @ qw + qb).reshape(B, S, N_HEADS, HEAD_DIM).transpose(0, 2, 1, 3)
            k = (x @ kw + kb).reshape(B, S, N_KV, HEAD_DIM).transpose(0, 2, 1, 3)
            v = (x @ vw + vb).reshape(B, S, N_KV, HEAD_DIM).transpose(0, 2, 1, 3)
            k = jnp.repeat(k, NUM_REP, axis=1)
            v = jnp.repeat(v, NUM_REP, axis=1)
            scores = jnp.einsum('bhqd,bhkd->bhqk', q, k) / np.sqrt(HEAD_DIM).astype(np.float32)
            attn = jax.nn.softmax(scores, axis=-1)
            out = jnp.einsum('bhqk,bhkd->bhqd', attn, v)
            out = out.transpose(0, 2, 1, 3).reshape(B, S, D)
            return out @ ow + ob

        def _moe(x, gate_w, w1, w2):
            B, S, D = x.shape
            T = B * S
            x_flat = x.reshape(T, D)
            capacity = int(CAP_FACTOR * T * TOP_K / N_EXPERTS)
            logits = x_flat @ gate_w
            probs = jax.nn.sigmoid(logits)
            _, sel = jax.lax.top_k(probs, TOP_K)
            w_topk = jnp.take_along_axis(probs, sel, axis=1)
            w_topk = w_topk / (jnp.sum(w_topk, axis=-1, keepdims=True) + 1e-06)
            flat_sel = sel.reshape(-1)
            em = jax.nn.one_hot(flat_sel, N_EXPERTS, dtype=jnp.int32)
            ranks = jnp.take_along_axis(jnp.cumsum(em, axis=0), flat_sel[:, None], axis=1)[:, 0] - 1
            valid = ranks < capacity
            slot = flat_sel * capacity + ranks
            scatter_idx = jnp.where(valid, slot, N_EXPERTS * capacity)
            x_rep = jnp.repeat(x_flat, TOP_K, axis=0)
            padded = jnp.zeros((N_EXPERTS * capacity + 1, D), x.dtype).at[scatter_idx].set(x_rep)
            padded_x = padded[:N_EXPERTS * capacity].reshape(N_EXPERTS, capacity, D)
            h = jax.nn.gelu(jnp.einsum('ecd,edf->ecf', padded_x, w1), approximate=False)
            out_padded = jnp.einsum('ecf,efd->ecd', h, w2).reshape(N_EXPERTS * capacity, D)
            gather_idx = jnp.where(valid, slot, 0)
            out_rep = jnp.where(valid[:, None], out_padded[gather_idx], 0.0)
            out_w = out_rep * w_topk.reshape(-1)[:, None]
            return out_w.reshape(T, TOP_K, D).sum(axis=1).reshape(B, S, D)
        src = x + _gqa(x, qw, qb, kw, kb, vw, vb, ow, ob)
        src = _rmsnorm(src, norm1_w)
        src = src + _moe(src, gate_w, w1, w2)
        return _rmsnorm(src, norm2_w)

    def _L1_attn_ref(x, Wq, bq, Wk, bk, Wv, bv, Wo, bo, W1, b1, W2, b2, g1, beta1, g2, beta2):
        import jax, jax.numpy as jnp
        import numpy as np
        D_MODEL = 256
        NUM_HEADS = 16
        HEAD_DIM = D_MODEL // NUM_HEADS
        D_FF = 1024
        EPS = 1e-05

        def layer_norm(x, gamma, beta):
            mu = jnp.mean(x, axis=-1, keepdims=True)
            var = jnp.mean((x - mu) ** 2, axis=-1, keepdims=True)
            return (x - mu) * jax.lax.rsqrt(var + EPS) * gamma + beta

        def apply_rope(t):
            S, d = (t.shape[-2], t.shape[-1])
            inv_freq = 1.0 / 10000.0 ** (jnp.arange(0, d, 2, dtype=jnp.float32) / d)
            angles = jnp.arange(S, dtype=jnp.float32)[:, None] * inv_freq[None, :]
            sin, cos = (jnp.sin(angles), jnp.cos(angles))
            tp = t.reshape(*t.shape[:-1], d // 2, 2)
            t0, t1 = (tp[..., 0], tp[..., 1])
            rot = jnp.stack([t0 * cos - t1 * sin, t0 * sin + t1 * cos], axis=-1)
            return rot.reshape(t.shape)
        B, S, d = x.shape
        H, hd = (NUM_HEADS, HEAD_DIM)
        x_norm = layer_norm(x, g1, beta1)
        q = (x_norm @ Wq + bq).reshape(B, S, H, hd).transpose(0, 2, 1, 3)
        k = (x_norm @ Wk + bk).reshape(B, S, H, hd).transpose(0, 2, 1, 3)
        v = (x_norm @ Wv + bv).reshape(B, S, H, hd).transpose(0, 2, 1, 3)
        q = apply_rope(q)
        k = apply_rope(k)
        q = q * (1.0 / jnp.sqrt(jnp.float32(hd)))
        scores = jnp.einsum('bhqd,bhkd->bhqk', q, k)
        attn = jax.nn.softmax(scores, axis=-1)
        out = jnp.einsum('bhqk,bhkd->bhqd', attn, v)
        out = out.transpose(0, 2, 1, 3).reshape(B, S, d)
        attn_out = out @ Wo + bo
        x = x + attn_out
        x_norm2 = layer_norm(x, g2, beta2)
        ffn = jax.nn.relu(x_norm2 @ W1 + b1) @ W2 + b2
        return x + ffn

    def _L1_ffn_ref(x, w1, conv_w, conv_b, w2):
        import jax, jax.numpy as jnp
        import numpy as np
        B, S, D_MODEL, D_HIDDEN = (4, 512, 256, 1024)

        def act_quant(x):
            scale = 127.0 / jnp.clip(jnp.max(jnp.abs(x), axis=-1, keepdims=True), 1e-05)
            return jnp.clip(jnp.round(x * scale), -128, 127) / scale

        def weight_quant(w):
            scale = 1.0 / jnp.clip(jnp.mean(jnp.abs(w)), 1e-05)
            return jnp.clip(jnp.round(w * scale), -1, 1) / scale

        def bit_linear(x, w):
            xq = x + jax.lax.stop_gradient(act_quant(x) - x)
            wq = w + jax.lax.stop_gradient(weight_quant(w) - w)
            return jnp.einsum('bsd,hd->bsh', xq, wq)

        def depthwise_conv1d(x_bcl, w, b):
            y = jax.lax.conv_general_dilated(x_bcl, w, window_strides=(1,), padding=[(1, 1)], dimension_numbers=('NCH', 'OIH', 'NCH'), feature_group_count=x_bcl.shape[1])
            return y + b[None, :, None]
        h = bit_linear(x, w1)
        h = depthwise_conv1d(h.transpose(0, 2, 1), conv_w, conv_b)
        h = h.transpose(0, 2, 1)
        h = jax.nn.silu(h)
        return bit_linear(h, w2)

    def _L2_attn_ref(x, q, k, log_decay, norm_weight, o_w):
        import jax, jax.numpy as jnp
        import numpy as np
        H = 16
        EPS = 1e-06
        b, n, dm = x.shape
        dh = dm // H
        qh = q.reshape(H, dh)
        kh = k.reshape(H, dh)
        v = x.reshape(b, n, H, dh)
        lam = jax.nn.sigmoid(log_decay)

        def step(S, v_t):
            S = lam[None, :, None, None] * S + kh[None, :, :, None] * v_t[:, :, None, :]
            o_t = jnp.einsum('hd,bhdv->bhv', qh, S)
            return (S, o_t)
        S0 = jnp.zeros((b, H, dh, dh), dtype=x.dtype)
        _, o = jax.lax.scan(step, S0, jnp.moveaxis(v, 1, 0))
        o = jnp.moveaxis(o, 0, 1).reshape(b, n, dm)
        o = o * jax.lax.rsqrt(jnp.mean(o * o, axis=-1, keepdims=True) + EPS) * norm_weight
        return o @ o_w.T

    def _L2_ffn_ref(x, gate_w, bias, W1, W3, W2, sw1, sw3, sw2):
        import jax, jax.numpy as jnp
        import numpy as np
        D = 256
        I = 128
        E = 32
        K = 4
        T = 2 * 512
        C = 2 * T * K // E
        X = x.reshape(-1, D)
        logits = (X @ gate_w.T).astype(jnp.float32)
        scores = jax.nn.sigmoid(logits)
        _, idx = jax.lax.top_k(scores + bias[None, :], K)
        w = jnp.take_along_axis(scores, idx, axis=-1)
        w = w / jnp.clip(jnp.sum(w, axis=-1, keepdims=True), 1e-12, None)
        w = w.astype(x.dtype)
        eid = idx.reshape(-1)
        onehot = (eid[:, None] == jnp.arange(E)[None, :]).astype(jnp.int32)
        pos = jnp.take_along_axis(jnp.cumsum(onehot, axis=0) - 1, eid[:, None], axis=1)[:, 0]
        valid = pos < C
        posc = jnp.minimum(pos, C - 1)
        Xrep = jnp.repeat(X, K, axis=0)
        xe = jnp.zeros((E, C, D), x.dtype).at[eid, posc].add(jnp.where(valid[:, None], Xrep, jnp.zeros((), x.dtype)))
        h = jax.nn.silu(jnp.einsum('ecd,edi->eci', xe, W1)) * jnp.einsum('ecd,edi->eci', xe, W3)
        ye = jnp.einsum('eci,eid->ecd', h, W2)
        gflat = jnp.where(valid, w.reshape(-1), jnp.zeros((), x.dtype))
        yrows = ye[eid, posc] * gflat[:, None]
        out = yrows.reshape(-1, K, D).sum(axis=1)
        out = out + jax.nn.silu(X @ sw1.T) * (X @ sw3.T) @ sw2.T
        return out.reshape(x.shape)

    def _L3_attn_ref(x, in_proj_w, in_proj_b, short_w, short_b, fw1, fb1, fw2, fb2, fw3, fb3, out_w, out_b):
        import jax, jax.numpy as jnp
        import numpy as np
        from jax import lax
        D_MODEL = 256
        SEQ_LEN = 2048
        ORDER = 2
        BATCH = 2

        def _hyena_fwd(x, in_proj_w, in_proj_b, short_w, short_b, fw1, fb1, fw2, fb2, fw3, fb3, out_w, out_b):
            B, L, C = x.shape
            proj = (x @ in_proj_w + in_proj_b).reshape(B, L, C, ORDER + 1)
            v = proj[..., 0]
            x_branches = [proj[..., i] for i in range(1, ORDER + 1)]
            vc = v.transpose(0, 2, 1)
            vc = lax.conv_general_dilated(vc, short_w, window_strides=(1,), padding=((1, 1),), feature_group_count=C, dimension_numbers=('NCH', 'OIH', 'NCH'))
            v = (vc + short_b[None, :, None]).transpose(0, 2, 1)
            pos = jnp.linspace(0.0, 1.0, L, dtype=x.dtype)[:, None]
            h = jax.nn.gelu(pos @ fw1 + fb1, approximate=False)
            h = jax.nn.gelu(h @ fw2 + fb2, approximate=False)
            coefs = (h @ fw3 + fb3).reshape(L, C, ORDER)
            n = 2 * L
            v_fft = jnp.fft.rfft(v, n=n, axis=1)
            output = v
            for i in range(ORDER):
                h_fft = jnp.fft.rfft(coefs[:, :, i], n=n, axis=0)
                conv = jnp.fft.irfft(v_fft * h_fft[None], n=n, axis=1)[:, :L, :]
                output = x_branches[i] * conv
            return output @ out_w + out_b
        return _hyena_fwd(x, in_proj_w, in_proj_b, short_w, short_b, fw1, fb1, fw2, fb2, fw3, fb3, out_w, out_b)

    def _L3_ffn_ref(inputs, gate_w, gate_b, expert_w, expert_b):
        import jax, jax.numpy as jnp
        import numpy as np
        THRESHOLD = 0.1
        d = inputs.shape[-1]
        x = inputs.reshape(-1, d)
        gate_logits = jax.nn.softmax(x @ gate_w + gate_b, axis=-1)
        selected = (gate_logits >= THRESHOLD).astype(x.dtype)
        weights = gate_logits * selected
        wsum = jnp.sum(weights, axis=-1, keepdims=True)
        weights = weights / jnp.where(wsum == 0, jnp.ones_like(wsum), wsum)
        E = expert_w.shape[0]
        out = jnp.zeros((x.shape[0], expert_w.shape[-1]), dtype=x.dtype)
        for e in range(E):
            out = out + weights[:, e:e + 1] * (x @ expert_w[e] + expert_b[e])
        return out.reshape(*inputs.shape[:-1], out.shape[-1])
    h = _L0_tok_ref(x, L0_tok_level_emb)
    h = h + _L0_attn_ref(_layernorm(h, axis=-1), L0_attn_query_mat, L0_attn_key_mat, L0_attn_value_mat, L0_attn_linear_m1)
    h = h + _L0_ffn_ref(_layernorm(h, axis=-1), L0_ffn_qw, L0_ffn_qb, L0_ffn_kw, L0_ffn_kb, L0_ffn_vw, L0_ffn_vb, L0_ffn_ow, L0_ffn_ob, L0_ffn_gate_w, L0_ffn_w1, L0_ffn_w2, L0_ffn_norm1_w, L0_ffn_norm2_w)
    h = h + _L1_attn_ref(_layernorm(h, axis=-1), L1_attn_Wq, L1_attn_bq, L1_attn_Wk, L1_attn_bk, L1_attn_Wv, L1_attn_bv, L1_attn_Wo, L1_attn_bo, L1_attn_W1, L1_attn_b1, L1_attn_W2, L1_attn_b2, L1_attn_g1, L1_attn_beta1, L1_attn_g2, L1_attn_beta2)
    h = h + _L1_ffn_ref(_layernorm(h, axis=-1), L1_ffn_w1, L1_ffn_conv_w, L1_ffn_conv_b, L1_ffn_w2)
    h = h + _L2_attn_ref(_layernorm(h, axis=-1), L2_attn_q, L2_attn_k, L2_attn_log_decay, L2_attn_norm_weight, L2_attn_o_w)
    h = h + _L2_ffn_ref(_layernorm(h, axis=-1), L2_ffn_gate_w, L2_ffn_bias, L2_ffn_W1, L2_ffn_W3, L2_ffn_W2, L2_ffn_sw1, L2_ffn_sw3, L2_ffn_sw2)
    h = h + _L3_attn_ref(_layernorm(h, axis=-1), L3_attn_in_proj_w, L3_attn_in_proj_b, L3_attn_short_w, L3_attn_short_b, L3_attn_fw1, L3_attn_fb1, L3_attn_fw2, L3_attn_fb2, L3_attn_fw3, L3_attn_fb3, L3_attn_out_w, L3_attn_out_b)
    h = h + _L3_ffn_ref(_layernorm(h, axis=-1), L3_ffn_gate_w, L3_ffn_gate_b, L3_ffn_expert_w, L3_ffn_expert_b)
    return h

_drawn_inputs = setup_inputs


def setup_inputs(seed=0):
    import zlib

    import numpy as np

    out = dict(_drawn_inputs(seed))
    spreads = {'L0_ffn_qb': (0.0, 0.8),
     'L0_ffn_kb': (0.0, 2.0),
     'L0_ffn_vb': (0.0, 0.478),
     'L0_ffn_ob': (0.0, 0.1),
     'L0_ffn_norm1_w': (1.0, 0.2),
     'L0_ffn_norm2_w': (1.0, 0.2),
     'L1_attn_bq': (0.0, 0.8),
     'L1_attn_bk': (0.0, 2.0),
     'L1_attn_bv': (0.0, 0.62),
     'L1_attn_bo': (0.0, 0.1),
     'L1_attn_b1': (0.0, 0.495),
     'L1_attn_b2': (0.0, 0.1),
     'L1_attn_g1': (1.0, 0.6),
     'L1_attn_beta1': (0.0, 0.8),
     'L1_attn_g2': (1.0, 0.6),
     'L1_attn_beta2': (0.0, 0.8),
     'L2_attn_norm_weight': (1.0, 0.6),
     'L2_ffn_bias': (0.0, 0.8),
     'L3_ffn_gate_b': (0.0, 2.0),
     'L3_ffn_expert_b': (0.0, 2.0)}
    factors = {'L0_ffn_qw': 8.0,
     'L0_ffn_kw': 8.0,
     'L0_ffn_gate_w': 2.705,
     'L1_attn_Wq': 8.0,
     'L1_attn_Wk': 8.0,
     'L2_ffn_gate_w': 8.0,
     'L2_ffn_W1': 8.0,
     'L2_ffn_W3': 8.0,
     'L2_ffn_W2': 8.0,
     'L2_ffn_sw1': 8.0,
     'L2_ffn_sw3': 8.0,
     'L2_ffn_sw2': 8.0,
     'L3_attn_in_proj_w': 2.675,
     'L3_attn_in_proj_b': 8.0,
     'L3_attn_short_b': 8.0,
     'L3_attn_fw1': 2.942,
     'L3_attn_fb1': 8.0,
     'L3_attn_fw2': 3.297,
     'L3_attn_fb2': 8.0,
     'L3_attn_fw3': 3.418,
     'L3_attn_fb3': 5.178,
     'L3_attn_out_w': 2.669,
     'L3_attn_out_b': 64.0,
     'L3_ffn_gate_w': 8.0,
     'L3_ffn_expert_w': 8.0}
    for name, (base, spread) in spreads.items():
        noise = np.random.default_rng([zlib.crc32(name.encode()), seed]).standard_normal(out[name].shape)
        drawn = base * np.exp(spread * noise) if base else spread * noise
        out[name] = jnp.asarray(drawn.astype(out[name].dtype))
    for name, factor in factors.items():
        out[name] = (out[name] * factor).astype(out[name].dtype)
    return out
```

```python
from contextlib import ExitStack

import numpy as np

import concourse.bass as bass
from concourse import mybir
from concourse.alu_op_type import AluOpType as ALU

ACT = mybir.ActivationFunctionType
F32 = mybir.dt.float32
BF16 = mybir.dt.bfloat16
I32 = mybir.dt.int32
U32 = mybir.dt.uint32
AX_X = mybir.AxisListType.X

B, S, D = 16, 128, 256
P = 128
TILES = B
KT = D // P
LANES = 2
HEADSTART = 16
CHUNK = 4
CHUNKS = TILES // CHUNK
HEADS, HD = 16, 16
LEVELS = 32
LN_EPS = 1e-5
RMS_EPS = 1e-6
BIG = 1e30
ROUND = 12582912.0

CONST_PARTS = [
    ("ident", P), ("causal", P), ("before", P), ("ones", P), ("iota", LEVELS),
    ("pairmask", 2), ("cos", D), ("sin", D), ("lag", P), ("dft_re", P), ("dft_im", P),
    ("dft_im0", P), ("dft_re1", P), ("inv_re", P), ("inv_im", P), ("edges", P), ("pos", P),
]
CONST_AT = {}
_n = 0
for _name, _width in CONST_PARTS:
    CONST_AT[_name] = (_n, _width)
    _n += _width
CONST_COLS = _n


def shape_constants():
    c = {}
    i = np.arange(P)
    c["ident"] = np.eye(P)
    c["causal"] = (i[:, None] <= i[None, :])
    c["before"] = (i[:, None] < i[None, :])
    c["ones"] = np.ones((P, P))
    c["iota"] = np.tile(np.arange(LEVELS), (P, 1))
    c["pairmask"] = (i[:, None] % 32) // 16 == np.arange(2)[None, :]
    inv_freq = (1.0 / np.float32(10000.0) ** (np.arange(0, HD, 2, dtype=np.float32) / np.float32(HD))).astype(np.float32)
    angle = (np.arange(S, dtype=np.float32)[:, None] * inv_freq[None, :]).astype(np.float64)
    cos, sin = np.repeat(np.cos(angle), 2, axis=1), np.repeat(np.sin(angle), 2, axis=1)
    sin[:, 0::2] *= -1.0
    c["cos"], c["sin"] = np.tile(cos, (1, HEADS)), np.tile(sin, (1, HEADS))
    c["lag"] = np.maximum(i[None, :] - i[:, None], 0)
    n = 2 * S
    w = 2 * np.pi * np.outer(i, i) / n
    re, im = np.cos(w), -np.sin(w)
    im0 = im.copy()
    im0[:, 0] = 0.0
    nyquist = np.cos(np.pi * i)
    packed = im.copy()
    packed[:, 0] = nyquist
    re1 = re.copy()
    re1[:, 0] = nyquist
    c["dft_re"], c["dft_im"], c["dft_im0"], c["dft_re1"] = re, packed, im0, re1
    both = np.where(i == 0, 1.0, 2.0)[:, None] / n
    c["inv_re"] = both * np.cos(w)
    inv_im = -2.0 / n * np.sin(w)
    inv_im[0] = nyquist / n
    c["inv_im"] = inv_im
    edges = np.ones((P, P))
    edges[0, 0] = 0.0
    edges[2, P - 1] = 0.0
    c["edges"] = edges
    c["pos"] = np.tile(np.linspace(0.0, 1.0, S, dtype=np.float32), (P, 1))
    return np.concatenate([np.asarray(c[name], np.float32) for name, _ in CONST_PARTS], axis=1)


SIGNALS = [
    "biased", "blocks", "clipped", "combined", "converted", "counts", "den", "diag", "expert_done",
    "first_tap", "hidden", "hidden_ps", "highest", "k_pair", "kept", "last_T", "last_rows",
    "last_turned", "level", "logits", "masked", "middle_tap", "moments", "moments_b", "moments_c",
    "normed", "o", "oT", "oT_ps", "onehot", "ones_set", "out", "pT", "pT_ps", "padded", "picked",
    "powers", "probs", "proj", "pv", "qT", "qk", "qkT_ps", "ranks", "recip", "rotated", "rounded",
    "rstd", "rstd_b", "rstd_c", "scaled", "scores", "shifted", "shifted_var", "shifted_var_b",
    "shifted_var_c", "silu", "squares", "stats", "stats_b", "stats_c", "stored", "taps", "top",
    "top_ps", "turned", "unit", "unit_ps", "v1", "weighed", "x", "x2", "xT", "xn", "y_ps",
]


class Signal:

    def __init__(self, sem):
        self.sem, self.base = sem, HEADSTART

    def nth(self, n):
        return n + (self.base + 1)

    def before(self, n):
        return n + (self.base + 1 - LANES)

    def advance(self, n):
        self.base += n


class Loads:

    def __init__(self, sem):
        self.sem, self.count = sem, 0

    def more(self, n=1):
        self.count += n

    def all(self):
        return 16 * self.count


def scratch(nc, ctx, phase):
    def sb(name, shape, dt=F32):
        return ctx.enter_context(nc.sbuf_tensor(f"{phase}_{name}", shape, dt))

    def ps(name, shape, dt=F32):
        return ctx.enter_context(nc.psum_tensor(f"{phase}_{name}", shape, dt))
    return sb, ps


def spread(ap, shape):
    return ap.broadcast_to(shape)


def transposes(nc, out, blocks, ident):
    last = None
    for o, x in zip(out, blocks):
        last = nc.tensor.transpose(o, x, ident[0:x.shape[0], 0:x.shape[0]])
    return last


def level_tables(nc, k):
    with ExitStack() as ctx:
        sb, ps = scratch(nc, ctx, "level_tables")
        tok = sb("tok", [B, S], I32)
        tokf = sb("tokf", [B, S])
        opens, closes = sb("opens", [B, S]), sb("closes", [B, S])
        depth, low, high = sb("depth", [B, S]), sb("low", [B, S]), sb("high", [B, S])
        level = sb("level", [B, S])
        emb = sb("emb", [LEVELS, D])
        stats, mom = sb("stats0", [LEVELS, 6]), sb("mom0", [LEVELS, 2])
        rstd = sb("rstd0", [LEVELS, 1])
        xn = sb("xn0", [LEVELS, D])
        xnT = sb("xnT0", [P, KT, LEVELS])
        qT = sb("qT0", [P, 8, LEVELS])
        k_pairs = sb("k_pairs", [P, 8, 2 * LEVELS])
        v_quads = sb("v_quads", [P, 4, 2, P])
        turned = ps("turned0", [P, 512])
        q_ps, k_ps, v_ps = (ps(n, [P, 8, LEVELS]) for n in ("q_ps", "k_ps", "v_ps"))
        s_ps = ps("s_ps", [LEVELS, 512])
        m_ps = ps("m_ps", [P, 4, D])
        wq, wk, wv, m1 = (k.region_a[:, n * 2048:(n + 1) * 2048] for n in range(4))
        split = lambda w: w.rearrange("p (t n) -> p t n", t=KT)
        wq, wk, wv = split(wq), split(wk), split(wv)
        m1 = m1.rearrange("p (t n) -> p t n", n=D)
        C, sig = k.const, k.sig

        with nc.Block() as block:
            @block.sync
            def _(sp):
                sp.dma_start(tok[:], k.dram["x"]).then_inc(k.load_small.sem, 16)
                sp.dma_start(emb[:], k.dram["L0_tok_level_emb"]).then_inc(k.load_small.sem, 16)
                sp.dma_start(k.const_sb[:], k.dram["constants"]).then_inc(k.load_small.sem, 16)
                for w, name in ((wq, "query"), (wk, "key"), (wv, "value")):
                    sp.dma_start(w, k.dram[f"L0_attn_{name}_mat"].rearrange("(t p) h d -> p t (h d)", p=P)
                                 ).then_inc(k.load_a.sem, 16)
                sp.dma_start(m1, k.dram["L0_attn_linear_m1"].rearrange("(t p) n -> p t n", p=P)
                             ).then_inc(k.load_a.sem, 16)
            k.load_small.more(3)
            k.load_a.more(4)

            @block.vector
            def _(dve):
                link = k.chain(dve)
                dve.wait_ge(k.load_small.sem, k.load_small.all())
                link(nc.vector.tensor_scalar(k.emb_rows[:], emb[:], 0.15, None, ALU.mult))
                link(nc.vector.bn_stats(stats[:], k.emb_rows[:]))
                nc.vector.bn_aggr(mom[:], stats[:]).then_inc(sig("moments").sem, 1)
                link(nc.vector.tensor_copy(tokf[:], tok[:]))
                for count, ids in ((opens, (40., 91., 123.)), (closes, (41., 93., 125.))):
                    link(nc.vector.tensor_scalar(count[:], tokf[:], ids[0], None, ALU.is_equal))
                    for one in ids[1:]:
                        link(nc.vector.scalar_tensor_tensor(count[:], tokf[:], one, count[:],
                                                            ALU.is_equal, ALU.add))
                link(nc.vector.tensor_tensor(opens[:], opens[:], closes[:], ALU.subtract))
                link(nc.vector.memset(closes[:], 0.0))
                link(nc.vector.tensor_tensor_scan(depth[:], opens[:], closes[:], 0.0, ALU.add, ALU.add))
                link(nc.vector.tensor_scalar(low[:], depth[:], -1.0, None, ALU.mult))
                link(nc.vector.tensor_scalar(high[:], low[:], float(LEVELS - 1), None, ALU.add))
                link(nc.vector.tensor_tensor_scan(level[:], high[:], low[:], 0.0, ALU.min, ALU.max))
                nc.vector.tensor_tensor(level[:], level[:], depth[:], ALU.add).then_inc(sig("level").sem, 1)
                nc.vector.memset(k_pairs[:], 0.0)
                link(nc.vector.memset(v_quads[:], 0.0))
                dve.wait_ge(sig("rstd").sem, sig("rstd").nth(0))
                nc.vector.tensor_scalar(xn[:], k.emb_rows[:], mom[:, 0:1], rstd[:, 0:1], ALU.subtract,
                                        ALU.mult).then_inc(sig("xn").sem, 1)
                dve.wait_ge(sig("xT").sem, sig("xT").nth(0))
                nc.vector.tensor_copy(k.level_cols[:], turned[:, 256:256 + B])
                dve.wait_ge(sig("proj").sem, sig("proj").nth(0))
                kp = k_ps[:]
                vp = v_ps[:].rearrange("p (c u) l -> p c u l", u=2)
                for j in range(2):
                    rows = slice(64 * j, 64 * j + 64)
                    nc.vector.tensor_copy(k_pairs[rows, :, LEVELS * j:LEVELS * (j + 1)], kp[rows])
                    for u in range(2):
                        at = LEVELS * (2 * u + j)
                        last = nc.vector.tensor_copy(v_quads[rows, :, u, at:at + LEVELS], vp[rows, :, u, :])
                last.then_inc(sig("blocks").sem, 1)
                dve.wait_ge(sig("out").sem, sig("out").nth(0))
                nc.vector.tensor_copy(k.value_rows[:], m_ps[:])

            @block.gpsimd
            def _(pool):
                nc.gpsimd.memset(k.minus_half[:], -0.5)
                nc.gpsimd.memset(k.eps_ln[:], LN_EPS)
                nc.gpsimd.memset(k.eps_rms[:], RMS_EPS)
                pool.wait_ge(sig("moments").sem, sig("moments").nth(0))
                rsqrt(nc, pool, k, rstd[:], mom[:, 1:2], 1.0, LN_EPS, 0).then_inc(sig("rstd").sem, 1)

            @block.tensor
            def _(pe):
                pe.wait_ge(k.load_small.sem, k.load_small.all())
                pe.wait_ge(sig("level").sem, sig("level").nth(0))
                nc.tensor.transpose(turned[:, 256:256 + B], level[:], C("ident")[0:B, 0:B])
                pe.wait_ge(sig("xn").sem, sig("xn").nth(0))
                for t in range(KT):
                    last = nc.tensor.transpose(turned[:, LEVELS * t:LEVELS * (t + 1)], xn[:, P * t:P * (t + 1)],
                                               C("ident")[0:LEVELS, 0:LEVELS])
                last.then_inc(sig("turned").sem, 1)
                pe.wait_ge(k.load_a.sem, k.load_a.all())
                pe.wait_ge(sig("xT").sem, sig("xT").nth(0))
                for w, o in ((wq, q_ps), (wk, k_ps), (wv, v_ps)):
                    for m in range(8):
                        for t in range(KT):
                            last = nc.tensor.matmul(o[:, m, :], w[:, t, P * m:P * (m + 1)], xnT[:, t, :],
                                                    start=(t == 0), stop=(t == KT - 1))
                last.then_inc(sig("proj").sem, 1)
                pe.wait_ge(sig("blocks").sem, sig("blocks").nth(0))
                pe.wait_ge(sig("qk").sem, sig("qk").nth(0))
                for m in range(8):
                    last = nc.tensor.matmul(s_ps[:, 64 * m:64 * m + 64], qT[:, m, :], k_pairs[:, m, :],
                                            start=True, stop=True)
                last.then_inc(sig("scores").sem, 1)
                for c in range(4):
                    for u in range(2):
                        last = nc.tensor.matmul(m_ps[:, c, :], v_quads[:, c, u, :], m1[:, 2 * c + u, :],
                                                start=(u == 0), stop=(u == 1))
                last.then_inc(sig("out").sem, 1)

            @block.scalar
            def _(act):
                act.wait_ge(sig("turned").sem, sig("turned").nth(0))
                nc.scalar.copy(xnT[:], turned[:, 0:KT * LEVELS].rearrange("p (t l) -> p t l", t=KT)
                               ).then_inc(sig("xT").sem, 1)
                act.wait_ge(sig("proj").sem, sig("proj").nth(0))
                nc.scalar.mul(qT[:], q_ps[:], 8.0).then_inc(sig("qk").sem, 1)
                act.wait_ge(sig("scores").sem, sig("scores").nth(0))
                nc.scalar.copy(k.score_rows[:], s_ps[:])
        for name in ("moments", "level", "shifted_var", "rstd", "xn", "turned", "xT", "proj", "blocks", "qk", "scores", "out"):
            sig(name).advance(1)


def rsqrt(nc, pool, k, out, in_, scale, eps, t):
    nc.gpsimd.tensor_scalar(out, in_, scale, eps, ALU.mult, ALU.add).then_inc(k.sig("shifted_var").sem, 1)
    pool.wait_ge(k.sig("shifted_var").sem, k.sig("shifted_var").nth(t))
    return nc.gpsimd.tensor_tensor(out, out, spread(k.minus_half[0:out.shape[0], 0:1], out.shape), ALU.pow)


def level_attention(nc, k):
    with ExitStack() as ctx:
        sb, ps = scratch(nc, ctx, "level_attention")
        onehot = sb("onehot", [P, LANES, LEVELS])
        onehotT = sb("onehotT", [LEVELS, LANES, P])
        count = sb("count", [P, LANES, LEVELS])
        absent = sb("absent", [P, LANES, LEVELS])
        w = sb("weights", [P, LANES, HEADS, LEVELS])
        top, den = sb("top", [P, LANES, HEADS]), sb("den", [P, LANES, HEADS])
        wT = sb("wT", [P, LANES, 4, P])
        small_ps = [ps(f"small_ps{i}", [P, 512]) for i in range(LANES)]
        score_ps = [ps(f"score_ps{i}", [P, HEADS, LEVELS]) for i in range(LANES)]
        turn_ps = [ps(f"turn_ps{i}", [P, 4, P]) for i in range(LANES)]
        C, sig = k.const, k.sig
        names = ("onehot", "turned", "xT", "counts", "scores", "masked", "top", "shifted", "probs",
                 "weighed", "den", "recip", "normed", "pT_ps", "pT", "out", "stored")

        def each(eng):
            return eng.Fori(0, TILES // LANES)

        with nc.Block() as block:
            @block.vector
            def _(dve):
                with each(dve) as i:
                    lanes = [(n, i * LANES + n) for n in range(LANES)]
                    for n, t in lanes:
                        dve.wait_ge(sig("stored").sem, sig("stored").before(t))
                        nc.vector.tensor_scalar(onehot[:, n, :], C("iota"), k.level_cols[:, bass.ds(t, 1)], None,
                                                ALU.is_equal).then_inc(sig("onehot").sem, 1)
                    for n, t in lanes:
                        dve.wait_ge(sig("xT").sem, sig("xT").nth(t))
                        nc.vector.tensor_copy(count[:, n, :], small_ps[n][:, P:P + LEVELS])
                        nc.vector.tensor_scalar(absent[:, n, :], small_ps[n][:, P:P + LEVELS], 0.0, -BIG,
                                                ALU.is_equal, ALU.mult).then_inc(sig("counts").sem, 1)
                    for n, t in lanes:
                        dve.wait_ge(sig("scores").sem, sig("scores").nth(t))
                        dve.wait_ge(sig("counts").sem, sig("counts").nth(t))
                        nc.vector.tensor_tensor(w[:, n], score_ps[n][:],
                                                spread(absent[:, n, :].unsqueeze(1), [P, HEADS, LEVELS]),
                                                ALU.add).then_inc(sig("masked").sem, 1)
                    for n, t in lanes:
                        dve.wait_ge(sig("masked").sem, sig("masked").nth(t))
                        nc.vector.tensor_reduce(top[:, n, :], w[:, n], AX_X, ALU.max).then_inc(sig("top").sem, 1)
                    for n, t in lanes:
                        dve.wait_ge(sig("top").sem, sig("top").nth(t))
                        nc.vector.tensor_tensor(w[:, n], w[:, n],
                                                spread(top[:, n, :].unsqueeze(2), [P, HEADS, LEVELS]),
                                                ALU.subtract).then_inc(sig("shifted").sem, 1)
                    for n, t in lanes:
                        dve.wait_ge(sig("probs").sem, sig("probs").nth(t))
                        nc.vector.tensor_tensor(w[:, n], w[:, n],
                                                spread(count[:, n, :].unsqueeze(1), [P, HEADS, LEVELS]),
                                                ALU.mult).then_inc(sig("weighed").sem, 1)
                    for n, t in lanes:
                        dve.wait_ge(sig("weighed").sem, sig("weighed").nth(t))
                        nc.vector.tensor_reduce(den[:, n, :], w[:, n], AX_X, ALU.add).then_inc(sig("den").sem, 1)
                    for n, t in lanes:
                        dve.wait_ge(sig("den").sem, sig("den").nth(t))
                        nc.vector.reciprocal(top[:, n, :], den[:, n, :]).then_inc(sig("recip").sem, 1)
                    for n, t in lanes:
                        dve.wait_ge(sig("recip").sem, sig("recip").nth(t))
                        nc.vector.tensor_tensor(w[:, n], w[:, n],
                                                spread(top[:, n, :].unsqueeze(2), [P, HEADS, LEVELS]),
                                                ALU.mult).then_inc(sig("normed").sem, 1)

            @block.tensor
            def _(pe):
                with each(pe) as i:
                    lanes = [(n, i * LANES + n) for n in range(LANES)]
                    for n, t in lanes:
                        pe.wait_ge(sig("onehot").sem, sig("onehot").nth(t))
                        nc.tensor.transpose(small_ps[n][0:LEVELS, 0:P], onehot[:, n, :], C("ident"))
                        nc.tensor.matmul(small_ps[n][:, P:P + LEVELS], C("causal"), onehot[:, n, :], start=True,
                                         stop=True).then_inc(sig("turned").sem, 1)
                    for n, t in lanes:
                        pe.wait_ge(sig("xT").sem, sig("xT").nth(t))
                        nc.tensor.matmul(score_ps[n][:].rearrange("p h l -> p (h l)"), onehotT[:, n, :],
                                         k.score_rows[:], start=True, stop=True).then_inc(sig("scores").sem, 1)
                    for n, t in lanes:
                        pe.wait_ge(sig("normed").sem, sig("normed").nth(t))
                        for c in range(4):
                            last = nc.tensor.transpose(turn_ps[n][:, c, :], w[:, n, 4 * c:4 * c + 4, :].rearrange(
                                "p h l -> p (h l)"), C("ident"))
                        last.then_inc(sig("pT_ps").sem, 1)
                    for n, t in lanes:
                        out = small_ps[n][:, 256:512]
                        nc.tensor.matmul(out, onehotT[:, n, :], k.emb_rows[:], start=True, stop=False)
                        pe.wait_ge(sig("pT").sem, sig("pT").nth(t))
                        for c in range(4):
                            last = nc.tensor.matmul(out, wT[:, n, c, :], k.value_rows[:, c, :], start=False,
                                                    stop=(c == 3))
                        last.then_inc(sig("out").sem, 1)

            @block.scalar
            def _(act):
                with each(act) as i:
                    lanes = [(n, i * LANES + n) for n in range(LANES)]
                    for n, t in lanes:
                        act.wait_ge(sig("turned").sem, sig("turned").nth(t))
                        nc.scalar.copy(onehotT[:, n, :], small_ps[n][0:LEVELS, 0:P]).then_inc(sig("xT").sem, 1)
                    for n, t in lanes:
                        act.wait_ge(sig("shifted").sem, sig("shifted").nth(t))
                        nc.scalar.activation(w[:, n], w[:, n], ACT.Exp).then_inc(sig("probs").sem, 1)
                    for n, t in lanes:
                        act.wait_ge(sig("pT_ps").sem, sig("pT_ps").nth(t))
                        nc.scalar.copy(wT[:, n], turn_ps[n][:]).then_inc(sig("pT").sem, 1)
                    for n, t in lanes:
                        act.wait_ge(sig("out").sem, sig("out").nth(t))
                        nc.scalar.copy(k.h[:, t, :], small_ps[n][:, 256:512]).then_inc(sig("stored").sem, 1)

            @block.sync
            def _(sp):
                load_gqa(k, sp)
        for name in names:
            sig(name).advance(TILES)


def attention_weights(region):
    at = {"wqk": (0, 1024), "wv": (1024, 512), "wo": (1536, 512), "bqk": (2048, 512), "bv": (2560, 256),
          "bo": (2816, 256), "row": (3072, 256), "gate": (3328, 16), "k_raw": (3344, 128), "v_raw": (3472, 128),
          "kb_raw": (3600, 64), "vb_raw": (3664, 64), "g1": (3744, 2), "beta1": (3746, 2), "g2": (3748, 2),
          "beta2": (3750, 2), "b1": (3752, 8)}
    w = {name: region[:, a:a + n] for name, (a, n) in at.items()}
    for name in ("wqk", "wv", "wo", "gate", "k_raw", "v_raw"):
        w[name] = w[name].rearrange("p (t n) -> p t n", t=KT)
    for name in ("bqk", "bv", "bo", "kb_raw", "vb_raw"):
        w[name] = w[name][0:1]
    return w


def by_rows(ap):
    return ap.rearrange("(t p) n -> p t n", p=P)


def as_row(ap):
    return ap.rearrange("(a n) -> a n", a=1)


def as_columns(ap):
    return ap.rearrange("(t p) -> p t", p=P)


def to_all(ap):
    return ap.partition_broadcast(P)


def load_gqa(k, sp):
    w, d = attention_weights(k.region_b), k.dram
    pairs = [
        (w["wqk"][:, :, 0:D], by_rows(d["L0_ffn_qw"])), (w["k_raw"], by_rows(d["L0_ffn_kw"])),
        (w["v_raw"], by_rows(d["L0_ffn_vw"])), (w["wo"], by_rows(d["L0_ffn_ow"])),
        (w["gate"], by_rows(d["L0_ffn_gate_w"])), (w["bqk"][:, 0:D], as_row(d["L0_ffn_qb"])),
        (w["kb_raw"], as_row(d["L0_ffn_kb"])), (w["vb_raw"], as_row(d["L0_ffn_vb"])),
        (w["bo"], as_row(d["L0_ffn_ob"])), (w["row"], to_all(d["L0_ffn_norm1_w"])),
    ]
    for to, source in pairs:
        sp.dma_start(to, source).then_inc(k.load_b.sem, 16)
    k.load_b.more(len(pairs))


def load_mha(k, sp):
    w, d = attention_weights(k.region_a), k.dram
    pairs = [
        (w["wqk"][:, :, 0:D], by_rows(d["L1_attn_Wq"])), (w["wqk"][:, :, D:2 * D], by_rows(d["L1_attn_Wk"])),
        (w["wv"], by_rows(d["L1_attn_Wv"])), (w["wo"], by_rows(d["L1_attn_Wo"])),
        (w["bqk"][:, 0:D], as_row(d["L1_attn_bq"])), (w["bqk"][:, D:2 * D], as_row(d["L1_attn_bk"])),
        (w["bv"], as_row(d["L1_attn_bv"])), (w["bo"], as_row(d["L1_attn_bo"])),
        (w["row"], to_all(d["L1_attn_b2"])), (w["g1"], as_columns(d["L1_attn_g1"])),
        (w["beta1"], as_columns(d["L1_attn_beta1"])), (w["g2"], as_columns(d["L1_attn_g2"])),
        (w["beta2"], as_columns(d["L1_attn_beta2"])), (w["b1"], as_columns(d["L1_attn_b1"])),
    ]
    for to, source in pairs:
        sp.dma_start(to, source, allow_slow_non_contiguous=True).then_inc(k.load_a.sem, 16)
    k.load_a.more(len(pairs))


def repeat_heads(nc, k):
    w = attention_weights(k.region_b)
    r4 = lambda ap: ap.rearrange("p (g r d) -> p g r d", g=4, r=4)
    with nc.Block() as block:
        @block.gpsimd
        def _(pool):
            pool.wait_ge(k.load_b.sem, k.load_b.all())
            for to, raw in ((w["wqk"][:, 0, D:], w["k_raw"][:, 0, :]), (w["wqk"][:, 1, D:], w["k_raw"][:, 1, :]),
                            (w["wv"][:, 0, :], w["v_raw"][:, 0, :]), (w["wv"][:, 1, :], w["v_raw"][:, 1, :]),
                            (w["bqk"][:, D:], w["kb_raw"]), (w["bv"], w["vb_raw"])):
                n = raw.shape[0]
                nc.gpsimd.tensor_copy(r4(to), spread(raw.rearrange("p (g d) -> p g d", g=4).unsqueeze(2),
                                                     [n, 4, 4, HD]))


def self_attention(nc, k, rope):
    w = attention_weights(k.region_a if rope else k.region_b)
    loads = k.load_a if rope else k.load_b
    with ExitStack() as ctx:
        sb, ps = scratch(nc, ctx, ("mha" if rope else "gqa"))
        stats, mom = sb("stats", [P, LANES, 6]), sb("mom", [P, LANES, 2])
        rstd = sb("rstd", [P, LANES, 1])
        x = sb("x_rows", [P, LANES, D])
        xn = sb("xn", [P, LANES, D]) if rope else x
        xT = sb("x_turned", [P, LANES, KT, P])
        qk = sb("qk", [P, LANES, 2, D])
        swapped = sb("qk_swapped", [P, LANES, 2, D]) if rope else None
        v1 = sb("v_and_one", [P, LANES, HEADS, HD + 1])
        qT = sb("qT", [P, LANES, KT, P])
        k_pair = sb("k_pair", [P, LANES, KT, 2, P])
        e = sb("e", [P, LANES, HEADS, P])
        top, den = sb("top", [P, LANES, HEADS]), sb("den", [P, LANES, HEADS])
        o = sb("o", [P, LANES, D])
        oT = sb("oT", [P, LANES, KT, P])
        last_rows = sb("last_rows", [P, LANES, D])
        score_ps = ps("score_ps", [P, 4, KT, 2, P])
        a_ps = [ps(f"a_ps{n}", [P, 512]) for n in range(LANES)]
        b_ps = [ps(f"b_ps{n}", [P, 512]) for n in range(LANES)]
        C, sig = k.const, k.sig
        turn = lambda bank: bank[:, 0:D].rearrange("p (t n) -> p t n", t=KT)

        def each(eng):
            return eng.Fori(0, TILES // LANES)

        def lanes(i):
            return [(n, i * LANES + n) for n in range(LANES)]

        with nc.Block() as block:
            @block.vector
            def _(dve):
                dve.wait_ge(loads.sem, loads.all())
                nc.vector.memset(v1[:], 1.0).then_inc(sig("ones_set").sem, 1)
                with each(dve) as i:
                    for n, t in lanes(i):
                        dve.wait_ge(sig("stored").sem, sig("stored").before(t))
                        dve.wait_ge(sig("kept").sem, sig("kept").before(t))
                        nc.vector.bn_stats(stats[:, n], k.h[:, t, :]).then_inc(sig("stats").sem, 1)
                    for n, t in lanes(i):
                        dve.wait_ge(sig("stats").sem, sig("stats").nth(t))
                        nc.vector.memset(k.idle[:, n:n + 1], 0.0)
                        nc.vector.bn_aggr(mom[:, n], stats[:, n]).then_inc(sig("moments").sem, 1)
                    for n, t in lanes(i):
                        dve.wait_ge(sig("rstd").sem, sig("rstd").nth(t))
                        nc.vector.tensor_scalar(x[:, n], k.h[:, t, :], mom[:, n, 0:1], rstd[:, n], ALU.subtract,
                                                ALU.mult).then_inc(sig("x").sem, 1)
                    if rope:
                        for n, t in lanes(i):
                            dve.wait_ge(sig("x").sem, sig("x").nth(t))
                            nc.vector.bn_stats(stats[:, n], x[:, n]).then_inc(sig("stats_b").sem, 1)
                        for n, t in lanes(i):
                            dve.wait_ge(sig("stats_b").sem, sig("stats_b").nth(t))
                            nc.vector.memset(k.idle[:, n:n + 1], 0.0)
                            nc.vector.bn_aggr(mom[:, n], stats[:, n]).then_inc(sig("moments_b").sem, 1)
                        for n, t in lanes(i):
                            dve.wait_ge(sig("rstd_b").sem, sig("rstd_b").nth(t))
                            nc.vector.tensor_scalar(xn[:, n], x[:, n], mom[:, n, 0:1], rstd[:, n], ALU.subtract,
                                                    ALU.mult).then_inc(sig("xn").sem, 1)
                        for n, t in lanes(i):
                            dve.wait_ge(sig("proj").sem, sig("proj").nth(t))
                            pairs = a_ps[n][:].rearrange("p (s f two) -> p s f two", s=2, two=2)
                            nc.vector.tensor_tensor(qk[:, n], a_ps[n][:].rearrange("p (s f) -> p s f", s=2),
                                                    spread(C("cos").unsqueeze(1), [P, 2, D]), ALU.mult)
                            for s in range(2):
                                last = nc.vector.tensor_tensor(
                                    swapped[:, n, s].rearrange("p (f two) -> p f two", two=2),
                                    pairs[:, s, :, ::-1], C("sin").rearrange("p (f two) -> p f two", two=2),
                                    ALU.mult)
                            last.then_inc(sig("rotated").sem, 1)
                    for n, t in lanes(i):
                        dve.wait_ge(sig("qT").sem, sig("qT").nth(t))
                        for f in range(KT):
                            last = nc.vector.tensor_tensor(
                                k_pair[:, n, f], spread(a_ps[n][:, P * (KT + f):P * (KT + f + 1)].unsqueeze(1), [P, 2, P]),
                                spread(C("pairmask").unsqueeze(2), [P, 2, P]), ALU.mult)
                        last.then_inc(sig("k_pair").sem, 1)
                    for n, t in lanes(i):
                        dve.wait_ge(sig("scores").sem, sig("scores").nth(t))
                        all_heads = score_ps[:].rearrange("p g f j z -> p (g f j) z")
                        nc.vector.tensor_reduce(top[:, n], all_heads, AX_X, ALU.max).then_inc(sig("top").sem, 1)
                        dve.wait_ge(sig("top").sem, sig("top").nth(t))
                        nc.vector.tensor_tensor(e[:, n], all_heads, spread(top[:, n].unsqueeze(2), [P, HEADS, P]),
                                                ALU.subtract).then_inc(sig("shifted").sem, 1)
                    for n, t in lanes(i):
                        dve.wait_ge(sig("pv").sem, sig("pv").nth(t))
                        heads = a_ps[n][:, 0:HEADS * (HD + 1)].rearrange("p (h d) -> p h d", h=HEADS)
                        nc.vector.reciprocal(den[:, n], heads[:, :, HD]).then_inc(sig("recip").sem, 1)
                        dve.wait_ge(sig("recip").sem, sig("recip").nth(t))
                        nc.vector.tensor_tensor(o[:, n].rearrange("p (h d) -> p h d", h=HEADS), heads[:, :, 0:HD],
                                                spread(den[:, n].unsqueeze(2), [P, HEADS, HD]),
                                                ALU.mult).then_inc(sig("o").sem, 1)
                    for n, t in lanes(i):
                        dve.wait_ge(sig("out").sem, sig("out").nth(t))
                        nc.vector.tensor_tensor(x[:, n], a_ps[n][:, 0:D], x[:, n], ALU.add).then_inc(sig("x2").sem, 1)
                    if rope:
                        for n, t in lanes(i):
                            dve.wait_ge(sig("x2").sem, sig("x2").nth(t))
                            nc.vector.bn_stats(stats[:, n], x[:, n]).then_inc(sig("stats_c").sem, 1)
                        for n, t in lanes(i):
                            dve.wait_ge(sig("stats_c").sem, sig("stats_c").nth(t))
                            nc.vector.memset(k.idle[:, n:n + 1], 0.0)
                            nc.vector.bn_aggr(mom[:, n], stats[:, n]).then_inc(sig("moments_c").sem, 1)
                        for n, t in lanes(i):
                            dve.wait_ge(sig("rstd_c").sem, sig("rstd_c").nth(t))
                            nc.vector.tensor_scalar(last_rows[:, n], x[:, n], mom[:, n, 0:1], rstd[:, n],
                                                    ALU.subtract, ALU.mult).then_inc(sig("last_rows").sem, 1)
                    else:
                        for n, t in lanes(i):
                            dve.wait_ge(sig("rstd_c").sem, sig("rstd_c").nth(t))
                            nc.vector.scalar_tensor_tensor(last_rows[:, n], x[:, n], rstd[:, n], w["row"], ALU.mult,
                                                           ALU.mult).then_inc(sig("last_rows").sem, 1)

            @block.gpsimd
            def _(pool):
                pool.wait_ge(loads.sem, loads.all())
                with each(pool) as i:
                    for n, t in lanes(i):
                        pool.wait_ge(sig("moments").sem, sig("moments").nth(t))
                        nc.gpsimd.tensor_tensor(rstd[:, n], mom[:, n, 1:2], k.eps_ln[:], ALU.add).then_inc(sig("shifted_var").sem, 1)
                        pool.wait_ge(sig("shifted_var").sem, sig("shifted_var").nth(t))
                        nc.gpsimd.tensor_tensor(rstd[:, n], rstd[:, n], k.minus_half[:],
                                                ALU.pow).then_inc(sig("rstd").sem, 1)
                    if rope:
                        for n, t in lanes(i):
                            pool.wait_ge(sig("moments_b").sem, sig("moments_b").nth(t))
                            nc.gpsimd.tensor_tensor(rstd[:, n], mom[:, n, 1:2], k.eps_ln[:], ALU.add).then_inc(sig("shifted_var_b").sem, 1)
                            pool.wait_ge(sig("shifted_var_b").sem, sig("shifted_var_b").nth(t))
                            nc.gpsimd.tensor_tensor(rstd[:, n], rstd[:, n], k.minus_half[:],
                                                    ALU.pow).then_inc(sig("rstd_b").sem, 1)
                        for n, t in lanes(i):
                            pool.wait_ge(sig("rotated").sem, sig("rotated").nth(t))
                            nc.gpsimd.tensor_tensor(qk[:, n], qk[:, n], swapped[:, n],
                                                    ALU.add).then_inc(sig("qk").sem, 1)
                    for n, t in lanes(i):
                        if rope:
                            pool.wait_ge(sig("moments_c").sem, sig("moments_c").nth(t))
                        else:
                            pool.wait_ge(sig("squares").sem, sig("squares").nth(t))
                        nc.gpsimd.tensor_tensor(rstd[:, n], mom[:, n, 1:2], (k.eps_ln if rope else k.eps_rms)[:],
                                                ALU.add).then_inc(sig("shifted_var_c").sem, 1)
                        pool.wait_ge(sig("shifted_var_c").sem, sig("shifted_var_c").nth(t))
                        nc.gpsimd.tensor_tensor(rstd[:, n], rstd[:, n], k.minus_half[:],
                                                ALU.pow).then_inc(sig("rstd_c").sem, 1)
                    for n, t in lanes(i):
                        pool.wait_ge(sig("last_rows").sem, sig("last_rows").nth(t))
                        if rope:
                            nc.gpsimd.tensor_tensor(o[:, n], x[:, n], w["row"], ALU.add
                                                    ).then_inc(sig("biased").sem, 1)
                            pool.wait_ge(sig("biased").sem, sig("biased").nth(t))
                            nc.gpsimd.tensor_tensor(k.h[:, t, :], k.h[:, t, :], o[:, n],
                                                    ALU.add).then_inc(sig("kept").sem, 1)
                        else:
                            nc.gpsimd.tensor_copy(k.rows[:, t, :], last_rows[:, n]).then_inc(sig("kept").sem, 1)

            @block.tensor
            def _(pe):
                pe.wait_ge(loads.sem, loads.all())
                with each(pe) as i:
                    for n, t in lanes(i):
                        ready = sig("xn") if rope else sig("x")
                        pe.wait_ge(ready.sem, ready.nth(t))
                        for f in range(KT):
                            last = nc.tensor.transpose(turn(a_ps[n])[:, f], xn[:, n, P * f:P * (f + 1)], C("ident"))
                        last.then_inc(sig("turned").sem, 1)
                    for n, t in lanes(i):
                        pe.wait_ge(sig("xT").sem, sig("xT").nth(t))
                        for bank, width, name, bias in ((a_ps[n], 2 * D, "wqk", "bqk"), (b_ps[n], D, "wv", "bv")):
                            nc.tensor.matmul(bank[:, 0:width], C("ones")[0:1, :], w[bias], start=True, stop=False)
                            for f in range(KT):
                                last = nc.tensor.matmul(bank[:, 0:width], xT[:, n, f], w[name][:, f, :],
                                                        start=False, stop=(f == KT - 1))
                        last.then_inc(sig("proj").sem, 1)
                    for n, t in lanes(i):
                        pe.wait_ge(sig("qk").sem, sig("qk").nth(t))
                        for f in range(2 * KT):
                            last = nc.tensor.transpose(a_ps[n][:, P * f:P * (f + 1)],
                                                       qk[:, n, f // KT, P * (f % KT):P * (f % KT + 1)], C("ident"))
                        last.then_inc(sig("qkT_ps").sem, 1)
                    for n, t in lanes(i):
                        pe.wait_ge(sig("k_pair").sem, sig("k_pair").nth(t))
                        pe.wait_ge(sig("shifted").sem, sig("shifted").nth(t - 1))
                        for f in range(KT):
                            for g in range(4):
                                rows = slice(32 * g, 32 * g + 32)
                                last = nc.tensor.matmul(score_ps[:, g, f].rearrange("p j z -> p (j z)"),
                                                        qT[rows, n, f, :],
                                                        k_pair[rows, n, f].rearrange("p j z -> p (j z)"),
                                                        start=True, stop=True)
                        last.then_inc(sig("scores").sem, 1)
                    for r in range(4):
                        for n, t in lanes(i):
                            if r == 0:
                                pe.wait_ge(sig("probs").sem, sig("probs").nth(t))
                            else:
                                pe.wait_ge(sig("pT").sem, sig("pT").nth(i * 4 * LANES + (r - 1) * LANES + n))
                            bank = (a_ps, b_ps)[r % 2][n]
                            for m in range(4):
                                last = nc.tensor.transpose(bank[:, P * m:P * (m + 1)], e[:, n, 4 * r + m, :],
                                                           C("ident"))
                            last.then_inc(sig("pT_ps").sem, 1)
                    for n, t in lanes(i):
                        pe.wait_ge(sig("pT").sem, sig("pT").nth(i * 4 * LANES + 3 * LANES + n))
                        for m in range(HEADS):
                            g, f, j = m // 4, m // 2 % 2, m % 2
                            head = 8 * f + 2 * g + j
                            last = nc.tensor.matmul(a_ps[n][:, head * (HD + 1):(head + 1) * (HD + 1)], e[:, n, m, :],
                                                    v1[:, n, head, :], start=True, stop=True)
                        last.then_inc(sig("pv").sem, 1)
                    for n, t in lanes(i):
                        pe.wait_ge(sig("o").sem, sig("o").nth(t))
                        for f in range(KT):
                            last = nc.tensor.transpose(turn(b_ps[n])[:, f], o[:, n, P * f:P * (f + 1)], C("ident"))
                        last.then_inc(sig("oT_ps").sem, 1)
                    for n, t in lanes(i):
                        pe.wait_ge(sig("oT").sem, sig("oT").nth(t))
                        nc.tensor.matmul(a_ps[n][:, 0:D], C("ones")[0:1, :], w["bo"], start=True, stop=False)
                        for f in range(KT):
                            last = nc.tensor.matmul(a_ps[n][:, 0:D], oT[:, n, f], w["wo"][:, f, :], start=False,
                                                    stop=(f == KT - 1))
                        last.then_inc(sig("out").sem, 1)
                    for n, t in lanes(i):
                        pe.wait_ge(sig("last_rows").sem, sig("last_rows").nth(t))
                        for f in range(KT):
                            last = nc.tensor.transpose(turn(b_ps[n])[:, f], last_rows[:, n, P * f:P * (f + 1)],
                                                       C("ident"))
                        last.then_inc(sig("last_turned").sem, 1)
                    if not rope:
                        for n, t in lanes(i):
                            pe.wait_ge(sig("last_T").sem, sig("last_T").nth(t))
                            for f in range(KT):
                                last = nc.tensor.matmul(b_ps[n][:, 0:8], xT[:, n, f], w["gate"][:, f, :],
                                                        start=(f == 0), stop=(f == KT - 1))
                            last.then_inc(sig("logits").sem, 1)

            @block.scalar
            def _(act):
                act.wait_ge(loads.sem, loads.all())
                act.wait_ge(sig("ones_set").sem, sig("ones_set").nth(0))
                with each(act) as i:
                    for n, t in lanes(i):
                        act.wait_ge(sig("turned").sem, sig("turned").nth(t))
                        if rope:
                            for f in range(KT):
                                last = nc.scalar.activation(xT[:, n, f], turn(a_ps[n])[:, f], ACT.Identity,
                                                            bias=w["beta1"][:, f:f + 1], scale=w["g1"][:, f:f + 1])
                            last.then_inc(sig("xT").sem, 1)
                        else:
                            nc.scalar.copy(xT[:, n], turn(a_ps[n])).then_inc(sig("xT").sem, 1)
                    for n, t in lanes(i):
                        act.wait_ge(sig("proj").sem, sig("proj").nth(t))
                        if not rope:
                            nc.scalar.copy(qk[:, n], a_ps[n][:].rearrange("p (s f) -> p s f", s=2)
                                           ).then_inc(sig("qk").sem, 1)
                        nc.scalar.copy(v1[:, n, :, 0:HD], b_ps[n][:, 0:D].rearrange("p (h d) -> p h d", h=HEADS)
                                       ).then_inc(sig("v1").sem, 1)
                    for n, t in lanes(i):
                        act.wait_ge(sig("qkT_ps").sem, sig("qkT_ps").nth(t))
                        nc.scalar.copy(qT[:, n], turn(a_ps[n])).then_inc(sig("qT").sem, 1)
                    for n, t in lanes(i):
                        act.wait_ge(sig("shifted").sem, sig("shifted").nth(t))
                        nc.scalar.activation(e[:, n], e[:, n], ACT.Exp, scale=HD ** -0.5
                                             ).then_inc(sig("probs").sem, 1)
                    for r in range(4):
                        for n, t in lanes(i):
                            act.wait_ge(sig("pT_ps").sem, sig("pT_ps").nth(i * 4 * LANES + r * LANES + n))
                            bank = (a_ps, b_ps)[r % 2][n]
                            nc.scalar.copy(e[:, n, 4 * r:4 * r + 4, :], bank[:].rearrange("p (m q) -> p m q", m=4)
                                           ).then_inc(sig("pT").sem, 1)
                    for n, t in lanes(i):
                        act.wait_ge(sig("oT_ps").sem, sig("oT_ps").nth(t))
                        nc.scalar.copy(oT[:, n], turn(b_ps[n])).then_inc(sig("oT").sem, 1)
                    if not rope:
                        for n, t in lanes(i):
                            act.wait_ge(sig("x2").sem, sig("x2").nth(t))
                            nc.scalar.activation(o[:, n], x[:, n], ACT.Square, scale=D ** -0.5, accum_out=mom[:, n, 1:2]
                                                 ).then_inc(sig("squares").sem, 1)
                    for n, t in lanes(i):
                        act.wait_ge(sig("last_turned").sem, sig("last_turned").nth(t))
                        if rope:
                            for f in range(KT):
                                last = nc.scalar.activation(k.xT[:, f, bass.ds(t * P, P)], turn(b_ps[n])[:, f],
                                                            ACT.Identity, bias=w["beta2"][:, f:f + 1],
                                                            scale=w["g2"][:, f:f + 1])
                            last.then_inc(sig("stored").sem, 1)
                        else:
                            nc.scalar.copy(k.xT[:, :, bass.ds(t * P, P)], turn(b_ps[n]))
                            nc.scalar.copy(xT[:, n], turn(b_ps[n])).then_inc(sig("last_T").sem, 1)
                    if not rope:
                        for n, t in lanes(i):
                            act.wait_ge(sig("logits").sem, sig("logits").nth(t))
                            nc.scalar.copy(k.logits[:, t, 0:8], b_ps[n][:, 0:8]).then_inc(sig("stored").sem, 1)
        names = ["stats", "moments", "shifted_var", "rstd", "x", "turned", "xT", "proj", "qk", "v1", "qkT_ps", "qT",
                 "k_pair", "scores", "top", "shifted", "probs", "pv", "recip", "o", "oT_ps", "oT", "out", "x2",
                 "shifted_var_c", "rstd_c", "last_rows", "last_turned", "stored", "kept"]
        names += (["stats_b", "moments_b", "shifted_var_b", "rstd_b", "xn", "rotated", "stats_c", "moments_c",
                   "biased"] if rope else ["squares", "last_T", "logits"])
        for name in names:
            sig(name).advance(TILES)
        for name in ("pT_ps", "pT"):
            sig(name).advance(4 * TILES)
        sig("ones_set").advance(1)


def route(nc, k, experts, chosen, capacity, biased):
    with ExitStack() as ctx:
        sb, ps = scratch(nc, ctx, f"route{experts}")
        shape = [P, TILES, experts]
        probs, choice = sb("probs", shape), sb("choice", shape)
        best, index = sb("best", [P, TILES, 8]), sb("index", [P, TILES, 8], U32)
        indexf = sb("indexf", [P, TILES, 8])
        picked, hit, earlier = sb("picked", shape), sb("hit", shape), sb("earlier", shape)
        total = sb("total", [P, TILES])
        bias = sb("bias", [P, experts])
        rank_ps = ps("rank_ps", shape)
        C, sig = k.const, k.sig
        gates = k.gates[:, :, 0:experts]
        flat = lambda x: x[:].rearrange("p t e -> p (t e)")
        with nc.Block() as block:
            if biased:
                @block.sync
                def _(sp):
                    sp.dma_start(bias[:], to_all(k.dram["L2_ffn_bias"])).then_inc(k.load_small.sem, 16)
                k.load_small.more()

            @block.scalar
            def _(act):
                nc.scalar.activation(probs[:], k.logits[:, :, 0:experts], ACT.Exp, scale=-1.0
                                     ).then_inc(sig("probs").sem, 1)

            @block.vector
            def _(dve):
                link = k.chain(dve)
                nc.vector.memset(k.gates[:], 1.0)
                dve.wait_ge(sig("probs").sem, sig("probs").nth(0))
                link(nc.vector.tensor_scalar(probs[:], probs[:], 1.0, None, ALU.add))
                link(nc.vector.reciprocal(probs[:], probs[:]))
                if biased:
                    dve.wait_ge(k.load_small.sem, k.load_small.all())
                    link(nc.vector.tensor_tensor(choice[:], probs[:], spread(bias[:].unsqueeze(1), shape), ALU.add))
                else:
                    link(nc.vector.tensor_copy(choice[:], probs[:]))
                for t in range(TILES):
                    last = nc.vector.max(best[:, t], choice[:, t])
                link(last)
                for t in range(TILES):
                    last = nc.vector.max_index(index[:, t], best[:, t], choice[:, t])
                link(last)
                link(nc.vector.tensor_copy(indexf[:], index[:]))
                iota = spread(C("iota")[:, 0:experts].unsqueeze(1), shape)
                for j in range(chosen):
                    to = hit if j else picked
                    link(nc.vector.tensor_tensor(to[:], iota, spread(indexf[:, :, j:j + 1], shape), ALU.is_equal))
                    if j:
                        link(nc.vector.tensor_tensor(picked[:], picked[:], hit[:], ALU.add))
                link(nc.vector.memset(earlier[:, 0], 0.0))
                for t in range(1, TILES):
                    link(nc.vector.tensor_tensor(earlier[:, t], earlier[:, t - 1], picked[:, t - 1], ALU.add))
                nc.vector.tensor_tensor(hit[:], picked[:], probs[:], ALU.mult).then_inc(sig("picked").sem, 1)
                dve.wait_ge(sig("picked").sem, sig("picked").nth(0))
                link(nc.vector.tensor_reduce(total[:], hit[:], AX_X, ALU.add))
                if biased:
                    link(nc.vector.tensor_scalar(total[:], total[:], 1e-12, None, ALU.max))
                else:
                    link(nc.vector.tensor_scalar(total[:], total[:], 1e-6, None, ALU.add))
                link(nc.vector.reciprocal(total[:], total[:]))
                link(nc.vector.tensor_tensor(hit[:], hit[:], spread(total[:].unsqueeze(2), shape), ALU.mult))
                dve.wait_ge(sig("ranks").sem, sig("ranks").nth(0))
                nc.vector.scalar_tensor_tensor(gates, rank_ps[:], float(capacity), hit[:], ALU.is_lt, ALU.mult)

            @block.tensor
            def _(pe):
                pe.wait_ge(sig("picked").sem, sig("picked").nth(0))
                nc.tensor.matmul(flat(rank_ps), C("before"), flat(picked), start=True, stop=False)
                nc.tensor.matmul(flat(rank_ps), C("ones"), flat(earlier), start=False,
                                 stop=True).then_inc(sig("ranks").sem, 1)
        for name in ("probs", "picked", "ranks"):
            sig(name).advance(1)


def experts(nc, k, count, w1, w2, gated, target, hidden_bias, prefetch):
    F = 4
    WIDE = CHUNK * P
    with ExitStack() as ctx:
        sb, ps = scratch(nc, ctx, f"experts{count}")
        w1_sb, w2_sb = sb("w1", [P, LANES, KT, F * P]), sb("w2", [P, LANES, F, D])
        hid = [sb(f"hidden{n}", [P, F, WIDE]) for n in range(2)]
        hid_ps = ps("hidden_ps", [P, F, WIDE])
        y_ps = [ps(f"y_ps{n}", [P, CHUNK, D]) for n in range(2)]
        sig = k.sig
        rounds = count // LANES
        unit_order = [(n, c) for n in range(LANES) for c in range(CHUNKS)]
        PER = len(unit_order)

        with nc.Block() as block:
            @block.sync
            def _(sp):
                prefetch(k, sp)
                with sp.Fori(0, rounds) as i:
                    for n in range(LANES):
                        e = i * LANES + n
                        sp.wait_ge(sig("expert_done").sem, sig("expert_done").before(e))
                        sp.dma_start(w1_sb[:, n], w1[:, e]).then_inc(k.load_lane[n].sem, 16)
                        sp.dma_start(w2_sb[:, n], w2[:, e]).then_inc(k.load_lane[n].sem, 16)

            @block.tensor
            def _(pe):
                with pe.Fori(0, rounds) as i:
                    def first(n, c, u):
                        if c == 0:
                            pe.wait_ge(k.load_lane[n].sem, i * 32 + (k.load_lane[n].all() + 32))
                        for f in range(F):
                            pe.wait_ge(sig("hidden").sem, i * (F * PER) + (sig("hidden").nth(F * u + f) - F))
                            for t in range(KT):
                                last = nc.tensor.matmul(hid_ps[:, f], w1_sb[:, n, t, P * f:P * (f + 1)],
                                                        k.xT[:, t, c * WIDE:(c + 1) * WIDE], start=(t == 0),
                                                        stop=(t == KT - 1))
                            last.then_inc(sig("hidden_ps").sem, 1)

                    def second(n, c, u):
                        pe.wait_ge(sig("hidden").sem, i * (F * PER) + sig("hidden").nth(F * u + F - 1))
                        pe.wait_ge(sig("combined").sem, i * PER + sig("combined").before(u))
                        for j in range(CHUNK):
                            for f in range(F):
                                last = nc.tensor.matmul(y_ps[u % 2][:, j], hid[u % 2][:, f, P * j:P * (j + 1)],
                                                        w2_sb[:, n, f, :], start=(f == 0), stop=(f == F - 1))
                        last.then_inc(sig("y_ps").sem, 1)
                    for u, (n, c) in enumerate(unit_order):
                        first(n, c, u)
                        if u:
                            second(*unit_order[u - 1], u - 1)
                    second(*unit_order[-1], PER - 1)

            @block.scalar
            def _(act):
                with act.Fori(0, rounds) as i:
                    for u, (n, c) in enumerate(unit_order):
                        act.wait_ge(sig("y_ps").sem, i * PER + sig("y_ps").before(u))
                        for f in range(F):
                            act.wait_ge(sig("hidden_ps").sem, i * (F * PER) + sig("hidden_ps").nth(F * u + f))
                            if hidden_bias is None:
                                last = nc.scalar.activation(hid[u % 2][:, f], hid_ps[:, f], ACT.Gelu)
                            else:
                                column = (i * LANES + n) * F + f
                                last = nc.scalar.activation(hid[u % 2][:, f], hid_ps[:, f], ACT.Relu,
                                                            bias=hidden_bias[:, bass.ds(column, 1)])
                            last.then_inc(sig("hidden").sem, 1)

            @block.vector
            def _(dve):
                with dve.Fori(0, rounds) as i:
                    for u, (n, c) in enumerate(unit_order):
                        dve.wait_ge(sig("y_ps").sem, i * PER + sig("y_ps").nth(u))
                        dve.wait_ge(sig("combined").sem, i * PER + (sig("combined").nth(u) - 1))
                        for j in range(CHUNK):
                            t = CHUNK * c + j
                            if gated:
                                last = nc.vector.scalar_tensor_tensor(
                                    target[:, t], y_ps[u % 2][:, j], k.gates[:, t, bass.ds(i * LANES + n, 1)],
                                    target[:, t], ALU.mult, ALU.add)
                            else:
                                last = nc.vector.tensor_tensor(target[:, t], y_ps[u % 2][:, j], target[:, t],
                                                               ALU.add)
                        last.then_inc(sig("combined").sem, 1)
                        if c == CHUNKS - 1:
                            dve.sem_inc(sig("expert_done").sem, 1)
        for n in range(LANES):
            k.load_lane[n].more(2 * rounds)
        units = rounds * PER
        for name, n in (("hidden", F * units), ("hidden_ps", F * units), ("y_ps", units), ("combined", units),
                        ("expert_done", count)):
            sig(name).advance(n)


def close_gqa(nc, k):
    with ExitStack() as ctx:
        sb, ps = scratch(nc, ctx, "close_gqa")
        norm2 = sb("norm2", [P, D])
        squares, normed = sb("squares", [P, LANES, D]), sb("normed", [P, LANES, D])
        mean, rstd = sb("mean", [P, TILES]), sb("rstd", [P, TILES])
        sig = k.sig
        with nc.Block() as block:
            @block.sync
            def _(sp):
                sp.dma_start(norm2[:], to_all(k.dram["L0_ffn_norm2_w"])).then_inc(k.load_small.sem, 16)
            k.load_small.more()

            @block.scalar
            def _(act):
                for t in range(TILES):
                    if t >= LANES:
                        act.wait_ge(sig("squares").sem, sig("squares").nth(t - LANES))
                    last = nc.scalar.activation(squares[:, t % LANES], k.rows[:, t], ACT.Square, scale=D ** -0.5,
                                                accum_out=mean[:, t:t + 1])
                    last.then_inc(sig("squares").sem, 1)

            @block.gpsimd
            def _(pool):
                pool.wait_ge(sig("squares").sem, sig("squares").nth(TILES - 1))
                nc.gpsimd.tensor_tensor(rstd[:], mean[:], spread(k.eps_rms[:], [P, TILES]),
                                        ALU.add).then_inc(sig("shifted_var").sem, 1)
                pool.wait_ge(sig("shifted_var").sem, sig("shifted_var").nth(0))
                nc.gpsimd.tensor_tensor(rstd[:], rstd[:], spread(k.minus_half[:], [P, TILES]),
                                        ALU.pow).then_inc(sig("rstd").sem, 1)
                with pool.Fori(0, TILES // LANES) as i:
                    for n in range(LANES):
                        t = i * LANES + n
                        pool.wait_ge(sig("xn").sem, sig("xn").nth(t))
                        nc.gpsimd.tensor_tensor(k.h[:, t, :], k.h[:, t, :], normed[:, n],
                                                ALU.add).then_inc(sig("kept").sem, 1)

            @block.vector
            def _(dve):
                dve.wait_ge(k.load_small.sem, k.load_small.all())
                dve.wait_ge(sig("rstd").sem, sig("rstd").nth(0))
                with dve.Fori(0, TILES // LANES) as i:
                    for n in range(LANES):
                        t = i * LANES + n
                        dve.wait_ge(sig("kept").sem, sig("kept").before(t))
                        nc.vector.scalar_tensor_tensor(normed[:, n], k.rows[:, t, :], rstd[:, bass.ds(t, 1)],
                                                       norm2[:], ALU.mult, ALU.mult).then_inc(sig("xn").sem, 1)
        for name, n in (("squares", TILES), ("shifted_var", 1), ("rstd", 1), ("xn", TILES), ("kept", TILES)):
            sig(name).advance(n)


def norm_pieces(ctx, nc, phase):
    sb, _ = scratch(nc, ctx, phase)
    return sb("ln_stats", [P, LANES, 6]), sb("ln_mom", [P, LANES, 2]), sb("ln_rstd", [P, LANES, 1])


def norm_vector(nc, k, dve, lanes, pieces, out, free):
    stats, mom, rstd = pieces
    sig = k.sig
    for n, t in lanes:
        for name in free:
            dve.wait_ge(sig(name).sem, sig(name).before(t))
        nc.vector.bn_stats(stats[:, n], k.h[:, t, :]).then_inc(sig("stats").sem, 1)
    for n, t in lanes:
        dve.wait_ge(sig("stats").sem, sig("stats").nth(t))
        nc.vector.memset(k.idle[:, n:n + 1], 0.0)
        nc.vector.bn_aggr(mom[:, n], stats[:, n]).then_inc(sig("moments").sem, 1)
    for n, t in lanes:
        dve.wait_ge(sig("rstd").sem, sig("rstd").nth(t))
        nc.vector.tensor_scalar(out(n, t), k.h[:, t, :], mom[:, n, 0:1], rstd[:, n], ALU.subtract,
                                ALU.mult).then_inc(sig("x").sem, 1)


def norm_pool(nc, k, pool, lanes, pieces):
    stats, mom, rstd = pieces
    sig = k.sig
    for n, t in lanes:
        pool.wait_ge(sig("moments").sem, sig("moments").nth(t))
        nc.gpsimd.tensor_tensor(rstd[:, n], mom[:, n, 1:2], k.eps_ln[:], ALU.add).then_inc(sig("shifted_var").sem, 1)
        pool.wait_ge(sig("shifted_var").sem, sig("shifted_var").nth(t))
        nc.gpsimd.tensor_tensor(rstd[:, n], rstd[:, n], k.minus_half[:], ALU.pow).then_inc(sig("rstd").sem, 1)


NORM_SIGNALS = ["stats", "moments", "shifted_var", "rstd", "x"]


def by_lanes(eng):
    return eng.Fori(0, TILES // LANES)


def lanes_of(i):
    return [(n, i * LANES + n) for n in range(LANES)]


def load_bitlinear(k, sp):
    w1 = k.region_b[:, 0:2048].rearrange("p (t n) -> p t n", n=D)
    w2 = k.region_b[:, 2048:4096].rearrange("p (t n) -> p t n", n=1024)
    for to, source in ((w1, by_rows(k.dram["L1_ffn_w1"])), (w2, by_rows(k.dram["L1_ffn_w2"])),
                       (k.conv_w[:], k.dram["L1_ffn_conv_w"].rearrange("(t p) a j -> p t (a j)", p=P)),
                       (k.conv_b[:], as_columns(k.dram["L1_ffn_conv_b"]))):
        sp.dma_start(to, source, allow_slow_non_contiguous=True).then_inc(k.load_b.sem, 16)
    k.load_b.more(4)


def load_decay(k, sp):
    r = k.region_a
    bf = r[:, 2048:4096].bitcast(BF16)
    d = k.dram
    pairs = [
        (r[:, 0:512].rearrange("p (t n) -> p t n", t=KT), by_rows(d["L2_attn_o_w"])),
        (r[:, 512:768], to_all(d["L2_attn_q"])), (r[:, 768:1024], to_all(d["L2_attn_k"])),
        (r[:, 1024:1280], to_all(d["L2_attn_norm_weight"])), (r[:, 1280:1296], to_all(d["L2_attn_log_decay"])),
        (bf[0:32, 0:256], d["L2_ffn_gate_w"]), (bf[:, 256:512], d["L2_ffn_sw1"]), (bf[:, 512:768], d["L2_ffn_sw3"]),
        (bf[:, 768:1024].rearrange("p (t n) -> p t n", t=KT), by_rows(d["L2_ffn_sw2"])),
    ]
    for to, source in pairs:
        sp.dma_start(to, source).then_inc(k.load_a.sem, 16)
    k.load_a.more(len(pairs))


def bitlinear(nc, k):
    CT = 8
    WIDE = CHUNK * P
    with ExitStack() as ctx:
        sb, ps = scratch(nc, ctx, "bitlinear")
        w1T, w2T = sb("w1T", [P, KT, CT * P], BF16), sb("w2T", [P, CT, D], BF16)
        mean = sb("weight_mean", [P, 2])
        unit = sb("weight_unit", [P, 2])
        w1 = k.region_b[:, 0:2048].rearrange("p (t n) -> p t n", n=D)
        w2 = k.region_b[:, 2048:4096].rearrange("p (t n) -> p t n", n=1024)
        unit_bc = k.xT[:, 0, :]
        qT = k.xT[:, 1, :].bitcast(BF16).rearrange("p (t n) -> p t n", t=KT)
        C, sig = k.const, k.sig

        with ExitStack() as ctx2, nc.Block() as block:
            sb2, ps2 = scratch(nc, ctx2, "bit_weights")
            ternary = sb2("ternary", [P, 2, 2048], BF16)
            scaled = sb2("scaled", [P, 2048])
            mean_ps = ps2("mean_ps", [P, 2])
            turned = [ps2(f"turned{n}", [P, CT, P], BF16) for n in range(4)]
            t1 = ternary[:, 0].rearrange("p (t n) -> p t n", n=D)
            t2 = ternary[:, 1].rearrange("p (t n) -> p t n", n=1024)

            @block.vector
            def _(dve):
                link = k.chain(dve)
                nc.vector.tensor_copy(k.ident16[:], C("ident"))
                dve.wait_ge(k.load_b.sem, k.load_b.all())
                for n in range(2):
                    last = nc.vector.tensor_reduce(mean[:, n:n + 1], k.region_b[:, 2048 * n:2048 * (n + 1)], AX_X,
                                                   ALU.add, apply_absolute_value=True)
                last.then_inc(sig("stats").sem, 1)
                dve.wait_ge(sig("moments").sem, sig("moments").nth(0))
                link(nc.vector.tensor_scalar(mean[:], mean_ps[:], 1.0 / (1024 * D), 1e-5, ALU.mult, ALU.max))
                link(nc.vector.reciprocal(unit[:], mean[:]))
                for n in range(2):
                    link(nc.vector.tensor_scalar(scaled[:], k.region_b[:, 2048 * n:2048 * (n + 1)], unit[:, n:n + 1],
                                                 ROUND, ALU.mult, ALU.add))
                    link(nc.vector.tensor_scalar(scaled[:], scaled[:], ROUND, 1.0, ALU.subtract, ALU.min))
                    link(nc.vector.tensor_scalar(ternary[:, n], scaled[:], -1.0, None, ALU.max))
                last = nc.vector.memset(k.idle[:], 0.0)
                last.then_inc(sig("x").sem, 1)

            @block.tensor
            def _(pe):
                pe.wait_ge(sig("stats").sem, sig("stats").nth(0))
                nc.tensor.matmul(mean_ps[:], C("ones"), mean[:], start=True, stop=True).then_inc(
                    sig("moments").sem, 1)
                pe.wait_ge(sig("x").sem, sig("x").nth(0))
                for half in range(2):
                    for c in range(CT):
                        nc.tensor.transpose(turned[half][:, c], t1[:, c, P * half:P * (half + 1)], k.ident16[:])
                        last = nc.tensor.transpose(turned[2 + half][:, c], t2[:, half, P * c:P * (c + 1)],
                                                   k.ident16[:])
                last.then_inc(sig("turned").sem, 1)

            @block.scalar
            def _(act):
                act.wait_ge(sig("turned").sem, sig("turned").nth(0))
                for half in range(2):
                    nc.scalar.copy(w1T[:, half].rearrange("p (c n) -> p c n", c=CT), turned[half][:])
                    nc.scalar.copy(w2T[:, :, P * half:P * (half + 1)], turned[2 + half][:])

            @block.sync
            def _(sp):
                load_decay(k, sp)
        for name in ("stats", "moments", "x", "turned"):
            sig(name).advance(1)

        with ExitStack() as ctx2, nc.Block() as block:
            sb2, ps2 = scratch(nc, ctx2, "bit_input")
            pieces = norm_pieces(ctx2, nc, "bit_input")
            x = sb2("x", [P, LANES, D])
            top, inv, f = (sb2(name, [P, LANES, 1]) for name in ("top", "inv", "unit"))
            q = sb2("q", [P, LANES, D], BF16)
            diag = sb2("diag", [P, LANES, P])
            bc_ps = [ps2(f"bc_ps{n}", [P, P]) for n in range(LANES)]
            q_ps = [ps2(f"q_ps{n}", [P, KT, P], BF16) for n in range(LANES)]

            @block.vector
            def _(dve):
                with by_lanes(dve) as i:
                    norm_vector(nc, k, dve, lanes_of(i), pieces, lambda n, t: x[:, n], ["stored"])
                    for n, t in lanes_of(i):
                        dve.wait_ge(sig("x").sem, sig("x").nth(t))
                        nc.vector.tensor_reduce(top[:, n], x[:, n], AX_X, ALU.max, apply_absolute_value=True
                                                ).then_inc(sig("top").sem, 1)
                    for n, t in lanes_of(i):
                        dve.wait_ge(sig("top").sem, sig("top").nth(t))
                        nc.vector.tensor_scalar(top[:, n], top[:, n], 1e-5, None, ALU.max
                                                ).then_inc(sig("clipped").sem, 1)
                    for n, t in lanes_of(i):
                        dve.wait_ge(sig("clipped").sem, sig("clipped").nth(t))
                        nc.vector.reciprocal(inv[:, n], top[:, n])
                        nc.vector.tensor_scalar(f[:, n], top[:, n], 1.0 / 127.0, mean[:, 0:1], ALU.mult, ALU.mult
                                                ).then_inc(sig("recip").sem, 1)
                    for n, t in lanes_of(i):
                        dve.wait_ge(sig("recip").sem, sig("recip").nth(t))
                        nc.vector.tensor_scalar(diag[:, n], C("ident"), f[:, n], None, ALU.mult
                                                ).then_inc(sig("diag").sem, 1)
                        nc.vector.tensor_scalar(x[:, n], x[:, n], inv[:, n], 127.0, ALU.mult, ALU.mult
                                                ).then_inc(sig("scaled").sem, 1)
                    for n, t in lanes_of(i):
                        dve.wait_ge(sig("scaled").sem, sig("scaled").nth(t))
                        nc.vector.tensor_scalar(x[:, n], x[:, n], 127.0, -128.0, ALU.min, ALU.max
                                                ).then_inc(sig("shifted").sem, 1)
                    for n, t in lanes_of(i):
                        dve.wait_ge(sig("shifted").sem, sig("shifted").nth(t))
                        nc.vector.tensor_scalar(q[:, n], x[:, n], ROUND, ROUND, ALU.add, ALU.subtract
                                                ).then_inc(sig("rounded").sem, 1)

            @block.gpsimd
            def _(pool):
                with by_lanes(pool) as i:
                    norm_pool(nc, k, pool, lanes_of(i), pieces)

            @block.tensor
            def _(pe):
                with by_lanes(pe) as i:
                    for n, t in lanes_of(i):
                        pe.wait_ge(sig("diag").sem, sig("diag").nth(t))
                        nc.tensor.matmul(bc_ps[n][:], C("ones"), diag[:, n], start=True, stop=True
                                         ).then_inc(sig("unit_ps").sem, 1)
                    for n, t in lanes_of(i):
                        pe.wait_ge(sig("rounded").sem, sig("rounded").nth(t))
                        for j in range(KT):
                            last = nc.tensor.transpose(q_ps[n][:, j], q[:, n, P * j:P * (j + 1)], k.ident16[:])
                        last.then_inc(sig("turned").sem, 1)

            @block.scalar
            def _(act):
                with by_lanes(act) as i:
                    for n, t in lanes_of(i):
                        act.wait_ge(sig("unit_ps").sem, sig("unit_ps").nth(t))
                        nc.scalar.copy(unit_bc[:, bass.ds(t * P, P)], bc_ps[n][:])
                    for n, t in lanes_of(i):
                        act.wait_ge(sig("turned").sem, sig("turned").nth(t))
                        nc.scalar.copy(qT[:, :, bass.ds(t * P, P)], q_ps[n][:]).then_inc(sig("stored").sem, 1)
        for name in NORM_SIGNALS + ["top", "clipped", "recip", "diag", "scaled", "shifted", "rounded", "unit_ps",
                                    "turned", "stored"]:
            sig(name).advance(TILES)

        with ExitStack() as ctx2, nc.Block() as block:
            sb2, ps2 = scratch(nc, ctx2, "bit_layers")
            padded = [sb2(f"padded{n}", [P, CHUNK, S + 2]) for n in range(2)]
            taps = [sb2(f"taps{n}", [P, CHUNK, S]) for n in range(2)]
            act_h = sb2("hidden", [P, CT, WIDE])
            q = sb2("q", [P, CT, WIDE], BF16)
            highest = sb2("highest", [P, WIDE])
            top, inv, f = (sb2(name, [P, CHUNK]) for name in ("top", "inv", "unit"))
            diag = sb2("diag", [P, CHUNK, P])
            scale_bc = sb2("scale_bc", [P, WIDE])
            h_ps = [ps2(f"h_ps{n}", [P, WIDE]) for n in range(2)]
            top_ps, scale_ps = ps2("top_ps", [P, CHUNK, P]), ps2("scale_ps", [P, WIDE])
            y_ps = ps2("y_ps", [P, CHUNK, D])
            by_seq = lambda x: x.rearrange("p (b s) -> p b s", b=CHUNK)

            @block.tensor
            def _(pe):
                with pe.Fori(0, CHUNKS) as c:
                    for m in range(CT):
                        u = c * CT + m
                        pe.wait_ge(sig("padded").sem, sig("padded").before(u))
                        for t in range(KT):
                            last = nc.tensor.matmul(h_ps[m % 2][:], w1T[:, t, P * m:P * (m + 1)],
                                                    qT[:, t, bass.ds(c * WIDE, WIDE)], start=(t == 0),
                                                    stop=(t == KT - 1))
                        last.then_inc(sig("hidden_ps").sem, 1)
                    pe.wait_ge(sig("highest").sem, sig("highest").nth(c))
                    for j in range(CHUNK):
                        last = nc.tensor.transpose(top_ps[:, j], highest[:, P * j:P * (j + 1)], C("ident"))
                    last.then_inc(sig("top_ps").sem, 1)
                    pe.wait_ge(sig("diag").sem, sig("diag").nth(c))
                    nc.tensor.matmul(scale_ps[:], C("ones"), diag[:].rearrange("p j q -> p (j q)"), start=True,
                                     stop=True).then_inc(sig("unit_ps").sem, 1)
                    pe.wait_ge(sig("rounded").sem, sig("rounded").nth(c))
                    for j in range(CHUNK):
                        for m in range(CT):
                            last = nc.tensor.matmul(y_ps[:, j], q[:, m, P * j:P * (j + 1)], w2T[:, m, :],
                                                    start=(m == 0), stop=(m == CT - 1))
                    last.then_inc(sig("y_ps").sem, 1)

            @block.scalar
            def _(act):
                with act.Fori(0, CHUNKS) as c:
                    for m in range(CT):
                        u = c * CT + m
                        act.wait_ge(sig("padded").sem, sig("padded").nth(u))
                        nc.scalar.activation(taps[m % 2][:], padded[m % 2][:, :, 1:S + 1], ACT.Identity,
                                             bias=k.conv_b[:, m:m + 1], scale=k.conv_w[:, m, 1:2]
                                             ).then_inc(sig("middle_tap").sem, 1)
                        act.wait_ge(sig("taps").sem, sig("taps").nth(u))
                        nc.scalar.activation(by_seq(act_h[:, m]), taps[m % 2][:], ACT.Silu
                                             ).then_inc(sig("hidden").sem, 1)
                    act.wait_ge(sig("unit_ps").sem, sig("unit_ps").nth(c))
                    nc.scalar.copy(scale_bc[:], scale_ps[:]).then_inc(sig("recip").sem, 1)

            @block.vector
            def _(dve):
                link = k.chain(dve)
                for n in range(2):
                    last = nc.vector.memset(padded[n][:], 0.0)
                link(last)
                with dve.Fori(0, CHUNKS) as c:
                    for m in range(CT):
                        u = c * CT + m
                        dve.wait_ge(sig("hidden").sem, sig("hidden").before(u))
                        dve.wait_ge(sig("hidden_ps").sem, sig("hidden_ps").nth(u))
                        nc.vector.tensor_tensor(padded[m % 2][:, :, 1:S + 1], by_seq(h_ps[m % 2][:]),
                                                by_seq(unit_bc[:, bass.ds(c * WIDE, WIDE)]), ALU.mult
                                                ).then_inc(sig("padded").sem, 1)
                        dve.wait_ge(sig("middle_tap").sem, sig("middle_tap").nth(u))
                        nc.vector.scalar_tensor_tensor(taps[m % 2][:], padded[m % 2][:, :, 0:S],
                                                       k.conv_w[:, m, 0:1], taps[m % 2][:], ALU.mult, ALU.add
                                                       ).then_inc(sig("first_tap").sem, 1)
                        dve.wait_ge(sig("first_tap").sem, sig("first_tap").nth(u))
                        nc.vector.scalar_tensor_tensor(taps[m % 2][:], padded[m % 2][:, :, 2:S + 2],
                                                       k.conv_w[:, m, 2:3], taps[m % 2][:], ALU.mult, ALU.add
                                                       ).then_inc(sig("taps").sem, 1)
                    dve.wait_ge(sig("hidden").sem, c * CT + sig("hidden").nth(CT - 1))
                    nc.vector.tensor_reduce(highest[:], act_h[:].rearrange("p m t -> p t m"), AX_X, ALU.max,
                                            apply_absolute_value=True).then_inc(sig("highest").sem, 1)
                    dve.wait_ge(sig("top_ps").sem, sig("top_ps").nth(c))
                    nc.vector.tensor_reduce(top[:], top_ps[:], AX_X, ALU.max).then_inc(sig("top").sem, 1)
                    dve.wait_ge(sig("top").sem, sig("top").nth(c))
                    nc.vector.tensor_scalar(top[:], top[:], 1e-5, None, ALU.max).then_inc(sig("clipped").sem, 1)
                    dve.wait_ge(sig("clipped").sem, sig("clipped").nth(c))
                    nc.vector.reciprocal(inv[:], top[:])
                    nc.vector.tensor_scalar(f[:], top[:], 1.0 / 127.0, mean[:, 1:2], ALU.mult, ALU.mult
                                            ).then_inc(sig("unit").sem, 1)
                    dve.wait_ge(sig("unit").sem, sig("unit").nth(c))
                    nc.vector.tensor_tensor(diag[:], spread(C("ident").unsqueeze(1), [P, CHUNK, P]),
                                            spread(inv[:].unsqueeze(2), [P, CHUNK, P]), ALU.mult
                                            ).then_inc(sig("diag").sem, 1)
                    dve.wait_ge(sig("recip").sem, sig("recip").nth(c))
                    nc.vector.tensor_tensor(act_h[:], act_h[:], spread(scale_bc[:].unsqueeze(1), [P, CT, WIDE]),
                                            ALU.mult).then_inc(sig("scaled").sem, 1)
                    dve.wait_ge(sig("scaled").sem, sig("scaled").nth(c))
                    nc.vector.tensor_scalar(act_h[:], act_h[:], 127.0, ROUND, ALU.mult, ALU.add
                                            ).then_inc(sig("shifted").sem, 1)
                    dve.wait_ge(sig("shifted").sem, sig("shifted").nth(c))
                    nc.vector.tensor_scalar(q[:], act_h[:], ROUND, 127.0, ALU.subtract, ALU.min
                                            ).then_inc(sig("rounded").sem, 1)
                    dve.wait_ge(sig("y_ps").sem, sig("y_ps").nth(c))
                    for j in range(CHUNK):
                        t = c * CHUNK + j
                        last = nc.vector.scalar_tensor_tensor(k.h[:, t, :], y_ps[:, j], f[:, j:j + 1], k.h[:, t, :],
                                                              ALU.mult, ALU.add)
                    last.then_inc(sig("stored").sem, 1)
        for name in ("padded", "hidden_ps", "middle_tap", "first_tap", "taps", "hidden"):
            sig(name).advance(CHUNKS * CT)
        for name in ("highest", "top_ps", "top", "clipped", "unit", "diag", "unit_ps", "recip", "scaled", "shifted",
                     "rounded", "y_ps", "stored"):
            sig(name).advance(CHUNKS)


def decay_attention(nc, k):
    r = k.region_a
    o_w = r[:, 0:512].rearrange("p (t n) -> p t n", t=KT)
    q, kk, norm_w, log_decay = r[:, 512:768], r[:, 768:1024], r[:, 1024:1280], r[:, 1280:1296]
    all_out = k.xT[:].rearrange("p t (n d) -> p (t n) d", d=D)
    C, sig = k.const, k.sig
    with ExitStack() as ctx:
        sb, ps = scratch(nc, ctx, "decay")
        powers = sb("powers", [P, HEADS, P])
        qk, per_head = sb("qk", [P, D]), sb("per_head", [P, HEADS])
        ln_decay, size, soft = (sb(name, [P, HEADS]) for name in ("ln_decay", "size", "soft"))
        o_wT = sb("o_wT", [P, KT, D])
        pieces = norm_pieces(ctx, nc, "decay")
        turned = ps("turned", [P, KT, D])
        out_ps = [ps(f"out_ps{n}", [P, TILES, HD]) for n in range(4)]

        with nc.Block() as block:
            @block.vector
            def _(dve):
                link = k.chain(dve)
                dve.wait_ge(k.load_a.sem, k.load_a.all())
                link(nc.vector.tensor_scalar(soft[:], log_decay, -1.0, None, ALU.mult))
                nc.vector.tensor_tensor(size[:], soft[:], log_decay, ALU.max).then_inc(sig("top").sem, 1)
                link(nc.vector.tensor_scalar(ln_decay[:], log_decay, -1.0, 0.0, ALU.mult, ALU.max))
                link(nc.vector.tensor_tensor(qk[:], q, kk, ALU.mult))
                link(nc.vector.tensor_reduce(per_head[:], qk[:].rearrange("p (h d) -> p h d", h=HEADS), AX_X,
                                             ALU.add))
                dve.wait_ge(sig("unit").sem, sig("unit").nth(0))
                link(nc.vector.tensor_tensor(ln_decay[:], ln_decay[:], soft[:], ALU.add))
                nc.vector.tensor_scalar(ln_decay[:], ln_decay[:], -1.0, None, ALU.mult).then_inc(sig("recip").sem, 1)
                for h in range(HEADS):
                    dve.wait_ge(sig("powers").sem, sig("powers").nth(h))
                    nc.vector.scalar_tensor_tensor(powers[:, h], powers[:, h], per_head[:, h:h + 1], C("causal"),
                                                   ALU.mult, ALU.mult)
                with by_lanes(dve) as i:
                    norm_vector(nc, k, dve, lanes_of(i), pieces, lambda n, t: k.rows[:, t, :], [])

            @block.gpsimd
            def _(pool):
                with by_lanes(pool) as i:
                    norm_pool(nc, k, pool, lanes_of(i), pieces)

            @block.scalar
            def _(act):
                act.wait_ge(sig("top").sem, sig("top").nth(0))
                nc.scalar.activation(soft[:], size[:], ACT.Exp, scale=-1.0).then_inc(sig("probs").sem, 1)
                act.wait_ge(sig("probs").sem, sig("probs").nth(0))
                nc.scalar.activation(soft[:], soft[:], ACT.Ln, bias=1.0).then_inc(sig("unit").sem, 1)
                act.wait_ge(sig("turned").sem, sig("turned").nth(0))
                nc.scalar.copy(o_wT[:], turned[:])
                act.wait_ge(sig("recip").sem, sig("recip").nth(0))
                for h in range(HEADS):
                    nc.scalar.activation(powers[:, h], C("lag"), ACT.Exp, scale=ln_decay[:, h:h + 1]
                                         ).then_inc(sig("powers").sem, 1)

            @block.tensor
            def _(pe):
                pe.wait_ge(k.load_a.sem, k.load_a.all())
                for a in range(KT):
                    for b in range(KT):
                        last = nc.tensor.transpose(turned[:, b, P * a:P * (a + 1)], o_w[:, a, P * b:P * (b + 1)],
                                                   C("ident"))
                last.then_inc(sig("turned").sem, 1)
        for name in ("top", "unit", "recip", "probs", "turned"):
            sig(name).advance(1)
        sig("powers").advance(HEADS)
        for name in NORM_SIGNALS:
            sig(name).advance(TILES)

        with nc.Block() as block:
            @block.tensor
            def _(pe):
                for h in range(HEADS):
                    if h >= 4:
                        pe.wait_ge(sig("stored").sem, sig("stored").nth(h - 4))
                    nc.tensor.matmul(out_ps[h % 4][:], powers[:, h], k.rows[:, :, HD * h:HD * (h + 1)], start=True,
                                     stop=True).then_inc(sig("out").sem, 1)

            @block.scalar
            def _(act):
                for h in range(HEADS):
                    act.wait_ge(sig("out").sem, sig("out").nth(h))
                    nc.scalar.copy(all_out[:, :, HD * h:HD * (h + 1)], out_ps[h % 4][:]
                                   ).then_inc(sig("stored").sem, 1)
        sig("out").advance(HEADS)
        sig("stored").advance(HEADS)

        with ExitStack() as ctx2, nc.Block() as block:
            sb2, ps2 = scratch(nc, ctx2, "decay_out")
            squares, normed = sb2("squares", [P, LANES, D]), sb2("normed", [P, LANES, D])
            mean, rstd = sb2("mean", [P, LANES, 1]), sb2("rstd", [P, LANES, 1])
            normedT = sb2("normedT", [P, LANES, KT, P])
            bank = [ps2(f"bank{n}", [P, KT, P]) for n in range(2)]

            @block.scalar
            def _(act):
                with by_lanes(act) as i:
                    for n, t in lanes_of(i):
                        act.wait_ge(sig("kept").sem, sig("kept").before(t))
                        nc.scalar.activation(squares[:, n], all_out[:, t, :], ACT.Square, scale=D ** -0.5,
                                             accum_out=mean[:, n]).then_inc(sig("squares").sem, 1)
                    for n, t in lanes_of(i):
                        act.wait_ge(sig("turned").sem, sig("turned").nth(t))
                        nc.scalar.copy(normedT[:, n], bank[n][:]).then_inc(sig("xT").sem, 1)

            @block.gpsimd
            def _(pool):
                with by_lanes(pool) as i:
                    for n, t in lanes_of(i):
                        pool.wait_ge(sig("squares").sem, sig("squares").nth(t))
                        nc.gpsimd.tensor_tensor(rstd[:, n], mean[:, n], k.eps_rms[:], ALU.add
                                                ).then_inc(sig("shifted_var").sem, 1)
                        pool.wait_ge(sig("shifted_var").sem, sig("shifted_var").nth(t))
                        nc.gpsimd.tensor_tensor(rstd[:, n], rstd[:, n], k.minus_half[:], ALU.pow
                                                ).then_inc(sig("rstd").sem, 1)

            @block.vector
            def _(dve):
                with by_lanes(dve) as i:
                    for n, t in lanes_of(i):
                        dve.wait_ge(sig("rstd").sem, sig("rstd").nth(t))
                        nc.vector.scalar_tensor_tensor(normed[:, n], all_out[:, t, :], rstd[:, n], norm_w, ALU.mult,
                                                       ALU.mult).then_inc(sig("xn").sem, 1)
                    for n, t in lanes_of(i):
                        dve.wait_ge(sig("out").sem, sig("out").nth(t))
                        nc.vector.tensor_tensor(k.h[:, t, :], bank[n][:].rearrange("p t n -> p (t n)"),
                                                k.h[:, t, :], ALU.add).then_inc(sig("kept").sem, 1)

            @block.tensor
            def _(pe):
                with by_lanes(pe) as i:
                    for n, t in lanes_of(i):
                        pe.wait_ge(sig("xn").sem, sig("xn").nth(t))
                        for f in range(KT):
                            last = nc.tensor.transpose(bank[n][:, f], normed[:, n, P * f:P * (f + 1)], C("ident"))
                        last.then_inc(sig("turned").sem, 1)
                    for n, t in lanes_of(i):
                        pe.wait_ge(sig("xT").sem, sig("xT").nth(t))
                        for f in range(KT):
                            last = nc.tensor.matmul(bank[n][:].rearrange("p t n -> p (t n)"), normedT[:, n, f],
                                                    o_wT[:, f, :], start=(f == 0), stop=(f == KT - 1))
                        last.then_inc(sig("out").sem, 1)
        for name in ("squares", "xT", "shifted_var", "rstd", "xn", "kept", "turned", "out"):
            sig(name).advance(TILES)


def load_hyena(k, sp):
    r, d = k.region_b, k.dram
    w = hyena_weights(k)
    pairs = [
        (w["in_proj"], by_rows(d["L3_attn_in_proj_w"])), (w["out_w"], by_rows(d["L3_attn_out_w"])),
        (w["fw3"], d["L3_attn_fw3"]), (w["fw2"], d["L3_attn_fw2"]),
        (w["in_bias"], d["L3_attn_in_proj_b"].partition_broadcast(3)), (w["out_b"], as_row(d["L3_attn_out_b"])),
        (w["fb3"], as_row(d["L3_attn_fb3"])), (w["fw1"], d["L3_attn_fw1"]),
        (w["fb1"], d["L3_attn_fb1"].rearrange("(n a) -> n a", a=1)),
        (w["fb2"], d["L3_attn_fb2"].rearrange("(n a) -> n a", a=1)),
        (w["short_w"], to_all(d["L3_attn_short_w"].rearrange("c a j -> (c a j)"))),
        (w["taps_T"], d["L3_attn_short_w"].rearrange("c a j -> j (a c)")),
        (k.v_bias[3:4, :], as_row(d["L3_attn_short_b"])),
    ]
    for to, source in pairs:
        sp.dma_start(to, source, allow_slow_non_contiguous=True).then_inc(k.load_b.sem, 16)
    k.load_b.more(len(pairs))


def hyena_weights(k):
    r = k.region_b
    return {
        "in_proj": r[:, 0:1536].rearrange("p (t n) -> p t n", t=KT),
        "out_w": r[:, 1536:2048].rearrange("p (t n) -> p t n", t=KT),
        "fw3": r[:, 2048:2560], "fw2": r[0:64, 2560:2688], "in_bias": r[0:3, 2688:3456], "out_b": r[0:1, 3456:3712],
        "fb3": r[0:1, 3712:4224], "fw1": r[0:1, 4224:4288], "fb1": r[0:64, 4288:4289], "fb2": r[:, 4289:4290],
        "short_w": r[:, 4290:5058], "taps_T": r[0:3, 5058:5314],
    }


def load_mixture(k, sp):
    r, d = k.region_a, k.dram
    pairs = [
        (r[:, 0:4096].rearrange("p (e t n) -> p e t n", e=8, t=KT),
         d["L3_ffn_expert_w"].rearrange("e (t p) n -> p e t n", p=P)),
        (r[:, 4096:4112].rearrange("p (t n) -> p t n", t=KT), by_rows(d["L3_ffn_gate_w"])),
        (r[0:1, 4112:4120], as_row(d["L3_ffn_gate_b"])),
        (r[0:1, 4120:6168], d["L3_ffn_expert_b"].rearrange("(a e) n -> a (e n)", a=1)),
    ]
    for to, source in pairs:
        sp.dma_start(to, source).then_inc(k.load_a.sem, 16)
    k.load_a.more(len(pairs))


def swiglu_gates(nc, k, shared):
    bf = k.region_a[:, 2048:4096].bitcast(BF16)
    gate_raw, sw1, sw3 = bf[0:32, 0:256], bf[:, 256:512], bf[:, 512:768]
    sw2 = bf[:, 768:1024].rearrange("p (t n) -> p t n", t=KT)
    C, sig = k.const, k.sig
    with ExitStack() as ctx:
        sb, ps = scratch(nc, ctx, "swiglu_gates")
        pieces = norm_pieces(ctx, nc, "swiglu_gates")
        x, xT = sb("x", [P, LANES, D]), sb("xT", [P, LANES, KT, P])
        gate_wT = sb("gate_wT", [P, KT, 32])
        raw_ps = ps("raw_ps", [P, 8, P], BF16)
        bank = [ps(f"bank{n}", [P, KT, P]) for n in range(2)]
        with nc.Block() as block:
            @block.vector
            def _(dve):
                with by_lanes(dve) as i:
                    norm_vector(nc, k, dve, lanes_of(i), pieces, lambda n, t: x[:, n], ["stored"])

            @block.gpsimd
            def _(pool):
                with by_lanes(pool) as i:
                    norm_pool(nc, k, pool, lanes_of(i), pieces)

            @block.tensor
            def _(pe):
                pe.wait_ge(k.load_a.sem, k.load_a.all())
                for t in range(KT):
                    cols = slice(P * t, P * (t + 1))
                    nc.tensor.transpose(raw_ps[:, t, 0:32], gate_raw[:, cols], k.ident16[0:32, 0:32])
                    nc.tensor.transpose(raw_ps[:, 2 + t], sw1[:, cols], k.ident16[:])
                    nc.tensor.transpose(raw_ps[:, 4 + t], sw3[:, cols], k.ident16[:])
                    last = nc.tensor.transpose(raw_ps[:, 6 + t], sw2[:, t], k.ident16[:])
                last.then_inc(sig("proj").sem, 1)
                with by_lanes(pe) as i:
                    for n, t in lanes_of(i):
                        pe.wait_ge(sig("x").sem, sig("x").nth(t))
                        for f in range(KT):
                            last = nc.tensor.transpose(bank[n][:, f], x[:, n, P * f:P * (f + 1)], C("ident"))
                        last.then_inc(sig("turned").sem, 1)
                    for n, t in lanes_of(i):
                        pe.wait_ge(sig("xT").sem, sig("xT").nth(t))
                        for f in range(KT):
                            last = nc.tensor.matmul(bank[n][:, 0, 0:32], xT[:, n, f], gate_wT[:, f], start=(f == 0),
                                                    stop=(f == KT - 1))
                        last.then_inc(sig("logits").sem, 1)

            @block.scalar
            def _(act):
                act.wait_ge(sig("proj").sem, sig("proj").nth(0))
                nc.scalar.copy(gate_wT[:], raw_ps[:, 0:2, 0:32])
                nc.scalar.copy(shared.rearrange("p (m n) -> p m n", n=P), raw_ps[:, 2:8])
                with by_lanes(act) as i:
                    for n, t in lanes_of(i):
                        act.wait_ge(sig("turned").sem, sig("turned").nth(t))
                        nc.scalar.copy(k.xT[:, :, bass.ds(t * P, P)], bank[n][:])
                        nc.scalar.copy(xT[:, n], bank[n][:]).then_inc(sig("xT").sem, 1)
                    for n, t in lanes_of(i):
                        act.wait_ge(sig("logits").sem, sig("logits").nth(t))
                        nc.scalar.copy(k.logits[:, t, :], bank[n][:, 0, 0:32]).then_inc(sig("stored").sem, 1)
        sig("proj").advance(1)
        for name in NORM_SIGNALS + ["turned", "xT", "logits", "stored"]:
            sig(name).advance(TILES)


def swiglu_experts(nc, k, shared):
    E, I = 32, 128
    WIDE = CHUNK * P
    W = 2 * KT * I + D
    d = k.dram
    w1 = d["L2_ffn_W1"].rearrange("e (t p) i -> p e t i", p=P)
    w3 = d["L2_ffn_W3"].rearrange("e (t p) i -> p e t i", p=P)
    w2 = d["L2_ffn_W2"].rearrange("e p n -> p e n")
    rounds = E // LANES
    order = [(n, c) for n in range(LANES) for c in range(CHUNKS)]
    PER = len(order)
    sig = k.sig
    with ExitStack() as ctx:
        sb, ps = scratch(nc, ctx, "swiglu")
        raw = sb("raw", [P, LANES, W], BF16)
        w = sb("w", [P, LANES, W])
        zero = sb("zero", [P, 1], BF16)
        gate_h = [sb(f"gate{n}", [P, WIDE]) for n in range(2)]
        hid = [sb(f"hidden{n}", [P, WIDE]) for n in range(2)]
        a_ps = [ps(f"a_ps{n}", [P, WIDE]) for n in range(2)]
        b_ps = [ps(f"b_ps{n}", [P, WIDE]) for n in range(2)]
        y_ps = [ps(f"y_ps{n}", [P, CHUNK, D]) for n in range(2)]

        def weights(n):
            one = w[:, n] if n < LANES else shared
            return (one[:, 0:KT * I].rearrange("p (t i) -> p t i", t=KT),
                    one[:, KT * I:2 * KT * I].rearrange("p (t i) -> p t i", t=KT), one[:, 2 * KT * I:])

        with nc.Block() as block:
            @block.sync
            def _(sp):
                load_hyena(k, sp)
                with sp.Fori(0, rounds) as i:
                    for n in range(LANES):
                        e = i * LANES + n
                        sp.wait_ge(sig("converted").sem, sig("converted").before(e))
                        for source, at in ((w1, 0), (w3, KT * I)):
                            sp.dma_start(raw[:, n, at:at + KT * I].rearrange("p (t i) -> p t i", t=KT),
                                         source[:, e]).then_inc(k.load_lane[n].sem, 16)
                        sp.dma_start(raw[:, n, 2 * KT * I:], w2[:, e]).then_inc(k.load_lane[n].sem, 16)

            @block.gpsimd
            def _(pool):
                nc.gpsimd.memset(zero[:], 0.0).then_inc(sig("ones_set").sem, 1)
                pool.wait_ge(sig("ones_set").sem, sig("ones_set").nth(0))
                with pool.Fori(0, rounds) as i:
                    for n in range(LANES):
                        e = i * LANES + n
                        pool.wait_ge(k.load_lane[n].sem, i * 48 + (k.load_lane[n].all() + 48))
                        pool.wait_ge(sig("expert_done").sem, sig("expert_done").before(e))
                        nc.gpsimd.tensor_tensor(w[:, n], raw[:, n], spread(zero[:], [P, W]), ALU.add
                                                ).then_inc(sig("converted").sem, 1)

            @block.tensor
            def _(pe):
                def units(i, order):
                    def first(n, c, u):
                        if c == 0 and n < LANES:
                            pe.wait_ge(sig("converted").sem, sig("converted").nth(i * LANES + n))
                        w1, w3, _ = weights(n)
                        pe.wait_ge(sig("hidden").sem, i * PER + sig("hidden").before(u))
                        for bank, part in ((a_ps, w1), (b_ps, w3)):
                            for t in range(KT):
                                last = nc.tensor.matmul(bank[u % 2][:], part[:, t, :],
                                                        k.xT[:, t, c * WIDE:(c + 1) * WIDE], start=(t == 0),
                                                        stop=(t == KT - 1))
                        last.then_inc(sig("hidden_ps").sem, 1)

                    def second(n, c, u):
                        pe.wait_ge(sig("hidden").sem, i * PER + sig("hidden").nth(u))
                        pe.wait_ge(sig("combined").sem, i * PER + sig("combined").before(u))
                        for j in range(CHUNK):
                            last = nc.tensor.matmul(y_ps[u % 2][:, j], hid[u % 2][:, P * j:P * (j + 1)],
                                                    weights(n)[2], start=True, stop=True)
                        last.then_inc(sig("y_ps").sem, 1)
                    for u, (n, c) in enumerate(order):
                        first(n, c, u)
                        if u:
                            second(*order[u - 1], u - 1)
                    second(*order[-1], len(order) - 1)
                with pe.Fori(0, rounds) as i:
                    units(i, order)
                units(rounds, [(LANES, c) for c in range(CHUNKS)])

            @block.scalar
            def _(act):
                def units(i, order):
                    for u, (n, c) in enumerate(order):
                        act.wait_ge(sig("hidden").sem, i * PER + sig("hidden").before(u))
                        act.wait_ge(sig("hidden_ps").sem, i * PER + sig("hidden_ps").nth(u))
                        nc.scalar.activation(gate_h[u % 2][:], a_ps[u % 2][:], ACT.Silu).then_inc(sig("silu").sem, 1)
                with act.Fori(0, rounds) as i:
                    units(i, order)
                units(rounds, [(LANES, c) for c in range(CHUNKS)])

            @block.vector
            def _(dve):
                def units(i, order):
                    def product(u):
                        dve.wait_ge(sig("silu").sem, i * PER + sig("silu").nth(u))
                        dve.wait_ge(sig("y_ps").sem, i * PER + sig("y_ps").before(u))
                        nc.vector.tensor_tensor(hid[u % 2][:], gate_h[u % 2][:], b_ps[u % 2][:], ALU.mult
                                                ).then_inc(sig("hidden").sem, 1)

                    def combine(n, c, u):
                        dve.wait_ge(sig("y_ps").sem, i * PER + sig("y_ps").nth(u))
                        dve.wait_ge(sig("combined").sem, i * PER + (sig("combined").nth(u) - 1))
                        for j in range(CHUNK):
                            t = CHUNK * c + j
                            column = bass.ds(i * LANES + n, 1) if n < LANES else slice(E, E + 1)
                            last = nc.vector.scalar_tensor_tensor(k.h[:, t], y_ps[u % 2][:, j],
                                                                  k.gates[:, t, column], k.h[:, t], ALU.mult,
                                                                  ALU.add)
                        last.then_inc(sig("combined").sem, 1)
                        if c == CHUNKS - 1:
                            dve.sem_inc(sig("expert_done").sem, 1)
                    for u, (n, c) in enumerate(order):
                        product(u)
                        if u:
                            combine(*order[u - 1], u - 1)
                    combine(*order[-1], len(order) - 1)
                with dve.Fori(0, rounds) as i:
                    units(i, order)
                units(rounds, [(LANES, c) for c in range(CHUNKS)])
        for n in range(LANES):
            k.load_lane[n].more(3 * rounds)
        total = rounds * PER + CHUNKS
        for name in ("hidden", "hidden_ps", "silu", "y_ps", "combined"):
            sig(name).advance(total)
        sig("converted").advance(E)
        sig("ones_set").advance(1)
        sig("expert_done").advance(E + 1)


def hyena(nc, k):
    w = hyena_weights(k)
    C, sig = k.const, k.sig
    with ExitStack() as ctx:
        sb, ps = scratch(nc, ctx, "hyena")
        pieces = norm_pieces(ctx, nc, "hyena")
        w_taps = sb("w_taps", [P, 3, KT, D])
        w_branch = sb("w_branch", [P, KT, D])
        f1, f2 = sb("filter1", [64, P]), sb("filter2", [P, P])
        coefs = sb("coefs", [P, D])
        H13, H22 = sb("H13", [P, 2, D]), sb("H22", [P, 2, D])
        x = sb("x", [P, LANES, D])
        padded = sb("padded", [P, LANES, KT, S + 2])
        v, branch = sb("v", [P, LANES, D]), sb("branch", [P, LANES, D])
        y1, y2 = sb("y1", [P, LANES, 2, D]), sb("y2", [P, LANES, 2, D])
        z, zT = sb("z", [P, LANES, D]), sb("zT", [P, LANES, KT, P])
        a_ps, b_ps, c_ps = ([ps(f"{c}_ps{n}", [P, 512]) for n in range(LANES)] for c in "abc")
        in_proj = w["in_proj"].rearrange("p t (c i) -> p t c i", i=3)
        taps = w["short_w"].rearrange("p (c j) -> p c j", j=3)

        with nc.Block() as block:
            @block.vector
            def _(dve):
                dve.wait_ge(k.load_b.sem, k.load_b.all())
                nc.vector.memset(padded[:], 0.0)
                bias = w["in_bias"].rearrange("p (c i) -> p c i", i=3)
                nc.vector.tensor_tensor(k.v_bias[0:3, :], bias[:, :, 0], w["taps_T"], ALU.mult)
                for t in range(KT):
                    nc.vector.tensor_copy(w_branch[:, t], in_proj[:, t, :, 2])
                    for j in range(3):
                        nc.vector.tensor_tensor(w_taps[:, j, t], in_proj[:, t, :, 0], taps[:, :, j], ALU.mult)
                dve.wait_ge(sig("out").sem, sig("out").nth(0))
                nc.vector.tensor_copy(H13[:, 0], a_ps[0][:, 0:D])
                nc.vector.tensor_copy(H13[:, 1], b_ps[0][:, 0:D])
                nc.vector.tensor_copy(H22[:, 1], c_ps[0][:, 0:D])
                nc.vector.tensor_scalar(H22[:, 0], c_ps[0][:, 0:D], -1.0, None, ALU.mult)

            @block.tensor
            def _(pe):
                pe.wait_ge(k.load_b.sem, k.load_b.all())
                nc.tensor.matmul(a_ps[0][0:64, 0:P], w["fw1"], C("pos")[0:1, :], start=True, stop=True
                                 ).then_inc(sig("hidden_ps").sem, 1)
                pe.wait_ge(sig("hidden").sem, sig("hidden").nth(0))
                nc.tensor.matmul(a_ps[0][:, 0:P], w["fw2"], f1[:], start=True, stop=True
                                 ).then_inc(sig("hidden_ps").sem, 1)
                pe.wait_ge(sig("hidden").sem, sig("hidden").nth(1))
                odd = lambda ap: ap.rearrange("p (c i) -> p c i", i=2)[:, :, 1]
                nc.tensor.matmul(a_ps[0][:, 0:D], C("ones")[0:1, :], odd(w["fb3"]), start=True, stop=False)
                nc.tensor.matmul(a_ps[0][:, 0:D], f2[:], odd(w["fw3"]), start=False, stop=True
                                 ).then_inc(sig("hidden_ps").sem, 1)
                pe.wait_ge(sig("hidden").sem, sig("hidden").nth(2))
                for bank, name in ((a_ps, "dft_re"), (b_ps, "dft_re1"), (c_ps, "dft_im0")):
                    last = nc.tensor.matmul(bank[0][:, 0:D], C(name), coefs[:], start=True, stop=True)
                last.then_inc(sig("out").sem, 1)

            @block.scalar
            def _(act):
                act.wait_ge(k.load_b.sem, k.load_b.all())
                act.wait_ge(sig("hidden_ps").sem, sig("hidden_ps").nth(0))
                nc.scalar.activation(f1[:], a_ps[0][0:64, 0:P], ACT.Gelu, bias=w["fb1"]).then_inc(sig("hidden").sem, 1)
                act.wait_ge(sig("hidden_ps").sem, sig("hidden_ps").nth(1))
                nc.scalar.activation(f2[:], a_ps[0][:, 0:P], ACT.Gelu, bias=w["fb2"]).then_inc(sig("hidden").sem, 1)
                act.wait_ge(sig("hidden_ps").sem, sig("hidden_ps").nth(2))
                nc.scalar.copy(coefs[:], a_ps[0][:, 0:D]).then_inc(sig("hidden").sem, 1)

            @block.sync
            def _(sp):
                load_mixture(k, sp)
        sig("out").advance(1)
        sig("hidden").advance(3)
        sig("hidden_ps").advance(3)

        with nc.Block() as block:
            @block.vector
            def _(dve):
                with by_lanes(dve) as i:
                    norm_vector(nc, k, dve, lanes_of(i), pieces, lambda n, t: x[:, n], ["kept"])
                    for n, t in lanes_of(i):
                        dve.wait_ge(sig("scores").sem, sig("scores").nth(t))
                        spectrum = c_ps[n][:].rearrange("p (s c) -> p s c", s=2)
                        nc.vector.tensor_tensor(y1[:, n], spectrum, H13[:], ALU.mult)
                        nc.vector.tensor_tensor(y2[:, n], spectrum[:, ::-1, :], H22[:], ALU.mult
                                                ).then_inc(sig("rotated").sem, 1)
                    for n, t in lanes_of(i):
                        dve.wait_ge(sig("pv").sem, sig("pv").nth(t))
                        nc.vector.tensor_tensor(z[:, n], a_ps[n][:, 0:D], branch[:, n], ALU.mult
                                                ).then_inc(sig("o").sem, 1)
                    for n, t in lanes_of(i):
                        dve.wait_ge(sig("out").sem, sig("out").nth(t))
                        nc.vector.tensor_tensor(k.h[:, t, :], a_ps[n][:, 0:D], k.h[:, t, :], ALU.add
                                                ).then_inc(sig("kept").sem, 1)

            @block.gpsimd
            def _(pool):
                with by_lanes(pool) as i:
                    norm_pool(nc, k, pool, lanes_of(i), pieces)
                    for n, t in lanes_of(i):
                        pool.wait_ge(sig("rotated").sem, sig("rotated").nth(t))
                        nc.gpsimd.tensor_tensor(y1[:, n], y1[:, n], y2[:, n], ALU.add).then_inc(sig("qk").sem, 1)

            @block.tensor
            def _(pe):
                branch_bias = w["in_bias"][0:1].rearrange("p (c i) -> p c i", i=3)[:, :, 2]
                with by_lanes(pe) as i:
                    for n, t in lanes_of(i):
                        pe.wait_ge(sig("x").sem, sig("x").nth(t))
                        for f in range(KT):
                            last = nc.tensor.transpose(a_ps[n][:, P * f:P * (f + 1)], x[:, n, P * f:P * (f + 1)],
                                                       C("ident"))
                        last.then_inc(sig("turned").sem, 1)
                    for n, t in lanes_of(i):
                        pe.wait_ge(sig("xT").sem, sig("xT").nth(t))
                        nc.tensor.matmul(a_ps[n][:, 0:D], C("edges")[0:4, :], k.v_bias[:], start=True, stop=False)
                        for j in range(3):
                            for f in range(KT):
                                nc.tensor.matmul(a_ps[n][:, 0:D], padded[:, n, f, j:j + S], w_taps[:, j, f],
                                                 start=False, stop=(j == 2 and f == KT - 1))
                        nc.tensor.matmul(b_ps[n][:, 0:D], C("ones")[0:1, :], branch_bias, start=True, stop=False)
                        for f in range(KT):
                            last = nc.tensor.matmul(b_ps[n][:, 0:D], padded[:, n, f, 1:S + 1], w_branch[:, f],
                                                    start=False, stop=(f == KT - 1))
                        last.then_inc(sig("proj").sem, 1)
                    for n, t in lanes_of(i):
                        pe.wait_ge(sig("v1").sem, sig("v1").nth(t))
                        nc.tensor.matmul(c_ps[n][:, 0:D], C("dft_re"), v[:, n], start=True, stop=True)
                        nc.tensor.matmul(c_ps[n][:, D:2 * D], C("dft_im"), v[:, n], start=True, stop=True
                                         ).then_inc(sig("scores").sem, 1)
                    for n, t in lanes_of(i):
                        pe.wait_ge(sig("qk").sem, sig("qk").nth(t))
                        nc.tensor.matmul(a_ps[n][:, 0:D], C("inv_re"), y1[:, n, 0], start=True, stop=False)
                        nc.tensor.matmul(a_ps[n][:, 0:D], C("inv_im"), y1[:, n, 1], start=False, stop=True
                                         ).then_inc(sig("pv").sem, 1)
                    for n, t in lanes_of(i):
                        pe.wait_ge(sig("o").sem, sig("o").nth(t))
                        for f in range(KT):
                            last = nc.tensor.transpose(b_ps[n][:, P * f:P * (f + 1)], z[:, n, P * f:P * (f + 1)],
                                                       C("ident"))
                        last.then_inc(sig("oT_ps").sem, 1)
                    for n, t in lanes_of(i):
                        pe.wait_ge(sig("oT").sem, sig("oT").nth(t))
                        nc.tensor.matmul(a_ps[n][:, 0:D], C("ones")[0:1, :], w["out_b"], start=True, stop=False)
                        for f in range(KT):
                            last = nc.tensor.matmul(a_ps[n][:, 0:D], zT[:, n, f], w["out_w"][:, f, :], start=False,
                                                    stop=(f == KT - 1))
                        last.then_inc(sig("out").sem, 1)

            @block.scalar
            def _(act):
                halves = lambda bank: bank[:, 0:D].rearrange("p (t n) -> p t n", t=KT)
                with by_lanes(act) as i:
                    for n, t in lanes_of(i):
                        act.wait_ge(sig("turned").sem, sig("turned").nth(t))
                        nc.scalar.copy(padded[:, n, :, 1:S + 1], halves(a_ps[n])).then_inc(sig("xT").sem, 1)
                    for n, t in lanes_of(i):
                        act.wait_ge(sig("proj").sem, sig("proj").nth(t))
                        nc.scalar.copy(branch[:, n], b_ps[n][:, 0:D])
                        nc.scalar.copy(v[:, n], a_ps[n][:, 0:D]).then_inc(sig("v1").sem, 1)
                    for n, t in lanes_of(i):
                        act.wait_ge(sig("oT_ps").sem, sig("oT_ps").nth(t))
                        nc.scalar.copy(zT[:, n], halves(b_ps[n])).then_inc(sig("oT").sem, 1)
        for name in NORM_SIGNALS + ["scores", "rotated", "pv", "o", "out", "kept", "qk", "turned", "xT", "proj", "v1",
                                    "oT_ps", "oT"]:
            sig(name).advance(TILES)


def mixture(nc, k):
    E = 8
    r = k.region_a
    expert_w = r[:, 0:4096].rearrange("p (e t n) -> p e t n", e=E, t=KT)
    gate_w = r[:, 4096:4112].rearrange("p (t n) -> p t n", t=KT)
    gate_b, expert_b = r[0:1, 4112:4120], r[0:1, 4120:6168].rearrange("p (e n) -> p e n", e=E)
    C, sig = k.const, k.sig
    with ExitStack() as ctx:
        sb, ps = scratch(nc, ctx, "mixture")
        pieces = norm_pieces(ctx, nc, "mixture")
        x, xT = sb("x", [P, LANES, D]), sb("xT", [P, LANES, KT, P])
        gate, kept = sb("gate", [P, LANES, E]), sb("kept", [P, LANES, E])
        top, den, inv, none = (sb(name, [P, LANES, 1]) for name in ("top", "den", "inv", "none"))
        a_ps = [ps(f"a_ps{n}", [P, 2, D]) for n in range(LANES)]
        pair_ps = [[ps(f"pair_ps{n}_{q}", [P, 2, D]) for q in range(3)] + [a_ps[n]] for n in range(LANES)]
        with nc.Block() as block:
            @block.vector
            def _(dve):
                with by_lanes(dve) as i:
                    norm_vector(nc, k, dve, lanes_of(i), pieces, lambda n, t: x[:, n], [])
                    for n, t in lanes_of(i):
                        dve.wait_ge(sig("logits").sem, sig("logits").nth(t))
                        nc.vector.tensor_reduce(top[:, n], a_ps[n][:, 0, 0:E], AX_X, ALU.max
                                                ).then_inc(sig("top").sem, 1)
                    for n, t in lanes_of(i):
                        dve.wait_ge(sig("top").sem, sig("top").nth(t))
                        nc.vector.tensor_scalar(gate[:, n], a_ps[n][:, 0, 0:E], top[:, n], None, ALU.subtract
                                                ).then_inc(sig("shifted").sem, 1)
                    for n, t in lanes_of(i):
                        dve.wait_ge(sig("probs").sem, sig("probs").nth(t))
                        nc.vector.tensor_reduce(den[:, n], gate[:, n], AX_X, ALU.add).then_inc(sig("den").sem, 1)
                    for n, t in lanes_of(i):
                        dve.wait_ge(sig("den").sem, sig("den").nth(t))
                        nc.vector.reciprocal(inv[:, n], den[:, n]).then_inc(sig("recip").sem, 1)
                    for n, t in lanes_of(i):
                        dve.wait_ge(sig("recip").sem, sig("recip").nth(t))
                        nc.vector.tensor_scalar(gate[:, n], gate[:, n], inv[:, n], None, ALU.mult
                                                ).then_inc(sig("normed").sem, 1)
                    for n, t in lanes_of(i):
                        dve.wait_ge(sig("normed").sem, sig("normed").nth(t))
                        nc.vector.scalar_tensor_tensor(kept[:, n], gate[:, n], 0.1, gate[:, n], ALU.is_ge, ALU.mult
                                                       ).then_inc(sig("picked").sem, 1)
                    for n, t in lanes_of(i):
                        dve.wait_ge(sig("picked").sem, sig("picked").nth(t))
                        nc.vector.tensor_reduce(den[:, n], kept[:, n], AX_X, ALU.add).then_inc(sig("clipped").sem, 1)
                    for n, t in lanes_of(i):
                        dve.wait_ge(sig("clipped").sem, sig("clipped").nth(t))
                        nc.vector.scalar_tensor_tensor(none[:, n], den[:, n], 0.0, den[:, n], ALU.is_equal, ALU.add
                                                       ).then_inc(sig("unit").sem, 1)
                    for n, t in lanes_of(i):
                        dve.wait_ge(sig("unit").sem, sig("unit").nth(t))
                        nc.vector.reciprocal(inv[:, n], none[:, n]).then_inc(sig("rounded").sem, 1)
                    for n, t in lanes_of(i):
                        dve.wait_ge(sig("rounded").sem, sig("rounded").nth(t))
                        nc.vector.tensor_scalar(gate[:, n], kept[:, n], inv[:, n], None, ALU.mult
                                                ).then_inc(sig("weighed").sem, 1)
                    for e in range(E):
                        for n, t in lanes_of(i):
                            if e % 2 == 0:
                                pair = i * 4 * LANES + e // 2 * LANES + n
                                dve.wait_ge(sig("y_ps").sem, sig("y_ps").nth(pair))
                            item = i * E * LANES + e * LANES + n
                            if e == 0:
                                dve.wait_ge(sig("weighed").sem, sig("weighed").nth(t))
                            else:
                                dve.wait_ge(sig("combined").sem, sig("combined").before(item))
                            nc.vector.scalar_tensor_tensor(k.h[:, t, :], pair_ps[n][e // 2][:, e % 2],
                                                           gate[:, n, e:e + 1], k.h[:, t, :], ALU.mult, ALU.add
                                                           ).then_inc(sig("combined").sem, 1)

            @block.gpsimd
            def _(pool):
                with by_lanes(pool) as i:
                    norm_pool(nc, k, pool, lanes_of(i), pieces)

            @block.tensor
            def _(pe):
                pe.wait_ge(k.load_a.sem, k.load_a.all())
                with by_lanes(pe) as i:
                    for n, t in lanes_of(i):
                        pe.wait_ge(sig("x").sem, sig("x").nth(t))
                        pe.wait_ge(sig("combined").sem, i * E * LANES + (sig("combined").nth(n) - LANES))
                        for f in range(KT):
                            last = nc.tensor.transpose(a_ps[n][:, 0, P * f:P * (f + 1)], x[:, n, P * f:P * (f + 1)],
                                                       C("ident"))
                        last.then_inc(sig("turned").sem, 1)
                    for n, t in lanes_of(i):
                        pe.wait_ge(sig("xT").sem, sig("xT").nth(t))
                        nc.tensor.matmul(a_ps[n][:, 0, 0:E], C("ones")[0:1, :], gate_b, start=True, stop=False)
                        for f in range(KT):
                            last = nc.tensor.matmul(a_ps[n][:, 0, 0:E], xT[:, n, f], gate_w[:, f, :], start=False,
                                                    stop=(f == KT - 1))
                        last.then_inc(sig("logits").sem, 1)
                    for q in range(E // 2):
                        for n, t in lanes_of(i):
                            if q == 3:
                                pe.wait_ge(sig("shifted").sem, sig("shifted").nth(t))
                            out = pair_ps[n][q][:].rearrange("p e n -> p (e n)")
                            nc.tensor.matmul(out, C("ones")[0:1, :], expert_b[:, 2 * q:2 * q + 2].rearrange(
                                "p e n -> p (e n)"), start=True, stop=False)
                            for f in range(KT):
                                last = nc.tensor.matmul(out.rearrange("p (e n) -> p e n", e=2), xT[:, n, f],
                                                        expert_w[:, 2 * q:2 * q + 2, f, :],
                                                        start=False, stop=(f == KT - 1))
                            last.then_inc(sig("y_ps").sem, 1)

            @block.scalar
            def _(act):
                with by_lanes(act) as i:
                    for n, t in lanes_of(i):
                        act.wait_ge(sig("turned").sem, sig("turned").nth(t))
                        nc.scalar.copy(xT[:, n], a_ps[n][:, 0].rearrange("p (t n) -> p t n", t=KT)
                                       ).then_inc(sig("xT").sem, 1)
                    for n, t in lanes_of(i):
                        act.wait_ge(sig("shifted").sem, sig("shifted").nth(t))
                        nc.scalar.activation(gate[:, n], gate[:, n], ACT.Exp).then_inc(sig("probs").sem, 1)
        for name in NORM_SIGNALS + ["logits", "top", "shifted", "probs", "den", "recip", "normed", "picked", "clipped",
                                    "unit", "rounded", "weighed", "turned", "xT"]:
            sig(name).advance(TILES)
        sig("combined").advance(TILES * E)
        sig("y_ps").advance(TILES * E // 2)


class Context:
    pass


def tower(nc, dram, out):
    k = Context()
    k.dram = dram
    with ExitStack() as ctx:
        sb = lambda name, shape, dt=F32: ctx.enter_context(nc.sbuf_tensor(name, shape, dt))
        k.const_sb = sb("const_sb", [P, CONST_COLS])
        k.h = sb("h", [P, TILES, D])
        k.rows = sb("rows", [P, TILES, D])
        k.xT = sb("xT", [P, KT, TILES * S])
        k.region_a = sb("region_a", [P, 10240])
        k.region_b = sb("region_b", [P, 5376])
        k.logits = sb("logits", [P, TILES, 32])
        k.gates = sb("gates", [P, TILES, 33])
        k.minus_half, k.eps_ln, k.eps_rms = (sb(name, [P, 1]) for name in ("minus_half", "eps_ln", "eps_rms"))
        k.ident16 = sb("ident16", [P, P], BF16)
        k.conv_w, k.conv_b = sb("conv_w", [P, 8, 3]), sb("conv_b", [P, 8])
        k.shared = sb("shared", [P, 6 * P])
        k.v_bias = sb("v_bias", [4, D])
        k.idle = sb("idle", [P, LANES])
        k.emb_rows = sb("emb_rows", [LEVELS, D])
        k.level_cols = sb("level_cols", [P, B])
        k.score_rows = sb("score_rows", [LEVELS, 512])
        k.value_rows = sb("value_rows", [P, 4, D])
        k.const = lambda name: k.const_sb[:, CONST_AT[name][0]:CONST_AT[name][0] + CONST_AT[name][1]]
        signals = {}

        def sig(name):
            if name not in signals:
                signals[name] = Signal(ctx.enter_context(nc.semaphore("s_" + name)))
            return signals[name]
        k.sig = sig
        k.load_small, k.load_a, k.load_b, k.store = (
            Loads(ctx.enter_context(nc.semaphore(name))) for name in ("load_small", "load_a", "load_b", "store"))
        chain_sem = ctx.enter_context(nc.semaphore("vector_step"))
        steps = [0]

        def chain(dve):
            def link(ins):
                steps[0] += 1
                ins.then_inc(chain_sem, 1)
                dve.wait_ge(chain_sem, steps[0])
            return link
        k.chain = chain
        k.load_lane = [Loads(ctx.enter_context(nc.semaphore(f"load_lane{n}"))) for n in range(LANES)]
        for name in SIGNALS:
            sig(name)
        with nc.Block() as block:
            @block.sync
            def _(sp):
                for name in SIGNALS:
                    sp.sem_inc(sig(name).sem, HEADSTART)
        level_tables(nc, k)
        level_attention(nc, k)
        repeat_heads(nc, k)
        self_attention(nc, k, rope=False)
        route(nc, k, 8, 2, int(1.25 * B * S * 2 / 8), biased=False)
        experts(nc, k, 8, dram["L0_ffn_w1"].rearrange("e (t p) f -> p e t f", p=P),
                dram["L0_ffn_w2"].rearrange("e (t p) n -> p e t n", p=P), gated=True, target=k.rows[:],
                hidden_bias=None, prefetch=load_mha)
        close_gqa(nc, k)
        self_attention(nc, k, rope=True)
        experts(nc, k, 2, dram["L1_attn_W1"].rearrange("(t p) (e f) -> p e t f", p=P, e=2),
                dram["L1_attn_W2"].rearrange("(e t p) n -> p e t n", p=P, e=2), gated=False, target=k.h[:],
                hidden_bias=attention_weights(k.region_a)["b1"], prefetch=load_bitlinear)
        bitlinear(nc, k)
        decay_attention(nc, k)
        swiglu_gates(nc, k, k.shared[:])
        route(nc, k, 32, 4, 2 * 2 * 512 * 4 // 32, biased=True)
        swiglu_experts(nc, k, k.shared[:])
        hyena(nc, k)
        mixture(nc, k)
        store(nc, k, out)


def store(nc, k, out):
    with nc.Block() as block:
        @block.sync
        def _(sp):
            sp.dma_start(out.rearrange("b s d -> s b d"), k.h[:]).then_inc(k.store.sem, 16)
            k.store.more()
            for loads in (k.load_a, k.load_b, k.load_small, *k.load_lane):
                if loads.count:
                    sp.wait_ge(loads.sem, loads.all())
            sp.wait_ge(k.store.sem, k.store.all())


_INS = [
    "x", "L0_tok_level_emb", "L0_attn_query_mat", "L0_attn_key_mat", "L0_attn_value_mat", "L0_attn_linear_m1",
    "L0_ffn_qw", "L0_ffn_qb", "L0_ffn_kw", "L0_ffn_kb", "L0_ffn_vw", "L0_ffn_vb", "L0_ffn_ow", "L0_ffn_ob",
    "L0_ffn_gate_w", "L0_ffn_w1", "L0_ffn_w2", "L0_ffn_norm1_w", "L0_ffn_norm2_w",
    "L1_attn_Wq", "L1_attn_bq", "L1_attn_Wk", "L1_attn_bk", "L1_attn_Wv", "L1_attn_bv", "L1_attn_Wo",
    "L1_attn_bo", "L1_attn_W1", "L1_attn_b1", "L1_attn_W2", "L1_attn_b2", "L1_attn_g1", "L1_attn_beta1",
    "L1_attn_g2", "L1_attn_beta2", "L1_ffn_w1", "L1_ffn_conv_w", "L1_ffn_conv_b", "L1_ffn_w2",
    "L2_attn_q", "L2_attn_k", "L2_attn_log_decay", "L2_attn_norm_weight", "L2_attn_o_w",
    "L2_ffn_gate_w", "L2_ffn_bias", "L2_ffn_W1", "L2_ffn_W3", "L2_ffn_W2", "L2_ffn_sw1", "L2_ffn_sw3",
    "L2_ffn_sw2", "L3_attn_in_proj_w", "L3_attn_in_proj_b", "L3_attn_short_w", "L3_attn_short_b",
    "L3_attn_fw1", "L3_attn_fb1", "L3_attn_fw2", "L3_attn_fb2", "L3_attn_fw3", "L3_attn_fb3",
    "L3_attn_out_w", "L3_attn_out_b", "L3_ffn_gate_w", "L3_ffn_gate_b", "L3_ffn_expert_w", "L3_ffn_expert_b",
]


def kernel(**inputs):
    from concourse import bacc
    from concourse.bass_utils import run_bass_kernel_spmd

    nc = bacc.Bacc("TRN2", target_bir_lowering=False, num_devices=1)
    arrays, dram = {}, {}
    for name in _INS:
        a = np.ascontiguousarray(inputs[name])
        arrays[f"in_{name}"] = a
        dram[name] = nc.dram_tensor(f"in_{name}", a.shape, mybir.dt.from_np(a.dtype), kind="ExternalInput").ap()
    arrays["in_constants"] = shape_constants()
    dram["constants"] = nc.dram_tensor("in_constants", [P, CONST_COLS], F32, kind="ExternalInput").ap()
    out = nc.dram_tensor("out_h", [B, S, D], F32, kind="ExternalOutput").ap()
    tower(nc, dram, out)
    return run_bass_kernel_spmd(nc, [arrays], core_ids=[0]).results[0]["out_h"]
```

```python
from contextlib import ExitStack

import numpy as np

import concourse.bass as bass
from concourse import mybir
from concourse.alu_op_type import AluOpType as ALU

ACT = mybir.ActivationFunctionType
F32 = mybir.dt.float32
BF16 = mybir.dt.bfloat16
F32R = mybir.dt.float32r
I32 = mybir.dt.int32
U32 = mybir.dt.uint32
AX_X = mybir.AxisListType.X

B, S, D = 16, 128, 256
P = 128
TILES = B
KT = D // P
LANES = 2
HEADSTART = 16
CHUNK = 4
CHUNKS = TILES // CHUNK
HEADS, HD = 16, 16
LEVELS = 32
LN_EPS = 1e-5
RMS_EPS = 1e-6
BIG = 1e30
ROUND = 12582912.0

CONST_PARTS = [
    ("ident", P), ("causal", P), ("before", P), ("ones", P), ("iota", LEVELS),
    ("pairmask", 2), ("cos", D), ("sin", D), ("lag", P), ("dft_re", P), ("dft_im", P),
    ("dft_im0", P), ("dft_re1", P), ("inv_re", P), ("inv_im", P), ("edges", P), ("pos", P),
]
CONST_AT = {}
_n = 0
for _name, _width in CONST_PARTS:
    CONST_AT[_name] = (_n, _width)
    _n += _width
CONST_COLS = _n


def shape_constants():
    c = {}
    i = np.arange(P)
    c["ident"] = np.eye(P)
    c["causal"] = (i[:, None] <= i[None, :])
    c["before"] = (i[:, None] < i[None, :])
    c["ones"] = np.ones((P, P))
    c["iota"] = np.tile(np.arange(LEVELS), (P, 1))
    c["pairmask"] = (i[:, None] % 32) // 16 == np.arange(2)[None, :]
    inv_freq = (1.0 / np.float32(10000.0) ** (np.arange(0, HD, 2, dtype=np.float32) / np.float32(HD))).astype(np.float32)
    angle = (np.arange(S, dtype=np.float32)[:, None] * inv_freq[None, :]).astype(np.float64)
    cos, sin = np.repeat(np.cos(angle), 2, axis=1), np.repeat(np.sin(angle), 2, axis=1)
    sin[:, 0::2] *= -1.0
    c["cos"], c["sin"] = np.tile(cos, (1, HEADS)), np.tile(sin, (1, HEADS))
    c["lag"] = np.maximum(i[None, :] - i[:, None], 0)
    n = 2 * S
    w = 2 * np.pi * np.outer(i, i) / n
    re, im = np.cos(w), -np.sin(w)
    im0 = im.copy()
    im0[:, 0] = 0.0
    nyquist = np.cos(np.pi * i)
    packed = im.copy()
    packed[:, 0] = nyquist
    re1 = re.copy()
    re1[:, 0] = nyquist
    c["dft_re"], c["dft_im"], c["dft_im0"], c["dft_re1"] = re, packed, im0, re1
    both = np.where(i == 0, 1.0, 2.0)[:, None] / n
    c["inv_re"] = both * np.cos(w)
    inv_im = -2.0 / n * np.sin(w)
    inv_im[0] = nyquist / n
    c["inv_im"] = inv_im
    edges = np.ones((P, P))
    edges[0, 0] = 0.0
    edges[2, P - 1] = 0.0
    c["edges"] = edges
    c["pos"] = np.tile(np.linspace(0.0, 1.0, S, dtype=np.float32), (P, 1))
    return np.concatenate([np.asarray(c[name], np.float32) for name, _ in CONST_PARTS], axis=1)


SIGNALS = [
    "biased", "blocks", "clipped", "combined", "converted", "counts", "den", "diag", "expert_done",
    "first_tap", "hidden", "hidden_ps", "high", "highest", "k_pair", "kept", "last_T", "last_rows",
    "last_turned", "level", "logits", "low", "masked", "middle_tap", "moments", "moments_b",
    "moments_c", "normed", "o", "oT", "oT_ps", "onehot", "ones_set", "out", "pT", "pT_ps", "padded",
    "picked", "powers", "probs", "proj", "pv", "qT", "qk", "qkT_ps", "qk_raw", "ranks", "recip",
    "rotated", "rounded", "rstd", "rstd_b", "rstd_c", "scaled", "scores", "shifted", "shifted_var",
    "shifted_var_b", "shifted_var_c", "silu", "squares", "stats", "stats_b", "stats_c", "stored",
    "taps", "top", "top_ps", "turned", "unit", "unit_ps", "v1", "weighed", "x", "x2", "xT", "x_bo",
    "xn", "y_ps",
]


class Signal:

    def __init__(self, sem):
        self.sem, self.base = sem, HEADSTART

    def nth(self, n):
        return n + (self.base + 1)

    def before(self, n):
        return n + (self.base + 1 - LANES)

    def advance(self, n):
        self.base += n


class Loads:

    def __init__(self, sem):
        self.sem, self.count = sem, 0

    def more(self, n=1):
        self.count += n

    def all(self):
        return 16 * self.count


def scratch(nc, ctx, phase):
    def sb(name, shape, dt=F32):
        return ctx.enter_context(nc.sbuf_tensor(f"{phase}_{name}", shape, dt))

    def ps(name, shape, dt=F32):
        return ctx.enter_context(nc.psum_tensor(f"{phase}_{name}", shape, dt))
    return sb, ps


def spread(ap, shape):
    return ap.broadcast_to(shape)


def transposes(nc, out, blocks, ident):
    last = None
    for o, x in zip(out, blocks):
        last = nc.tensor.transpose(o, x, ident[0:x.shape[0], 0:x.shape[0]])
    return last


def level_tables(nc, k):
    with ExitStack() as ctx:
        sb, ps = scratch(nc, ctx, "level_tables")
        tok = sb("tok", [B, S], I32)
        tokf = sb("tokf", [B, S])
        opens, closes = sb("opens", [B, S]), sb("closes", [B, S])
        depth, low, high = sb("depth", [B, S]), sb("low", [B, S]), sb("high", [B, S])
        level = sb("level", [B, S])
        emb = sb("emb", [LEVELS, D])
        stats, mom = sb("stats0", [LEVELS, 6]), sb("mom0", [LEVELS, 2])
        rstd = sb("rstd0", [LEVELS, 1])
        xn = sb("xn0", [LEVELS, D])
        xnT = sb("xnT0", [P, KT, LEVELS])
        qT = sb("qT0", [P, 8, LEVELS])
        k_pairs = sb("k_pairs", [P, 8, 2 * LEVELS])
        v_quads = sb("v_quads", [P, 4, 2, P])
        turned = ps("turned0", [P, 512])
        q_ps, k_ps, v_ps = (ps(n, [P, 8, LEVELS]) for n in ("q_ps", "k_ps", "v_ps"))
        s_ps = ps("s_ps", [LEVELS, 512])
        m_ps = ps("m_ps", [P, 4, D])
        wq, wk, wv, m1 = (k.region_a[:, n * 2048:(n + 1) * 2048] for n in range(4))
        split = lambda w: w.rearrange("p (t n) -> p t n", t=KT)
        wq, wk, wv = split(wq), split(wk), split(wv)
        m1 = m1.rearrange("p (t n) -> p t n", n=D)
        C, sig = k.const, k.sig

        with nc.Block() as block:
            @block.sync
            def _(sp):
                sp.dma_start(tok[:], k.dram["x"]).then_inc(k.load_small.sem, 16)
                sp.dma_start(emb[:], k.dram["L0_tok_level_emb"]).then_inc(k.load_small.sem, 16)
                sp.dma_start(k.const_sb[:], k.dram["constants"]).then_inc(k.load_small.sem, 16)
                for w, name in ((wq, "query"), (wk, "key"), (wv, "value")):
                    sp.dma_start(w, k.dram[f"L0_attn_{name}_mat"].rearrange("(t p) h d -> p t (h d)", p=P)
                                 ).then_inc(k.load_a.sem, 16)
                sp.dma_start(m1, k.dram["L0_attn_linear_m1"].rearrange("(t p) n -> p t n", p=P)
                             ).then_inc(k.load_a.sem, 16)
            k.load_small.more(3)
            k.load_a.more(4)

            @block.vector
            def _(dve):
                link = k.chain(dve)
                dve.wait_ge(k.load_small.sem, k.load_small.all())
                link(nc.vector.tensor_scalar(k.emb_rows[:], emb[:], 0.15, None, ALU.mult))
                link(nc.vector.bn_stats(stats[:], k.emb_rows[:]))
                nc.vector.bn_aggr(mom[:], stats[:]).then_inc(sig("moments").sem, 1)
                link(nc.vector.tensor_copy(tokf[:], tok[:]))
                for count, ids in ((opens, (40., 91., 123.)), (closes, (41., 93., 125.))):
                    link(nc.vector.tensor_scalar(count[:], tokf[:], ids[0], None, ALU.is_equal))
                    for one in ids[1:]:
                        link(nc.vector.scalar_tensor_tensor(count[:], tokf[:], one, count[:],
                                                            ALU.is_equal, ALU.add))
                link(nc.vector.tensor_tensor(opens[:], opens[:], closes[:], ALU.subtract))
                link(nc.vector.memset(closes[:], 0.0))
                link(nc.vector.tensor_tensor_scan(depth[:], opens[:], closes[:], 0.0, ALU.add, ALU.add))
                link(nc.vector.tensor_scalar(low[:], depth[:], -1.0, None, ALU.mult))
                link(nc.vector.tensor_scalar(high[:], low[:], float(LEVELS - 1), None, ALU.add))
                link(nc.vector.tensor_tensor_scan(level[:], high[:], low[:], 0.0, ALU.min, ALU.max))
                nc.vector.tensor_tensor(level[:], level[:], depth[:], ALU.add).then_inc(sig("level").sem, 1)
                nc.vector.memset(k_pairs[:], 0.0)
                link(nc.vector.memset(v_quads[:], 0.0))
                dve.wait_ge(sig("rstd").sem, sig("rstd").nth(0))
                nc.vector.tensor_scalar(xn[:], k.emb_rows[:], mom[:, 0:1], rstd[:, 0:1], ALU.subtract,
                                        ALU.mult).then_inc(sig("xn").sem, 1)
                dve.wait_ge(sig("xT").sem, sig("xT").nth(0))
                nc.vector.tensor_copy(k.level_cols[:], turned[:, 256:256 + B])
                dve.wait_ge(sig("proj").sem, sig("proj").nth(0))
                kp = k_ps[:]
                vp = v_ps[:].rearrange("p (c u) l -> p c u l", u=2)
                for j in range(2):
                    rows = slice(64 * j, 64 * j + 64)
                    nc.vector.tensor_copy(k_pairs[rows, :, LEVELS * j:LEVELS * (j + 1)], kp[rows])
                    for u in range(2):
                        at = LEVELS * (2 * u + j)
                        last = nc.vector.tensor_copy(v_quads[rows, :, u, at:at + LEVELS], vp[rows, :, u, :])
                last.then_inc(sig("blocks").sem, 1)
                dve.wait_ge(sig("out").sem, sig("out").nth(0))
                nc.vector.tensor_copy(k.value_rows[:], m_ps[:])

            @block.gpsimd
            def _(pool):
                nc.gpsimd.memset(k.minus_half[:], -0.5)
                nc.gpsimd.memset(k.eps_ln[:], LN_EPS)
                nc.gpsimd.memset(k.eps_rms[:], RMS_EPS)
                pool.wait_ge(sig("moments").sem, sig("moments").nth(0))
                rsqrt(nc, pool, k, rstd[:], mom[:, 1:2], 1.0, LN_EPS, 0).then_inc(sig("rstd").sem, 1)

            @block.tensor
            def _(pe):
                pe.wait_ge(k.load_small.sem, k.load_small.all())
                pe.wait_ge(sig("level").sem, sig("level").nth(0))
                nc.tensor.transpose(turned[:, 256:256 + B], level[:], C("ident")[0:B, 0:B])
                pe.wait_ge(sig("xn").sem, sig("xn").nth(0))
                for t in range(KT):
                    last = nc.tensor.transpose(turned[:, LEVELS * t:LEVELS * (t + 1)], xn[:, P * t:P * (t + 1)],
                                               C("ident")[0:LEVELS, 0:LEVELS])
                last.then_inc(sig("turned").sem, 1)
                pe.wait_ge(k.load_a.sem, k.load_a.all())
                pe.wait_ge(sig("xT").sem, sig("xT").nth(0))
                for w, o in ((wq, q_ps), (wk, k_ps), (wv, v_ps)):
                    for m in range(8):
                        for t in range(KT):
                            last = nc.tensor.matmul(o[:, m, :], w[:, t, P * m:P * (m + 1)], xnT[:, t, :],
                                                    start=(t == 0), stop=(t == KT - 1))
                last.then_inc(sig("proj").sem, 1)
                pe.wait_ge(sig("blocks").sem, sig("blocks").nth(0))
                pe.wait_ge(sig("qk").sem, sig("qk").nth(0))
                for m in range(8):
                    last = nc.tensor.matmul(s_ps[:, 64 * m:64 * m + 64], qT[:, m, :], k_pairs[:, m, :],
                                            start=True, stop=True)
                last.then_inc(sig("scores").sem, 1)
                for c in range(4):
                    for u in range(2):
                        last = nc.tensor.matmul(m_ps[:, c, :], v_quads[:, c, u, :], m1[:, 2 * c + u, :],
                                                start=(u == 0), stop=(u == 1))
                last.then_inc(sig("out").sem, 1)

            @block.scalar
            def _(act):
                act.wait_ge(sig("turned").sem, sig("turned").nth(0))
                nc.scalar.copy(xnT[:], turned[:, 0:KT * LEVELS].rearrange("p (t l) -> p t l", t=KT)
                               ).then_inc(sig("xT").sem, 1)
                act.wait_ge(sig("proj").sem, sig("proj").nth(0))
                nc.scalar.mul(qT[:], q_ps[:], 8.0).then_inc(sig("qk").sem, 1)
                act.wait_ge(sig("scores").sem, sig("scores").nth(0))
                nc.scalar.copy(k.score_rows[:], s_ps[:])
        for name in ("moments", "level", "shifted_var", "rstd", "xn", "turned", "xT", "proj", "blocks", "qk", "scores", "out"):
            sig(name).advance(1)


def rsqrt(nc, pool, k, out, in_, scale, eps, t):
    nc.gpsimd.tensor_scalar(out, in_, scale, eps, ALU.mult, ALU.add).then_inc(k.sig("shifted_var").sem, 1)
    pool.wait_ge(k.sig("shifted_var").sem, k.sig("shifted_var").nth(t))
    return nc.gpsimd.tensor_tensor(out, out, spread(k.minus_half[0:out.shape[0], 0:1], out.shape), ALU.pow)


def level_attention(nc, k):
    with ExitStack() as ctx:
        sb, ps = scratch(nc, ctx, "level_attention")
        onehot = sb("onehot", [P, LANES, LEVELS])
        onehotT = sb("onehotT", [LEVELS, LANES, P])
        count = sb("count", [P, LANES, LEVELS])
        absent = sb("absent", [P, LANES, LEVELS])
        w = sb("weights", [P, LANES, HEADS, LEVELS])
        top, den = sb("top", [P, LANES, HEADS]), sb("den", [P, LANES, HEADS])
        wT = sb("wT", [P, LANES, 4, P])
        small_ps = [ps(f"small_ps{i}", [P, 512]) for i in range(LANES)]
        score_ps = [ps(f"score_ps{i}", [P, HEADS, LEVELS]) for i in range(LANES)]
        turn_ps = [ps(f"turn_ps{i}", [P, 4, P]) for i in range(LANES)]
        C, sig = k.const, k.sig
        names = ("onehot", "turned", "xT", "counts", "scores", "masked", "top", "shifted", "probs",
                 "weighed", "den", "recip", "normed", "pT_ps", "pT", "out", "stored")

        def each(eng):
            return eng.Fori(0, TILES // LANES)

        with nc.Block() as block:
            @block.vector
            def _(dve):
                with each(dve) as i:
                    lanes = [(n, i * LANES + n) for n in range(LANES)]
                    for n, t in lanes:
                        dve.wait_ge(sig("stored").sem, sig("stored").before(t))
                        nc.vector.tensor_scalar(onehot[:, n, :], C("iota"), k.level_cols[:, bass.ds(t, 1)], None,
                                                ALU.is_equal).then_inc(sig("onehot").sem, 1)
                    for n, t in lanes:
                        dve.wait_ge(sig("xT").sem, sig("xT").nth(t))
                        nc.vector.tensor_copy(count[:, n, :], small_ps[n][:, P:P + LEVELS])
                        nc.vector.tensor_scalar(absent[:, n, :], small_ps[n][:, P:P + LEVELS], 0.0, -BIG,
                                                ALU.is_equal, ALU.mult).then_inc(sig("counts").sem, 1)
                    for n, t in lanes:
                        dve.wait_ge(sig("scores").sem, sig("scores").nth(t))
                        dve.wait_ge(sig("counts").sem, sig("counts").nth(t))
                        nc.vector.tensor_tensor(w[:, n], score_ps[n][:],
                                                spread(absent[:, n, :].unsqueeze(1), [P, HEADS, LEVELS]),
                                                ALU.add).then_inc(sig("masked").sem, 1)
                    for n, t in lanes:
                        dve.wait_ge(sig("masked").sem, sig("masked").nth(t))
                        nc.vector.tensor_reduce(top[:, n, :], w[:, n], AX_X, ALU.max).then_inc(sig("top").sem, 1)
                    for n, t in lanes:
                        dve.wait_ge(sig("top").sem, sig("top").nth(t))
                        nc.vector.tensor_tensor(w[:, n], w[:, n],
                                                spread(top[:, n, :].unsqueeze(2), [P, HEADS, LEVELS]),
                                                ALU.subtract).then_inc(sig("shifted").sem, 1)
                    for n, t in lanes:
                        dve.wait_ge(sig("probs").sem, sig("probs").nth(t))
                        nc.vector.tensor_tensor(w[:, n], w[:, n],
                                                spread(count[:, n, :].unsqueeze(1), [P, HEADS, LEVELS]),
                                                ALU.mult).then_inc(sig("weighed").sem, 1)
                    for n, t in lanes:
                        dve.wait_ge(sig("weighed").sem, sig("weighed").nth(t))
                        nc.vector.tensor_reduce(den[:, n, :], w[:, n], AX_X, ALU.add).then_inc(sig("den").sem, 1)
                    for n, t in lanes:
                        dve.wait_ge(sig("den").sem, sig("den").nth(t))
                        nc.vector.reciprocal(top[:, n, :], den[:, n, :]).then_inc(sig("recip").sem, 1)
                    for n, t in lanes:
                        dve.wait_ge(sig("recip").sem, sig("recip").nth(t))
                        nc.vector.tensor_tensor(w[:, n], w[:, n],
                                                spread(top[:, n, :].unsqueeze(2), [P, HEADS, LEVELS]),
                                                ALU.mult).then_inc(sig("normed").sem, 1)

            @block.tensor
            def _(pe):
                with each(pe) as i:
                    lanes = [(n, i * LANES + n) for n in range(LANES)]
                    for n, t in lanes:
                        pe.wait_ge(sig("onehot").sem, sig("onehot").nth(t))
                        nc.tensor.transpose(small_ps[n][0:LEVELS, 0:P], onehot[:, n, :], C("ident"))
                        nc.tensor.matmul(small_ps[n][:, P:P + LEVELS], C("causal"), onehot[:, n, :], start=True,
                                         stop=True).then_inc(sig("turned").sem, 1)
                    for n, t in lanes:
                        pe.wait_ge(sig("xT").sem, sig("xT").nth(t))
                        nc.tensor.matmul(score_ps[n][:].rearrange("p h l -> p (h l)"), onehotT[:, n, :],
                                         k.score_rows[:], start=True, stop=True).then_inc(sig("scores").sem, 1)
                    for n, t in lanes:
                        pe.wait_ge(sig("normed").sem, sig("normed").nth(t))
                        for c in range(4):
                            last = nc.tensor.transpose(turn_ps[n][:, c, :], w[:, n, 4 * c:4 * c + 4, :].rearrange(
                                "p h l -> p (h l)"), C("ident"))
                        last.then_inc(sig("pT_ps").sem, 1)
                    for n, t in lanes:
                        out = small_ps[n][:, 256:512]
                        nc.tensor.matmul(out, onehotT[:, n, :], k.emb_rows[:], start=True, stop=False)
                        pe.wait_ge(sig("pT").sem, sig("pT").nth(t))
                        for c in range(4):
                            last = nc.tensor.matmul(out, wT[:, n, c, :], k.value_rows[:, c, :], start=False,
                                                    stop=(c == 3))
                        last.then_inc(sig("out").sem, 1)

            @block.scalar
            def _(act):
                with each(act) as i:
                    lanes = [(n, i * LANES + n) for n in range(LANES)]
                    for n, t in lanes:
                        act.wait_ge(sig("turned").sem, sig("turned").nth(t))
                        nc.scalar.copy(onehotT[:, n, :], small_ps[n][0:LEVELS, 0:P]).then_inc(sig("xT").sem, 1)
                    for n, t in lanes:
                        act.wait_ge(sig("shifted").sem, sig("shifted").nth(t))
                        nc.scalar.activation(w[:, n], w[:, n], ACT.Exp).then_inc(sig("probs").sem, 1)
                    for n, t in lanes:
                        act.wait_ge(sig("pT_ps").sem, sig("pT_ps").nth(t))
                        nc.scalar.copy(wT[:, n], turn_ps[n][:]).then_inc(sig("pT").sem, 1)
                    for n, t in lanes:
                        act.wait_ge(sig("out").sem, sig("out").nth(t))
                        nc.scalar.copy(k.h[:, t, :], small_ps[n][:, 256:512]).then_inc(sig("stored").sem, 1)

            @block.sync
            def _(sp):
                load_gqa(k, sp)
        for name in names:
            sig(name).advance(TILES)


def attention_weights(region):
    at = {"wqk": (0, 1024), "wv": (1024, 512), "wo": (1536, 512), "bqk": (2048, 512), "bv": (2560, 256),
          "bo": (2816, 256), "row": (3072, 256), "gate": (3328, 16), "k_raw": (3344, 128), "v_raw": (3472, 128),
          "kb_raw": (3600, 64), "vb_raw": (3664, 64), "g1": (3744, 2), "beta1": (3746, 2), "g2": (3748, 2),
          "beta2": (3750, 2), "b1": (3752, 8)}
    w = {name: region[:, a:a + n] for name, (a, n) in at.items()}
    for name in ("wqk", "wv", "wo", "gate", "k_raw", "v_raw"):
        w[name] = w[name].rearrange("p (t n) -> p t n", t=KT)
    return w


def by_rows(ap):
    return ap.rearrange("(t p) n -> p t n", p=P)


def as_row(ap):
    return ap.rearrange("(a n) -> a n", a=1)


def as_columns(ap):
    return ap.rearrange("(t p) -> p t", p=P)


def to_all(ap):
    return ap.partition_broadcast(P)


def load_gqa(k, sp):
    w, d = attention_weights(k.region_b), k.dram
    pairs = [
        (w["wqk"][:, :, 0:D], by_rows(d["L0_ffn_qw"])), (w["k_raw"], by_rows(d["L0_ffn_kw"])),
        (w["v_raw"], by_rows(d["L0_ffn_vw"])), (w["wo"], by_rows(d["L0_ffn_ow"])),
        (w["gate"], by_rows(d["L0_ffn_gate_w"])), (w["bqk"][:, 0:D], to_all(d["L0_ffn_qb"])),
        (w["kb_raw"], to_all(d["L0_ffn_kb"])), (w["vb_raw"], to_all(d["L0_ffn_vb"])),
        (w["bo"], to_all(d["L0_ffn_ob"])), (w["row"], to_all(d["L0_ffn_norm1_w"])),
    ]
    for to, source in pairs:
        sp.dma_start(to, source).then_inc(k.load_b.sem, 16)
    k.load_b.more(len(pairs))


def load_mha(k, sp):
    w, d = attention_weights(k.region_a), k.dram
    pairs = [
        (w["wqk"][:, :, 0:D], by_rows(d["L1_attn_Wq"])), (w["wqk"][:, :, D:2 * D], by_rows(d["L1_attn_Wk"])),
        (w["wv"], by_rows(d["L1_attn_Wv"])), (w["wo"], by_rows(d["L1_attn_Wo"])),
        (w["bqk"][:, 0:D], to_all(d["L1_attn_bq"])), (w["bqk"][:, D:2 * D], to_all(d["L1_attn_bk"])),
        (w["bv"], to_all(d["L1_attn_bv"])), (w["bo"], to_all(d["L1_attn_bo"])),
        (w["row"], to_all(d["L1_attn_b2"])), (w["g1"], as_columns(d["L1_attn_g1"])),
        (w["beta1"], as_columns(d["L1_attn_beta1"])), (w["g2"], as_columns(d["L1_attn_g2"])),
        (w["beta2"], as_columns(d["L1_attn_beta2"])), (w["b1"], as_columns(d["L1_attn_b1"])),
    ]
    for to, source in pairs:
        sp.dma_start(to, source, allow_slow_non_contiguous=True).then_inc(k.load_a.sem, 16)
    k.load_a.more(len(pairs))


def repeat_heads(nc, k):
    w = attention_weights(k.region_b)
    r4 = lambda ap: ap.rearrange("p (g r d) -> p g r d", g=4, r=4)
    with nc.Block() as block:
        @block.gpsimd
        def _(pool):
            pool.wait_ge(k.load_b.sem, k.load_b.all())
            for to, raw in ((w["wqk"][:, 0, D:], w["k_raw"][:, 0, :]), (w["wqk"][:, 1, D:], w["k_raw"][:, 1, :]),
                            (w["wv"][:, 0, :], w["v_raw"][:, 0, :]), (w["wv"][:, 1, :], w["v_raw"][:, 1, :]),
                            (w["bqk"][:, D:], w["kb_raw"]), (w["bv"], w["vb_raw"])):
                n = raw.shape[0]
                nc.gpsimd.tensor_copy(r4(to), spread(raw.rearrange("p (g d) -> p g d", g=4).unsqueeze(2),
                                                     [n, 4, 4, HD]))


def pipelined(eng, rounds, per, tail, ops):
    def issue(i, units, valid):
        for u in units:
            for lag, op in ops:
                if valid(u - lag):
                    op(i, u - lag)
    longest = max(lag for lag, _ in ops)
    issue(0, range(per), lambda v: v >= 0)
    with eng.Fori(1, rounds) as i:
        issue(i, range(per), lambda v: True)
    issue(rounds, range(tail + longest), lambda v: v < tail)


def self_attention(nc, k, rope):
    w = attention_weights(k.region_a if rope else k.region_b)
    loads = k.load_a if rope else k.load_b
    DEPTH = 2 * LANES
    with ExitStack() as ctx:
        sb, ps = scratch(nc, ctx, ("mha" if rope else "gqa"))
        stats, mom = sb("stats", [P, LANES, 6]), sb("mom", [P, LANES, 2])
        rstd = sb("rstd", [P, LANES, 1])
        stats_c, mom_c = sb("stats_c", [P, LANES, 6]), sb("mom_c", [P, LANES, 2])
        rstd_c = sb("rstd_c", [P, LANES, 1])
        x = sb("x_rows", [P, DEPTH, D])
        x_bo = sb("x_plus_bo", [P, LANES, D])
        xn = sb("xn", [P, LANES, D]) if rope else None
        xT = sb("x_turned", [P, LANES, KT, P])
        qk = sb("qk", [P, LANES, 2, D])
        qk_raw = sb("qk_raw", [P, LANES, 2, D]) if rope else qk
        swapped = sb("qk_swapped", [P, LANES, 2, D]) if rope else None
        v1 = sb("v_and_one", [P, LANES, HEADS, HD + 1])
        qT = sb("qT", [P, LANES, KT, P])
        k_pair = sb("k_pair", [P, LANES, KT, 2, P])
        e = sb("e", [P, LANES, HEADS, P])
        top, den = sb("top", [P, LANES, HEADS]), sb("den", [P, LANES, HEADS])
        o = sb("o", [P, LANES, D])
        oT = sb("oT", [P, LANES, KT, P])
        last_rows = sb("last_rows", [P, LANES, D])
        last_T = None if rope else sb("last_T", [P, LANES, KT, P])
        score_ps = ps("score_ps", [P, 4, KT, 2, P])
        a_ps = [ps(f"a_ps{n}", [P, 512]) for n in range(LANES)]
        b_ps = [ps(f"b_ps{n}", [P, 512]) for n in range(LANES)]
        C, sig = k.const, k.sig
        turn = lambda bank: bank[:, 0:D].rearrange("p (t n) -> p t n", t=KT)
        by_half = lambda bank: bank[:].rearrange("p (s f) -> p s f", s=2)
        by_head = lambda ap: ap.rearrange("p (h d) -> p h d", h=HEADS)

        def run(eng, ops):
            def of_tile(op):
                return lambda i, v: op(v % LANES, v % DEPTH, i * DEPTH + v)
            pipelined(eng, TILES // DEPTH, DEPTH, 0, [(lag, of_tile(op)) for lag, op in ops])

        with nc.Block() as block:
            @block.vector
            def _(dve):
                def stats_of(name, out, row):
                    def op(n, r, t):
                        if name:
                            dve.wait_ge(sig(name[0]).sem, sig(name[0]).nth(t))
                        nc.vector.bn_stats(out[0][:, n], row(n, r, t)).then_inc(sig(name[1] if name else "stats").sem, 1)
                        dve.wait_ge(sig(name[1] if name else "stats").sem, sig(name[1] if name else "stats").nth(t))
                        nc.vector.memset(k.idle[:, n:n + 1], 0.0)
                        nc.vector.bn_aggr(out[1][:, n], out[0][:, n]).then_inc(
                            sig(name[2] if name else "moments").sem, 1)
                    return op

                def norm_h(n, r, t):
                    dve.wait_ge(sig("kept").sem, sig("kept").nth(t) - DEPTH)
                    dve.wait_ge(sig("rstd").sem, sig("rstd").nth(t))
                    nc.vector.tensor_scalar(x[:, r], k.h[:, t, :], mom[:, n, 0:1], rstd[:, n], ALU.subtract,
                                            ALU.mult).then_inc(sig("x").sem, 1)

                def norm_x(n, r, t):
                    dve.wait_ge(sig("turned").sem, sig("turned").before(t))
                    dve.wait_ge(sig("rstd_b").sem, sig("rstd_b").nth(t))
                    nc.vector.tensor_scalar(xn[:, n], x[:, r], mom[:, n, 0:1], rstd[:, n], ALU.subtract,
                                            ALU.mult).then_inc(sig("xn").sem, 1)

                def biases(n, r, t):
                    dve.wait_ge(sig("proj").sem, sig("proj").nth(t))
                    if rope:
                        dve.wait_ge(sig("qk").sem, sig("qk").before(t))
                    nc.vector.tensor_tensor(qk_raw[:, n], by_half(a_ps[n]), w["bqk"].rearrange("p (s f) -> p s f", s=2),
                                            ALU.add).then_inc(sig("qk_raw" if rope else "qk").sem, 1)
                    nc.vector.tensor_tensor(v1[:, n, :, 0:HD], by_head(b_ps[n][:, 0:D]), by_head(w["bv"]),
                                            ALU.add).then_inc(sig("v1").sem, 1)

                def rotate(n, r, t):
                    dve.wait_ge(sig("qk_raw").sem, sig("qk_raw").nth(t))
                    for s in range(2):
                        nc.vector.tensor_tensor(
                            swapped[:, n, s].rearrange("p (f two) -> p f two", two=2),
                            qk_raw[:, n, s].rearrange("p (f two) -> p f two", two=2)[:, :, ::-1],
                            C("sin").rearrange("p (f two) -> p f two", two=2), ALU.mult)
                    nc.vector.tensor_tensor(qk[:, n], qk_raw[:, n], spread(C("cos").unsqueeze(1), [P, 2, D]),
                                            ALU.mult).then_inc(sig("rotated").sem, 1)

                def key_pairs(n, r, t):
                    dve.wait_ge(sig("qT").sem, sig("qT").nth(t))
                    for f in range(KT):
                        last = nc.vector.tensor_tensor(
                            k_pair[:, n, f],
                            spread(a_ps[n][:, P * (KT + f):P * (KT + f + 1)].unsqueeze(1), [P, 2, P]),
                            spread(C("pairmask").unsqueeze(2), [P, 2, P]), ALU.mult)
                    last.then_inc(sig("k_pair").sem, 1)

                def shift(n, r, t):
                    dve.wait_ge(sig("scores").sem, sig("scores").nth(t))
                    all_heads = score_ps[:].rearrange("p g f j z -> p (g f j) z")
                    nc.vector.tensor_reduce(top[:, n], all_heads, AX_X, ALU.max).then_inc(sig("top").sem, 1)
                    dve.wait_ge(sig("top").sem, sig("top").nth(t))
                    nc.vector.tensor_tensor(e[:, n], all_heads, spread(top[:, n].unsqueeze(2), [P, HEADS, P]),
                                            ALU.subtract).then_inc(sig("shifted").sem, 1)

                def normalise(n, r, t):
                    dve.wait_ge(sig("kept").sem, sig("kept").before(t))
                    dve.wait_ge(sig("stored").sem, sig("stored").before(t))
                    dve.wait_ge(sig("pv").sem, sig("pv").nth(t))
                    heads = by_head(a_ps[n][:, 0:HEADS * (HD + 1)])
                    nc.vector.reciprocal(den[:, n], heads[:, :, HD]).then_inc(sig("recip").sem, 1)
                    dve.wait_ge(sig("recip").sem, sig("recip").nth(t))
                    nc.vector.tensor_tensor(by_head(o[:, n]), heads[:, :, 0:HD],
                                            spread(den[:, n].unsqueeze(2), [P, HEADS, HD]),
                                            ALU.mult).then_inc(sig("o").sem, 1)

                def add_output(n, r, t):
                    dve.wait_ge(sig("x_bo").sem, sig("x_bo").nth(t))
                    dve.wait_ge(sig("out").sem, sig("out").nth(t))
                    nc.vector.tensor_tensor(x[:, r], a_ps[n][:, 0:D], x_bo[:, n], ALU.add).then_inc(sig("x2").sem, 1)

                def norm_output(n, r, t):
                    dve.wait_ge(sig("rstd_c").sem, sig("rstd_c").nth(t))
                    if rope:
                        last = nc.vector.tensor_scalar(last_rows[:, n], x[:, r], mom_c[:, n, 0:1], rstd_c[:, n],
                                                       ALU.subtract, ALU.mult)
                    else:
                        last = nc.vector.scalar_tensor_tensor(last_rows[:, n], x[:, r], rstd_c[:, n], w["row"],
                                                              ALU.mult, ALU.mult)
                    last.then_inc(sig("last_rows").sem, 1)

                stats_h = stats_of(None, (stats, mom), lambda n, r, t: k.h[:, t, :])
                dve.wait_ge(loads.sem, loads.all())
                nc.vector.memset(v1[:], 1.0).then_inc(sig("ones_set").sem, 1)
                dve.wait_ge(sig("ones_set").sem, sig("ones_set").nth(0))
                if rope:
                    stats_x = stats_of(("x", "stats_b", "moments_b"), (stats, mom), lambda n, r, t: x[:, r])
                    stats_x2 = stats_of(("x2", "stats_c", "moments_c"), (stats_c, mom_c), lambda n, r, t: x[:, r])
                    run(dve, [(2, shift), (0, stats_h), (1, biases), (1, rotate), (0, norm_h), (0, stats_x),
                              (1, key_pairs), (0, norm_x), (2, normalise), (2, add_output), (2, stats_x2),
                              (2, norm_output)])
                else:
                    run(dve, [(2, shift), (0, stats_h), (1, biases), (0, norm_h), (1, key_pairs), (2, normalise),
                              (2, add_output), (2, norm_output)])

            @block.gpsimd
            def _(pool):
                def inverse_root(source, shifted, done, out, variance, eps):
                    def op(n, r, t):
                        pool.wait_ge(sig(source).sem, sig(source).nth(t))
                        nc.gpsimd.tensor_tensor(out[:, n], variance[:, n, 1:2], eps[:], ALU.add
                                                ).then_inc(sig(shifted).sem, 1)
                        pool.wait_ge(sig(shifted).sem, sig(shifted).nth(t))
                        nc.gpsimd.tensor_tensor(out[:, n], out[:, n], k.minus_half[:], ALU.pow
                                                ).then_inc(sig(done).sem, 1)
                    return op

                def add_pairs(n, r, t):
                    pool.wait_ge(sig("rotated").sem, sig("rotated").nth(t))
                    nc.gpsimd.tensor_tensor(qk[:, n], qk[:, n], swapped[:, n], ALU.add).then_inc(sig("qk").sem, 1)

                def add_output_bias(n, r, t):
                    pool.wait_ge(sig("x2").sem, sig("x2").before(t))
                    pool.wait_ge(sig("x").sem, sig("x").nth(t))
                    nc.gpsimd.tensor_tensor(x_bo[:, n], x[:, r], w["bo"], ALU.add).then_inc(sig("x_bo").sem, 1)

                def keep(n, r, t):
                    pool.wait_ge(sig("last_rows").sem, sig("last_rows").nth(t))
                    if rope:
                        nc.gpsimd.tensor_tensor(o[:, n], x[:, r], w["row"], ALU.add).then_inc(sig("biased").sem, 1)
                        pool.wait_ge(sig("biased").sem, sig("biased").nth(t))
                        nc.gpsimd.tensor_tensor(k.h[:, t, :], k.h[:, t, :], o[:, n], ALU.add
                                                ).then_inc(sig("kept").sem, 1)
                    else:
                        nc.gpsimd.tensor_copy(k.rows[:, t, :], last_rows[:, n]).then_inc(sig("kept").sem, 1)

                pool.wait_ge(loads.sem, loads.all())
                root_h = inverse_root("moments", "shifted_var", "rstd", rstd, mom, k.eps_ln)
                if rope:
                    root_x = inverse_root("moments_b", "shifted_var_b", "rstd_b", rstd, mom, k.eps_ln)
                    root_x2 = inverse_root("moments_c", "shifted_var_c", "rstd_c", rstd_c, mom_c, k.eps_ln)
                    run(pool, [(0, root_h), (1, add_pairs), (0, root_x), (1, add_output_bias), (2, root_x2),
                               (2, keep)])
                else:
                    root_x2 = inverse_root("squares", "shifted_var_c", "rstd_c", rstd_c, mom_c, k.eps_rms)
                    run(pool, [(0, root_h), (1, add_output_bias), (2, root_x2), (2, keep)])

            @block.tensor
            def _(pe):
                def turn_x(n, r, t):
                    ready = sig("xn") if rope else sig("x")
                    pe.wait_ge(ready.sem, ready.nth(t))
                    pe.wait_ge(sig("x2").sem, sig("x2").before(t))
                    rows = xn[:, n] if rope else x[:, r]
                    for f in range(KT):
                        last = nc.tensor.transpose(turn(a_ps[n])[:, f], rows[:, P * f:P * (f + 1)], C("ident"))
                    last.then_inc(sig("turned").sem, 1)

                def project(n, r, t):
                    pe.wait_ge(sig("stored").sem, sig("stored").before(t))
                    pe.wait_ge(sig("xT").sem, sig("xT").nth(t))
                    for bank, width, name in ((a_ps[n], 2 * D, "wqk"), (b_ps[n], D, "wv")):
                        for f in range(KT):
                            last = nc.tensor.matmul(bank[:, 0:width], xT[:, n, f], w[name][:, f, :],
                                                    start=(f == 0), stop=(f == KT - 1))
                    last.then_inc(sig("proj").sem, 1)

                def turn_qk(n, r, t):
                    pe.wait_ge(sig("v1").sem, sig("v1").nth(t))
                    pe.wait_ge(sig("qk").sem, sig("qk").nth(t))
                    for f in range(2 * KT):
                        last = nc.tensor.transpose(a_ps[n][:, P * f:P * (f + 1)],
                                                   qk[:, n, f // KT, P * (f % KT):P * (f % KT + 1)], C("ident"))
                    last.then_inc(sig("qkT_ps").sem, 1)

                def scores(parts):
                    def op(n, r, t):
                        if parts[0] == 0:
                            pe.wait_ge(sig("k_pair").sem, sig("k_pair").nth(t))
                            pe.wait_ge(sig("shifted").sem, sig("shifted").nth(t) - 1)
                        for m in parts:
                            f, g = m // 4, m % 4
                            rows = slice(32 * g, 32 * g + 32)
                            last = nc.tensor.matmul(score_ps[:, g, f].rearrange("p j z -> p (j z)"),
                                                    qT[rows, n, f, :],
                                                    k_pair[rows, n, f].rearrange("p j z -> p (j z)"),
                                                    start=True, stop=True)
                        if parts[-1] == 7:
                            last.then_inc(sig("scores").sem, 1)
                    return op

                def turn_probs(q):
                    def op(n, r, t):
                        if q == 0:
                            pe.wait_ge(sig("probs").sem, sig("probs").nth(t))
                        if q >= 2:
                            pe.wait_ge(sig("pT").sem, sig("pT").nth(t * 4 + (q - 2)))
                        bank = (a_ps, b_ps)[q % 2][n]
                        for m in range(4):
                            last = nc.tensor.transpose(bank[:, P * m:P * (m + 1)], e[:, n, 4 * q + m, :], C("ident"))
                        last.then_inc(sig("pT_ps").sem, 1)
                    return op

                def weigh(n, r, t):
                    pe.wait_ge(sig("pT").sem, sig("pT").nth(t * 4 + 3))
                    for m in range(HEADS):
                        g, f, j = m // 4, m // 2 % 2, m % 2
                        head = 8 * f + 2 * g + j
                        last = nc.tensor.matmul(a_ps[n][:, head * (HD + 1):(head + 1) * (HD + 1)], e[:, n, m, :],
                                                v1[:, n, head, :], start=True, stop=True)
                    last.then_inc(sig("pv").sem, 1)

                def turn_o(n, r, t):
                    pe.wait_ge(sig("o").sem, sig("o").nth(t))
                    for f in range(KT):
                        last = nc.tensor.transpose(turn(b_ps[n])[:, f], o[:, n, P * f:P * (f + 1)], C("ident"))
                    last.then_inc(sig("oT_ps").sem, 1)

                def output(n, r, t):
                    pe.wait_ge(sig("oT").sem, sig("oT").nth(t))
                    for f in range(KT):
                        last = nc.tensor.matmul(a_ps[n][:, 0:D], oT[:, n, f], w["wo"][:, f, :], start=(f == 0),
                                                stop=(f == KT - 1))
                    last.then_inc(sig("out").sem, 1)

                def turn_last(n, r, t):
                    pe.wait_ge(sig("last_rows").sem, sig("last_rows").nth(t))
                    for f in range(KT):
                        last = nc.tensor.transpose(turn(b_ps[n])[:, f], last_rows[:, n, P * f:P * (f + 1)],
                                                   C("ident"))
                    last.then_inc(sig("last_turned").sem, 1)

                def logits(n, r, t):
                    pe.wait_ge(sig("last_T").sem, sig("last_T").nth(t))
                    for f in range(KT):
                        last = nc.tensor.matmul(b_ps[n][:, 0:8], last_T[:, n, f], w["gate"][:, f, :],
                                                start=(f == 0), stop=(f == KT - 1))
                    last.then_inc(sig("logits").sem, 1)

                pe.wait_ge(loads.sem, loads.all())
                run(pe, [(1, turn_x), (1, project), (2, turn_probs(0)), (2, turn_probs(1)), (1, turn_qk),
                         (2, turn_probs(2)), (2, turn_probs(3)), (2, weigh), (1, scores((0, 1))), (2, turn_o),
                         (1, scores((2, 3))), (2, output), (1, scores((4, 5, 6, 7))), (2, turn_last)]
                    + ([] if rope else [(2, logits)]))

            @block.scalar
            def _(act):
                def keep_xT(n, r, t):
                    act.wait_ge(sig("turned").sem, sig("turned").nth(t))
                    if rope:
                        for f in range(KT):
                            last = nc.scalar.activation(xT[:, n, f], turn(a_ps[n])[:, f], ACT.Identity,
                                                        bias=w["beta1"][:, f:f + 1], scale=w["g1"][:, f:f + 1])
                        last.then_inc(sig("xT").sem, 1)
                    else:
                        nc.scalar.copy(xT[:, n], turn(a_ps[n])).then_inc(sig("xT").sem, 1)

                def exponents(n, r, t):
                    act.wait_ge(sig("shifted").sem, sig("shifted").nth(t))
                    nc.scalar.activation(e[:, n], e[:, n], ACT.Exp, scale=HD ** -0.5).then_inc(sig("probs").sem, 1)

                def keep_probs(q):
                    def op(n, r, t):
                        act.wait_ge(sig("pT_ps").sem, sig("pT_ps").nth(t * 4 + q))
                        bank = (a_ps, b_ps)[q % 2][n]
                        nc.scalar.copy(e[:, n, 4 * q:4 * q + 4, :], bank[:].rearrange("p (m q) -> p m q", m=4)
                                       ).then_inc(sig("pT").sem, 1)
                    return op

                def keep_qT(n, r, t):
                    act.wait_ge(sig("qkT_ps").sem, sig("qkT_ps").nth(t))
                    nc.scalar.copy(qT[:, n], turn(a_ps[n])).then_inc(sig("qT").sem, 1)

                def keep_oT(n, r, t):
                    act.wait_ge(sig("oT_ps").sem, sig("oT_ps").nth(t))
                    nc.scalar.copy(oT[:, n], turn(b_ps[n])).then_inc(sig("oT").sem, 1)

                def mean_square(n, r, t):
                    act.wait_ge(sig("x2").sem, sig("x2").nth(t))
                    nc.scalar.activation(o[:, n], x[:, r], ACT.Square, scale=D ** -0.5, accum_out=mom_c[:, n, 1:2]
                                         ).then_inc(sig("squares").sem, 1)

                def keep_last(n, r, t):
                    act.wait_ge(sig("last_turned").sem, sig("last_turned").nth(t))
                    if rope:
                        for f in range(KT):
                            last = nc.scalar.activation(k.xT[:, f, bass.ds(t * P, P)], turn(b_ps[n])[:, f],
                                                        ACT.Identity, bias=w["beta2"][:, f:f + 1],
                                                        scale=w["g2"][:, f:f + 1])
                        last.then_inc(sig("stored").sem, 1)
                    else:
                        nc.scalar.copy(k.xT[:, :, bass.ds(t * P, P)], turn(b_ps[n]))
                        nc.scalar.copy(last_T[:, n], turn(b_ps[n])).then_inc(sig("last_T").sem, 1)

                def keep_logits(n, r, t):
                    act.wait_ge(sig("logits").sem, sig("logits").nth(t))
                    nc.scalar.copy(k.logits[:, t, 0:8], b_ps[n][:, 0:8]).then_inc(sig("stored").sem, 1)

                act.wait_ge(loads.sem, loads.all())
                ops = [(1, keep_xT), (2, exponents), (2, keep_probs(0)), (2, keep_probs(1)), (1, keep_qT),
                       (2, keep_probs(2)), (2, keep_probs(3)), (2, keep_oT)]
                run(act, ops + ([(2, keep_last)] if rope else [(2, mean_square), (2, keep_last), (2, keep_logits)]))
        names = ["stats", "moments", "shifted_var", "rstd", "x", "turned", "xT", "proj", "qk", "v1", "qkT_ps", "qT",
                 "k_pair", "scores", "top", "shifted", "probs", "pv", "recip", "o", "oT_ps", "oT", "out", "x_bo", "x2",
                 "shifted_var_c", "rstd_c", "last_rows", "last_turned", "stored", "kept"]
        names += (["stats_b", "moments_b", "shifted_var_b", "rstd_b", "xn", "qk_raw", "rotated", "stats_c",
                   "moments_c", "biased"] if rope else ["squares", "last_T", "logits"])
        for name in names:
            sig(name).advance(TILES)
        for name in ("pT_ps", "pT"):
            sig(name).advance(4 * TILES)
        sig("ones_set").advance(1)


def route(nc, k, experts, chosen, capacity, biased):
    with ExitStack() as ctx:
        sb, ps = scratch(nc, ctx, f"route{experts}")
        shape = [P, TILES, experts]
        probs, choice = sb("probs", shape), sb("choice", shape)
        best, index = sb("best", [P, TILES, 8]), sb("index", [P, TILES, 8], U32)
        indexf = sb("indexf", [P, TILES, 8])
        picked, hit, earlier = sb("picked", shape), sb("hit", shape), sb("earlier", shape)
        total = sb("total", [P, TILES])
        bias = sb("bias", [P, experts])
        rank_ps = ps("rank_ps", shape)
        C, sig = k.const, k.sig
        gates = k.gates[:, :, 0:experts]
        flat = lambda x: x[:].rearrange("p t e -> p (t e)")
        with nc.Block() as block:
            if biased:
                @block.sync
                def _(sp):
                    sp.dma_start(bias[:], to_all(k.dram["L2_ffn_bias"])).then_inc(k.load_small.sem, 16)
                k.load_small.more()

            @block.scalar
            def _(act):
                nc.scalar.activation(probs[:], k.logits[:, :, 0:experts], ACT.Exp, scale=-1.0
                                     ).then_inc(sig("probs").sem, 1)

            @block.vector
            def _(dve):
                link = k.chain(dve)
                nc.vector.memset(k.gates[:], 1.0)
                dve.wait_ge(sig("probs").sem, sig("probs").nth(0))
                link(nc.vector.tensor_scalar(probs[:], probs[:], 1.0, None, ALU.add))
                link(nc.vector.reciprocal(probs[:], probs[:]))
                if biased:
                    dve.wait_ge(k.load_small.sem, k.load_small.all())
                    link(nc.vector.tensor_tensor(choice[:], probs[:], spread(bias[:].unsqueeze(1), shape), ALU.add))
                else:
                    link(nc.vector.tensor_copy(choice[:], probs[:]))
                for t in range(TILES):
                    last = nc.vector.max(best[:, t], choice[:, t])
                link(last)
                for t in range(TILES):
                    last = nc.vector.max_index(index[:, t], best[:, t], choice[:, t])
                link(last)
                link(nc.vector.tensor_copy(indexf[:], index[:]))
                iota = spread(C("iota")[:, 0:experts].unsqueeze(1), shape)
                for j in range(chosen):
                    to = hit if j else picked
                    link(nc.vector.tensor_tensor(to[:], iota, spread(indexf[:, :, j:j + 1], shape), ALU.is_equal))
                    if j:
                        link(nc.vector.tensor_tensor(picked[:], picked[:], hit[:], ALU.add))
                link(nc.vector.memset(earlier[:, 0], 0.0))
                for t in range(1, TILES):
                    link(nc.vector.tensor_tensor(earlier[:, t], earlier[:, t - 1], picked[:, t - 1], ALU.add))
                nc.vector.tensor_tensor(hit[:], picked[:], probs[:], ALU.mult).then_inc(sig("picked").sem, 1)
                dve.wait_ge(sig("picked").sem, sig("picked").nth(0))
                link(nc.vector.tensor_reduce(total[:], hit[:], AX_X, ALU.add))
                if biased:
                    link(nc.vector.tensor_scalar(total[:], total[:], 1e-12, None, ALU.max))
                else:
                    link(nc.vector.tensor_scalar(total[:], total[:], 1e-6, None, ALU.add))
                link(nc.vector.reciprocal(total[:], total[:]))
                link(nc.vector.tensor_tensor(hit[:], hit[:], spread(total[:].unsqueeze(2), shape), ALU.mult))
                dve.wait_ge(sig("ranks").sem, sig("ranks").nth(0))
                nc.vector.scalar_tensor_tensor(gates, rank_ps[:], float(capacity), hit[:], ALU.is_lt, ALU.mult)

            @block.tensor
            def _(pe):
                pe.wait_ge(sig("picked").sem, sig("picked").nth(0))
                nc.tensor.matmul(flat(rank_ps), C("before"), flat(picked), start=True, stop=False)
                nc.tensor.matmul(flat(rank_ps), C("ones"), flat(earlier), start=False,
                                 stop=True).then_inc(sig("ranks").sem, 1)
        for name in ("probs", "picked", "ranks"):
            sig(name).advance(1)


def experts(nc, k, count, w1, w2, gated, target, hidden_bias, prefetch):
    F = 4
    WIDE = CHUNK * P
    with ExitStack() as ctx:
        sb, ps = scratch(nc, ctx, f"experts{count}")
        w1_sb, w2_sb = sb("w1", [P, LANES, KT, F * P]), sb("w2", [P, LANES, F, D])
        hid = [sb(f"hidden{n}", [P, F, WIDE]) for n in range(2)]
        hid_ps = ps("hidden_ps", [P, F, WIDE])
        y_ps = [ps(f"y_ps{n}", [P, CHUNK, D]) for n in range(2)]
        sig = k.sig
        rounds = count // LANES
        unit_order = [(n, c) for n in range(LANES) for c in range(CHUNKS)]
        PER = len(unit_order)

        with nc.Block() as block:
            @block.sync
            def _(sp):
                prefetch(k, sp)
                with sp.Fori(0, rounds) as i:
                    for n in range(LANES):
                        e = i * LANES + n
                        sp.wait_ge(sig("expert_done").sem, sig("expert_done").before(e))
                        sp.dma_start(w1_sb[:, n], w1[:, e]).then_inc(k.load_lane[n].sem, 16)
                        sp.dma_start(w2_sb[:, n], w2[:, e]).then_inc(k.load_lane[n].sem, 16)

            @block.tensor
            def _(pe):
                with pe.Fori(0, rounds) as i:
                    def first(n, c, u):
                        if c == 0:
                            pe.wait_ge(k.load_lane[n].sem, i * 32 + (k.load_lane[n].all() + 32))
                        for f in range(F):
                            pe.wait_ge(sig("hidden").sem, i * (F * PER) + (sig("hidden").nth(F * u + f) - F))
                            for t in range(KT):
                                last = nc.tensor.matmul(hid_ps[:, f], w1_sb[:, n, t, P * f:P * (f + 1)],
                                                        k.xT[:, t, c * WIDE:(c + 1) * WIDE], start=(t == 0),
                                                        stop=(t == KT - 1))
                            last.then_inc(sig("hidden_ps").sem, 1)

                    def second(n, c, u):
                        pe.wait_ge(sig("hidden").sem, i * (F * PER) + sig("hidden").nth(F * u + F - 1))
                        pe.wait_ge(sig("combined").sem, i * PER + sig("combined").before(u))
                        for j in range(CHUNK):
                            for f in range(F):
                                last = nc.tensor.matmul(y_ps[u % 2][:, j], hid[u % 2][:, f, P * j:P * (j + 1)],
                                                        w2_sb[:, n, f, :], start=(f == 0), stop=(f == F - 1))
                        last.then_inc(sig("y_ps").sem, 1)
                    for u, (n, c) in enumerate(unit_order):
                        first(n, c, u)
                        if u:
                            second(*unit_order[u - 1], u - 1)
                    second(*unit_order[-1], PER - 1)

            @block.scalar
            def _(act):
                with act.Fori(0, rounds) as i:
                    for u, (n, c) in enumerate(unit_order):
                        act.wait_ge(sig("y_ps").sem, i * PER + sig("y_ps").before(u))
                        for f in range(F):
                            act.wait_ge(sig("hidden_ps").sem, i * (F * PER) + sig("hidden_ps").nth(F * u + f))
                            if hidden_bias is None:
                                last = nc.scalar.activation(hid[u % 2][:, f], hid_ps[:, f], ACT.Gelu)
                            else:
                                column = (i * LANES + n) * F + f
                                last = nc.scalar.activation(hid[u % 2][:, f], hid_ps[:, f], ACT.Relu,
                                                            bias=hidden_bias[:, bass.ds(column, 1)])
                            last.then_inc(sig("hidden").sem, 1)

            @block.vector
            def _(dve):
                with dve.Fori(0, rounds) as i:
                    for u, (n, c) in enumerate(unit_order):
                        dve.wait_ge(sig("y_ps").sem, i * PER + sig("y_ps").nth(u))
                        dve.wait_ge(sig("combined").sem, i * PER + (sig("combined").nth(u) - 1))
                        for j in range(CHUNK):
                            t = CHUNK * c + j
                            if gated:
                                last = nc.vector.scalar_tensor_tensor(
                                    target[:, t], y_ps[u % 2][:, j], k.gates[:, t, bass.ds(i * LANES + n, 1)],
                                    target[:, t], ALU.mult, ALU.add)
                            else:
                                last = nc.vector.tensor_tensor(target[:, t], y_ps[u % 2][:, j], target[:, t],
                                                               ALU.add)
                        last.then_inc(sig("combined").sem, 1)
                        if c == CHUNKS - 1:
                            dve.sem_inc(sig("expert_done").sem, 1)
        for n in range(LANES):
            k.load_lane[n].more(2 * rounds)
        units = rounds * PER
        for name, n in (("hidden", F * units), ("hidden_ps", F * units), ("y_ps", units), ("combined", units),
                        ("expert_done", count)):
            sig(name).advance(n)


def close_gqa(nc, k):
    with ExitStack() as ctx:
        sb, ps = scratch(nc, ctx, "close_gqa")
        norm2 = sb("norm2", [P, D])
        squares, normed = sb("squares", [P, LANES, D]), sb("normed", [P, LANES, D])
        mean, rstd = sb("mean", [P, TILES]), sb("rstd", [P, TILES])
        sig = k.sig
        with nc.Block() as block:
            @block.sync
            def _(sp):
                sp.dma_start(norm2[:], to_all(k.dram["L0_ffn_norm2_w"])).then_inc(k.load_small.sem, 16)
            k.load_small.more()

            @block.scalar
            def _(act):
                for t in range(TILES):
                    if t >= LANES:
                        act.wait_ge(sig("squares").sem, sig("squares").nth(t - LANES))
                    last = nc.scalar.activation(squares[:, t % LANES], k.rows[:, t], ACT.Square, scale=D ** -0.5,
                                                accum_out=mean[:, t:t + 1])
                    last.then_inc(sig("squares").sem, 1)

            @block.gpsimd
            def _(pool):
                pool.wait_ge(sig("squares").sem, sig("squares").nth(TILES - 1))
                nc.gpsimd.tensor_tensor(rstd[:], mean[:], spread(k.eps_rms[:], [P, TILES]),
                                        ALU.add).then_inc(sig("shifted_var").sem, 1)
                pool.wait_ge(sig("shifted_var").sem, sig("shifted_var").nth(0))
                nc.gpsimd.tensor_tensor(rstd[:], rstd[:], spread(k.minus_half[:], [P, TILES]),
                                        ALU.pow).then_inc(sig("rstd").sem, 1)
                with pool.Fori(0, TILES // LANES) as i:
                    for n in range(LANES):
                        t = i * LANES + n
                        pool.wait_ge(sig("xn").sem, sig("xn").nth(t))
                        nc.gpsimd.tensor_tensor(k.h[:, t, :], k.h[:, t, :], normed[:, n],
                                                ALU.add).then_inc(sig("kept").sem, 1)

            @block.vector
            def _(dve):
                dve.wait_ge(k.load_small.sem, k.load_small.all())
                dve.wait_ge(sig("rstd").sem, sig("rstd").nth(0))
                with dve.Fori(0, TILES // LANES) as i:
                    for n in range(LANES):
                        t = i * LANES + n
                        dve.wait_ge(sig("kept").sem, sig("kept").before(t))
                        nc.vector.scalar_tensor_tensor(normed[:, n], k.rows[:, t, :], rstd[:, bass.ds(t, 1)],
                                                       norm2[:], ALU.mult, ALU.mult).then_inc(sig("xn").sem, 1)
        for name, n in (("squares", TILES), ("shifted_var", 1), ("rstd", 1), ("xn", TILES), ("kept", TILES)):
            sig(name).advance(n)


def norm_pieces(ctx, nc, phase):
    sb, _ = scratch(nc, ctx, phase)
    return sb("ln_stats", [P, LANES, 6]), sb("ln_mom", [P, LANES, 2]), sb("ln_rstd", [P, LANES, 1])


def norm_vector(nc, k, dve, lanes, pieces, out, free):
    stats, mom, rstd = pieces
    sig = k.sig
    for n, t in lanes:
        for name in free:
            dve.wait_ge(sig(name).sem, sig(name).before(t))
        nc.vector.bn_stats(stats[:, n], k.h[:, t, :]).then_inc(sig("stats").sem, 1)
    for n, t in lanes:
        dve.wait_ge(sig("stats").sem, sig("stats").nth(t))
        nc.vector.memset(k.idle[:, n:n + 1], 0.0)
        nc.vector.bn_aggr(mom[:, n], stats[:, n]).then_inc(sig("moments").sem, 1)
    for n, t in lanes:
        dve.wait_ge(sig("rstd").sem, sig("rstd").nth(t))
        nc.vector.tensor_scalar(out(n, t), k.h[:, t, :], mom[:, n, 0:1], rstd[:, n], ALU.subtract,
                                ALU.mult).then_inc(sig("x").sem, 1)


def norm_pool(nc, k, pool, lanes, pieces):
    stats, mom, rstd = pieces
    sig = k.sig
    for n, t in lanes:
        pool.wait_ge(sig("moments").sem, sig("moments").nth(t))
        nc.gpsimd.tensor_tensor(rstd[:, n], mom[:, n, 1:2], k.eps_ln[:], ALU.add).then_inc(sig("shifted_var").sem, 1)
        pool.wait_ge(sig("shifted_var").sem, sig("shifted_var").nth(t))
        nc.gpsimd.tensor_tensor(rstd[:, n], rstd[:, n], k.minus_half[:], ALU.pow).then_inc(sig("rstd").sem, 1)


NORM_SIGNALS = ["stats", "moments", "shifted_var", "rstd", "x"]


def by_lanes(eng):
    return eng.Fori(0, TILES // LANES)


def lanes_of(i):
    return [(n, i * LANES + n) for n in range(LANES)]


def load_bitlinear(k, sp):
    w1 = k.region_b[:, 0:2048].rearrange("p (t n) -> p t n", n=D)
    w2 = k.region_b[:, 2048:4096].rearrange("p (t n) -> p t n", n=1024)
    for to, source in ((w1, by_rows(k.dram["L1_ffn_w1"])), (w2, by_rows(k.dram["L1_ffn_w2"])),
                       (k.conv_w[:], k.dram["L1_ffn_conv_w"].rearrange("(t p) a j -> p t (a j)", p=P)),
                       (k.conv_b[:], as_columns(k.dram["L1_ffn_conv_b"]))):
        sp.dma_start(to, source, allow_slow_non_contiguous=True).then_inc(k.load_b.sem, 16)
    k.load_b.more(4)


def load_decay(k, sp):
    r = k.region_a
    bf = r[:, 2048:4096].bitcast(BF16)
    d = k.dram
    pairs = [
        (r[:, 0:512].rearrange("p (t n) -> p t n", t=KT), by_rows(d["L2_attn_o_w"])),
        (r[:, 512:768], to_all(d["L2_attn_q"])), (r[:, 768:1024], to_all(d["L2_attn_k"])),
        (r[:, 1024:1280], to_all(d["L2_attn_norm_weight"])), (r[:, 1280:1296], to_all(d["L2_attn_log_decay"])),
        (bf[0:32, 0:256], d["L2_ffn_gate_w"]), (bf[:, 256:512], d["L2_ffn_sw1"]), (bf[:, 512:768], d["L2_ffn_sw3"]),
        (bf[:, 768:1024].rearrange("p (t n) -> p t n", t=KT), by_rows(d["L2_ffn_sw2"])),
    ]
    for to, source in pairs:
        sp.dma_start(to, source).then_inc(k.load_a.sem, 16)
    k.load_a.more(len(pairs))


def bitlinear(nc, k):
    CT = 8
    WIDE = CHUNK * P
    with ExitStack() as ctx:
        sb, ps = scratch(nc, ctx, "bitlinear")
        w1T, w2T = sb("w1T", [P, KT, CT * P], BF16), sb("w2T", [P, CT, D], BF16)
        mean = sb("weight_mean", [P, 2])
        unit = sb("weight_unit", [P, 2])
        w1 = k.region_b[:, 0:2048].rearrange("p (t n) -> p t n", n=D)
        w2 = k.region_b[:, 2048:4096].rearrange("p (t n) -> p t n", n=1024)
        unit_bc = k.xT[:, 0, :]
        qT = k.xT[:, 1, :].bitcast(BF16).rearrange("p (t n) -> p t n", t=KT)
        C, sig = k.const, k.sig

        with ExitStack() as ctx2, nc.Block() as block:
            sb2, ps2 = scratch(nc, ctx2, "bit_weights")
            ternary = sb2("ternary", [P, 2, 2048], BF16)
            scaled = sb2("scaled", [P, 2048])
            mean_ps = ps2("mean_ps", [P, 2])
            turned = [ps2(f"turned{n}", [P, CT, P], BF16) for n in range(4)]
            t1 = ternary[:, 0].rearrange("p (t n) -> p t n", n=D)
            t2 = ternary[:, 1].rearrange("p (t n) -> p t n", n=1024)

            @block.vector
            def _(dve):
                link = k.chain(dve)
                nc.vector.tensor_copy(k.ident16[:], C("ident"))
                dve.wait_ge(k.load_b.sem, k.load_b.all())
                for n in range(2):
                    last = nc.vector.tensor_reduce(mean[:, n:n + 1], k.region_b[:, 2048 * n:2048 * (n + 1)], AX_X,
                                                   ALU.add, apply_absolute_value=True)
                last.then_inc(sig("stats").sem, 1)
                dve.wait_ge(sig("moments").sem, sig("moments").nth(0))
                link(nc.vector.tensor_scalar(mean[:], mean_ps[:], 1.0 / (1024 * D), 1e-5, ALU.mult, ALU.max))
                link(nc.vector.reciprocal(unit[:], mean[:]))
                for n in range(2):
                    link(nc.vector.tensor_scalar(scaled[:], k.region_b[:, 2048 * n:2048 * (n + 1)], unit[:, n:n + 1],
                                                 ROUND, ALU.mult, ALU.add))
                    link(nc.vector.tensor_scalar(scaled[:], scaled[:], ROUND, 1.0, ALU.subtract, ALU.min))
                    link(nc.vector.tensor_scalar(ternary[:, n], scaled[:], -1.0, None, ALU.max))
                last = nc.vector.memset(k.idle[:], 0.0)
                last.then_inc(sig("x").sem, 1)

            @block.tensor
            def _(pe):
                pe.wait_ge(sig("stats").sem, sig("stats").nth(0))
                nc.tensor.matmul(mean_ps[:], C("ones"), mean[:], start=True, stop=True).then_inc(
                    sig("moments").sem, 1)
                pe.wait_ge(sig("x").sem, sig("x").nth(0))
                for half in range(2):
                    for c in range(CT):
                        nc.tensor.transpose(turned[half][:, c], t1[:, c, P * half:P * (half + 1)], k.ident16[:])
                        last = nc.tensor.transpose(turned[2 + half][:, c], t2[:, half, P * c:P * (c + 1)],
                                                   k.ident16[:])
                last.then_inc(sig("turned").sem, 1)

            @block.scalar
            def _(act):
                act.wait_ge(sig("turned").sem, sig("turned").nth(0))
                for half in range(2):
                    nc.scalar.copy(w1T[:, half].rearrange("p (c n) -> p c n", c=CT), turned[half][:])
                    nc.scalar.copy(w2T[:, :, P * half:P * (half + 1)], turned[2 + half][:])

            @block.sync
            def _(sp):
                load_decay(k, sp)
        for name in ("stats", "moments", "x", "turned"):
            sig(name).advance(1)

        with ExitStack() as ctx2, nc.Block() as block:
            sb2, ps2 = scratch(nc, ctx2, "bit_input")
            pieces = norm_pieces(ctx2, nc, "bit_input")
            x = sb2("x", [P, LANES, D])
            top, inv, f = (sb2(name, [P, LANES, 1]) for name in ("top", "inv", "unit"))
            q = sb2("q", [P, LANES, D], BF16)
            diag = sb2("diag", [P, LANES, P])
            bc_ps = [ps2(f"bc_ps{n}", [P, P]) for n in range(LANES)]
            q_ps = [ps2(f"q_ps{n}", [P, KT, P], BF16) for n in range(LANES)]

            @block.vector
            def _(dve):
                with by_lanes(dve) as i:
                    norm_vector(nc, k, dve, lanes_of(i), pieces, lambda n, t: x[:, n], ["stored"])
                    for n, t in lanes_of(i):
                        dve.wait_ge(sig("x").sem, sig("x").nth(t))
                        nc.vector.tensor_reduce(top[:, n], x[:, n], AX_X, ALU.max, apply_absolute_value=True
                                                ).then_inc(sig("top").sem, 1)
                    for n, t in lanes_of(i):
                        dve.wait_ge(sig("top").sem, sig("top").nth(t))
                        nc.vector.tensor_scalar(top[:, n], top[:, n], 1e-5, None, ALU.max
                                                ).then_inc(sig("clipped").sem, 1)
                    for n, t in lanes_of(i):
                        dve.wait_ge(sig("clipped").sem, sig("clipped").nth(t))
                        nc.vector.reciprocal(inv[:, n], top[:, n])
                        nc.vector.tensor_scalar(f[:, n], top[:, n], 1.0 / 127.0, mean[:, 0:1], ALU.mult, ALU.mult
                                                ).then_inc(sig("recip").sem, 1)
                    for n, t in lanes_of(i):
                        dve.wait_ge(sig("recip").sem, sig("recip").nth(t))
                        nc.vector.tensor_scalar(diag[:, n], C("ident"), f[:, n], None, ALU.mult
                                                ).then_inc(sig("diag").sem, 1)
                        nc.vector.tensor_scalar(x[:, n], x[:, n], inv[:, n], 127.0, ALU.mult, ALU.mult
                                                ).then_inc(sig("scaled").sem, 1)
                    for n, t in lanes_of(i):
                        dve.wait_ge(sig("scaled").sem, sig("scaled").nth(t))
                        nc.vector.tensor_scalar(x[:, n], x[:, n], 127.0, -128.0, ALU.min, ALU.max
                                                ).then_inc(sig("shifted").sem, 1)
                    for n, t in lanes_of(i):
                        dve.wait_ge(sig("shifted").sem, sig("shifted").nth(t))
                        nc.vector.tensor_scalar(q[:, n], x[:, n], ROUND, ROUND, ALU.add, ALU.subtract
                                                ).then_inc(sig("rounded").sem, 1)

            @block.gpsimd
            def _(pool):
                with by_lanes(pool) as i:
                    norm_pool(nc, k, pool, lanes_of(i), pieces)

            @block.tensor
            def _(pe):
                with by_lanes(pe) as i:
                    for n, t in lanes_of(i):
                        pe.wait_ge(sig("diag").sem, sig("diag").nth(t))
                        nc.tensor.matmul(bc_ps[n][:], C("ones"), diag[:, n], start=True, stop=True
                                         ).then_inc(sig("unit_ps").sem, 1)
                    for n, t in lanes_of(i):
                        pe.wait_ge(sig("rounded").sem, sig("rounded").nth(t))
                        for j in range(KT):
                            last = nc.tensor.transpose(q_ps[n][:, j], q[:, n, P * j:P * (j + 1)], k.ident16[:])
                        last.then_inc(sig("turned").sem, 1)

            @block.scalar
            def _(act):
                with by_lanes(act) as i:
                    for n, t in lanes_of(i):
                        act.wait_ge(sig("unit_ps").sem, sig("unit_ps").nth(t))
                        nc.scalar.copy(unit_bc[:, bass.ds(t * P, P)], bc_ps[n][:])
                    for n, t in lanes_of(i):
                        act.wait_ge(sig("turned").sem, sig("turned").nth(t))
                        nc.scalar.copy(qT[:, :, bass.ds(t * P, P)], q_ps[n][:]).then_inc(sig("stored").sem, 1)
        for name in NORM_SIGNALS + ["top", "clipped", "recip", "diag", "scaled", "shifted", "rounded", "unit_ps",
                                    "turned", "stored"]:
            sig(name).advance(TILES)

        with ExitStack() as ctx2, nc.Block() as block:
            sb2, ps2 = scratch(nc, ctx2, "bit_layers")
            padded = [sb2(f"padded{n}", [P, CHUNK, S + 2]) for n in range(2)]
            taps = [sb2(f"taps{n}", [P, CHUNK, S]) for n in range(2)]
            act_h = sb2("hidden", [P, CT, WIDE])
            q = sb2("q", [P, CT, WIDE], BF16)
            highest = sb2("highest", [P, WIDE])
            top, inv, f = (sb2(name, [P, CHUNK]) for name in ("top", "inv", "unit"))
            diag = sb2("diag", [P, CHUNK, P])
            scale_bc = sb2("scale_bc", [P, WIDE])
            h_ps = [ps2(f"h_ps{n}", [P, WIDE]) for n in range(2)]
            top_ps, scale_ps = ps2("top_ps", [P, CHUNK, P]), ps2("scale_ps", [P, WIDE])
            y_ps = ps2("y_ps", [P, CHUNK, D])
            by_seq = lambda x: x.rearrange("p (b s) -> p b s", b=CHUNK)

            @block.tensor
            def _(pe):
                with pe.Fori(0, CHUNKS) as c:
                    for m in range(CT):
                        u = c * CT + m
                        pe.wait_ge(sig("padded").sem, sig("padded").before(u))
                        for t in range(KT):
                            last = nc.tensor.matmul(h_ps[m % 2][:], w1T[:, t, P * m:P * (m + 1)],
                                                    qT[:, t, bass.ds(c * WIDE, WIDE)], start=(t == 0),
                                                    stop=(t == KT - 1))
                        last.then_inc(sig("hidden_ps").sem, 1)
                    pe.wait_ge(sig("highest").sem, sig("highest").nth(c))
                    for j in range(CHUNK):
                        last = nc.tensor.transpose(top_ps[:, j], highest[:, P * j:P * (j + 1)], C("ident"))
                    last.then_inc(sig("top_ps").sem, 1)
                    pe.wait_ge(sig("diag").sem, sig("diag").nth(c))
                    nc.tensor.matmul(scale_ps[:], C("ones"), diag[:].rearrange("p j q -> p (j q)"), start=True,
                                     stop=True).then_inc(sig("unit_ps").sem, 1)
                    pe.wait_ge(sig("rounded").sem, sig("rounded").nth(c))
                    for j in range(CHUNK):
                        for m in range(CT):
                            last = nc.tensor.matmul(y_ps[:, j], q[:, m, P * j:P * (j + 1)], w2T[:, m, :],
                                                    start=(m == 0), stop=(m == CT - 1))
                    last.then_inc(sig("y_ps").sem, 1)

            @block.scalar
            def _(act):
                with act.Fori(0, CHUNKS) as c:
                    for m in range(CT):
                        u = c * CT + m
                        act.wait_ge(sig("padded").sem, sig("padded").nth(u))
                        nc.scalar.activation(taps[m % 2][:], padded[m % 2][:, :, 1:S + 1], ACT.Identity,
                                             bias=k.conv_b[:, m:m + 1], scale=k.conv_w[:, m, 1:2]
                                             ).then_inc(sig("middle_tap").sem, 1)
                        act.wait_ge(sig("taps").sem, sig("taps").nth(u))
                        nc.scalar.activation(by_seq(act_h[:, m]), taps[m % 2][:], ACT.Silu
                                             ).then_inc(sig("hidden").sem, 1)
                    act.wait_ge(sig("unit_ps").sem, sig("unit_ps").nth(c))
                    nc.scalar.copy(scale_bc[:], scale_ps[:]).then_inc(sig("recip").sem, 1)

            @block.vector
            def _(dve):
                link = k.chain(dve)
                for n in range(2):
                    last = nc.vector.memset(padded[n][:], 0.0)
                link(last)
                with dve.Fori(0, CHUNKS) as c:
                    for m in range(CT):
                        u = c * CT + m
                        dve.wait_ge(sig("hidden").sem, sig("hidden").before(u))
                        dve.wait_ge(sig("hidden_ps").sem, sig("hidden_ps").nth(u))
                        nc.vector.tensor_tensor(padded[m % 2][:, :, 1:S + 1], by_seq(h_ps[m % 2][:]),
                                                by_seq(unit_bc[:, bass.ds(c * WIDE, WIDE)]), ALU.mult
                                                ).then_inc(sig("padded").sem, 1)
                        dve.wait_ge(sig("middle_tap").sem, sig("middle_tap").nth(u))
                        nc.vector.scalar_tensor_tensor(taps[m % 2][:], padded[m % 2][:, :, 0:S],
                                                       k.conv_w[:, m, 0:1], taps[m % 2][:], ALU.mult, ALU.add
                                                       ).then_inc(sig("first_tap").sem, 1)
                        dve.wait_ge(sig("first_tap").sem, sig("first_tap").nth(u))
                        nc.vector.scalar_tensor_tensor(taps[m % 2][:], padded[m % 2][:, :, 2:S + 2],
                                                       k.conv_w[:, m, 2:3], taps[m % 2][:], ALU.mult, ALU.add
                                                       ).then_inc(sig("taps").sem, 1)
                    dve.wait_ge(sig("hidden").sem, c * CT + sig("hidden").nth(CT - 1))
                    nc.vector.tensor_reduce(highest[:], act_h[:].rearrange("p m t -> p t m"), AX_X, ALU.max,
                                            apply_absolute_value=True).then_inc(sig("highest").sem, 1)
                    dve.wait_ge(sig("top_ps").sem, sig("top_ps").nth(c))
                    nc.vector.tensor_reduce(top[:], top_ps[:], AX_X, ALU.max).then_inc(sig("top").sem, 1)
                    dve.wait_ge(sig("top").sem, sig("top").nth(c))
                    nc.vector.tensor_scalar(top[:], top[:], 1e-5, None, ALU.max).then_inc(sig("clipped").sem, 1)
                    dve.wait_ge(sig("clipped").sem, sig("clipped").nth(c))
                    nc.vector.reciprocal(inv[:], top[:])
                    nc.vector.tensor_scalar(f[:], top[:], 1.0 / 127.0, mean[:, 1:2], ALU.mult, ALU.mult
                                            ).then_inc(sig("unit").sem, 1)
                    dve.wait_ge(sig("unit").sem, sig("unit").nth(c))
                    nc.vector.tensor_tensor(diag[:], spread(C("ident").unsqueeze(1), [P, CHUNK, P]),
                                            spread(inv[:].unsqueeze(2), [P, CHUNK, P]), ALU.mult
                                            ).then_inc(sig("diag").sem, 1)
                    dve.wait_ge(sig("recip").sem, sig("recip").nth(c))
                    nc.vector.tensor_tensor(act_h[:], act_h[:], spread(scale_bc[:].unsqueeze(1), [P, CT, WIDE]),
                                            ALU.mult).then_inc(sig("scaled").sem, 1)
                    dve.wait_ge(sig("scaled").sem, sig("scaled").nth(c))
                    nc.vector.tensor_scalar(act_h[:], act_h[:], 127.0, ROUND, ALU.mult, ALU.add
                                            ).then_inc(sig("shifted").sem, 1)
                    dve.wait_ge(sig("shifted").sem, sig("shifted").nth(c))
                    nc.vector.tensor_scalar(q[:], act_h[:], ROUND, 127.0, ALU.subtract, ALU.min
                                            ).then_inc(sig("rounded").sem, 1)
                    dve.wait_ge(sig("y_ps").sem, sig("y_ps").nth(c))
                    for j in range(CHUNK):
                        t = c * CHUNK + j
                        last = nc.vector.scalar_tensor_tensor(k.h[:, t, :], y_ps[:, j], f[:, j:j + 1], k.h[:, t, :],
                                                              ALU.mult, ALU.add)
                    last.then_inc(sig("stored").sem, 1)
        for name in ("padded", "hidden_ps", "middle_tap", "first_tap", "taps", "hidden"):
            sig(name).advance(CHUNKS * CT)
        for name in ("highest", "top_ps", "top", "clipped", "unit", "diag", "unit_ps", "recip", "scaled", "shifted",
                     "rounded", "y_ps", "stored"):
            sig(name).advance(CHUNKS)


def decay_attention(nc, k):
    r = k.region_a
    o_w = r[:, 0:512].rearrange("p (t n) -> p t n", t=KT)
    q, kk, norm_w, log_decay = r[:, 512:768], r[:, 768:1024], r[:, 1024:1280], r[:, 1280:1296]
    all_out = k.xT[:].rearrange("p t (n d) -> p (t n) d", d=D)
    C, sig = k.const, k.sig
    with ExitStack() as ctx:
        sb, ps = scratch(nc, ctx, "decay")
        powers = sb("powers", [P, HEADS, P])
        qk, per_head = sb("qk", [P, D]), sb("per_head", [P, HEADS])
        ln_decay, size, soft = (sb(name, [P, HEADS]) for name in ("ln_decay", "size", "soft"))
        o_wT = sb("o_wT", [P, KT, D])
        pieces = norm_pieces(ctx, nc, "decay")
        turned = ps("turned", [P, KT, D])
        out_ps = [ps(f"out_ps{n}", [P, TILES, HD]) for n in range(4)]

        with nc.Block() as block:
            @block.vector
            def _(dve):
                link = k.chain(dve)
                dve.wait_ge(k.load_a.sem, k.load_a.all())
                link(nc.vector.tensor_scalar(soft[:], log_decay, -1.0, None, ALU.mult))
                nc.vector.tensor_tensor(size[:], soft[:], log_decay, ALU.max).then_inc(sig("top").sem, 1)
                link(nc.vector.tensor_scalar(ln_decay[:], log_decay, -1.0, 0.0, ALU.mult, ALU.max))
                link(nc.vector.tensor_tensor(qk[:], q, kk, ALU.mult))
                link(nc.vector.tensor_reduce(per_head[:], qk[:].rearrange("p (h d) -> p h d", h=HEADS), AX_X,
                                             ALU.add))
                dve.wait_ge(sig("unit").sem, sig("unit").nth(0))
                link(nc.vector.tensor_tensor(ln_decay[:], ln_decay[:], soft[:], ALU.add))
                nc.vector.tensor_scalar(ln_decay[:], ln_decay[:], -1.0, None, ALU.mult).then_inc(sig("recip").sem, 1)
                for h in range(HEADS):
                    dve.wait_ge(sig("powers").sem, sig("powers").nth(h))
                    nc.vector.scalar_tensor_tensor(powers[:, h], powers[:, h], per_head[:, h:h + 1], C("causal"),
                                                   ALU.mult, ALU.mult)
                with by_lanes(dve) as i:
                    norm_vector(nc, k, dve, lanes_of(i), pieces, lambda n, t: k.rows[:, t, :], [])

            @block.gpsimd
            def _(pool):
                with by_lanes(pool) as i:
                    norm_pool(nc, k, pool, lanes_of(i), pieces)

            @block.scalar
            def _(act):
                act.wait_ge(sig("top").sem, sig("top").nth(0))
                nc.scalar.activation(soft[:], size[:], ACT.Exp, scale=-1.0).then_inc(sig("probs").sem, 1)
                act.wait_ge(sig("probs").sem, sig("probs").nth(0))
                nc.scalar.activation(soft[:], soft[:], ACT.Ln, bias=1.0).then_inc(sig("unit").sem, 1)
                act.wait_ge(sig("turned").sem, sig("turned").nth(0))
                nc.scalar.copy(o_wT[:], turned[:])
                act.wait_ge(sig("recip").sem, sig("recip").nth(0))
                for h in range(HEADS):
                    nc.scalar.activation(powers[:, h], C("lag"), ACT.Exp, scale=ln_decay[:, h:h + 1]
                                         ).then_inc(sig("powers").sem, 1)

            @block.tensor
            def _(pe):
                pe.wait_ge(k.load_a.sem, k.load_a.all())
                for a in range(KT):
                    for b in range(KT):
                        last = nc.tensor.transpose(turned[:, b, P * a:P * (a + 1)], o_w[:, a, P * b:P * (b + 1)],
                                                   C("ident"))
                last.then_inc(sig("turned").sem, 1)
        for name in ("top", "unit", "recip", "probs", "turned"):
            sig(name).advance(1)
        sig("powers").advance(HEADS)
        for name in NORM_SIGNALS:
            sig(name).advance(TILES)

        with nc.Block() as block:
            @block.tensor
            def _(pe):
                for h in range(HEADS):
                    if h >= 4:
                        pe.wait_ge(sig("stored").sem, sig("stored").nth(h - 4))
                    nc.tensor.matmul(out_ps[h % 4][:], powers[:, h], k.rows[:, :, HD * h:HD * (h + 1)], start=True,
                                     stop=True).then_inc(sig("out").sem, 1)

            @block.scalar
            def _(act):
                for h in range(HEADS):
                    act.wait_ge(sig("out").sem, sig("out").nth(h))
                    nc.scalar.copy(all_out[:, :, HD * h:HD * (h + 1)], out_ps[h % 4][:]
                                   ).then_inc(sig("stored").sem, 1)
        sig("out").advance(HEADS)
        sig("stored").advance(HEADS)

        with ExitStack() as ctx2, nc.Block() as block:
            sb2, ps2 = scratch(nc, ctx2, "decay_out")
            squares, normed = sb2("squares", [P, LANES, D]), sb2("normed", [P, LANES, D])
            mean, rstd = sb2("mean", [P, LANES, 1]), sb2("rstd", [P, LANES, 1])
            normedT = sb2("normedT", [P, LANES, KT, P])
            bank = [ps2(f"bank{n}", [P, KT, P]) for n in range(2)]

            @block.scalar
            def _(act):
                with by_lanes(act) as i:
                    for n, t in lanes_of(i):
                        act.wait_ge(sig("kept").sem, sig("kept").before(t))
                        nc.scalar.activation(squares[:, n], all_out[:, t, :], ACT.Square, scale=D ** -0.5,
                                             accum_out=mean[:, n]).then_inc(sig("squares").sem, 1)
                    for n, t in lanes_of(i):
                        act.wait_ge(sig("turned").sem, sig("turned").nth(t))
                        nc.scalar.copy(normedT[:, n], bank[n][:]).then_inc(sig("xT").sem, 1)

            @block.gpsimd
            def _(pool):
                with by_lanes(pool) as i:
                    for n, t in lanes_of(i):
                        pool.wait_ge(sig("squares").sem, sig("squares").nth(t))
                        nc.gpsimd.tensor_tensor(rstd[:, n], mean[:, n], k.eps_rms[:], ALU.add
                                                ).then_inc(sig("shifted_var").sem, 1)
                        pool.wait_ge(sig("shifted_var").sem, sig("shifted_var").nth(t))
                        nc.gpsimd.tensor_tensor(rstd[:, n], rstd[:, n], k.minus_half[:], ALU.pow
                                                ).then_inc(sig("rstd").sem, 1)

            @block.vector
            def _(dve):
                with by_lanes(dve) as i:
                    for n, t in lanes_of(i):
                        dve.wait_ge(sig("rstd").sem, sig("rstd").nth(t))
                        nc.vector.scalar_tensor_tensor(normed[:, n], all_out[:, t, :], rstd[:, n], norm_w, ALU.mult,
                                                       ALU.mult).then_inc(sig("xn").sem, 1)
                    for n, t in lanes_of(i):
                        dve.wait_ge(sig("out").sem, sig("out").nth(t))
                        nc.vector.tensor_tensor(k.h[:, t, :], bank[n][:].rearrange("p t n -> p (t n)"),
                                                k.h[:, t, :], ALU.add).then_inc(sig("kept").sem, 1)

            @block.tensor
            def _(pe):
                with by_lanes(pe) as i:
                    for n, t in lanes_of(i):
                        pe.wait_ge(sig("xn").sem, sig("xn").nth(t))
                        for f in range(KT):
                            last = nc.tensor.transpose(bank[n][:, f], normed[:, n, P * f:P * (f + 1)], C("ident"))
                        last.then_inc(sig("turned").sem, 1)
                    for n, t in lanes_of(i):
                        pe.wait_ge(sig("xT").sem, sig("xT").nth(t))
                        for f in range(KT):
                            last = nc.tensor.matmul(bank[n][:].rearrange("p t n -> p (t n)"), normedT[:, n, f],
                                                    o_wT[:, f, :], start=(f == 0), stop=(f == KT - 1))
                        last.then_inc(sig("out").sem, 1)
        for name in ("squares", "xT", "shifted_var", "rstd", "xn", "kept", "turned", "out"):
            sig(name).advance(TILES)


def load_hyena(k, sp):
    r, d = k.region_b, k.dram
    w = hyena_weights(k)
    pairs = [
        (w["in_proj"], by_rows(d["L3_attn_in_proj_w"])), (w["out_w"], by_rows(d["L3_attn_out_w"])),
        (w["fw3"], d["L3_attn_fw3"]), (w["fw2"], d["L3_attn_fw2"]),
        (w["in_bias"], d["L3_attn_in_proj_b"].partition_broadcast(3)), (w["out_b"], as_row(d["L3_attn_out_b"])),
        (w["fb3"], as_row(d["L3_attn_fb3"])), (w["fw1"], d["L3_attn_fw1"]),
        (w["fb1"], d["L3_attn_fb1"].rearrange("(n a) -> n a", a=1)),
        (w["fb2"], d["L3_attn_fb2"].rearrange("(n a) -> n a", a=1)),
        (w["short_w"], to_all(d["L3_attn_short_w"].rearrange("c a j -> (c a j)"))),
        (w["taps_T"], d["L3_attn_short_w"].rearrange("c a j -> j (a c)")),
        (k.v_bias[3:4, :], as_row(d["L3_attn_short_b"])),
    ]
    for to, source in pairs:
        sp.dma_start(to, source, allow_slow_non_contiguous=True).then_inc(k.load_b.sem, 16)
    k.load_b.more(len(pairs))


def hyena_weights(k):
    r = k.region_b
    return {
        "in_proj": r[:, 0:1536].rearrange("p (t n) -> p t n", t=KT),
        "out_w": r[:, 1536:2048].rearrange("p (t n) -> p t n", t=KT),
        "fw3": r[:, 2048:2560], "fw2": r[0:64, 2560:2688], "in_bias": r[0:3, 2688:3456], "out_b": r[0:1, 3456:3712],
        "fb3": r[0:1, 3712:4224], "fw1": r[0:1, 4224:4288], "fb1": r[0:64, 4288:4289], "fb2": r[:, 4289:4290],
        "short_w": r[:, 4290:5058], "taps_T": r[0:3, 5058:5314],
    }


def load_mixture(k, sp):
    r, d = k.region_a, k.dram
    pairs = [
        (r[:, 0:4096].rearrange("p (e t n) -> p e t n", e=8, t=KT),
         d["L3_ffn_expert_w"].rearrange("e (t p) n -> p e t n", p=P)),
        (r[:, 4096:4112].rearrange("p (t n) -> p t n", t=KT), by_rows(d["L3_ffn_gate_w"])),
        (r[0:1, 4112:4120], as_row(d["L3_ffn_gate_b"])),
        (r[0:1, 4120:6168], d["L3_ffn_expert_b"].rearrange("(a e) n -> a (e n)", a=1)),
    ]
    for to, source in pairs:
        sp.dma_start(to, source).then_inc(k.load_a.sem, 16)
    k.load_a.more(len(pairs))


def swiglu_gates(nc, k, shared, x_high, x_low):
    bf = k.region_a[:, 2048:4096].bitcast(BF16)
    gate_raw, sw1, sw3 = bf[0:32, 0:256], bf[:, 256:512], bf[:, 512:768]
    sw2 = bf[:, 768:1024].rearrange("p (t n) -> p t n", t=KT)
    C, sig = k.const, k.sig
    with ExitStack() as ctx:
        sb, ps = scratch(nc, ctx, "swiglu_gates")
        pieces = norm_pieces(ctx, nc, "swiglu_gates")
        x, xT = sb("x", [P, LANES, D]), sb("xT", [P, LANES, KT, P])
        gate_wT = sb("gate_wT", [P, KT, 32])
        raw_ps = ps("raw_ps", [P, 8, P], BF16)
        bank = [ps(f"bank{n}", [P, KT, P]) for n in range(2)]
        with nc.Block() as block:
            @block.vector
            def _(dve):
                with by_lanes(dve) as i:
                    norm_vector(nc, k, dve, lanes_of(i), pieces, lambda n, t: x[:, n], ["stored"])

            @block.gpsimd
            def _(pool):
                with by_lanes(pool) as i:
                    norm_pool(nc, k, pool, lanes_of(i), pieces)
                    for n, t in lanes_of(i):
                        pool.wait_ge(sig("xT").sem, sig("xT").nth(t))
                        at = bass.ds(t * P, P)
                        nc.gpsimd.tensor_tensor(x_low[:, :, at], xT[:, n], x_high[:, :, at].bitcast(F32),
                                                ALU.subtract).then_inc(sig("low").sem, 1)

            @block.tensor
            def _(pe):
                pe.wait_ge(k.load_a.sem, k.load_a.all())
                for t in range(KT):
                    cols = slice(P * t, P * (t + 1))
                    nc.tensor.transpose(raw_ps[:, t, 0:32], gate_raw[:, cols], k.ident16[0:32, 0:32])
                    nc.tensor.transpose(raw_ps[:, 2 + t], sw1[:, cols], k.ident16[:])
                    nc.tensor.transpose(raw_ps[:, 4 + t], sw3[:, cols], k.ident16[:])
                    last = nc.tensor.transpose(raw_ps[:, 6 + t], sw2[:, t], k.ident16[:])
                last.then_inc(sig("proj").sem, 1)
                with by_lanes(pe) as i:
                    for n, t in lanes_of(i):
                        pe.wait_ge(sig("x").sem, sig("x").nth(t))
                        for f in range(KT):
                            last = nc.tensor.transpose(bank[n][:, f], x[:, n, P * f:P * (f + 1)], C("ident"))
                        last.then_inc(sig("turned").sem, 1)
                    for n, t in lanes_of(i):
                        pe.wait_ge(sig("xT").sem, sig("xT").nth(t))
                        for f in range(KT):
                            last = nc.tensor.matmul(bank[n][:, 0, 0:32], xT[:, n, f], gate_wT[:, f], start=(f == 0),
                                                    stop=(f == KT - 1))
                        last.then_inc(sig("logits").sem, 1)

            @block.scalar
            def _(act):
                act.wait_ge(sig("proj").sem, sig("proj").nth(0))
                nc.scalar.copy(gate_wT[:], raw_ps[:, 0:2, 0:32])
                nc.scalar.copy(shared.rearrange("p (m n) -> p m n", n=P), raw_ps[:, 2:8])
                with by_lanes(act) as i:
                    for n, t in lanes_of(i):
                        act.wait_ge(sig("turned").sem, sig("turned").nth(t))
                        act.wait_ge(sig("low").sem, sig("low").before(t))
                        nc.scalar.copy(x_high[:, :, bass.ds(t * P, P)], bank[n][:])
                        nc.scalar.copy(xT[:, n], bank[n][:]).then_inc(sig("xT").sem, 1)
                    for n, t in lanes_of(i):
                        act.wait_ge(sig("logits").sem, sig("logits").nth(t))
                        nc.scalar.copy(k.logits[:, t, :], bank[n][:, 0, 0:32]).then_inc(sig("stored").sem, 1)
        sig("proj").advance(1)
        for name in NORM_SIGNALS + ["turned", "xT", "low", "logits", "stored"]:
            sig(name).advance(TILES)


def swiglu_experts(nc, k, x_high, x_low, shared):
    E, I = 32, 128
    WIDE = CHUNK * P
    W = 2 * KT * I + D
    d = k.dram
    w1 = d["L2_ffn_W1"].rearrange("e (t p) i -> p e t i", p=P)
    w3 = d["L2_ffn_W3"].rearrange("e (t p) i -> p e t i", p=P)
    w2 = d["L2_ffn_W2"].rearrange("e p n -> p e n")
    rounds = E // LANES
    PER = LANES * CHUNKS
    HIDS = 4
    sig = k.sig

    def item(signal, i, v, back=0):
        return i * PER + (signal.nth(v) - back)

    with ExitStack() as ctx:
        sb, ps = scratch(nc, ctx, "swiglu")
        raw = sb("raw", [P, LANES, W], BF16)
        zero = sb("zero", [P, 1], BF16)
        w = sb("w", [P, LANES, W], F32R)
        gate_h = [sb(f"gate{n}", [P, WIDE]) for n in range(2)]
        hid = [sb(f"hidden{n}", [P, WIDE]) for n in range(HIDS)]
        high = [sb(f"high{n}", [P, WIDE], F32R) for n in range(HIDS)]
        low = [sb(f"low{n}", [P, WIDE], F32R) for n in range(HIDS)]
        a_ps = [ps(f"a_ps{n}", [P, WIDE]) for n in range(2)]
        b_ps = [ps(f"b_ps{n}", [P, WIDE]) for n in range(2)]
        y_ps = [ps(f"y_ps{n}", [P, CHUNK, D]) for n in range(2)]

        def weights(v):
            one = w[:, v // CHUNKS % LANES]
            return (one[:, 0:KT * I].rearrange("p (t i) -> p t i", t=KT),
                    one[:, KT * I:2 * KT * I].rearrange("p (t i) -> p t i", t=KT), one[:, 2 * KT * I:])

        with nc.Block() as block:
            @block.sync
            def _(sp):
                load_hyena(k, sp)
                with sp.Fori(0, rounds) as i:
                    for n in range(LANES):
                        e = i * LANES + n
                        sp.wait_ge(sig("converted").sem, sig("converted").before(e))
                        for source, at in ((w1, 0), (w3, KT * I)):
                            sp.dma_start(raw[:, n, at:at + KT * I].rearrange("p (t i) -> p t i", t=KT),
                                         source[:, e]).then_inc(k.load_lane[n].sem, 16)
                        sp.dma_start(raw[:, n, 2 * KT * I:], w2[:, e]).then_inc(k.load_lane[n].sem, 16)

            @block.gpsimd
            def _(pool):
                nc.gpsimd.memset(zero[:], 0.0).then_inc(sig("ones_set").sem, 1)
                pool.wait_ge(sig("ones_set").sem, sig("ones_set").nth(0))

                def convert(n, source):
                    nc.gpsimd.tensor_tensor(w[:, n], source, spread(zero[:], [P, W]), ALU.add
                                            ).then_inc(sig("converted").sem, 1)

                def next_expert(i, v):
                    if v % CHUNKS == 1:
                        n = (v // CHUNKS + 1) % LANES
                        pool.wait_ge(sig("y_ps").sem, item(sig("y_ps"), i, v, 2))
                        if n:
                            pool.wait_ge(k.load_lane[n].sem, i * 48 + (k.load_lane[n].all() + 48))
                            convert(n, raw[:, n])
                        elif i is last_round:
                            convert(0, shared)
                        else:
                            pool.wait_ge(k.load_lane[0].sem, i * 48 + (k.load_lane[0].all() + 96))
                            convert(0, raw[:, 0])

                def low_part(i, v):
                    pool.wait_ge(sig("high").sem, item(sig("high"), i, v))
                    pool.wait_ge(sig("y_ps").sem, item(sig("y_ps"), i, v, HIDS))
                    nc.gpsimd.tensor_tensor(low[v % HIDS][:], hid[v % HIDS][:], high[v % HIDS][:].bitcast(F32),
                                            ALU.subtract).then_inc(sig("low").sem, 1)

                last_round = rounds - 1
                pool.wait_ge(k.load_lane[0].sem, k.load_lane[0].all() + 48)
                convert(0, raw[:, 0])
                with pool.Fori(0, last_round) as i:
                    for v in range(PER):
                        low_part(i, v)
                        next_expert(i, v)
                for v in range(PER):
                    low_part(last_round, v)
                    next_expert(last_round, v)
                for v in range(CHUNKS):
                    low_part(rounds, v)

            @block.tensor
            def _(pe):
                def first(i, v):
                    c = v % CHUNKS
                    if c == 0:
                        pe.wait_ge(sig("converted").sem, i * LANES + sig("converted").nth(v // CHUNKS))
                    w1, w3, _ = weights(v)
                    pe.wait_ge(sig("hidden").sem, item(sig("hidden"), i, v, 2))
                    for bank, part in ((a_ps, w1), (b_ps, w3)):
                        for x in (x_high, x_low):
                            for t in range(KT):
                                last = nc.tensor.matmul(bank[v % 2][:], part[:, t, :],
                                                        x[:, t, c * WIDE:(c + 1) * WIDE],
                                                        start=(x is x_high and t == 0),
                                                        stop=(x is x_low and t == KT - 1))
                    last.then_inc(sig("hidden_ps").sem, 1)

                def second(i, v):
                    pe.wait_ge(sig("low").sem, item(sig("low"), i, v))
                    pe.wait_ge(sig("combined").sem, item(sig("combined"), i, v, 2))
                    for j in range(CHUNK):
                        for part in (high, low):
                            last = nc.tensor.matmul(y_ps[v % 2][:, j], part[v % HIDS][:, P * j:P * (j + 1)],
                                                    weights(v)[2], start=(part is high), stop=(part is low))
                    last.then_inc(sig("y_ps").sem, 1)
                pipelined(pe, rounds, PER, CHUNKS, [(0, first), (2, second)])

            @block.scalar
            def _(act):
                def silu(i, v):
                    act.wait_ge(sig("hidden").sem, item(sig("hidden"), i, v, 2))
                    act.wait_ge(sig("hidden_ps").sem, item(sig("hidden_ps"), i, v))
                    nc.scalar.activation(gate_h[v % 2][:], a_ps[v % 2][:], ACT.Silu).then_inc(sig("silu").sem, 1)

                def high_part(i, v):
                    act.wait_ge(sig("hidden").sem, item(sig("hidden"), i, v))
                    act.wait_ge(sig("y_ps").sem, item(sig("y_ps"), i, v, HIDS))
                    nc.scalar.copy(high[v % HIDS][:], hid[v % HIDS][:]).then_inc(sig("high").sem, 1)
                pipelined(act, rounds, PER, CHUNKS, [(0, silu), (1, high_part)])

            @block.vector
            def _(dve):
                def product(i, v):
                    dve.wait_ge(sig("silu").sem, item(sig("silu"), i, v))
                    dve.wait_ge(sig("low").sem, item(sig("low"), i, v, HIDS))
                    nc.vector.tensor_tensor(hid[v % HIDS][:], gate_h[v % 2][:], b_ps[v % 2][:], ALU.mult
                                            ).then_inc(sig("hidden").sem, 1)

                def combine(i, v):
                    dve.wait_ge(sig("y_ps").sem, item(sig("y_ps"), i, v))
                    dve.wait_ge(sig("combined").sem, item(sig("combined"), i, v, 1))
                    for j in range(CHUNK):
                        t = CHUNK * (v % CHUNKS) + j
                        e = i * LANES + v // CHUNKS
                        column = bass.ds(e, 1)
                        last = nc.vector.scalar_tensor_tensor(k.h[:, t], y_ps[v % 2][:, j], k.gates[:, t, column],
                                                              k.h[:, t], ALU.mult, ALU.add)
                    last.then_inc(sig("combined").sem, 1)
                pipelined(dve, rounds, PER, CHUNKS, [(0, product), (3, combine)])
        for n in range(LANES):
            k.load_lane[n].more(3 * rounds)
        total = rounds * PER + CHUNKS
        for name in ("hidden", "hidden_ps", "silu", "high", "low", "y_ps", "combined"):
            sig(name).advance(total)
        sig("converted").advance(E + 1)
        sig("ones_set").advance(1)


def hyena(nc, k):
    w = hyena_weights(k)
    C, sig = k.const, k.sig
    with ExitStack() as ctx:
        sb, ps = scratch(nc, ctx, "hyena")
        pieces = norm_pieces(ctx, nc, "hyena")
        w_taps = sb("w_taps", [P, 3, KT, D])
        w_branch = sb("w_branch", [P, KT, D])
        f1, f2 = sb("filter1", [64, P]), sb("filter2", [P, P])
        coefs = sb("coefs", [P, D])
        H13, H22 = sb("H13", [P, 2, D]), sb("H22", [P, 2, D])
        x = sb("x", [P, LANES, D])
        padded = sb("padded", [P, LANES, KT, S + 2])
        v, branch = sb("v", [P, LANES, D]), sb("branch", [P, LANES, D])
        y1, y2 = sb("y1", [P, LANES, 2, D]), sb("y2", [P, LANES, 2, D])
        z, zT = sb("z", [P, LANES, D]), sb("zT", [P, LANES, KT, P])
        a_ps, b_ps, c_ps = ([ps(f"{c}_ps{n}", [P, 512]) for n in range(LANES)] for c in "abc")
        in_proj = w["in_proj"].rearrange("p t (c i) -> p t c i", i=3)
        taps = w["short_w"].rearrange("p (c j) -> p c j", j=3)

        with nc.Block() as block:
            @block.vector
            def _(dve):
                dve.wait_ge(k.load_b.sem, k.load_b.all())
                nc.vector.memset(padded[:], 0.0)
                bias = w["in_bias"].rearrange("p (c i) -> p c i", i=3)
                nc.vector.tensor_tensor(k.v_bias[0:3, :], bias[:, :, 0], w["taps_T"], ALU.mult)
                for t in range(KT):
                    nc.vector.tensor_copy(w_branch[:, t], in_proj[:, t, :, 2])
                    for j in range(3):
                        nc.vector.tensor_tensor(w_taps[:, j, t], in_proj[:, t, :, 0], taps[:, :, j], ALU.mult)
                dve.wait_ge(sig("out").sem, sig("out").nth(0))
                nc.vector.tensor_copy(H13[:, 0], a_ps[0][:, 0:D])
                nc.vector.tensor_copy(H13[:, 1], b_ps[0][:, 0:D])
                nc.vector.tensor_copy(H22[:, 1], c_ps[0][:, 0:D])
                nc.vector.tensor_scalar(H22[:, 0], c_ps[0][:, 0:D], -1.0, None, ALU.mult)

            @block.tensor
            def _(pe):
                pe.wait_ge(k.load_b.sem, k.load_b.all())
                nc.tensor.matmul(a_ps[0][0:64, 0:P], w["fw1"], C("pos")[0:1, :], start=True, stop=True
                                 ).then_inc(sig("hidden_ps").sem, 1)
                pe.wait_ge(sig("hidden").sem, sig("hidden").nth(0))
                nc.tensor.matmul(a_ps[0][:, 0:P], w["fw2"], f1[:], start=True, stop=True
                                 ).then_inc(sig("hidden_ps").sem, 1)
                pe.wait_ge(sig("hidden").sem, sig("hidden").nth(1))
                odd = lambda ap: ap.rearrange("p (c i) -> p c i", i=2)[:, :, 1]
                nc.tensor.matmul(a_ps[0][:, 0:D], C("ones")[0:1, :], odd(w["fb3"]), start=True, stop=False)
                nc.tensor.matmul(a_ps[0][:, 0:D], f2[:], odd(w["fw3"]), start=False, stop=True
                                 ).then_inc(sig("hidden_ps").sem, 1)
                pe.wait_ge(sig("hidden").sem, sig("hidden").nth(2))
                for bank, name in ((a_ps, "dft_re"), (b_ps, "dft_re1"), (c_ps, "dft_im0")):
                    last = nc.tensor.matmul(bank[0][:, 0:D], C(name), coefs[:], start=True, stop=True)
                last.then_inc(sig("out").sem, 1)

            @block.scalar
            def _(act):
                act.wait_ge(k.load_b.sem, k.load_b.all())
                act.wait_ge(sig("hidden_ps").sem, sig("hidden_ps").nth(0))
                nc.scalar.activation(f1[:], a_ps[0][0:64, 0:P], ACT.Gelu, bias=w["fb1"]).then_inc(sig("hidden").sem, 1)
                act.wait_ge(sig("hidden_ps").sem, sig("hidden_ps").nth(1))
                nc.scalar.activation(f2[:], a_ps[0][:, 0:P], ACT.Gelu, bias=w["fb2"]).then_inc(sig("hidden").sem, 1)
                act.wait_ge(sig("hidden_ps").sem, sig("hidden_ps").nth(2))
                nc.scalar.copy(coefs[:], a_ps[0][:, 0:D]).then_inc(sig("hidden").sem, 1)

            @block.sync
            def _(sp):
                load_mixture(k, sp)
        sig("out").advance(1)
        sig("hidden").advance(3)
        sig("hidden_ps").advance(3)

        with nc.Block() as block:
            @block.vector
            def _(dve):
                with by_lanes(dve) as i:
                    norm_vector(nc, k, dve, lanes_of(i), pieces, lambda n, t: x[:, n], ["kept"])
                    for n, t in lanes_of(i):
                        dve.wait_ge(sig("scores").sem, sig("scores").nth(t))
                        spectrum = c_ps[n][:].rearrange("p (s c) -> p s c", s=2)
                        nc.vector.tensor_tensor(y1[:, n], spectrum, H13[:], ALU.mult)
                        nc.vector.tensor_tensor(y2[:, n], spectrum[:, ::-1, :], H22[:], ALU.mult
                                                ).then_inc(sig("rotated").sem, 1)
                    for n, t in lanes_of(i):
                        dve.wait_ge(sig("pv").sem, sig("pv").nth(t))
                        nc.vector.tensor_tensor(z[:, n], a_ps[n][:, 0:D], branch[:, n], ALU.mult
                                                ).then_inc(sig("o").sem, 1)
                    for n, t in lanes_of(i):
                        dve.wait_ge(sig("out").sem, sig("out").nth(t))
                        nc.vector.tensor_tensor(k.h[:, t, :], a_ps[n][:, 0:D], k.h[:, t, :], ALU.add
                                                ).then_inc(sig("kept").sem, 1)

            @block.gpsimd
            def _(pool):
                with by_lanes(pool) as i:
                    norm_pool(nc, k, pool, lanes_of(i), pieces)
                    for n, t in lanes_of(i):
                        pool.wait_ge(sig("rotated").sem, sig("rotated").nth(t))
                        nc.gpsimd.tensor_tensor(y1[:, n], y1[:, n], y2[:, n], ALU.add).then_inc(sig("qk").sem, 1)

            @block.tensor
            def _(pe):
                branch_bias = w["in_bias"][0:1].rearrange("p (c i) -> p c i", i=3)[:, :, 2]
                with by_lanes(pe) as i:
                    for n, t in lanes_of(i):
                        pe.wait_ge(sig("x").sem, sig("x").nth(t))
                        for f in range(KT):
                            last = nc.tensor.transpose(a_ps[n][:, P * f:P * (f + 1)], x[:, n, P * f:P * (f + 1)],
                                                       C("ident"))
                        last.then_inc(sig("turned").sem, 1)
                    for n, t in lanes_of(i):
                        pe.wait_ge(sig("xT").sem, sig("xT").nth(t))
                        nc.tensor.matmul(a_ps[n][:, 0:D], C("edges")[0:4, :], k.v_bias[:], start=True, stop=False)
                        for j in range(3):
                            for f in range(KT):
                                nc.tensor.matmul(a_ps[n][:, 0:D], padded[:, n, f, j:j + S], w_taps[:, j, f],
                                                 start=False, stop=(j == 2 and f == KT - 1))
                        nc.tensor.matmul(b_ps[n][:, 0:D], C("ones")[0:1, :], branch_bias, start=True, stop=False)
                        for f in range(KT):
                            last = nc.tensor.matmul(b_ps[n][:, 0:D], padded[:, n, f, 1:S + 1], w_branch[:, f],
                                                    start=False, stop=(f == KT - 1))
                        last.then_inc(sig("proj").sem, 1)
                    for n, t in lanes_of(i):
                        pe.wait_ge(sig("v1").sem, sig("v1").nth(t))
                        nc.tensor.matmul(c_ps[n][:, 0:D], C("dft_re"), v[:, n], start=True, stop=True)
                        nc.tensor.matmul(c_ps[n][:, D:2 * D], C("dft_im"), v[:, n], start=True, stop=True
                                         ).then_inc(sig("scores").sem, 1)
                    for n, t in lanes_of(i):
                        pe.wait_ge(sig("qk").sem, sig("qk").nth(t))
                        nc.tensor.matmul(a_ps[n][:, 0:D], C("inv_re"), y1[:, n, 0], start=True, stop=False)
                        nc.tensor.matmul(a_ps[n][:, 0:D], C("inv_im"), y1[:, n, 1], start=False, stop=True
                                         ).then_inc(sig("pv").sem, 1)
                    for n, t in lanes_of(i):
                        pe.wait_ge(sig("o").sem, sig("o").nth(t))
                        for f in range(KT):
                            last = nc.tensor.transpose(b_ps[n][:, P * f:P * (f + 1)], z[:, n, P * f:P * (f + 1)],
                                                       C("ident"))
                        last.then_inc(sig("oT_ps").sem, 1)
                    for n, t in lanes_of(i):
                        pe.wait_ge(sig("oT").sem, sig("oT").nth(t))
                        nc.tensor.matmul(a_ps[n][:, 0:D], C("ones")[0:1, :], w["out_b"], start=True, stop=False)
                        for f in range(KT):
                            last = nc.tensor.matmul(a_ps[n][:, 0:D], zT[:, n, f], w["out_w"][:, f, :], start=False,
                                                    stop=(f == KT - 1))
                        last.then_inc(sig("out").sem, 1)

            @block.scalar
            def _(act):
                halves = lambda bank: bank[:, 0:D].rearrange("p (t n) -> p t n", t=KT)
                with by_lanes(act) as i:
                    for n, t in lanes_of(i):
                        act.wait_ge(sig("turned").sem, sig("turned").nth(t))
                        nc.scalar.copy(padded[:, n, :, 1:S + 1], halves(a_ps[n])).then_inc(sig("xT").sem, 1)
                    for n, t in lanes_of(i):
                        act.wait_ge(sig("proj").sem, sig("proj").nth(t))
                        nc.scalar.copy(branch[:, n], b_ps[n][:, 0:D])
                        nc.scalar.copy(v[:, n], a_ps[n][:, 0:D]).then_inc(sig("v1").sem, 1)
                    for n, t in lanes_of(i):
                        act.wait_ge(sig("oT_ps").sem, sig("oT_ps").nth(t))
                        nc.scalar.copy(zT[:, n], halves(b_ps[n])).then_inc(sig("oT").sem, 1)
        for name in NORM_SIGNALS + ["scores", "rotated", "pv", "o", "out", "kept", "qk", "turned", "xT", "proj", "v1",
                                    "oT_ps", "oT"]:
            sig(name).advance(TILES)


def mixture(nc, k):
    E = 8
    r = k.region_a
    expert_w = r[:, 0:4096].rearrange("p (e t n) -> p e t n", e=E, t=KT)
    gate_w = r[:, 4096:4112].rearrange("p (t n) -> p t n", t=KT)
    gate_b, expert_b = r[0:1, 4112:4120], r[0:1, 4120:6168].rearrange("p (e n) -> p e n", e=E)
    C, sig = k.const, k.sig
    with ExitStack() as ctx:
        sb, ps = scratch(nc, ctx, "mixture")
        pieces = norm_pieces(ctx, nc, "mixture")
        x, xT = sb("x", [P, LANES, D]), sb("xT", [P, LANES, KT, P])
        gate, kept = sb("gate", [P, LANES, E]), sb("kept", [P, LANES, E])
        top, den, inv, none = (sb(name, [P, LANES, 1]) for name in ("top", "den", "inv", "none"))
        a_ps = [ps(f"a_ps{n}", [P, 2, D]) for n in range(LANES)]
        pair_ps = [[ps(f"pair_ps{n}_{q}", [P, 2, D]) for q in range(3)] + [a_ps[n]] for n in range(LANES)]
        with nc.Block() as block:
            @block.vector
            def _(dve):
                with by_lanes(dve) as i:
                    norm_vector(nc, k, dve, lanes_of(i), pieces, lambda n, t: x[:, n], [])
                    for n, t in lanes_of(i):
                        dve.wait_ge(sig("logits").sem, sig("logits").nth(t))
                        nc.vector.tensor_reduce(top[:, n], a_ps[n][:, 0, 0:E], AX_X, ALU.max
                                                ).then_inc(sig("top").sem, 1)
                    for n, t in lanes_of(i):
                        dve.wait_ge(sig("top").sem, sig("top").nth(t))
                        nc.vector.tensor_scalar(gate[:, n], a_ps[n][:, 0, 0:E], top[:, n], None, ALU.subtract
                                                ).then_inc(sig("shifted").sem, 1)
                    for n, t in lanes_of(i):
                        dve.wait_ge(sig("probs").sem, sig("probs").nth(t))
                        nc.vector.tensor_reduce(den[:, n], gate[:, n], AX_X, ALU.add).then_inc(sig("den").sem, 1)
                    for n, t in lanes_of(i):
                        dve.wait_ge(sig("den").sem, sig("den").nth(t))
                        nc.vector.reciprocal(inv[:, n], den[:, n]).then_inc(sig("recip").sem, 1)
                    for n, t in lanes_of(i):
                        dve.wait_ge(sig("recip").sem, sig("recip").nth(t))
                        nc.vector.tensor_scalar(gate[:, n], gate[:, n], inv[:, n], None, ALU.mult
                                                ).then_inc(sig("normed").sem, 1)
                    for n, t in lanes_of(i):
                        dve.wait_ge(sig("normed").sem, sig("normed").nth(t))
                        nc.vector.scalar_tensor_tensor(kept[:, n], gate[:, n], 0.1, gate[:, n], ALU.is_ge, ALU.mult
                                                       ).then_inc(sig("picked").sem, 1)
                    for n, t in lanes_of(i):
                        dve.wait_ge(sig("picked").sem, sig("picked").nth(t))
                        nc.vector.tensor_reduce(den[:, n], kept[:, n], AX_X, ALU.add).then_inc(sig("clipped").sem, 1)
                    for n, t in lanes_of(i):
                        dve.wait_ge(sig("clipped").sem, sig("clipped").nth(t))
                        nc.vector.scalar_tensor_tensor(none[:, n], den[:, n], 0.0, den[:, n], ALU.is_equal, ALU.add
                                                       ).then_inc(sig("unit").sem, 1)
                    for n, t in lanes_of(i):
                        dve.wait_ge(sig("unit").sem, sig("unit").nth(t))
                        nc.vector.reciprocal(inv[:, n], none[:, n]).then_inc(sig("rounded").sem, 1)
                    for n, t in lanes_of(i):
                        dve.wait_ge(sig("rounded").sem, sig("rounded").nth(t))
                        nc.vector.tensor_scalar(gate[:, n], kept[:, n], inv[:, n], None, ALU.mult
                                                ).then_inc(sig("weighed").sem, 1)
                    for e in range(E):
                        for n, t in lanes_of(i):
                            if e % 2 == 0:
                                pair = i * 4 * LANES + e // 2 * LANES + n
                                dve.wait_ge(sig("y_ps").sem, sig("y_ps").nth(pair))
                            item = i * E * LANES + e * LANES + n
                            if e == 0:
                                dve.wait_ge(sig("weighed").sem, sig("weighed").nth(t))
                            else:
                                dve.wait_ge(sig("combined").sem, sig("combined").before(item))
                            nc.vector.scalar_tensor_tensor(k.h[:, t, :], pair_ps[n][e // 2][:, e % 2],
                                                           gate[:, n, e:e + 1], k.h[:, t, :], ALU.mult, ALU.add
                                                           ).then_inc(sig("combined").sem, 1)

            @block.gpsimd
            def _(pool):
                with by_lanes(pool) as i:
                    norm_pool(nc, k, pool, lanes_of(i), pieces)

            @block.tensor
            def _(pe):
                pe.wait_ge(k.load_a.sem, k.load_a.all())
                with by_lanes(pe) as i:
                    for n, t in lanes_of(i):
                        pe.wait_ge(sig("x").sem, sig("x").nth(t))
                        pe.wait_ge(sig("combined").sem, i * E * LANES + (sig("combined").nth(n) - LANES))
                        for f in range(KT):
                            last = nc.tensor.transpose(a_ps[n][:, 0, P * f:P * (f + 1)], x[:, n, P * f:P * (f + 1)],
                                                       C("ident"))
                        last.then_inc(sig("turned").sem, 1)
                    for n, t in lanes_of(i):
                        pe.wait_ge(sig("xT").sem, sig("xT").nth(t))
                        nc.tensor.matmul(a_ps[n][:, 0, 0:E], C("ones")[0:1, :], gate_b, start=True, stop=False)
                        for f in range(KT):
                            last = nc.tensor.matmul(a_ps[n][:, 0, 0:E], xT[:, n, f], gate_w[:, f, :], start=False,
                                                    stop=(f == KT - 1))
                        last.then_inc(sig("logits").sem, 1)
                    for q in range(E // 2):
                        for n, t in lanes_of(i):
                            if q == 3:
                                pe.wait_ge(sig("shifted").sem, sig("shifted").nth(t))
                            out = pair_ps[n][q][:].rearrange("p e n -> p (e n)")
                            nc.tensor.matmul(out, C("ones")[0:1, :], expert_b[:, 2 * q:2 * q + 2].rearrange(
                                "p e n -> p (e n)"), start=True, stop=False)
                            for f in range(KT):
                                last = nc.tensor.matmul(out.rearrange("p (e n) -> p e n", e=2), xT[:, n, f],
                                                        expert_w[:, 2 * q:2 * q + 2, f, :],
                                                        start=False, stop=(f == KT - 1))
                            last.then_inc(sig("y_ps").sem, 1)

            @block.scalar
            def _(act):
                with by_lanes(act) as i:
                    for n, t in lanes_of(i):
                        act.wait_ge(sig("turned").sem, sig("turned").nth(t))
                        nc.scalar.copy(xT[:, n], a_ps[n][:, 0].rearrange("p (t n) -> p t n", t=KT)
                                       ).then_inc(sig("xT").sem, 1)
                    for n, t in lanes_of(i):
                        act.wait_ge(sig("shifted").sem, sig("shifted").nth(t))
                        nc.scalar.activation(gate[:, n], gate[:, n], ACT.Exp).then_inc(sig("probs").sem, 1)
        for name in NORM_SIGNALS + ["logits", "top", "shifted", "probs", "den", "recip", "normed", "picked", "clipped",
                                    "unit", "rounded", "weighed", "turned", "xT"]:
            sig(name).advance(TILES)
        sig("combined").advance(TILES * E)
        sig("y_ps").advance(TILES * E // 2)


class Context:
    pass


def tower(nc, dram, out):
    k = Context()
    k.dram = dram
    with ExitStack() as ctx:
        sb = lambda name, shape, dt=F32: ctx.enter_context(nc.sbuf_tensor(name, shape, dt))
        k.const_sb = sb("const_sb", [P, CONST_COLS])
        k.h = sb("h", [P, TILES, D])
        k.rows = sb("rows", [P, TILES, D])
        k.xT = sb("xT", [P, KT, TILES * S])
        k.region_a = sb("region_a", [P, 10240])
        k.region_b = sb("region_b", [P, 5376])
        k.logits = sb("logits", [P, TILES, 32])
        k.gates = sb("gates", [P, TILES, 33])
        k.minus_half, k.eps_ln, k.eps_rms = (sb(name, [P, 1]) for name in ("minus_half", "eps_ln", "eps_rms"))
        k.ident16 = sb("ident16", [P, P], BF16)
        k.conv_w, k.conv_b = sb("conv_w", [P, 8, 3]), sb("conv_b", [P, 8])
        k.shared = sb("shared", [P, 6 * P])
        k.v_bias = sb("v_bias", [4, D])
        k.idle = sb("idle", [P, LANES])
        k.emb_rows = sb("emb_rows", [LEVELS, D])
        k.level_cols = sb("level_cols", [P, B])
        k.score_rows = sb("score_rows", [LEVELS, 512])
        k.value_rows = sb("value_rows", [P, 4, D])
        k.const = lambda name: k.const_sb[:, CONST_AT[name][0]:CONST_AT[name][0] + CONST_AT[name][1]]
        signals = {}

        def sig(name):
            if name not in signals:
                signals[name] = Signal(ctx.enter_context(nc.semaphore("s_" + name)))
            return signals[name]
        k.sig = sig
        k.load_small, k.load_a, k.load_b, k.store = (
            Loads(ctx.enter_context(nc.semaphore(name))) for name in ("load_small", "load_a", "load_b", "store"))
        chain_sem = ctx.enter_context(nc.semaphore("vector_step"))
        steps = [0]

        def chain(dve):
            def link(ins):
                steps[0] += 1
                ins.then_inc(chain_sem, 1)
                dve.wait_ge(chain_sem, steps[0])
            return link
        k.chain = chain
        k.load_lane = [Loads(ctx.enter_context(nc.semaphore(f"load_lane{n}"))) for n in range(LANES)]
        for name in SIGNALS:
            sig(name)
        with nc.Block() as block:
            @block.sync
            def _(sp):
                for name in SIGNALS:
                    sp.sem_inc(sig(name).sem, HEADSTART)
        level_tables(nc, k)
        level_attention(nc, k)
        repeat_heads(nc, k)
        self_attention(nc, k, rope=False)
        route(nc, k, 8, 2, int(1.25 * B * S * 2 / 8), biased=False)
        experts(nc, k, 8, dram["L0_ffn_w1"].rearrange("e (t p) f -> p e t f", p=P),
                dram["L0_ffn_w2"].rearrange("e (t p) n -> p e t n", p=P), gated=True, target=k.rows[:],
                hidden_bias=None, prefetch=load_mha)
        close_gqa(nc, k)
        self_attention(nc, k, rope=True)
        experts(nc, k, 2, dram["L1_attn_W1"].rearrange("(t p) (e f) -> p e t f", p=P, e=2),
                dram["L1_attn_W2"].rearrange("(e t p) n -> p e t n", p=P, e=2), gated=False, target=k.h[:],
                hidden_bias=attention_weights(k.region_a)["b1"], prefetch=load_bitlinear)
        bitlinear(nc, k)
        decay_attention(nc, k)
        with ExitStack() as layer:
            parts = [layer.enter_context(nc.sbuf_tensor(name, [P, KT, TILES * S], F32R)) for name in
                     ("x_high", "x_low")]
            swiglu_gates(nc, k, k.shared[:], *(x[:] for x in parts))
            route(nc, k, 32, 4, 2 * 2 * 512 * 4 // 32, biased=True)
            swiglu_experts(nc, k, *(x[:] for x in parts), k.shared[:])
        hyena(nc, k)
        mixture(nc, k)
        store(nc, k, out)


def store(nc, k, out):
    with nc.Block() as block:
        @block.sync
        def _(sp):
            sp.dma_start(out.rearrange("b s d -> s b d"), k.h[:]).then_inc(k.store.sem, 16)
            k.store.more()
            for loads in (k.load_a, k.load_b, k.load_small, *k.load_lane):
                if loads.count:
                    sp.wait_ge(loads.sem, loads.all())
            sp.wait_ge(k.store.sem, k.store.all())


_INS = [
    "x", "L0_tok_level_emb", "L0_attn_query_mat", "L0_attn_key_mat", "L0_attn_value_mat", "L0_attn_linear_m1",
    "L0_ffn_qw", "L0_ffn_qb", "L0_ffn_kw", "L0_ffn_kb", "L0_ffn_vw", "L0_ffn_vb", "L0_ffn_ow", "L0_ffn_ob",
    "L0_ffn_gate_w", "L0_ffn_w1", "L0_ffn_w2", "L0_ffn_norm1_w", "L0_ffn_norm2_w",
    "L1_attn_Wq", "L1_attn_bq", "L1_attn_Wk", "L1_attn_bk", "L1_attn_Wv", "L1_attn_bv", "L1_attn_Wo",
    "L1_attn_bo", "L1_attn_W1", "L1_attn_b1", "L1_attn_W2", "L1_attn_b2", "L1_attn_g1", "L1_attn_beta1",
    "L1_attn_g2", "L1_attn_beta2", "L1_ffn_w1", "L1_ffn_conv_w", "L1_ffn_conv_b", "L1_ffn_w2",
    "L2_attn_q", "L2_attn_k", "L2_attn_log_decay", "L2_attn_norm_weight", "L2_attn_o_w",
    "L2_ffn_gate_w", "L2_ffn_bias", "L2_ffn_W1", "L2_ffn_W3", "L2_ffn_W2", "L2_ffn_sw1", "L2_ffn_sw3",
    "L2_ffn_sw2", "L3_attn_in_proj_w", "L3_attn_in_proj_b", "L3_attn_short_w", "L3_attn_short_b",
    "L3_attn_fw1", "L3_attn_fb1", "L3_attn_fw2", "L3_attn_fb2", "L3_attn_fw3", "L3_attn_fb3",
    "L3_attn_out_w", "L3_attn_out_b", "L3_ffn_gate_w", "L3_ffn_gate_b", "L3_ffn_expert_w", "L3_ffn_expert_b",
]


def kernel(**inputs):
    from concourse import bacc
    from concourse.bass_utils import run_bass_kernel_spmd

    nc = bacc.Bacc("TRN2", target_bir_lowering=False, num_devices=1)
    arrays, dram = {}, {}
    for name in _INS:
        a = np.ascontiguousarray(inputs[name])
        arrays[f"in_{name}"] = a
        dram[name] = nc.dram_tensor(f"in_{name}", a.shape, mybir.dt.from_np(a.dtype), kind="ExternalInput").ap()
    arrays["in_constants"] = shape_constants()
    dram["constants"] = nc.dram_tensor("in_constants", [P, CONST_COLS], F32, kind="ExternalInput").ap()
    out = nc.dram_tensor("out_h", [B, S, D], F32, kind="ExternalOutput").ap()
    tower(nc, dram, out)
    return run_bass_kernel_spmd(nc, [arrays], core_ids=[0]).results[0]["out_h"]
```

```python
from contextlib import ExitStack

import numpy as np

import concourse.bass as bass
from concourse import mybir
from concourse.alu_op_type import AluOpType as ALU

ACT = mybir.ActivationFunctionType
F32 = mybir.dt.float32
BF16 = mybir.dt.bfloat16
F32R = mybir.dt.float32r
I32 = mybir.dt.int32
U32 = mybir.dt.uint32
AX_X = mybir.AxisListType.X

B, S, D = 16, 128, 256
P = 128
TILES = B
KT = D // P
LANES = 2
HEADSTART = 16
CHUNK = 4
CHUNKS = TILES // CHUNK
HEADS, HD = 16, 16
LEVELS = 32
LN_EPS = 1e-5
RMS_EPS = 1e-6
BIG = 1e30
ROUND = 12582912.0

CONST_PARTS = [
    ("ident", P), ("causal", P), ("before", P), ("ones", P), ("iota", LEVELS),
    ("headmask", P // HD), ("cos", D), ("sin", D), ("lag", P), ("dft_re", P), ("dft_im", P),
    ("dft_im0", P), ("dft_re1", P), ("inv_re", P), ("inv_im", P), ("edges", P), ("pos", P),
]
CONST_AT = {}
_n = 0
for _name, _width in CONST_PARTS:
    CONST_AT[_name] = (_n, _width)
    _n += _width
CONST_COLS = _n


def shape_constants():
    c = {}
    i = np.arange(P)
    c["ident"] = np.eye(P)
    c["causal"] = (i[:, None] <= i[None, :])
    c["before"] = (i[:, None] < i[None, :])
    c["ones"] = np.ones((P, P))
    c["iota"] = np.tile(np.arange(LEVELS), (P, 1))
    c["headmask"] = i[:, None] // HD == np.arange(P // HD)[None, :]
    exponent = np.arange(0, HD, 2, dtype=np.float32) / np.float32(HD)
    inv_freq = (1.0 / np.float32(10000.0) ** exponent).astype(np.float32)
    angle = (np.arange(S, dtype=np.float32)[:, None] * inv_freq[None, :]).astype(np.float64)
    cos, sin = np.repeat(np.cos(angle), 2, axis=1), np.repeat(np.sin(angle), 2, axis=1)
    sin[:, 0::2] *= -1.0
    c["cos"], c["sin"] = np.tile(cos, (1, HEADS)), np.tile(sin, (1, HEADS))
    c["lag"] = np.maximum(i[None, :] - i[:, None], 0)
    n = 2 * S
    w = 2 * np.pi * np.outer(i, i) / n
    re, im = np.cos(w), -np.sin(w)
    im0 = im.copy()
    im0[:, 0] = 0.0
    nyquist = np.cos(np.pi * i)
    packed = im.copy()
    packed[:, 0] = nyquist
    re1 = re.copy()
    re1[:, 0] = nyquist
    c["dft_re"], c["dft_im"], c["dft_im0"], c["dft_re1"] = re, packed, im0, re1
    both = np.where(i == 0, 1.0, 2.0)[:, None] / n
    c["inv_re"] = both * np.cos(w)
    inv_im = -2.0 / n * np.sin(w)
    inv_im[0] = nyquist / n
    c["inv_im"] = inv_im
    edges = np.ones((P, P))
    edges[0, 0] = 0.0
    edges[2, P - 1] = 0.0
    c["edges"] = edges
    c["pos"] = np.tile(np.linspace(0.0, 1.0, S, dtype=np.float32), (P, 1))
    return np.concatenate([np.asarray(c[name], np.float32) for name, _ in CONST_PARTS], axis=1)


SIGNALS = [
    "biased", "blocks", "branch", "clipped", "combined", "converted", "counts", "den", "diag",
    "expert_done", "first_tap", "hidden", "hidden_ps", "high", "highest", "k_apart", "kept",
    "last_T", "last_rows", "last_turned", "level", "logits", "low", "masked", "middle_tap",
    "moments", "moments_b", "moments_c", "normed", "o", "oT", "oT_ps", "onehot", "ones_set", "out",
    "pT", "pT_ps", "padded", "picked", "powers", "probs", "proj", "pv", "qT", "qk", "qkT_ps",
    "qk_raw", "ranks", "recip", "rotated", "rounded", "rstd", "rstd_b", "rstd_c", "scaled",
    "scores", "share", "share_T", "share_ps", "shifted", "shifted_var", "shifted_var_b",
    "shifted_var_c", "silu", "squares", "stats", "stats_b", "stats_c", "stored", "taps", "top",
    "top_ps", "turned", "unit", "unit_ps", "v1", "weighed", "x", "x2", "xT", "x_bo", "xn", "y_ps",
]


class Signal:

    def __init__(self, sem):
        self.sem, self.base = sem, HEADSTART

    def nth(self, n):
        return n + (self.base + 1)

    def before(self, n):
        return n + (self.base + 1 - LANES)

    def advance(self, n):
        self.base += n


class Loads:

    def __init__(self, sem):
        self.sem, self.count = sem, 0

    def more(self, n=1):
        self.count += n

    def all(self):
        return 16 * self.count


def scratch(nc, ctx, phase):
    def sb(name, shape, dt=F32):
        return ctx.enter_context(nc.sbuf_tensor(f"{phase}_{name}", shape, dt))

    def ps(name, shape, dt=F32):
        return ctx.enter_context(nc.psum_tensor(f"{phase}_{name}", shape, dt))
    return sb, ps


def spread(ap, shape):
    return ap.broadcast_to(shape)


def pipelined(eng, rounds, per, tail, ops, last_apart=False):
    def issue(i, units, valid):
        for u in units:
            for lag, op in ops:
                if valid(u - lag):
                    op(i, u - lag)
    longest = max(lag for lag, _ in ops)
    issue(0, range(per), lambda v: v >= 0)
    with eng.Fori(1, rounds - last_apart) as i:
        issue(i, range(per), lambda v: True)
    if last_apart:
        issue(rounds - 1, range(per), lambda v: True)
    issue(rounds, range(tail + longest), lambda v: v < tail)


def in_lanes(eng, ops):
    def of_tile(op):
        return lambda i, v: op(v % LANES, i * LANES + v)
    pipelined(eng, TILES // LANES, LANES, 0, [(lag, of_tile(op)) for lag, op in ops])


def level_tables(nc, k):
    with ExitStack() as ctx:
        sb, ps = scratch(nc, ctx, "level_tables")
        tok = sb("tok", [B, S], I32)
        tokf = sb("tokf", [B, S])
        opens, closes = sb("opens", [B, S]), sb("closes", [B, S])
        depth, low, high = sb("depth", [B, S]), sb("low", [B, S]), sb("high", [B, S])
        level = sb("level", [B, S])
        emb = sb("emb", [LEVELS, D])
        stats, mom = sb("stats0", [LEVELS, 6]), sb("mom0", [LEVELS, 2])
        rstd = sb("rstd0", [LEVELS, 1])
        xn = sb("xn0", [LEVELS, D])
        xnT = sb("xnT0", [P, KT, LEVELS])
        qT = sb("qT0", [P, 8, LEVELS])
        k_pairs = sb("k_pairs", [P, 8, 2 * LEVELS])
        v_quads = sb("v_quads", [P, 4, 2, P])
        turned = ps("turned0", [P, 512])
        q_ps, k_ps, v_ps = (ps(n, [P, 8, LEVELS]) for n in ("q_ps", "k_ps", "v_ps"))
        s_ps = ps("s_ps", [LEVELS, 512])
        m_ps = ps("m_ps", [P, 4, D])
        wq, wk, wv, m1 = (k.region_a[:, n * 2048:(n + 1) * 2048] for n in range(4))
        split = lambda w: w.rearrange("p (t n) -> p t n", t=KT)
        wq, wk, wv = split(wq), split(wk), split(wv)
        m1 = m1.rearrange("p (t n) -> p t n", n=D)
        C, sig = k.const, k.sig

        with nc.Block() as block:
            @block.sync
            def _(sp):
                sp.dma_start(tok[:], k.dram["x"]).then_inc(k.load_small.sem, 16)
                sp.dma_start(emb[:], k.dram["L0_tok_level_emb"]).then_inc(k.load_small.sem, 16)
                sp.dma_start(k.const_sb[:], k.dram["constants"]).then_inc(k.load_small.sem, 16)
                for w, name in ((wq, "query"), (wk, "key"), (wv, "value")):
                    sp.dma_start(w, k.dram[f"L0_attn_{name}_mat"].rearrange("(t p) h d -> p t (h d)", p=P)
                                 ).then_inc(k.load_a.sem, 16)
                sp.dma_start(m1, k.dram["L0_attn_linear_m1"].rearrange("(t p) n -> p t n", p=P)
                             ).then_inc(k.load_a.sem, 16)
            k.load_small.more(3)
            k.load_a.more(4)

            @block.vector
            def _(dve):
                link = k.chain(dve)
                dve.wait_ge(k.load_small.sem, k.load_small.all())
                link(nc.vector.tensor_scalar(k.emb_rows[:], emb[:], 0.15, None, ALU.mult))
                link(nc.vector.bn_stats(stats[:], k.emb_rows[:]))
                nc.vector.bn_aggr(mom[:], stats[:]).then_inc(sig("moments").sem, 1)
                link(nc.vector.tensor_copy(tokf[:], tok[:]))
                for count, ids in ((opens, (40., 91., 123.)), (closes, (41., 93., 125.))):
                    link(nc.vector.tensor_scalar(count[:], tokf[:], ids[0], None, ALU.is_equal))
                    for one in ids[1:]:
                        link(nc.vector.scalar_tensor_tensor(count[:], tokf[:], one, count[:],
                                                            ALU.is_equal, ALU.add))
                link(nc.vector.tensor_tensor(opens[:], opens[:], closes[:], ALU.subtract))
                link(nc.vector.memset(closes[:], 0.0))
                link(nc.vector.tensor_tensor_scan(depth[:], opens[:], closes[:], 0.0, ALU.add, ALU.add))
                link(nc.vector.tensor_scalar(low[:], depth[:], -1.0, None, ALU.mult))
                link(nc.vector.tensor_scalar(high[:], low[:], float(LEVELS - 1), None, ALU.add))
                link(nc.vector.tensor_tensor_scan(level[:], high[:], low[:], 0.0, ALU.min, ALU.max))
                nc.vector.tensor_tensor(level[:], level[:], depth[:], ALU.add).then_inc(sig("level").sem, 1)
                nc.vector.memset(k_pairs[:], 0.0)
                link(nc.vector.memset(v_quads[:], 0.0))
                dve.wait_ge(sig("rstd").sem, sig("rstd").nth(0))
                nc.vector.tensor_scalar(xn[:], k.emb_rows[:], mom[:, 0:1], rstd[:, 0:1], ALU.subtract,
                                        ALU.mult).then_inc(sig("xn").sem, 1)
                dve.wait_ge(sig("xT").sem, sig("xT").nth(0))
                nc.vector.tensor_copy(k.level_cols[:], turned[:, 256:256 + B])
                dve.wait_ge(sig("proj").sem, sig("proj").nth(0))
                kp = k_ps[:]
                vp = v_ps[:].rearrange("p (c u) l -> p c u l", u=2)
                for j in range(2):
                    rows = slice(64 * j, 64 * j + 64)
                    nc.vector.tensor_copy(k_pairs[rows, :, LEVELS * j:LEVELS * (j + 1)], kp[rows])
                    for u in range(2):
                        at = LEVELS * (2 * u + j)
                        last = nc.vector.tensor_copy(v_quads[rows, :, u, at:at + LEVELS], vp[rows, :, u, :])
                last.then_inc(sig("blocks").sem, 1)
                dve.wait_ge(sig("out").sem, sig("out").nth(0))
                nc.vector.tensor_copy(k.value_rows[:], m_ps[:])

            @block.gpsimd
            def _(pool):
                nc.gpsimd.memset(k.minus_half[:], -0.5)
                nc.gpsimd.memset(k.eps_ln[:], LN_EPS)
                nc.gpsimd.memset(k.eps_rms[:], RMS_EPS)
                pool.wait_ge(sig("moments").sem, sig("moments").nth(0))
                rsqrt(nc, pool, k, rstd[:], mom[:, 1:2], 1.0, LN_EPS, 0).then_inc(sig("rstd").sem, 1)

            @block.tensor
            def _(pe):
                pe.wait_ge(k.load_small.sem, k.load_small.all())
                pe.wait_ge(sig("level").sem, sig("level").nth(0))
                nc.tensor.transpose(turned[:, 256:256 + B], level[:], C("ident")[0:B, 0:B])
                pe.wait_ge(sig("xn").sem, sig("xn").nth(0))
                for t in range(KT):
                    last = nc.tensor.transpose(turned[:, LEVELS * t:LEVELS * (t + 1)], xn[:, P * t:P * (t + 1)],
                                               C("ident")[0:LEVELS, 0:LEVELS])
                last.then_inc(sig("turned").sem, 1)
                pe.wait_ge(k.load_a.sem, k.load_a.all())
                pe.wait_ge(sig("xT").sem, sig("xT").nth(0))
                for w, o in ((wq, q_ps), (wk, k_ps), (wv, v_ps)):
                    for m in range(8):
                        for t in range(KT):
                            last = nc.tensor.matmul(o[:, m, :], w[:, t, P * m:P * (m + 1)], xnT[:, t, :],
                                                    start=(t == 0), stop=(t == KT - 1))
                last.then_inc(sig("proj").sem, 1)
                pe.wait_ge(sig("blocks").sem, sig("blocks").nth(0))
                pe.wait_ge(sig("qk").sem, sig("qk").nth(0))
                for m in range(8):
                    last = nc.tensor.matmul(s_ps[:, 64 * m:64 * m + 64], qT[:, m, :], k_pairs[:, m, :],
                                            start=True, stop=True)
                last.then_inc(sig("scores").sem, 1)
                for c in range(4):
                    for u in range(2):
                        last = nc.tensor.matmul(m_ps[:, c, :], v_quads[:, c, u, :], m1[:, 2 * c + u, :],
                                                start=(u == 0), stop=(u == 1))
                last.then_inc(sig("out").sem, 1)

            @block.scalar
            def _(act):
                act.wait_ge(sig("turned").sem, sig("turned").nth(0))
                nc.scalar.copy(xnT[:], turned[:, 0:KT * LEVELS].rearrange("p (t l) -> p t l", t=KT)
                               ).then_inc(sig("xT").sem, 1)
                act.wait_ge(sig("proj").sem, sig("proj").nth(0))
                nc.scalar.mul(qT[:], q_ps[:], 8.0).then_inc(sig("qk").sem, 1)
                act.wait_ge(sig("scores").sem, sig("scores").nth(0))
                nc.scalar.copy(k.score_rows[:], s_ps[:])
        for name in ("moments", "level", "shifted_var", "rstd", "xn", "turned", "xT", "proj", "blocks", "qk",
                     "scores", "out"):
            sig(name).advance(1)


def rsqrt(nc, pool, k, out, in_, scale, eps, t):
    nc.gpsimd.tensor_scalar(out, in_, scale, eps, ALU.mult, ALU.add).then_inc(k.sig("shifted_var").sem, 1)
    pool.wait_ge(k.sig("shifted_var").sem, k.sig("shifted_var").nth(t))
    return nc.gpsimd.tensor_tensor(out, out, spread(k.minus_half[0:out.shape[0], 0:1], out.shape), ALU.pow)


def level_attention(nc, k):
    DEPTH = 2 * LANES
    with ExitStack() as ctx:
        sb, ps = scratch(nc, ctx, "level_attention")
        onehot = sb("onehot", [P, DEPTH, LEVELS])
        onehotT = sb("onehotT", [LEVELS, DEPTH, P])
        count = sb("count", [P, DEPTH, LEVELS])
        absent = sb("absent", [P, DEPTH, LEVELS])
        w = sb("weights", [P, DEPTH, HEADS, LEVELS])
        top, den = sb("top", [P, DEPTH, HEADS]), sb("den", [P, DEPTH, HEADS])
        wT = sb("wT", [P, DEPTH, 4, P])
        small_ps = [ps(f"small_ps{i}", [P, 512]) for i in range(DEPTH)]
        score_ps = [ps(f"score_ps{i}", [P, HEADS, LEVELS]) for i in range(LANES)]
        turn_ps = [ps(f"turn_ps{i}", [P, 4, P]) for i in range(LANES)]
        C, sig = k.const, k.sig
        all_levels = lambda ap: spread(ap.unsqueeze(2), [P, HEADS, LEVELS])
        all_heads = lambda ap: spread(ap.unsqueeze(1), [P, HEADS, LEVELS])

        def run(eng, ops):
            def of_tile(op):
                return lambda i, v: op(v % DEPTH, i * DEPTH + v)
            pipelined(eng, TILES // DEPTH, DEPTH, 0, [(lag, of_tile(op)) for lag, op in ops])

        with nc.Block() as block:
            @block.vector
            def _(dve):
                def levels(r, t):
                    dve.wait_ge(sig("turned").sem, sig("turned").nth(t) - DEPTH)
                    nc.vector.tensor_scalar(onehot[:, r, :], C("iota"), k.level_cols[:, bass.ds(t, 1)], None,
                                            ALU.is_equal).then_inc(sig("onehot").sem, 1)

                def counts(r, t):
                    dve.wait_ge(sig("xT").sem, sig("xT").nth(t))
                    nc.vector.tensor_copy(count[:, r, :], small_ps[r][:, P:P + LEVELS])
                    nc.vector.tensor_scalar(absent[:, r, :], small_ps[r][:, P:P + LEVELS], 0.0, -BIG,
                                            ALU.is_equal, ALU.mult).then_inc(sig("counts").sem, 1)

                def mask(r, t):
                    dve.wait_ge(sig("scores").sem, sig("scores").nth(t))
                    dve.wait_ge(sig("counts").sem, sig("counts").nth(t))
                    nc.vector.tensor_tensor(w[:, r], score_ps[r % LANES][:], all_heads(absent[:, r, :]),
                                            ALU.add).then_inc(sig("masked").sem, 1)

                def find_top(r, t):
                    dve.wait_ge(sig("masked").sem, sig("masked").nth(t))
                    nc.vector.tensor_reduce(top[:, r, :], w[:, r], AX_X, ALU.max).then_inc(sig("top").sem, 1)

                def shift(r, t):
                    dve.wait_ge(sig("top").sem, sig("top").nth(t))
                    nc.vector.tensor_tensor(w[:, r], w[:, r], all_levels(top[:, r, :]),
                                            ALU.subtract).then_inc(sig("shifted").sem, 1)

                def weigh(r, t):
                    dve.wait_ge(sig("probs").sem, sig("probs").nth(t))
                    nc.vector.tensor_tensor(w[:, r], w[:, r], all_heads(count[:, r, :]),
                                            ALU.mult).then_inc(sig("weighed").sem, 1)

                def add_up(r, t):
                    dve.wait_ge(sig("weighed").sem, sig("weighed").nth(t))
                    nc.vector.tensor_reduce(den[:, r, :], w[:, r], AX_X, ALU.add).then_inc(sig("den").sem, 1)

                def invert(r, t):
                    dve.wait_ge(sig("den").sem, sig("den").nth(t))
                    nc.vector.reciprocal(top[:, r, :], den[:, r, :]).then_inc(sig("recip").sem, 1)

                def normalise(r, t):
                    dve.wait_ge(sig("recip").sem, sig("recip").nth(t))
                    nc.vector.tensor_tensor(w[:, r], w[:, r], all_levels(top[:, r, :]),
                                            ALU.mult).then_inc(sig("normed").sem, 1)
                run(dve, [(0, levels), (2, weigh), (1, counts), (2, add_up), (1, mask), (2, invert), (1, find_top),
                          (2, normalise), (1, shift)])

            @block.tensor
            def _(pe):
                def turn_levels(r, t):
                    pe.wait_ge(sig("onehot").sem, sig("onehot").nth(t))
                    pe.wait_ge(sig("stored").sem, sig("stored").nth(t) - DEPTH)
                    nc.tensor.transpose(small_ps[r][0:LEVELS, 0:P], onehot[:, r, :], C("ident"))
                    nc.tensor.matmul(small_ps[r][:, P:P + LEVELS], C("causal"), onehot[:, r, :], start=True,
                                     stop=True).then_inc(sig("turned").sem, 1)

                def scores(r, t):
                    pe.wait_ge(sig("xT").sem, sig("xT").nth(t))
                    pe.wait_ge(sig("masked").sem, sig("masked").before(t))
                    nc.tensor.matmul(score_ps[r % LANES][:].rearrange("p h l -> p (h l)"), onehotT[:, r, :],
                                     k.score_rows[:], start=True, stop=True).then_inc(sig("scores").sem, 1)

                def turn_weights(r, t):
                    pe.wait_ge(sig("normed").sem, sig("normed").nth(t))
                    pe.wait_ge(sig("pT").sem, sig("pT").before(t))
                    for c in range(4):
                        last = nc.tensor.transpose(turn_ps[r % LANES][:, c, :], w[:, r, 4 * c:4 * c + 4, :].rearrange(
                            "p h l -> p (h l)"), C("ident"))
                    last.then_inc(sig("pT_ps").sem, 1)

                def output(r, t):
                    out = small_ps[r][:, 256:512]
                    pe.wait_ge(sig("counts").sem, sig("counts").nth(t))
                    nc.tensor.matmul(out, onehotT[:, r, :], k.emb_rows[:], start=True, stop=False)
                    pe.wait_ge(sig("pT").sem, sig("pT").nth(t))
                    for c in range(4):
                        last = nc.tensor.matmul(out, wT[:, r, c, :], k.value_rows[:, c, :], start=False,
                                                stop=(c == 3))
                    last.then_inc(sig("out").sem, 1)
                run(pe, [(3, turn_weights), (0, turn_levels), (1, scores), (3, output)])

            @block.scalar
            def _(act):
                def keep_levels(r, t):
                    act.wait_ge(sig("turned").sem, sig("turned").nth(t))
                    nc.scalar.copy(onehotT[:, r, :], small_ps[r][0:LEVELS, 0:P]).then_inc(sig("xT").sem, 1)

                def exponents(r, t):
                    act.wait_ge(sig("shifted").sem, sig("shifted").nth(t))
                    nc.scalar.activation(w[:, r], w[:, r], ACT.Exp).then_inc(sig("probs").sem, 1)

                def keep_weights(r, t):
                    act.wait_ge(sig("pT_ps").sem, sig("pT_ps").nth(t))
                    nc.scalar.copy(wT[:, r], turn_ps[r % LANES][:]).then_inc(sig("pT").sem, 1)

                def store_rows(r, t):
                    act.wait_ge(sig("out").sem, sig("out").nth(t))
                    nc.scalar.copy(k.h[:, t, :], small_ps[r][:, 256:512]).then_inc(sig("stored").sem, 1)
                run(act, [(2, exponents), (3, keep_weights), (0, keep_levels), (3, store_rows)])

            @block.gpsimd
            def _(pool):
                nc.gpsimd.memset(values_room(k, rope=False), 0.0)

            @block.sync
            def _(sp):
                load_gqa(k, sp)
        for name in ("onehot", "turned", "xT", "counts", "scores", "masked", "top", "shifted", "probs",
                     "weighed", "den", "recip", "normed", "pT_ps", "pT", "out", "stored"):
            sig(name).advance(TILES)


def attention_weights(region):
    at = {"wqk": (0, 1024), "wv": (1024, 512), "wo": (1536, 512), "bqk": (2048, 512), "bv": (2560, 256),
          "bo": (2816, 256), "row": (3072, 256), "gate": (3328, 16), "k_raw": (3344, 128), "v_raw": (3472, 128),
          "kb_raw": (3600, 64), "vb_raw": (3664, 64), "g1": (3744, 2), "beta1": (3746, 2), "g2": (3748, 2),
          "beta2": (3750, 2), "b1": (3752, 8)}
    w = {name: region[:, a:a + n] for name, (a, n) in at.items()}
    for name in ("wqk", "wv", "wo", "gate", "k_raw", "v_raw"):
        w[name] = w[name].rearrange("p (t n) -> p t n", t=KT)
    return w


def by_rows(ap):
    return ap.rearrange("(t p) n -> p t n", p=P)


def as_row(ap):
    return ap.rearrange("(a n) -> a n", a=1)


def as_columns(ap):
    return ap.rearrange("(t p) -> p t", p=P)


def to_all(ap):
    return ap.partition_broadcast(P)


def load_gqa(k, sp):
    w, d = attention_weights(k.region_b), k.dram
    pairs = [
        (w["wqk"][:, :, 0:D], by_rows(d["L0_ffn_qw"])), (w["k_raw"], by_rows(d["L0_ffn_kw"])),
        (w["v_raw"], by_rows(d["L0_ffn_vw"])), (w["wo"], by_rows(d["L0_ffn_ow"])),
        (w["gate"], by_rows(d["L0_ffn_gate_w"])), (w["bqk"][:, 0:D], to_all(d["L0_ffn_qb"])),
        (w["kb_raw"], to_all(d["L0_ffn_kb"])), (w["vb_raw"], to_all(d["L0_ffn_vb"])),
        (w["bo"], to_all(d["L0_ffn_ob"])), (w["row"], to_all(d["L0_ffn_norm1_w"])),
    ]
    for to, source in pairs:
        sp.dma_start(to, source).then_inc(k.load_b.sem, 16)
    k.load_b.more(len(pairs))


def load_mha(k, sp):
    w, d = attention_weights(k.region_a), k.dram
    pairs = [
        (w["wqk"][:, :, 0:D], by_rows(d["L1_attn_Wq"])), (w["wqk"][:, :, D:2 * D], by_rows(d["L1_attn_Wk"])),
        (w["wv"], by_rows(d["L1_attn_Wv"])), (w["wo"], by_rows(d["L1_attn_Wo"])),
        (w["bqk"][:, 0:D], to_all(d["L1_attn_bq"])), (w["bqk"][:, D:2 * D], to_all(d["L1_attn_bk"])),
        (w["bv"], to_all(d["L1_attn_bv"])), (w["bo"], to_all(d["L1_attn_bo"])),
        (w["row"], to_all(d["L1_attn_b2"])), (w["g1"], as_columns(d["L1_attn_g1"])),
        (w["beta1"], as_columns(d["L1_attn_beta1"])), (w["g2"], as_columns(d["L1_attn_g2"])),
        (w["beta2"], as_columns(d["L1_attn_beta2"])), (w["b1"], as_columns(d["L1_attn_b1"])),
    ]
    for to, source in pairs:
        sp.dma_start(to, source, allow_slow_non_contiguous=True).then_inc(k.load_a.sem, 16)
    k.load_a.more(len(pairs))


def repeat_heads(nc, k):
    w = attention_weights(k.region_b)
    r4 = lambda ap: ap.rearrange("p (g r d) -> p g r d", g=4, r=4)
    with nc.Block() as block:
        @block.gpsimd
        def _(pool):
            pool.wait_ge(k.load_b.sem, k.load_b.all())
            for to, raw in ((w["wqk"][:, 0, D:], w["k_raw"][:, 0, :]), (w["wqk"][:, 1, D:], w["k_raw"][:, 1, :]),
                            (w["wv"][:, 0, :], w["v_raw"][:, 0, :]), (w["wv"][:, 1, :], w["v_raw"][:, 1, :]),
                            (w["bqk"][:, D:], w["kb_raw"]), (w["bv"], w["vb_raw"])):
                n = raw.shape[0]
                nc.gpsimd.tensor_copy(r4(to), spread(raw.rearrange("p (g d) -> p g d", g=4).unsqueeze(2),
                                                     [n, 4, 4, HD]))


GROUP = P // HD
STEP = P + HD


def values_room(k, rope):
    return (k.region_b if rope else k.region_a)[:, 0:LANES * KT * GROUP * STEP]


def self_attention(nc, k, rope):
    w = attention_weights(k.region_a if rope else k.region_b)
    loads = k.load_a if rope else k.load_b
    DEPTH = 2 * LANES
    with ExitStack() as ctx:
        sb, ps = scratch(nc, ctx, ("mha" if rope else "gqa"))
        stats, mom = sb("stats", [P, LANES, 6]), sb("mom", [P, LANES, 2])
        rstd = sb("rstd", [P, LANES, 1])
        stats_c, mom_c = sb("stats_c", [P, LANES, 6]), sb("mom_c", [P, LANES, 2])
        rstd_c = sb("rstd_c", [P, LANES, 1])
        x = sb("x_rows", [P, DEPTH, D])
        x_bo = sb("x_plus_bo", [P, LANES, D])
        xn = sb("xn", [P, LANES, D]) if rope else None
        xT = sb("x_turned", [P, LANES, KT, P])
        qk = sb("qk", [P, LANES, 2, D])
        qk_raw = sb("qk_raw", [P, LANES, 2, D]) if rope else qk
        swapped = sb("qk_swapped", [P, LANES, 2, D]) if rope else None
        qT = sb("qT", [P, LANES, KT, P])
        in_k = GROUP * KT * P
        k_room = k.region_a[:, 10240 - LANES * in_k:]
        v_room = values_room(k, rope)
        k_apart = k_room.rearrange("p (n f j z) -> p n f j z", n=LANES, f=KT, j=GROUP)
        v_apart = v_room.rearrange("p (n f c) -> p n f c", n=LANES, f=KT)
        e = sb("e", [P, LANES, HEADS, P])
        eT = sb("eT", [P, LANES, HEADS, P])
        top, den = sb("top", [P, LANES, HEADS]), sb("den", [P, LANES, HEADS])
        share = sb("share", [P, LANES, D])
        scratch_rows = sb("scratch_rows", [P, LANES, D])
        share_T = sb("share_turned", [P, LANES, KT, P])
        oT = sb("oT", [P, LANES, KT, P])
        last_rows = sb("last_rows", [P, LANES, D])
        last_T = None if rope else sb("last_T", [P, LANES, KT, P])
        score_ps = ps("score_ps", [P, HEADS, P])
        a_ps = [ps(f"a_ps{n}", [P, 512]) for n in range(LANES)]
        b_ps = [ps(f"b_ps{n}", [P, 512]) for n in range(LANES)]
        C, sig = k.const, k.sig
        turn = lambda bank: bank[:, 0:D].rearrange("p (t n) -> p t n", t=KT)
        by_half = lambda bank: bank[:].rearrange("p (s f) -> p s f", s=2)
        by_head = lambda ap: ap.rearrange("p (h d) -> p h d", h=HEADS)

        def run(eng, ops):
            def of_tile(op):
                return lambda i, v: op(v % LANES, v % DEPTH, i * DEPTH + v)
            pipelined(eng, TILES // DEPTH, DEPTH, 0, [(lag, of_tile(op)) for lag, op in ops])

        with nc.Block() as block:
            @block.vector
            def _(dve):
                def moments_of(source, counted, done, to, row):
                    statistics, moments = to

                    def op(n, r, t):
                        if source:
                            dve.wait_ge(sig(source).sem, sig(source).nth(t))
                        nc.vector.bn_stats(statistics[:, n], row(n, r, t)).then_inc(sig(counted).sem, 1)
                        dve.wait_ge(sig(counted).sem, sig(counted).nth(t))
                        nc.vector.memset(k.idle[:, n:n + 1], 0.0)
                        nc.vector.bn_aggr(moments[:, n], statistics[:, n]).then_inc(sig(done).sem, 1)
                    return op

                def norm_h(n, r, t):
                    dve.wait_ge(sig("kept").sem, sig("kept").nth(t) - DEPTH)
                    dve.wait_ge(sig("rstd").sem, sig("rstd").nth(t))
                    nc.vector.tensor_scalar(x[:, r], k.h[:, t, :], mom[:, n, 0:1], rstd[:, n], ALU.subtract,
                                            ALU.mult).then_inc(sig("x").sem, 1)

                def norm_x(n, r, t):
                    dve.wait_ge(sig("turned").sem, sig("turned").before(t))
                    dve.wait_ge(sig("rstd_b").sem, sig("rstd_b").nth(t))
                    nc.vector.tensor_scalar(xn[:, n], x[:, r], mom[:, n, 0:1], rstd[:, n], ALU.subtract,
                                            ALU.mult).then_inc(sig("xn").sem, 1)

                def biases(n, r, t):
                    dve.wait_ge(sig("proj").sem, sig("proj").nth(t))
                    if rope:
                        dve.wait_ge(sig("qk").sem, sig("qk").before(t))
                    nc.vector.tensor_tensor(qk_raw[:, n], by_half(a_ps[n]), w["bqk"].rearrange("p (s f) -> p s f", s=2),
                                            ALU.add).then_inc(sig("qk_raw" if rope else "qk").sem, 1)
                    for f in range(KT):
                        cols = slice(P * f, P * (f + 1))
                        by_group = lambda ap: ap.rearrange("p (j d) -> p j d", j=GROUP)
                        last = nc.vector.tensor_tensor(by_group(v_apart[:, n, f])[:, :, 0:HD],
                                                       by_group(b_ps[n][:, cols]), by_group(w["bv"][:, cols]),
                                                       ALU.add)
                    last.then_inc(sig("v1").sem, 1)

                def rotate(n, r, t):
                    dve.wait_ge(sig("qk_raw").sem, sig("qk_raw").nth(t))
                    for s in range(2):
                        nc.vector.tensor_tensor(
                            swapped[:, n, s].rearrange("p (f two) -> p f two", two=2),
                            qk_raw[:, n, s].rearrange("p (f two) -> p f two", two=2)[:, :, ::-1],
                            C("sin").rearrange("p (f two) -> p f two", two=2), ALU.mult)
                    nc.vector.tensor_tensor(qk[:, n], qk_raw[:, n], spread(C("cos").unsqueeze(1), [P, 2, D]),
                                            ALU.mult).then_inc(sig("rotated").sem, 1)

                def keys_apart(n, r, t):
                    dve.wait_ge(sig("qT").sem, sig("qT").nth(t))
                    for f in range(KT):
                        last = nc.vector.tensor_tensor(
                            k_apart[:, n, f],
                            spread(a_ps[n][:, P * (KT + f):P * (KT + f + 1)].unsqueeze(1), [P, GROUP, P]),
                            spread(C("headmask").unsqueeze(2), [P, GROUP, P]), ALU.mult)
                    last.then_inc(sig("k_apart").sem, 1)

                def find_top(n, r, t):
                    dve.wait_ge(sig("scores").sem, sig("scores").nth(t))
                    nc.vector.tensor_reduce(top[:, n], score_ps[:], AX_X, ALU.max).then_inc(sig("top").sem, 1)

                def shift(n, r, t):
                    dve.wait_ge(sig("top").sem, sig("top").nth(t))
                    nc.vector.tensor_tensor(e[:, n], score_ps[:], spread(top[:, n].unsqueeze(2), [P, HEADS, P]),
                                            ALU.subtract).then_inc(sig("shifted").sem, 1)

                def sum_exponents(n, r, t):
                    dve.wait_ge(sig("probs").sem, sig("probs").nth(t))
                    nc.vector.tensor_reduce(den[:, n], e[:, n], AX_X, ALU.add).then_inc(sig("den").sem, 1)
                    dve.wait_ge(sig("den").sem, sig("den").nth(t))
                    nc.vector.reciprocal(den[:, n], den[:, n]).then_inc(sig("recip").sem, 1)
                    dve.wait_ge(sig("recip").sem, sig("recip").nth(t))
                    nc.vector.tensor_copy(by_head(share[:, n]), spread(den[:, n].unsqueeze(2), [P, HEADS, HD])
                                          ).then_inc(sig("share").sem, 1)

                def normalise(n, r, t):
                    dve.wait_ge(sig("share_T").sem, sig("share_T").nth(t))
                    dve.wait_ge(sig("pv").sem, sig("pv").nth(t))
                    nc.vector.tensor_tensor(oT[:, n], turn(a_ps[n]), share_T[:, n], ALU.mult).then_inc(sig("oT").sem, 1)

                def add_output(n, r, t):
                    dve.wait_ge(sig("x_bo").sem, sig("x_bo").nth(t))
                    dve.wait_ge(sig("out").sem, sig("out").nth(t))
                    nc.vector.tensor_tensor(x[:, r], a_ps[n][:, 0:D], x_bo[:, n], ALU.add).then_inc(sig("x2").sem, 1)

                def norm_output(n, r, t):
                    dve.wait_ge(sig("kept").sem, sig("kept").before(t))
                    dve.wait_ge(sig("stored").sem, sig("stored").before(t))
                    dve.wait_ge(sig("rstd_c").sem, sig("rstd_c").nth(t))
                    if rope:
                        last = nc.vector.tensor_scalar(last_rows[:, n], x[:, r], mom_c[:, n, 0:1], rstd_c[:, n],
                                                       ALU.subtract, ALU.mult)
                    else:
                        last = nc.vector.scalar_tensor_tensor(last_rows[:, n], x[:, r], rstd_c[:, n], w["row"],
                                                              ALU.mult, ALU.mult)
                    last.then_inc(sig("last_rows").sem, 1)

                stats_h = moments_of(None, "stats", "moments", (stats, mom), lambda n, r, t: k.h[:, t, :])
                dve.wait_ge(loads.sem, loads.all())
                if rope:
                    stats_x = moments_of("x", "stats_b", "moments_b", (stats, mom), lambda n, r, t: x[:, r])
                    stats_x2 = moments_of("x2", "stats_c", "moments_c", (stats_c, mom_c),
                                          lambda n, r, t: x[:, r])
                    run(dve, [(2, find_top), (2, shift), (0, stats_h), (1, biases), (1, rotate), (0, norm_h),
                              (2, sum_exponents), (0, stats_x), (1, keys_apart), (0, norm_x), (2, normalise),
                              (2, add_output), (2, stats_x2), (2, norm_output)])
                else:
                    run(dve, [(2, find_top), (2, shift), (0, stats_h), (1, biases), (0, norm_h), (2, sum_exponents),
                              (1, keys_apart), (2, normalise), (2, add_output), (2, norm_output)])

            @block.gpsimd
            def _(pool):
                def inverse_root(source, shifted, done, out, variance, eps):
                    def op(n, r, t):
                        pool.wait_ge(sig(source).sem, sig(source).nth(t))
                        nc.gpsimd.tensor_tensor(out[:, n], variance[:, n, 1:2], eps[:], ALU.add
                                                ).then_inc(sig(shifted).sem, 1)
                        pool.wait_ge(sig(shifted).sem, sig(shifted).nth(t))
                        nc.gpsimd.tensor_tensor(out[:, n], out[:, n], k.minus_half[:], ALU.pow
                                                ).then_inc(sig(done).sem, 1)
                    return op

                def add_pairs(n, r, t):
                    pool.wait_ge(sig("rotated").sem, sig("rotated").nth(t))
                    nc.gpsimd.tensor_tensor(qk[:, n], qk[:, n], swapped[:, n], ALU.add).then_inc(sig("qk").sem, 1)

                def add_output_bias(n, r, t):
                    pool.wait_ge(sig("x2").sem, sig("x2").before(t))
                    pool.wait_ge(sig("x").sem, sig("x").nth(t))
                    nc.gpsimd.tensor_tensor(x_bo[:, n], x[:, r], w["bo"], ALU.add).then_inc(sig("x_bo").sem, 1)

                def keep(n, r, t):
                    pool.wait_ge(sig("last_rows").sem, sig("last_rows").nth(t))
                    if rope:
                        nc.gpsimd.tensor_tensor(scratch_rows[:, n], x[:, r], w["row"], ALU.add
                                                ).then_inc(sig("biased").sem, 1)
                        pool.wait_ge(sig("biased").sem, sig("biased").nth(t))
                        nc.gpsimd.tensor_tensor(k.h[:, t, :], k.h[:, t, :], scratch_rows[:, n], ALU.add
                                                ).then_inc(sig("kept").sem, 1)
                    else:
                        nc.gpsimd.tensor_copy(k.rows[:, t, :], last_rows[:, n]).then_inc(sig("kept").sem, 1)

                pool.wait_ge(loads.sem, loads.all())
                root_h = inverse_root("moments", "shifted_var", "rstd", rstd, mom, k.eps_ln)
                if rope:
                    root_x = inverse_root("moments_b", "shifted_var_b", "rstd_b", rstd, mom, k.eps_ln)
                    root_x2 = inverse_root("moments_c", "shifted_var_c", "rstd_c", rstd_c, mom_c, k.eps_ln)
                    run(pool, [(0, root_h), (1, add_pairs), (0, root_x), (1, add_output_bias), (2, root_x2),
                               (2, keep)])
                else:
                    root_x2 = inverse_root("squares", "shifted_var_c", "rstd_c", rstd_c, mom_c, k.eps_rms)
                    run(pool, [(0, root_h), (1, add_output_bias), (2, root_x2), (2, keep)])

            @block.tensor
            def _(pe):
                def turn_x(n, r, t):
                    ready = sig("xn") if rope else sig("x")
                    pe.wait_ge(ready.sem, ready.nth(t))
                    pe.wait_ge(sig("x2").sem, sig("x2").before(t))
                    rows = xn[:, n] if rope else x[:, r]
                    for f in range(KT):
                        last = nc.tensor.transpose(turn(a_ps[n])[:, f], rows[:, P * f:P * (f + 1)], C("ident"))
                    last.then_inc(sig("turned").sem, 1)

                def project(n, r, t):
                    pe.wait_ge(sig("stored").sem, sig("stored").before(t))
                    pe.wait_ge(sig("xT").sem, sig("xT").nth(t))
                    for bank, width, name in ((a_ps[n], 2 * D, "wqk"), (b_ps[n], D, "wv")):
                        for f in range(KT):
                            last = nc.tensor.matmul(bank[:, 0:width], xT[:, n, f], w[name][:, f, :],
                                                    start=(f == 0), stop=(f == KT - 1))
                    last.then_inc(sig("proj").sem, 1)

                def turn_qk(n, r, t):
                    pe.wait_ge(sig("v1").sem, sig("v1").nth(t))
                    pe.wait_ge(sig("qk").sem, sig("qk").nth(t))
                    for f in range(2 * KT):
                        last = nc.tensor.transpose(a_ps[n][:, P * f:P * (f + 1)],
                                                   qk[:, n, f // KT, P * (f % KT):P * (f % KT + 1)], C("ident"))
                    last.then_inc(sig("qkT_ps").sem, 1)

                def scores(parts):
                    def op(n, r, t):
                        if parts[0] == 0:
                            pe.wait_ge(sig("k_apart").sem, sig("k_apart").nth(t))
                            pe.wait_ge(sig("shifted").sem, sig("shifted").nth(t) - 1)
                        for m in parts:
                            f, heads = m // 2, slice(m % 2 * 4, m % 2 * 4 + 4)
                            last = nc.tensor.matmul(score_ps[:, 4 * m:4 * m + 4].rearrange("p j z -> p (j z)"),
                                                    qT[:, n, f, :],
                                                    k_apart[:, n, f, heads].rearrange("p j z -> p (j z)"),
                                                    start=True, stop=True)
                        if parts[-1] == 3:
                            last.then_inc(sig("scores").sem, 1)
                    return op

                def turn_probs(q):
                    def op(n, r, t):
                        if q == 0:
                            pe.wait_ge(sig("probs").sem, sig("probs").nth(t))
                        if q >= 2:
                            pe.wait_ge(sig("pT").sem, sig("pT").nth(t * 4 + (q - 2)))
                        bank = (a_ps, b_ps)[q % 2][n]
                        for m in range(4):
                            last = nc.tensor.transpose(bank[:, P * m:P * (m + 1)], e[:, n, 4 * q + m, :], C("ident"))
                        last.then_inc(sig("pT_ps").sem, 1)
                    return op

                def turn_share(n, r, t):
                    pe.wait_ge(sig("share").sem, sig("share").nth(t))
                    for f in range(KT):
                        last = nc.tensor.transpose(turn(b_ps[n])[:, f], share[:, n, P * f:P * (f + 1)], C("ident"))
                    last.then_inc(sig("share_ps").sem, 1)

                def weigh(n, r, t):
                    pe.wait_ge(sig("pT").sem, sig("pT").nth(t * 4 + 3))
                    for h in range(HEADS):
                        f, j = h // GROUP, h % GROUP
                        last = nc.tensor.matmul(turn(a_ps[n])[:, f], v_apart[:, n, f, P * j:P * (j + 1)], eT[:, n, h],
                                                start=(j == 0), stop=(j == GROUP - 1))
                    last.then_inc(sig("pv").sem, 1)

                def output(n, r, t):
                    pe.wait_ge(sig("oT").sem, sig("oT").nth(t))
                    for f in range(KT):
                        last = nc.tensor.matmul(a_ps[n][:, 0:D], oT[:, n, f], w["wo"][:, f, :], start=(f == 0),
                                                stop=(f == KT - 1))
                    last.then_inc(sig("out").sem, 1)

                def turn_last(n, r, t):
                    pe.wait_ge(sig("last_rows").sem, sig("last_rows").nth(t))
                    for f in range(KT):
                        last = nc.tensor.transpose(turn(b_ps[n])[:, f], last_rows[:, n, P * f:P * (f + 1)],
                                                   C("ident"))
                    last.then_inc(sig("last_turned").sem, 1)

                def logits(n, r, t):
                    pe.wait_ge(sig("last_T").sem, sig("last_T").nth(t))
                    for f in range(KT):
                        last = nc.tensor.matmul(b_ps[n][:, 0:8], last_T[:, n, f], w["gate"][:, f, :],
                                                start=(f == 0), stop=(f == KT - 1))
                    last.then_inc(sig("logits").sem, 1)

                pe.wait_ge(loads.sem, loads.all())
                run(pe, [(1, project), (2, turn_probs(0)), (2, turn_probs(1)), (1, turn_qk),
                         (2, turn_probs(2)), (2, turn_probs(3)), (2, weigh), (2, turn_share),
                         (1, scores((0, 1))), (2, output), (1, scores((2, 3))),
                         (0, turn_x), (2, turn_last)] + ([] if rope else [(2, logits)]))

            @block.scalar
            def _(act):
                def keep_xT(n, r, t):
                    act.wait_ge(sig("turned").sem, sig("turned").nth(t))
                    if rope:
                        for f in range(KT):
                            last = nc.scalar.activation(xT[:, n, f], turn(a_ps[n])[:, f], ACT.Identity,
                                                        bias=w["beta1"][:, f:f + 1], scale=w["g1"][:, f:f + 1])
                        last.then_inc(sig("xT").sem, 1)
                    else:
                        nc.scalar.copy(xT[:, n], turn(a_ps[n])).then_inc(sig("xT").sem, 1)

                def exponents(n, r, t):
                    act.wait_ge(sig("shifted").sem, sig("shifted").nth(t))
                    nc.scalar.activation(e[:, n], e[:, n], ACT.Exp, scale=HD ** -0.5).then_inc(sig("probs").sem, 1)

                def keep_probs(q):
                    def op(n, r, t):
                        act.wait_ge(sig("pT_ps").sem, sig("pT_ps").nth(t * 4 + q))
                        bank = (a_ps, b_ps)[q % 2][n]
                        nc.scalar.copy(eT[:, n, 4 * q:4 * q + 4, :], bank[:].rearrange("p (m q) -> p m q", m=4)
                                       ).then_inc(sig("pT").sem, 1)
                    return op

                def keep_qT(n, r, t):
                    act.wait_ge(sig("qkT_ps").sem, sig("qkT_ps").nth(t))
                    nc.scalar.copy(qT[:, n], turn(a_ps[n])).then_inc(sig("qT").sem, 1)

                def keep_share(n, r, t):
                    act.wait_ge(sig("share_ps").sem, sig("share_ps").nth(t))
                    nc.scalar.copy(share_T[:, n], turn(b_ps[n])).then_inc(sig("share_T").sem, 1)

                def mean_square(n, r, t):
                    act.wait_ge(sig("x2").sem, sig("x2").nth(t))
                    nc.scalar.activation(scratch_rows[:, n], x[:, r], ACT.Square, scale=D ** -0.5,
                                         accum_out=mom_c[:, n, 1:2]
                                         ).then_inc(sig("squares").sem, 1)

                def keep_last(n, r, t):
                    act.wait_ge(sig("last_turned").sem, sig("last_turned").nth(t))
                    if rope:
                        for f in range(KT):
                            last = nc.scalar.activation(k.xT[:, f, bass.ds(t * P, P)], turn(b_ps[n])[:, f],
                                                        ACT.Identity, bias=w["beta2"][:, f:f + 1],
                                                        scale=w["g2"][:, f:f + 1])
                        last.then_inc(sig("stored").sem, 1)
                    else:
                        nc.scalar.copy(last_T[:, n], turn(b_ps[n])).then_inc(sig("last_T").sem, 1)

                def keep_logits(n, r, t):
                    act.wait_ge(sig("logits").sem, sig("logits").nth(t))
                    nc.scalar.copy(k.logits[:, t, 0:8], b_ps[n][:, 0:8]).then_inc(sig("stored").sem, 1)
                    nc.scalar.copy(k.xT[:, :, bass.ds(t * P, P)], last_T[:, n])

                act.wait_ge(loads.sem, loads.all())
                ops = [(2, exponents), (2, keep_probs(0)), (2, keep_probs(1)), (1, keep_qT),
                       (2, keep_probs(2)), (2, keep_probs(3)), (2, keep_share)]
                run(act, ops + ([(0, keep_xT), (2, keep_last)] if rope else
                                [(2, mean_square), (0, keep_xT), (2, keep_last), (2, keep_logits)]))
        names = ["stats", "moments", "shifted_var", "rstd", "x", "turned", "xT", "proj", "qk", "v1", "qkT_ps", "qT",
                 "k_apart", "scores", "top", "shifted", "probs", "den", "recip", "share", "share_ps", "share_T", "pv",
                 "oT", "out", "x_bo", "x2",
                 "shifted_var_c", "rstd_c", "last_rows", "last_turned", "stored", "kept"]
        names += (["stats_b", "moments_b", "shifted_var_b", "rstd_b", "xn", "qk_raw", "rotated", "stats_c",
                   "moments_c", "biased"] if rope else ["squares", "last_T", "logits"])
        for name in names:
            sig(name).advance(TILES)
        for name in ("pT_ps", "pT"):
            sig(name).advance(4 * TILES)


def route(nc, k, experts, chosen, capacity, biased):
    with ExitStack() as ctx:
        sb, ps = scratch(nc, ctx, f"route{experts}")
        shape = [P, TILES, experts]
        probs, choice = sb("probs", shape), sb("choice", shape)
        best, index = sb("best", [P, TILES, 8]), sb("index", [P, TILES, 8], U32)
        indexf = sb("indexf", [P, TILES, 8])
        picked, hit, earlier = sb("picked", shape), sb("hit", shape), sb("earlier", shape)
        total = sb("total", [P, TILES])
        bias = sb("bias", [P, experts])
        rank_ps = ps("rank_ps", shape)
        C, sig = k.const, k.sig
        gates = k.gates[:, :, 0:experts]
        flat = lambda x: x[:].rearrange("p t e -> p (t e)")
        with nc.Block() as block:
            if biased:
                @block.sync
                def _(sp):
                    sp.dma_start(bias[:], to_all(k.dram["L2_ffn_bias"])).then_inc(k.load_small.sem, 16)
                k.load_small.more()

            @block.scalar
            def _(act):
                nc.scalar.activation(probs[:], k.logits[:, :, 0:experts], ACT.Exp, scale=-1.0
                                     ).then_inc(sig("probs").sem, 1)

            @block.vector
            def _(dve):
                link = k.chain(dve)
                nc.vector.memset(k.gates[:], 1.0)
                dve.wait_ge(sig("probs").sem, sig("probs").nth(0))
                link(nc.vector.tensor_scalar(probs[:], probs[:], 1.0, None, ALU.add))
                link(nc.vector.reciprocal(probs[:], probs[:]))
                if biased:
                    dve.wait_ge(k.load_small.sem, k.load_small.all())
                    link(nc.vector.tensor_tensor(choice[:], probs[:], spread(bias[:].unsqueeze(1), shape), ALU.add))
                else:
                    link(nc.vector.tensor_copy(choice[:], probs[:]))
                for t in range(TILES):
                    last = nc.vector.max(best[:, t], choice[:, t])
                link(last)
                for t in range(TILES):
                    last = nc.vector.max_index(index[:, t], best[:, t], choice[:, t])
                link(last)
                link(nc.vector.tensor_copy(indexf[:], index[:]))
                iota = spread(C("iota")[:, 0:experts].unsqueeze(1), shape)
                for j in range(chosen):
                    to = hit if j else picked
                    link(nc.vector.tensor_tensor(to[:], iota, spread(indexf[:, :, j:j + 1], shape), ALU.is_equal))
                    if j:
                        link(nc.vector.tensor_tensor(picked[:], picked[:], hit[:], ALU.add))
                link(nc.vector.memset(earlier[:, 0], 0.0))
                for t in range(1, TILES):
                    link(nc.vector.tensor_tensor(earlier[:, t], earlier[:, t - 1], picked[:, t - 1], ALU.add))
                nc.vector.tensor_tensor(hit[:], picked[:], probs[:], ALU.mult).then_inc(sig("picked").sem, 1)
                dve.wait_ge(sig("picked").sem, sig("picked").nth(0))
                link(nc.vector.tensor_reduce(total[:], hit[:], AX_X, ALU.add))
                if biased:
                    link(nc.vector.tensor_scalar(total[:], total[:], 1e-12, None, ALU.max))
                else:
                    link(nc.vector.tensor_scalar(total[:], total[:], 1e-6, None, ALU.add))
                link(nc.vector.reciprocal(total[:], total[:]))
                link(nc.vector.tensor_tensor(hit[:], hit[:], spread(total[:].unsqueeze(2), shape), ALU.mult))
                dve.wait_ge(sig("ranks").sem, sig("ranks").nth(0))
                nc.vector.scalar_tensor_tensor(gates, rank_ps[:], float(capacity), hit[:], ALU.is_lt, ALU.mult)

            @block.tensor
            def _(pe):
                pe.wait_ge(sig("picked").sem, sig("picked").nth(0))
                nc.tensor.matmul(flat(rank_ps), C("before"), flat(picked), start=True, stop=False)
                nc.tensor.matmul(flat(rank_ps), C("ones"), flat(earlier), start=False,
                                 stop=True).then_inc(sig("ranks").sem, 1)
        for name in ("probs", "picked", "ranks"):
            sig(name).advance(1)


def experts(nc, k, count, w1, w2, gated, target, hidden_bias, prefetch):
    F = 4
    WIDE = CHUNK * P
    with ExitStack() as ctx:
        sb, ps = scratch(nc, ctx, f"experts{count}")
        w1_sb, w2_sb = sb("w1", [P, LANES, KT, F * P]), sb("w2", [P, LANES, F, D])
        hid = [sb(f"hidden{n}", [P, F, WIDE]) for n in range(2)]
        hid_ps = ps("hidden_ps", [P, F, WIDE])
        y_ps = [ps(f"y_ps{n}", [P, CHUNK, D]) for n in range(2)]
        sig = k.sig
        rounds = count // LANES
        unit_order = [(n, c) for n in range(LANES) for c in range(CHUNKS)]
        PER = len(unit_order)

        with nc.Block() as block:
            if gated:
                @block.gpsimd
                def _(pool):
                    nc.gpsimd.memset(values_room(k, rope=True), 0.0)

            @block.sync
            def _(sp):
                prefetch(k, sp)
                with sp.Fori(0, rounds) as i:
                    for n in range(LANES):
                        e = i * LANES + n
                        sp.wait_ge(sig("expert_done").sem, sig("expert_done").before(e))
                        sp.dma_start(w1_sb[:, n], w1[:, e]).then_inc(k.load_lane[n].sem, 16)
                        sp.dma_start(w2_sb[:, n], w2[:, e]).then_inc(k.load_lane[n].sem, 16)

            @block.tensor
            def _(pe):
                with pe.Fori(0, rounds) as i:
                    def first(n, c, u):
                        if c == 0:
                            pe.wait_ge(k.load_lane[n].sem, i * 32 + (k.load_lane[n].all() + 32))
                        for f in range(F):
                            pe.wait_ge(sig("hidden").sem, i * (F * PER) + (sig("hidden").nth(F * u + f) - F))
                            for t in range(KT):
                                last = nc.tensor.matmul(hid_ps[:, f], w1_sb[:, n, t, P * f:P * (f + 1)],
                                                        k.xT[:, t, c * WIDE:(c + 1) * WIDE], start=(t == 0),
                                                        stop=(t == KT - 1))
                            last.then_inc(sig("hidden_ps").sem, 1)

                    def second(n, c, u):
                        pe.wait_ge(sig("hidden").sem, i * (F * PER) + sig("hidden").nth(F * u + F - 1))
                        pe.wait_ge(sig("combined").sem, i * PER + sig("combined").before(u))
                        for j in range(CHUNK):
                            for f in range(F):
                                last = nc.tensor.matmul(y_ps[u % 2][:, j], hid[u % 2][:, f, P * j:P * (j + 1)],
                                                        w2_sb[:, n, f, :], start=(f == 0), stop=(f == F - 1))
                        last.then_inc(sig("y_ps").sem, 1)
                    for u, (n, c) in enumerate(unit_order):
                        first(n, c, u)
                        if u:
                            second(*unit_order[u - 1], u - 1)
                    second(*unit_order[-1], PER - 1)

            @block.scalar
            def _(act):
                with act.Fori(0, rounds) as i:
                    for u, (n, c) in enumerate(unit_order):
                        act.wait_ge(sig("y_ps").sem, i * PER + sig("y_ps").before(u))
                        for f in range(F):
                            act.wait_ge(sig("hidden_ps").sem, i * (F * PER) + sig("hidden_ps").nth(F * u + f))
                            if hidden_bias is None:
                                last = nc.scalar.activation(hid[u % 2][:, f], hid_ps[:, f], ACT.Gelu)
                            else:
                                column = (i * LANES + n) * F + f
                                last = nc.scalar.activation(hid[u % 2][:, f], hid_ps[:, f], ACT.Relu,
                                                            bias=hidden_bias[:, bass.ds(column, 1)])
                            last.then_inc(sig("hidden").sem, 1)

            @block.vector
            def _(dve):
                with dve.Fori(0, rounds) as i:
                    for u, (n, c) in enumerate(unit_order):
                        dve.wait_ge(sig("y_ps").sem, i * PER + sig("y_ps").nth(u))
                        dve.wait_ge(sig("combined").sem, i * PER + (sig("combined").nth(u) - 1))
                        for j in range(CHUNK):
                            t = CHUNK * c + j
                            if gated:
                                last = nc.vector.scalar_tensor_tensor(
                                    target[:, t], y_ps[u % 2][:, j], k.gates[:, t, bass.ds(i * LANES + n, 1)],
                                    target[:, t], ALU.mult, ALU.add)
                            else:
                                last = nc.vector.tensor_tensor(target[:, t], y_ps[u % 2][:, j], target[:, t],
                                                               ALU.add)
                        last.then_inc(sig("combined").sem, 1)
                        if c == CHUNKS - 1:
                            dve.sem_inc(sig("expert_done").sem, 1)
        for n in range(LANES):
            k.load_lane[n].more(2 * rounds)
        units = rounds * PER
        for name, n in (("hidden", F * units), ("hidden_ps", F * units), ("y_ps", units), ("combined", units),
                        ("expert_done", count)):
            sig(name).advance(n)


def close_gqa(nc, k):
    with ExitStack() as ctx:
        sb, ps = scratch(nc, ctx, "close_gqa")
        norm2 = sb("norm2", [P, D])
        squares, normed = sb("squares", [P, LANES, D]), sb("normed", [P, LANES, D])
        mean, rstd = sb("mean", [P, TILES]), sb("rstd", [P, TILES])
        sig = k.sig
        with nc.Block() as block:
            @block.sync
            def _(sp):
                sp.dma_start(norm2[:], to_all(k.dram["L0_ffn_norm2_w"])).then_inc(k.load_small.sem, 16)
            k.load_small.more()

            @block.scalar
            def _(act):
                for t in range(TILES):
                    if t >= LANES:
                        act.wait_ge(sig("squares").sem, sig("squares").nth(t - LANES))
                    last = nc.scalar.activation(squares[:, t % LANES], k.rows[:, t], ACT.Square, scale=D ** -0.5,
                                                accum_out=mean[:, t:t + 1])
                    last.then_inc(sig("squares").sem, 1)

            @block.gpsimd
            def _(pool):
                pool.wait_ge(sig("squares").sem, sig("squares").nth(TILES - 1))
                nc.gpsimd.tensor_tensor(rstd[:], mean[:], spread(k.eps_rms[:], [P, TILES]),
                                        ALU.add).then_inc(sig("shifted_var").sem, 1)
                pool.wait_ge(sig("shifted_var").sem, sig("shifted_var").nth(0))
                nc.gpsimd.tensor_tensor(rstd[:], rstd[:], spread(k.minus_half[:], [P, TILES]),
                                        ALU.pow).then_inc(sig("rstd").sem, 1)
                with pool.Fori(0, TILES // LANES) as i:
                    for n in range(LANES):
                        t = i * LANES + n
                        pool.wait_ge(sig("xn").sem, sig("xn").nth(t))
                        nc.gpsimd.tensor_tensor(k.h[:, t, :], k.h[:, t, :], normed[:, n],
                                                ALU.add).then_inc(sig("kept").sem, 1)

            @block.vector
            def _(dve):
                dve.wait_ge(k.load_small.sem, k.load_small.all())
                dve.wait_ge(sig("rstd").sem, sig("rstd").nth(0))
                with dve.Fori(0, TILES // LANES) as i:
                    for n in range(LANES):
                        t = i * LANES + n
                        dve.wait_ge(sig("kept").sem, sig("kept").before(t))
                        nc.vector.scalar_tensor_tensor(normed[:, n], k.rows[:, t, :], rstd[:, bass.ds(t, 1)],
                                                       norm2[:], ALU.mult, ALU.mult).then_inc(sig("xn").sem, 1)
        for name, n in (("squares", TILES), ("shifted_var", 1), ("rstd", 1), ("xn", TILES), ("kept", TILES)):
            sig(name).advance(n)


def norm_pieces(ctx, nc, phase):
    sb, _ = scratch(nc, ctx, phase)
    return sb("ln_stats", [P, LANES, 6]), sb("ln_mom", [P, LANES, 2]), sb("ln_rstd", [P, LANES, 1])


def norm_moments(nc, k, dve, n, t, pieces):
    stats, mom, rstd = pieces
    sig = k.sig
    nc.vector.bn_stats(stats[:, n], k.h[:, t, :]).then_inc(sig("stats").sem, 1)
    dve.wait_ge(sig("stats").sem, sig("stats").nth(t))
    nc.vector.memset(k.idle[:, n:n + 1], 0.0)
    nc.vector.bn_aggr(mom[:, n], stats[:, n]).then_inc(sig("moments").sem, 1)


def norm_rows(nc, k, dve, n, t, pieces, out, reader):
    stats, mom, rstd = pieces
    sig = k.sig
    if reader:
        dve.wait_ge(sig(reader).sem, sig(reader).before(t))
    dve.wait_ge(sig("rstd").sem, sig("rstd").nth(t))
    nc.vector.tensor_scalar(out, k.h[:, t, :], mom[:, n, 0:1], rstd[:, n], ALU.subtract, ALU.mult
                            ).then_inc(sig("x").sem, 1)


def norm_root(nc, k, pool, n, t, pieces):
    stats, mom, rstd = pieces
    sig = k.sig
    pool.wait_ge(sig("moments").sem, sig("moments").nth(t))
    nc.gpsimd.tensor_tensor(rstd[:, n], mom[:, n, 1:2], k.eps_ln[:], ALU.add).then_inc(sig("shifted_var").sem, 1)
    pool.wait_ge(sig("shifted_var").sem, sig("shifted_var").nth(t))
    nc.gpsimd.tensor_tensor(rstd[:, n], rstd[:, n], k.minus_half[:], ALU.pow).then_inc(sig("rstd").sem, 1)


NORM_SIGNALS = ["stats", "moments", "shifted_var", "rstd", "x"]


def load_bitlinear(k, sp):
    w1 = k.region_b[:, 0:2048].rearrange("p (t n) -> p t n", n=D)
    w2 = k.region_b[:, 2048:4096].rearrange("p (t n) -> p t n", n=1024)
    for to, source in ((w1, by_rows(k.dram["L1_ffn_w1"])), (w2, by_rows(k.dram["L1_ffn_w2"])),
                       (k.conv_w[:], k.dram["L1_ffn_conv_w"].rearrange("(t p) a j -> p t (a j)", p=P)),
                       (k.conv_b[:], as_columns(k.dram["L1_ffn_conv_b"]))):
        sp.dma_start(to, source, allow_slow_non_contiguous=True).then_inc(k.load_b.sem, 16)
    k.load_b.more(4)


def load_decay(k, sp):
    r = k.region_a
    bf = r[:, 2048:4096].bitcast(BF16)
    d = k.dram
    pairs = [
        (r[:, 0:512].rearrange("p (t n) -> p t n", t=KT), by_rows(d["L2_attn_o_w"])),
        (r[:, 512:768], to_all(d["L2_attn_q"])), (r[:, 768:1024], to_all(d["L2_attn_k"])),
        (r[:, 1024:1280], to_all(d["L2_attn_norm_weight"])), (r[:, 1280:1296], to_all(d["L2_attn_log_decay"])),
        (bf[0:32, 0:256], d["L2_ffn_gate_w"]), (bf[:, 256:512], d["L2_ffn_sw1"]), (bf[:, 512:768], d["L2_ffn_sw3"]),
        (bf[:, 768:1024].rearrange("p (t n) -> p t n", t=KT), by_rows(d["L2_ffn_sw2"])),
    ]
    for to, source in pairs:
        sp.dma_start(to, source).then_inc(k.load_a.sem, 16)
    k.load_a.more(len(pairs))


def bitlinear(nc, k):
    CT = 8
    WIDE = CHUNK * P
    with ExitStack() as ctx:
        sb, ps = scratch(nc, ctx, "bitlinear")
        w1T, w2T = sb("w1T", [P, KT, CT * P], BF16), sb("w2T", [P, CT, D], BF16)
        mean = sb("weight_mean", [P, 2])
        unit = sb("weight_unit", [P, 2])
        w1 = k.region_b[:, 0:2048].rearrange("p (t n) -> p t n", n=D)
        w2 = k.region_b[:, 2048:4096].rearrange("p (t n) -> p t n", n=1024)
        unit_bc = k.xT[:, 0, :]
        qT = k.xT[:, 1, :].bitcast(BF16).rearrange("p (t n) -> p t n", t=KT)
        C, sig = k.const, k.sig

        with ExitStack() as ctx2, nc.Block() as block:
            sb2, ps2 = scratch(nc, ctx2, "bit_weights")
            ternary = sb2("ternary", [P, 2, 2048], BF16)
            scaled = sb2("scaled", [P, 2048])
            mean_ps = ps2("mean_ps", [P, 2])
            turned = [ps2(f"turned{n}", [P, CT, P], BF16) for n in range(4)]
            t1 = ternary[:, 0].rearrange("p (t n) -> p t n", n=D)
            t2 = ternary[:, 1].rearrange("p (t n) -> p t n", n=1024)

            @block.vector
            def _(dve):
                link = k.chain(dve)
                nc.vector.tensor_copy(k.ident16[:], C("ident"))
                dve.wait_ge(k.load_b.sem, k.load_b.all())
                for n in range(2):
                    last = nc.vector.tensor_reduce(mean[:, n:n + 1], k.region_b[:, 2048 * n:2048 * (n + 1)], AX_X,
                                                   ALU.add, apply_absolute_value=True)
                last.then_inc(sig("stats").sem, 1)
                dve.wait_ge(sig("moments").sem, sig("moments").nth(0))
                link(nc.vector.tensor_scalar(mean[:], mean_ps[:], 1.0 / (1024 * D), 1e-5, ALU.mult, ALU.max))
                link(nc.vector.reciprocal(unit[:], mean[:]))
                for n in range(2):
                    link(nc.vector.tensor_scalar(scaled[:], k.region_b[:, 2048 * n:2048 * (n + 1)], unit[:, n:n + 1],
                                                 ROUND, ALU.mult, ALU.add))
                    link(nc.vector.tensor_scalar(scaled[:], scaled[:], ROUND, 1.0, ALU.subtract, ALU.min))
                    link(nc.vector.tensor_scalar(ternary[:, n], scaled[:], -1.0, None, ALU.max))
                last = nc.vector.memset(k.idle[:], 0.0)
                last.then_inc(sig("x").sem, 1)

            @block.tensor
            def _(pe):
                pe.wait_ge(sig("stats").sem, sig("stats").nth(0))
                nc.tensor.matmul(mean_ps[:], C("ones"), mean[:], start=True, stop=True).then_inc(
                    sig("moments").sem, 1)
                pe.wait_ge(sig("x").sem, sig("x").nth(0))
                for half in range(2):
                    for c in range(CT):
                        nc.tensor.transpose(turned[half][:, c], t1[:, c, P * half:P * (half + 1)], k.ident16[:])
                        last = nc.tensor.transpose(turned[2 + half][:, c], t2[:, half, P * c:P * (c + 1)],
                                                   k.ident16[:])
                last.then_inc(sig("turned").sem, 1)

            @block.scalar
            def _(act):
                act.wait_ge(sig("turned").sem, sig("turned").nth(0))
                for half in range(2):
                    nc.scalar.copy(w1T[:, half].rearrange("p (c n) -> p c n", c=CT), turned[half][:])
                    nc.scalar.copy(w2T[:, :, P * half:P * (half + 1)], turned[2 + half][:])

            @block.sync
            def _(sp):
                load_decay(k, sp)
        for name in ("stats", "moments", "x", "turned"):
            sig(name).advance(1)

        with ExitStack() as ctx2, nc.Block() as block:
            sb2, ps2 = scratch(nc, ctx2, "bit_input")
            pieces = norm_pieces(ctx2, nc, "bit_input")
            x = sb2("x", [P, LANES, D])
            top, inv, f = (sb2(name, [P, LANES, 1]) for name in ("top", "inv", "unit"))
            q = sb2("q", [P, LANES, D], BF16)
            diag = sb2("diag", [P, LANES, P])
            bc_ps = [ps2(f"bc_ps{n}", [P, P]) for n in range(LANES)]
            q_ps = [ps2(f"q_ps{n}", [P, KT, P], BF16) for n in range(LANES)]

            @block.vector
            def _(dve):
                def moments(n, t):
                    norm_moments(nc, k, dve, n, t, pieces)

                def norm(n, t):
                    norm_rows(nc, k, dve, n, t, pieces, x[:, n], "stored")

                def find_top(n, t):
                    dve.wait_ge(sig("x").sem, sig("x").nth(t))
                    nc.vector.tensor_reduce(top[:, n], x[:, n], AX_X, ALU.max, apply_absolute_value=True
                                            ).then_inc(sig("top").sem, 1)

                def clip_top(n, t):
                    dve.wait_ge(sig("top").sem, sig("top").nth(t))
                    nc.vector.tensor_scalar(top[:, n], top[:, n], 1e-5, None, ALU.max).then_inc(sig("clipped").sem, 1)

                def units(n, t):
                    dve.wait_ge(sig("clipped").sem, sig("clipped").nth(t))
                    nc.vector.reciprocal(inv[:, n], top[:, n])
                    nc.vector.tensor_scalar(f[:, n], top[:, n], 1.0 / 127.0, mean[:, 0:1], ALU.mult, ALU.mult
                                            ).then_inc(sig("recip").sem, 1)

                def scale(n, t):
                    dve.wait_ge(sig("recip").sem, sig("recip").nth(t))
                    nc.vector.tensor_scalar(diag[:, n], C("ident"), f[:, n], None, ALU.mult
                                            ).then_inc(sig("diag").sem, 1)
                    nc.vector.tensor_scalar(x[:, n], x[:, n], inv[:, n], 127.0, ALU.mult, ALU.mult
                                            ).then_inc(sig("scaled").sem, 1)

                def clamp(n, t):
                    dve.wait_ge(sig("scaled").sem, sig("scaled").nth(t))
                    nc.vector.tensor_scalar(x[:, n], x[:, n], 127.0, -128.0, ALU.min, ALU.max
                                            ).then_inc(sig("shifted").sem, 1)

                def round_off(n, t):
                    dve.wait_ge(sig("shifted").sem, sig("shifted").nth(t))
                    nc.vector.tensor_scalar(q[:, n], x[:, n], ROUND, ROUND, ALU.add, ALU.subtract
                                            ).then_inc(sig("rounded").sem, 1)
                in_lanes(dve, [(2, clip_top), (0, moments), (2, units), (1, norm), (2, scale), (1, find_top),
                               (2, clamp), (2, round_off)])

            @block.gpsimd
            def _(pool):
                in_lanes(pool, [(0, lambda n, t: norm_root(nc, k, pool, n, t, pieces))])

            @block.tensor
            def _(pe):
                def spread_unit(n, t):
                    pe.wait_ge(sig("diag").sem, sig("diag").nth(t))
                    nc.tensor.matmul(bc_ps[n][:], C("ones"), diag[:, n], start=True, stop=True
                                     ).then_inc(sig("unit_ps").sem, 1)

                def turn_q(n, t):
                    pe.wait_ge(sig("rounded").sem, sig("rounded").nth(t))
                    for j in range(KT):
                        last = nc.tensor.transpose(q_ps[n][:, j], q[:, n, P * j:P * (j + 1)], k.ident16[:])
                    last.then_inc(sig("turned").sem, 1)
                in_lanes(pe, [(2, spread_unit), (2, turn_q)])

            @block.scalar
            def _(act):
                def keep_unit(n, t):
                    act.wait_ge(sig("unit_ps").sem, sig("unit_ps").nth(t))
                    nc.scalar.copy(unit_bc[:, bass.ds(t * P, P)], bc_ps[n][:])

                def keep_q(n, t):
                    act.wait_ge(sig("turned").sem, sig("turned").nth(t))
                    nc.scalar.copy(qT[:, :, bass.ds(t * P, P)], q_ps[n][:]).then_inc(sig("stored").sem, 1)
                in_lanes(act, [(2, keep_unit), (2, keep_q)])
        for name in NORM_SIGNALS + ["top", "clipped", "recip", "diag", "scaled", "shifted", "rounded", "unit_ps",
                                    "turned", "stored"]:
            sig(name).advance(TILES)

        with ExitStack() as ctx2, nc.Block() as block:
            sb2, ps2 = scratch(nc, ctx2, "bit_layers")
            padded = [sb2(f"padded{n}", [P, CHUNK, S + 2]) for n in range(2)]
            taps = [sb2(f"taps{n}", [P, CHUNK, S]) for n in range(2)]
            act_h = [sb2(f"hidden{n}", [P, CT, WIDE]) for n in range(2)]
            q = sb2("q", [P, CT, WIDE], BF16)
            highest = sb2("highest", [P, WIDE])
            top, inv, f = (sb2(name, [P, CHUNK]) for name in ("top", "inv", "unit"))
            diag = sb2("diag", [P, CHUNK, P])
            scale_bc = sb2("scale_bc", [P, WIDE])
            h_ps = [ps2(f"h_ps{n}", [P, WIDE]) for n in range(2)]
            top_ps, scale_ps = ps2("top_ps", [P, CHUNK, P]), ps2("scale_ps", [P, WIDE])
            y_ps = ps2("y_ps", [P, CHUNK, D])
            by_seq = lambda x: x.rearrange("p (b s) -> p b s", b=CHUNK)

            def run(eng, ops):
                def of_chunk(op):
                    return lambda i, v: op(v % 2, i * 2 + v)
                pipelined(eng, CHUNKS // 2, 2, 0, [(lag, of_chunk(op)) for lag, op in ops])

            @block.tensor
            def _(pe):
                def hidden(m):
                    def op(n, c):
                        u = c * CT + m
                        pe.wait_ge(sig("padded").sem, sig("padded").before(u))
                        for t in range(KT):
                            last = nc.tensor.matmul(h_ps[m % 2][:], w1T[:, t, P * m:P * (m + 1)],
                                                    qT[:, t, bass.ds(c * WIDE, WIDE)], start=(t == 0),
                                                    stop=(t == KT - 1))
                        last.then_inc(sig("hidden_ps").sem, 1)
                    return op

                def turn_highest(n, c):
                    pe.wait_ge(sig("highest").sem, sig("highest").nth(c))
                    for j in range(CHUNK):
                        last = nc.tensor.transpose(top_ps[:, j], highest[:, P * j:P * (j + 1)], C("ident"))
                    last.then_inc(sig("top_ps").sem, 1)

                def spread_scale(n, c):
                    pe.wait_ge(sig("diag").sem, sig("diag").nth(c))
                    nc.tensor.matmul(scale_ps[:], C("ones"), diag[:].rearrange("p j q -> p (j q)"), start=True,
                                     stop=True).then_inc(sig("unit_ps").sem, 1)

                def output(n, c):
                    pe.wait_ge(sig("stored").sem, sig("stored").nth(c) - 1)
                    pe.wait_ge(sig("rounded").sem, sig("rounded").nth(c))
                    for j in range(CHUNK):
                        for m in range(CT):
                            last = nc.tensor.matmul(y_ps[:, j], q[:, m, P * j:P * (j + 1)], w2T[:, m, :],
                                                    start=(m == 0), stop=(m == CT - 1))
                    last.then_inc(sig("y_ps").sem, 1)
                run(pe, [(0, hidden(0)), (0, hidden(1)), (0, hidden(2)), (1, turn_highest), (0, hidden(3)),
                         (0, hidden(4)), (1, spread_scale), (0, hidden(5)), (0, hidden(6)), (0, hidden(7)),
                         (1, output)])

            @block.scalar
            def _(act):
                def middle_tap(m):
                    def op(n, c):
                        act.wait_ge(sig("padded").sem, sig("padded").nth(c * CT + m))
                        nc.scalar.activation(taps[m % 2][:], padded[m % 2][:, :, 1:S + 1], ACT.Identity,
                                             bias=k.conv_b[:, m:m + 1], scale=k.conv_w[:, m, 1:2]
                                             ).then_inc(sig("middle_tap").sem, 1)
                    return op

                def silu(m):
                    def op(n, c):
                        act.wait_ge(sig("taps").sem, sig("taps").nth(c * CT + m))
                        nc.scalar.activation(by_seq(act_h[n][:, m]), taps[m % 2][:], ACT.Silu
                                             ).then_inc(sig("hidden").sem, 1)
                    return op

                def keep_scale(n, c):
                    act.wait_ge(sig("unit_ps").sem, sig("unit_ps").nth(c))
                    nc.scalar.copy(scale_bc[:], scale_ps[:]).then_inc(sig("recip").sem, 1)
                ops = []
                for m in range(CT):
                    ops.append((0, middle_tap(m)))
                    if m:
                        ops.append((0, silu(m - 1)))
                    if m == 4:
                        ops.append((1, keep_scale))
                run(act, ops + [(0, silu(CT - 1))])

            @block.gpsimd
            def _(pool):
                def scale(n, c):
                    pool.wait_ge(sig("recip").sem, sig("recip").nth(c))
                    nc.gpsimd.tensor_tensor(act_h[n][:], act_h[n][:], spread(scale_bc[:].unsqueeze(1), [P, CT, WIDE]),
                                            ALU.mult).then_inc(sig("scaled").sem, 1)
                run(pool, [(1, scale)])

            @block.vector
            def _(dve):
                def pad(m):
                    def op(n, c):
                        u = c * CT + m
                        dve.wait_ge(sig("hidden").sem, sig("hidden").before(u))
                        dve.wait_ge(sig("hidden_ps").sem, sig("hidden_ps").nth(u))
                        nc.vector.tensor_tensor(padded[m % 2][:, :, 1:S + 1], by_seq(h_ps[m % 2][:]),
                                                by_seq(unit_bc[:, bass.ds(c * WIDE, WIDE)]), ALU.mult
                                                ).then_inc(sig("padded").sem, 1)
                    return op

                def outer_taps(m):
                    def op(n, c):
                        u = c * CT + m
                        dve.wait_ge(sig("middle_tap").sem, sig("middle_tap").nth(u))
                        nc.vector.scalar_tensor_tensor(taps[m % 2][:], padded[m % 2][:, :, 0:S],
                                                       k.conv_w[:, m, 0:1], taps[m % 2][:], ALU.mult, ALU.add
                                                       ).then_inc(sig("first_tap").sem, 1)
                        dve.wait_ge(sig("first_tap").sem, sig("first_tap").nth(u))
                        nc.vector.scalar_tensor_tensor(taps[m % 2][:], padded[m % 2][:, :, 2:S + 2],
                                                       k.conv_w[:, m, 2:3], taps[m % 2][:], ALU.mult, ALU.add
                                                       ).then_inc(sig("taps").sem, 1)
                    return op

                def find_highest(n, c):
                    dve.wait_ge(sig("hidden").sem, sig("hidden").nth(c * CT + (CT - 1)))
                    nc.vector.tensor_reduce(highest[:], act_h[n][:].rearrange("p m t -> p t m"), AX_X, ALU.max,
                                            apply_absolute_value=True).then_inc(sig("highest").sem, 1)

                def units(n, c):
                    dve.wait_ge(sig("top_ps").sem, sig("top_ps").nth(c))
                    nc.vector.tensor_reduce(top[:], top_ps[:], AX_X, ALU.max).then_inc(sig("top").sem, 1)
                    dve.wait_ge(sig("top").sem, sig("top").nth(c))
                    nc.vector.tensor_scalar(top[:], top[:], 1e-5, None, ALU.max).then_inc(sig("clipped").sem, 1)
                    dve.wait_ge(sig("clipped").sem, sig("clipped").nth(c))
                    nc.vector.reciprocal(inv[:], top[:])
                    nc.vector.tensor_scalar(f[:], top[:], 1.0 / 127.0, mean[:, 1:2], ALU.mult, ALU.mult
                                            ).then_inc(sig("unit").sem, 1)
                    dve.wait_ge(sig("unit").sem, sig("unit").nth(c))
                    nc.vector.tensor_tensor(diag[:], spread(C("ident").unsqueeze(1), [P, CHUNK, P]),
                                            spread(inv[:].unsqueeze(2), [P, CHUNK, P]), ALU.mult
                                            ).then_inc(sig("diag").sem, 1)

                def round_hidden(n, c):
                    dve.wait_ge(sig("scaled").sem, sig("scaled").nth(c))
                    nc.vector.tensor_scalar(act_h[n][:], act_h[n][:], 127.0, ROUND, ALU.mult, ALU.add
                                            ).then_inc(sig("shifted").sem, 1)
                    dve.wait_ge(sig("shifted").sem, sig("shifted").nth(c))
                    nc.vector.tensor_scalar(q[:], act_h[n][:], ROUND, 127.0, ALU.subtract, ALU.min
                                            ).then_inc(sig("rounded").sem, 1)

                def add_output(n, c):
                    dve.wait_ge(sig("y_ps").sem, sig("y_ps").nth(c))
                    for j in range(CHUNK):
                        t = c * CHUNK + j
                        last = nc.vector.scalar_tensor_tensor(k.h[:, t, :], y_ps[:, j], f[:, j:j + 1], k.h[:, t, :],
                                                              ALU.mult, ALU.add)
                    last.then_inc(sig("stored").sem, 1)
                link = k.chain(dve)
                for n in range(2):
                    last = nc.vector.memset(padded[n][:], 0.0)
                link(last)
                run(dve, [(0, pad(0)), (1, find_highest), (0, pad(1)), (0, outer_taps(0)), (0, pad(2)),
                          (0, outer_taps(1)), (2, add_output), (1, units), (0, pad(3)), (0, outer_taps(2)),
                          (0, pad(4)), (0, outer_taps(3)), (0, pad(5)), (0, outer_taps(4)), (0, pad(6)),
                          (0, outer_taps(5)), (0, pad(7)), (0, outer_taps(6)), (0, outer_taps(7)),
                          (1, round_hidden)])
        for name in ("padded", "hidden_ps", "middle_tap", "first_tap", "taps", "hidden"):
            sig(name).advance(CHUNKS * CT)
        for name in ("highest", "top_ps", "top", "clipped", "unit", "diag", "unit_ps", "recip", "scaled", "shifted",
                     "rounded", "y_ps", "stored"):
            sig(name).advance(CHUNKS)


def decay_attention(nc, k):
    r = k.region_a
    o_w = r[:, 0:512].rearrange("p (t n) -> p t n", t=KT)
    q, kk, norm_w, log_decay = r[:, 512:768], r[:, 768:1024], r[:, 1024:1280], r[:, 1280:1296]
    all_out = k.xT[:].rearrange("p t (n d) -> p (t n) d", d=D)
    C, sig = k.const, k.sig
    with ExitStack() as ctx:
        sb, ps = scratch(nc, ctx, "decay")
        powers = sb("powers", [P, HEADS, P])
        qk, per_head = sb("qk", [P, D]), sb("per_head", [P, HEADS])
        ln_decay, size, soft = (sb(name, [P, HEADS]) for name in ("ln_decay", "size", "soft"))
        o_wT = sb("o_wT", [P, KT, D])
        pieces = norm_pieces(ctx, nc, "decay")
        turned = ps("turned", [P, KT, D])
        out_ps = [ps(f"out_ps{n}", [P, TILES, HD]) for n in range(4)]

        with nc.Block() as block:
            @block.vector
            def _(dve):
                link = k.chain(dve)
                dve.wait_ge(k.load_a.sem, k.load_a.all())
                link(nc.vector.tensor_scalar(soft[:], log_decay, -1.0, None, ALU.mult))
                nc.vector.tensor_tensor(size[:], soft[:], log_decay, ALU.max).then_inc(sig("top").sem, 1)
                link(nc.vector.tensor_scalar(ln_decay[:], log_decay, -1.0, 0.0, ALU.mult, ALU.max))
                link(nc.vector.tensor_tensor(qk[:], q, kk, ALU.mult))
                link(nc.vector.tensor_reduce(per_head[:], qk[:].rearrange("p (h d) -> p h d", h=HEADS), AX_X,
                                             ALU.add))
                dve.wait_ge(sig("unit").sem, sig("unit").nth(0))
                link(nc.vector.tensor_tensor(ln_decay[:], ln_decay[:], soft[:], ALU.add))
                nc.vector.tensor_scalar(ln_decay[:], ln_decay[:], -1.0, None, ALU.mult).then_inc(sig("recip").sem, 1)
                for h in range(HEADS):
                    dve.wait_ge(sig("powers").sem, sig("powers").nth(h))
                    nc.vector.scalar_tensor_tensor(powers[:, h], powers[:, h], per_head[:, h:h + 1], C("causal"),
                                                   ALU.mult, ALU.mult)

                def moments(n, t):
                    norm_moments(nc, k, dve, n, t, pieces)

                def norm(n, t):
                    norm_rows(nc, k, dve, n, t, pieces, k.rows[:, t, :], None)
                in_lanes(dve, [(0, moments), (1, norm)])

            @block.gpsimd
            def _(pool):
                in_lanes(pool, [(0, lambda n, t: norm_root(nc, k, pool, n, t, pieces))])

            @block.scalar
            def _(act):
                act.wait_ge(sig("top").sem, sig("top").nth(0))
                nc.scalar.activation(soft[:], size[:], ACT.Exp, scale=-1.0).then_inc(sig("probs").sem, 1)
                act.wait_ge(sig("probs").sem, sig("probs").nth(0))
                nc.scalar.activation(soft[:], soft[:], ACT.Ln, bias=1.0).then_inc(sig("unit").sem, 1)
                act.wait_ge(sig("turned").sem, sig("turned").nth(0))
                nc.scalar.copy(o_wT[:], turned[:])
                act.wait_ge(sig("recip").sem, sig("recip").nth(0))
                for h in range(HEADS):
                    nc.scalar.activation(powers[:, h], C("lag"), ACT.Exp, scale=ln_decay[:, h:h + 1]
                                         ).then_inc(sig("powers").sem, 1)

            @block.tensor
            def _(pe):
                pe.wait_ge(k.load_a.sem, k.load_a.all())
                for a in range(KT):
                    for b in range(KT):
                        last = nc.tensor.transpose(turned[:, b, P * a:P * (a + 1)], o_w[:, a, P * b:P * (b + 1)],
                                                   C("ident"))
                last.then_inc(sig("turned").sem, 1)
        for name in ("top", "unit", "recip", "probs", "turned"):
            sig(name).advance(1)
        sig("powers").advance(HEADS)
        for name in NORM_SIGNALS:
            sig(name).advance(TILES)

        with nc.Block() as block:
            @block.tensor
            def _(pe):
                for h in range(HEADS):
                    if h >= 4:
                        pe.wait_ge(sig("stored").sem, sig("stored").nth(h - 4))
                    nc.tensor.matmul(out_ps[h % 4][:], powers[:, h], k.rows[:, :, HD * h:HD * (h + 1)], start=True,
                                     stop=True).then_inc(sig("out").sem, 1)

            @block.scalar
            def _(act):
                for h in range(HEADS):
                    act.wait_ge(sig("out").sem, sig("out").nth(h))
                    nc.scalar.copy(all_out[:, :, HD * h:HD * (h + 1)], out_ps[h % 4][:]
                                   ).then_inc(sig("stored").sem, 1)
        sig("out").advance(HEADS)
        sig("stored").advance(HEADS)

        with ExitStack() as ctx2, nc.Block() as block:
            sb2, ps2 = scratch(nc, ctx2, "decay_out")
            squares, normed = sb2("squares", [P, LANES, D]), sb2("normed", [P, LANES, D])
            mean, rstd = sb2("mean", [P, LANES, 1]), sb2("rstd", [P, LANES, 1])
            normedT = sb2("normedT", [P, LANES, KT, P])
            bank = [ps2(f"bank{n}", [P, KT, P]) for n in range(2)]

            @block.scalar
            def _(act):
                def mean_square(n, t):
                    act.wait_ge(sig("xn").sem, sig("xn").before(t))
                    nc.scalar.activation(squares[:, n], all_out[:, t, :], ACT.Square, scale=D ** -0.5,
                                         accum_out=mean[:, n]).then_inc(sig("squares").sem, 1)

                def keep_turned(n, t):
                    act.wait_ge(sig("turned").sem, sig("turned").nth(t))
                    nc.scalar.copy(normedT[:, n], bank[n][:]).then_inc(sig("xT").sem, 1)
                in_lanes(act, [(1, keep_turned), (0, mean_square)])

            @block.gpsimd
            def _(pool):
                def inverse_root(n, t):
                    pool.wait_ge(sig("squares").sem, sig("squares").nth(t))
                    nc.gpsimd.tensor_tensor(rstd[:, n], mean[:, n], k.eps_rms[:], ALU.add
                                            ).then_inc(sig("shifted_var").sem, 1)
                    pool.wait_ge(sig("shifted_var").sem, sig("shifted_var").nth(t))
                    nc.gpsimd.tensor_tensor(rstd[:, n], rstd[:, n], k.minus_half[:], ALU.pow
                                            ).then_inc(sig("rstd").sem, 1)
                in_lanes(pool, [(0, inverse_root)])

            @block.vector
            def _(dve):
                def norm(n, t):
                    dve.wait_ge(sig("turned").sem, sig("turned").before(t))
                    dve.wait_ge(sig("rstd").sem, sig("rstd").nth(t))
                    nc.vector.scalar_tensor_tensor(normed[:, n], all_out[:, t, :], rstd[:, n], norm_w, ALU.mult,
                                                   ALU.mult).then_inc(sig("xn").sem, 1)

                def add_output(n, t):
                    dve.wait_ge(sig("out").sem, sig("out").nth(t))
                    nc.vector.tensor_tensor(k.h[:, t, :], bank[n][:].rearrange("p t n -> p (t n)"),
                                            k.h[:, t, :], ALU.add).then_inc(sig("kept").sem, 1)
                in_lanes(dve, [(1, norm), (2, add_output)])

            @block.tensor
            def _(pe):
                def turn(n, t):
                    pe.wait_ge(sig("kept").sem, sig("kept").before(t))
                    pe.wait_ge(sig("xn").sem, sig("xn").nth(t))
                    for f in range(KT):
                        last = nc.tensor.transpose(bank[n][:, f], normed[:, n, P * f:P * (f + 1)], C("ident"))
                    last.then_inc(sig("turned").sem, 1)

                def output(n, t):
                    pe.wait_ge(sig("xT").sem, sig("xT").nth(t))
                    for f in range(KT):
                        last = nc.tensor.matmul(bank[n][:].rearrange("p t n -> p (t n)"), normedT[:, n, f],
                                                o_wT[:, f, :], start=(f == 0), stop=(f == KT - 1))
                    last.then_inc(sig("out").sem, 1)
                in_lanes(pe, [(2, output), (1, turn)])
        for name in ("squares", "xT", "shifted_var", "rstd", "xn", "kept", "turned", "out"):
            sig(name).advance(TILES)


def load_hyena(k, sp):
    r, d = k.region_b, k.dram
    w = hyena_weights(k)
    pairs = [
        (w["in_proj"], by_rows(d["L3_attn_in_proj_w"])), (w["out_w"], by_rows(d["L3_attn_out_w"])),
        (w["fw3"], d["L3_attn_fw3"]), (w["fw2"], d["L3_attn_fw2"]),
        (w["in_bias"], to_all(d["L3_attn_in_proj_b"])), (w["out_b"], to_all(d["L3_attn_out_b"])),
        (w["fb3"], as_row(d["L3_attn_fb3"])), (w["fw1"], d["L3_attn_fw1"]),
        (w["fb1"], d["L3_attn_fb1"].rearrange("(n a) -> n a", a=1)),
        (w["fb2"], d["L3_attn_fb2"].rearrange("(n a) -> n a", a=1)),
        (w["short_w"], to_all(d["L3_attn_short_w"].rearrange("c a j -> (c a j)"))),
        (w["taps_T"], d["L3_attn_short_w"].rearrange("c a j -> j (a c)")),
        (k.v_bias[3:4, :], as_row(d["L3_attn_short_b"])),
    ]
    for to, source in pairs:
        sp.dma_start(to, source, allow_slow_non_contiguous=True).then_inc(k.load_b.sem, 16)
    k.load_b.more(len(pairs))


def hyena_weights(k):
    r = k.region_b
    return {
        "in_proj": r[:, 0:1536].rearrange("p (t n) -> p t n", t=KT),
        "out_w": r[:, 1536:2048].rearrange("p (t n) -> p t n", t=KT),
        "fw3": r[:, 2048:2560], "fw2": r[0:64, 2560:2688], "in_bias": r[:, 2688:3456], "out_b": r[:, 3456:3712],
        "fb3": r[0:1, 3712:4224], "fw1": r[0:1, 4224:4288], "fb1": r[0:64, 4288:4289], "fb2": r[:, 4289:4290],
        "short_w": r[:, 4290:5058], "taps_T": r[0:3, 5058:5314],
    }


def load_mixture(k, sp):
    r, d = k.region_a, k.dram
    pairs = [
        (r[:, 0:4096].rearrange("p (e t n) -> p e t n", e=8, t=KT),
         d["L3_ffn_expert_w"].rearrange("e (t p) n -> p e t n", p=P)),
        (r[:, 4096:4112].rearrange("p (t n) -> p t n", t=KT), by_rows(d["L3_ffn_gate_w"])),
        (r[:, 4112:4120], to_all(d["L3_ffn_gate_b"])), (r[0:8, 4120:4376], d["L3_ffn_expert_b"]),
    ]
    for to, source in pairs:
        sp.dma_start(to, source).then_inc(k.load_a.sem, 16)
    k.load_a.more(len(pairs))


def swiglu_gates(nc, k, shared, x_high, x_low):
    bf = k.region_a[:, 2048:4096].bitcast(BF16)
    gate_raw, sw1, sw3 = bf[0:32, 0:256], bf[:, 256:512], bf[:, 512:768]
    sw2 = bf[:, 768:1024].rearrange("p (t n) -> p t n", t=KT)
    C, sig = k.const, k.sig
    with ExitStack() as ctx:
        sb, ps = scratch(nc, ctx, "swiglu_gates")
        pieces = norm_pieces(ctx, nc, "swiglu_gates")
        x, xT = sb("x", [P, LANES, D]), sb("xT", [P, LANES, KT, P])
        gate_wT = sb("gate_wT", [P, KT, 32])
        raw_ps = ps("raw_ps", [P, 8, P], BF16)
        bank = [ps(f"bank{n}", [P, KT, P]) for n in range(2)]
        with nc.Block() as block:
            @block.vector
            def _(dve):
                def moments(n, t):
                    norm_moments(nc, k, dve, n, t, pieces)

                def norm(n, t):
                    norm_rows(nc, k, dve, n, t, pieces, x[:, n], "turned")
                in_lanes(dve, [(0, moments), (1, norm)])

            @block.gpsimd
            def _(pool):
                def norm(n, t):
                    norm_root(nc, k, pool, n, t, pieces)

                def low_part(n, t):
                    pool.wait_ge(sig("xT").sem, sig("xT").nth(t))
                    at = bass.ds(t * P, P)
                    nc.gpsimd.tensor_tensor(x_low[:, :, at], xT[:, n], x_high[:, :, at].bitcast(F32),
                                            ALU.subtract).then_inc(sig("low").sem, 1)
                in_lanes(pool, [(0, norm), (2, low_part)])

            @block.tensor
            def _(pe):
                pe.wait_ge(k.load_a.sem, k.load_a.all())
                for t in range(KT):
                    cols = slice(P * t, P * (t + 1))
                    nc.tensor.transpose(raw_ps[:, t, 0:32], gate_raw[:, cols], k.ident16[0:32, 0:32])
                    nc.tensor.transpose(raw_ps[:, 2 + t], sw1[:, cols], k.ident16[:])
                    nc.tensor.transpose(raw_ps[:, 4 + t], sw3[:, cols], k.ident16[:])
                    last = nc.tensor.transpose(raw_ps[:, 6 + t], sw2[:, t], k.ident16[:])
                last.then_inc(sig("proj").sem, 1)

                def turn_x(n, t):
                    pe.wait_ge(sig("stored").sem, sig("stored").before(t))
                    pe.wait_ge(sig("x").sem, sig("x").nth(t))
                    for f in range(KT):
                        last = nc.tensor.transpose(bank[n][:, f], x[:, n, P * f:P * (f + 1)], C("ident"))
                    last.then_inc(sig("turned").sem, 1)

                def logits(n, t):
                    pe.wait_ge(sig("xT").sem, sig("xT").nth(t))
                    for f in range(KT):
                        last = nc.tensor.matmul(bank[n][:, 0, 0:32], xT[:, n, f], gate_wT[:, f], start=(f == 0),
                                                stop=(f == KT - 1))
                    last.then_inc(sig("logits").sem, 1)
                in_lanes(pe, [(1, turn_x), (2, logits)])

            @block.scalar
            def _(act):
                act.wait_ge(sig("proj").sem, sig("proj").nth(0))
                nc.scalar.copy(gate_wT[:], raw_ps[:, 0:2, 0:32])
                nc.scalar.copy(shared.rearrange("p (m n) -> p m n", n=P), raw_ps[:, 2:8])

                def keep_xT(n, t):
                    act.wait_ge(sig("turned").sem, sig("turned").nth(t))
                    act.wait_ge(sig("low").sem, sig("low").before(t))
                    nc.scalar.copy(x_high[:, :, bass.ds(t * P, P)], bank[n][:])
                    nc.scalar.copy(xT[:, n], bank[n][:]).then_inc(sig("xT").sem, 1)

                def keep_logits(n, t):
                    act.wait_ge(sig("logits").sem, sig("logits").nth(t))
                    nc.scalar.copy(k.logits[:, t, :], bank[n][:, 0, 0:32]).then_inc(sig("stored").sem, 1)
                in_lanes(act, [(2, keep_logits), (1, keep_xT)])
        sig("proj").advance(1)
        for name in NORM_SIGNALS + ["turned", "xT", "low", "logits", "stored"]:
            sig(name).advance(TILES)


def swiglu_experts(nc, k, x_high, x_low, shared):
    E, I = 32, 128
    WIDE = CHUNK * P
    W = 2 * KT * I + D
    d = k.dram
    w1 = d["L2_ffn_W1"].rearrange("e (t p) i -> p e t i", p=P)
    w3 = d["L2_ffn_W3"].rearrange("e (t p) i -> p e t i", p=P)
    w2 = d["L2_ffn_W2"].rearrange("e p n -> p e n")
    rounds = E // LANES
    PER = LANES * CHUNKS
    HIDS = 4
    sig = k.sig

    def item(signal, i, v, back=0):
        return i * PER + (signal.nth(v) - back)

    with ExitStack() as ctx:
        sb, ps = scratch(nc, ctx, "swiglu")
        raw = sb("raw", [P, LANES, W], BF16)
        w = sb("w", [P, LANES, W], F32R)
        gate_h = [sb(f"gate{n}", [P, WIDE]) for n in range(2)]
        hid = [sb(f"hidden{n}", [P, WIDE]) for n in range(HIDS)]
        high = [sb(f"high{n}", [P, WIDE], F32R) for n in range(HIDS)]
        low = [sb(f"low{n}", [P, WIDE], F32R) for n in range(HIDS)]
        a_ps = [ps(f"a_ps{n}", [P, WIDE]) for n in range(2)]
        b_ps = [ps(f"b_ps{n}", [P, WIDE]) for n in range(2)]
        y_ps = [ps(f"y_ps{n}", [P, CHUNK, D]) for n in range(2)]

        def weights(v):
            one = w[:, v // CHUNKS % LANES]
            return (one[:, 0:KT * I].rearrange("p (t i) -> p t i", t=KT),
                    one[:, KT * I:2 * KT * I].rearrange("p (t i) -> p t i", t=KT), one[:, 2 * KT * I:])

        with nc.Block() as block:
            @block.sync
            def _(sp):
                load_hyena(k, sp)
                with sp.Fori(0, rounds) as i:
                    for n in range(LANES):
                        e = i * LANES + n
                        sp.wait_ge(sig("converted").sem, sig("converted").before(e))
                        for source, at in ((w1, 0), (w3, KT * I)):
                            sp.dma_start(raw[:, n, at:at + KT * I].rearrange("p (t i) -> p t i", t=KT),
                                         source[:, e]).then_inc(k.load_lane[n].sem, 16)
                        sp.dma_start(raw[:, n, 2 * KT * I:], w2[:, e]).then_inc(k.load_lane[n].sem, 16)

            @block.gpsimd
            def _(pool):
                def low_part(i, v):
                    pool.wait_ge(sig("high").sem, item(sig("high"), i, v))
                    pool.wait_ge(sig("y_ps").sem, item(sig("y_ps"), i, v, HIDS))
                    nc.gpsimd.tensor_tensor(low[v % HIDS][:], hid[v % HIDS][:], high[v % HIDS][:].bitcast(F32),
                                            ALU.subtract).then_inc(sig("low").sem, 1)
                pipelined(pool, rounds, PER, CHUNKS, [(0, low_part)])

            @block.tensor
            def _(pe):
                def first(i, v):
                    c = v % CHUNKS
                    if c == 0:
                        pe.wait_ge(sig("converted").sem, i * LANES + sig("converted").nth(v // CHUNKS))
                    w1, w3, _ = weights(v)
                    pe.wait_ge(sig("hidden").sem, item(sig("hidden"), i, v, 2))
                    for bank, part in ((a_ps, w1), (b_ps, w3)):
                        for x in (x_high, x_low):
                            for t in range(KT):
                                last = nc.tensor.matmul(bank[v % 2][:], part[:, t, :],
                                                        x[:, t, c * WIDE:(c + 1) * WIDE],
                                                        start=(x is x_high and t == 0),
                                                        stop=(x is x_low and t == KT - 1))
                    last.then_inc(sig("hidden_ps").sem, 1)

                def second(i, v):
                    pe.wait_ge(sig("low").sem, item(sig("low"), i, v))
                    pe.wait_ge(sig("combined").sem, item(sig("combined"), i, v, 2))
                    for j in range(CHUNK):
                        for part in (high, low):
                            last = nc.tensor.matmul(y_ps[v % 2][:, j], part[v % HIDS][:, P * j:P * (j + 1)],
                                                    weights(v)[2], start=(part is high), stop=(part is low))
                    last.then_inc(sig("y_ps").sem, 1)
                pipelined(pe, rounds, PER, CHUNKS, [(0, first), (2, second)])

            @block.scalar
            def _(act):
                def silu(i, v):
                    act.wait_ge(sig("hidden").sem, item(sig("hidden"), i, v, 2))
                    act.wait_ge(sig("hidden_ps").sem, item(sig("hidden_ps"), i, v))
                    nc.scalar.activation(gate_h[v % 2][:], a_ps[v % 2][:], ACT.Silu).then_inc(sig("silu").sem, 1)

                def high_part(i, v):
                    act.wait_ge(sig("hidden").sem, item(sig("hidden"), i, v))
                    act.wait_ge(sig("y_ps").sem, item(sig("y_ps"), i, v, HIDS))
                    nc.scalar.copy(high[v % HIDS][:], hid[v % HIDS][:]).then_inc(sig("high").sem, 1)

                def convert(n, source):
                    nc.scalar.copy(w[:, n], source).then_inc(sig("converted").sem, 1)

                def next_expert(i, v):
                    in_round = i if isinstance(i, int) else 1
                    if v % CHUNKS == 1 and in_round < rounds:
                        n = (v // CHUNKS + 1) % LANES
                        shared_next = n == 0 and in_round == rounds - 1
                        act.wait_ge(sig("y_ps").sem, item(sig("y_ps"), i, v, 2))
                        if not shared_next:
                            loaded = k.load_lane[n].all() + (48 if n else 96)
                            act.wait_ge(k.load_lane[n].sem, i * 48 + loaded)
                        convert(n, shared if shared_next else raw[:, n])
                act.wait_ge(k.load_lane[0].sem, k.load_lane[0].all() + 48)
                convert(0, raw[:, 0])
                pipelined(act, rounds, PER, CHUNKS, [(1, high_part), (1, next_expert), (0, silu)], last_apart=True)

            @block.vector
            def _(dve):
                def product(i, v):
                    dve.wait_ge(sig("silu").sem, item(sig("silu"), i, v))
                    dve.wait_ge(sig("low").sem, item(sig("low"), i, v, HIDS))
                    nc.vector.tensor_tensor(hid[v % HIDS][:], gate_h[v % 2][:], b_ps[v % 2][:], ALU.mult
                                            ).then_inc(sig("hidden").sem, 1)

                def combine(i, v):
                    dve.wait_ge(sig("y_ps").sem, item(sig("y_ps"), i, v))
                    dve.wait_ge(sig("combined").sem, item(sig("combined"), i, v, 1))
                    for j in range(CHUNK):
                        t = CHUNK * (v % CHUNKS) + j
                        e = i * LANES + v // CHUNKS
                        column = bass.ds(e, 1)
                        last = nc.vector.scalar_tensor_tensor(k.h[:, t], y_ps[v % 2][:, j], k.gates[:, t, column],
                                                              k.h[:, t], ALU.mult, ALU.add)
                    last.then_inc(sig("combined").sem, 1)
                pipelined(dve, rounds, PER, CHUNKS, [(3, combine), (0, product)])
        for n in range(LANES):
            k.load_lane[n].more(3 * rounds)
        total = rounds * PER + CHUNKS
        for name in ("hidden", "hidden_ps", "silu", "high", "low", "y_ps", "combined"):
            sig(name).advance(total)
        sig("converted").advance(E + 1)


def hyena(nc, k):
    w = hyena_weights(k)
    C, sig = k.const, k.sig
    with ExitStack() as ctx:
        sb, ps = scratch(nc, ctx, "hyena")
        pieces = norm_pieces(ctx, nc, "hyena")
        w_taps = sb("w_taps", [P, 3, KT, D])
        w_branch = sb("w_branch", [P, KT, D])
        f1, f2 = sb("filter1", [64, P]), sb("filter2", [P, P])
        coefs = sb("coefs", [P, D])
        H13, H22 = sb("H13", [P, 2, D]), sb("H22", [P, 2, D])
        x = sb("x", [P, LANES, D])
        padded = sb("padded", [P, LANES, KT, S + 2])
        v, branch = sb("v", [P, LANES, D]), sb("branch", [P, LANES, D])
        y1, y2 = sb("y1", [P, LANES, 2, D]), sb("y2", [P, LANES, 2, D])
        z, zT = sb("z", [P, LANES, D]), sb("zT", [P, LANES, KT, P])
        a_ps, b_ps, c_ps, x_ps = ([ps(f"{c}_ps{n}", [P, 512]) for n in range(LANES)] for c in "abcx")
        in_proj = w["in_proj"].rearrange("p t (c i) -> p t c i", i=3)
        taps = w["short_w"].rearrange("p (c j) -> p c j", j=3)

        with nc.Block() as block:
            @block.vector
            def _(dve):
                dve.wait_ge(k.load_b.sem, k.load_b.all())
                nc.vector.memset(padded[:], 0.0)
                bias = w["in_bias"][0:3].rearrange("p (c i) -> p c i", i=3)
                nc.vector.tensor_tensor(k.v_bias[0:3, :], bias[:, :, 0], w["taps_T"], ALU.mult)
                for t in range(KT):
                    nc.vector.tensor_copy(w_branch[:, t], in_proj[:, t, :, 2])
                    for j in range(3):
                        nc.vector.tensor_tensor(w_taps[:, j, t], in_proj[:, t, :, 0], taps[:, :, j], ALU.mult)
                dve.wait_ge(sig("out").sem, sig("out").nth(0))
                nc.vector.tensor_copy(H13[:, 0], a_ps[0][:, 0:D])
                nc.vector.tensor_copy(H13[:, 1], b_ps[0][:, 0:D])
                nc.vector.tensor_copy(H22[:, 1], c_ps[0][:, 0:D])
                nc.vector.tensor_scalar(H22[:, 0], c_ps[0][:, 0:D], -1.0, None, ALU.mult)

            @block.tensor
            def _(pe):
                pe.wait_ge(k.load_b.sem, k.load_b.all())
                nc.tensor.matmul(a_ps[0][0:64, 0:P], w["fw1"], C("pos")[0:1, :], start=True, stop=True
                                 ).then_inc(sig("hidden_ps").sem, 1)
                pe.wait_ge(sig("hidden").sem, sig("hidden").nth(0))
                nc.tensor.matmul(a_ps[0][:, 0:P], w["fw2"], f1[:], start=True, stop=True
                                 ).then_inc(sig("hidden_ps").sem, 1)
                pe.wait_ge(sig("hidden").sem, sig("hidden").nth(1))
                odd = lambda ap: ap.rearrange("p (c i) -> p c i", i=2)[:, :, 1]
                nc.tensor.matmul(a_ps[0][:, 0:D], C("ones")[0:1, :], odd(w["fb3"]), start=True, stop=False)
                nc.tensor.matmul(a_ps[0][:, 0:D], f2[:], odd(w["fw3"]), start=False, stop=True
                                 ).then_inc(sig("hidden_ps").sem, 1)
                pe.wait_ge(sig("hidden").sem, sig("hidden").nth(2))
                for bank, name in ((a_ps, "dft_re"), (b_ps, "dft_re1"), (c_ps, "dft_im0")):
                    last = nc.tensor.matmul(bank[0][:, 0:D], C(name), coefs[:], start=True, stop=True)
                last.then_inc(sig("out").sem, 1)

            @block.scalar
            def _(act):
                act.wait_ge(k.load_b.sem, k.load_b.all())
                act.wait_ge(sig("hidden_ps").sem, sig("hidden_ps").nth(0))
                nc.scalar.activation(f1[:], a_ps[0][0:64, 0:P], ACT.Gelu, bias=w["fb1"]).then_inc(sig("hidden").sem, 1)
                act.wait_ge(sig("hidden_ps").sem, sig("hidden_ps").nth(1))
                nc.scalar.activation(f2[:], a_ps[0][:, 0:P], ACT.Gelu, bias=w["fb2"]).then_inc(sig("hidden").sem, 1)
                act.wait_ge(sig("hidden_ps").sem, sig("hidden_ps").nth(2))
                nc.scalar.copy(coefs[:], a_ps[0][:, 0:D]).then_inc(sig("hidden").sem, 1)

            @block.sync
            def _(sp):
                load_mixture(k, sp)
        sig("out").advance(1)
        sig("hidden").advance(3)
        sig("hidden_ps").advance(3)

        with nc.Block() as block:
            @block.vector
            def _(dve):
                def moments(n, t):
                    norm_moments(nc, k, dve, n, t, pieces)

                def norm(n, t):
                    norm_rows(nc, k, dve, n, t, pieces, x[:, n], "turned")

                def add_branch_bias(n, t):
                    dve.wait_ge(sig("proj").sem, sig("proj").nth(t))
                    branch_bias = w["in_bias"].rearrange("p (c i) -> p c i", i=3)[:, :, 2]
                    nc.vector.tensor_tensor(branch[:, n], b_ps[n][:, 0:D], branch_bias, ALU.add
                                            ).then_inc(sig("branch").sem, 1)

                def multiply(n, t):
                    dve.wait_ge(sig("scores").sem, sig("scores").nth(t))
                    spectrum = c_ps[n][:].rearrange("p (s c) -> p s c", s=2)
                    nc.vector.tensor_tensor(y1[:, n], spectrum, H13[:], ALU.mult)
                    nc.vector.tensor_tensor(y2[:, n], spectrum[:, ::-1, :], H22[:], ALU.mult
                                            ).then_inc(sig("rotated").sem, 1)

                def gate(n, t):
                    dve.wait_ge(sig("branch").sem, sig("branch").nth(t))
                    dve.wait_ge(sig("pv").sem, sig("pv").nth(t))
                    nc.vector.tensor_tensor(z[:, n], a_ps[n][:, 0:D], branch[:, n], ALU.mult
                                            ).then_inc(sig("o").sem, 1)

                def add_output(n, t):
                    dve.wait_ge(sig("out").sem, sig("out").nth(t))
                    nc.vector.tensor_tensor(k.h[:, t, :], a_ps[n][:, 0:D], k.h[:, t, :], ALU.add
                                            ).then_inc(sig("kept").sem, 1)
                in_lanes(dve, [(0, moments), (1, add_branch_bias), (2, gate), (1, multiply), (0, norm),
                               (2, add_output)])

            @block.gpsimd
            def _(pool):
                def norm(n, t):
                    norm_root(nc, k, pool, n, t, pieces)

                def add_parts(n, t):
                    pool.wait_ge(sig("rotated").sem, sig("rotated").nth(t))
                    nc.gpsimd.tensor_tensor(y1[:, n], y1[:, n], y2[:, n], ALU.add).then_inc(sig("qk").sem, 1)

                def add_output_bias(n, t):
                    pool.wait_ge(sig("kept").sem, sig("kept").nth(t))
                    nc.gpsimd.tensor_tensor(k.h[:, t, :], k.h[:, t, :], w["out_b"], ALU.add)
                in_lanes(pool, [(0, norm), (1, add_parts), (2, add_output_bias)])

            @block.tensor
            def _(pe):
                def turn_x(n, t):
                    pe.wait_ge(sig("x").sem, sig("x").nth(t))
                    pe.wait_ge(sig("xT").sem, sig("xT").before(t))
                    for f in range(KT):
                        last = nc.tensor.transpose(x_ps[n][:, P * f:P * (f + 1)], x[:, n, P * f:P * (f + 1)],
                                                   C("ident"))
                    last.then_inc(sig("turned").sem, 1)

                def project(n, t):
                    pe.wait_ge(sig("kept").sem, sig("kept").before(t))
                    pe.wait_ge(sig("xT").sem, sig("xT").nth(t))
                    nc.tensor.matmul(a_ps[n][:, 0:D], C("edges")[0:4, :], k.v_bias[:], start=True, stop=False)
                    for j in range(3):
                        for f in range(KT):
                            nc.tensor.matmul(a_ps[n][:, 0:D], padded[:, n, f, j:j + S], w_taps[:, j, f],
                                             start=False, stop=(j == 2 and f == KT - 1))
                    for f in range(KT):
                        last = nc.tensor.matmul(b_ps[n][:, 0:D], padded[:, n, f, 1:S + 1], w_branch[:, f],
                                                start=(f == 0), stop=(f == KT - 1))
                    last.then_inc(sig("proj").sem, 1)

                def transform(n, t):
                    pe.wait_ge(sig("v1").sem, sig("v1").nth(t))
                    nc.tensor.matmul(c_ps[n][:, 0:D], C("dft_re"), v[:, n], start=True, stop=True)
                    nc.tensor.matmul(c_ps[n][:, D:2 * D], C("dft_im"), v[:, n], start=True, stop=True
                                     ).then_inc(sig("scores").sem, 1)

                def transform_back(n, t):
                    pe.wait_ge(sig("qk").sem, sig("qk").nth(t))
                    nc.tensor.matmul(a_ps[n][:, 0:D], C("inv_re"), y1[:, n, 0], start=True, stop=False)
                    nc.tensor.matmul(a_ps[n][:, 0:D], C("inv_im"), y1[:, n, 1], start=False, stop=True
                                     ).then_inc(sig("pv").sem, 1)

                def turn_z(n, t):
                    pe.wait_ge(sig("o").sem, sig("o").nth(t))
                    for f in range(KT):
                        last = nc.tensor.transpose(b_ps[n][:, P * f:P * (f + 1)], z[:, n, P * f:P * (f + 1)],
                                                   C("ident"))
                    last.then_inc(sig("oT_ps").sem, 1)

                def output(n, t):
                    pe.wait_ge(sig("oT").sem, sig("oT").nth(t))
                    for f in range(KT):
                        last = nc.tensor.matmul(a_ps[n][:, 0:D], zT[:, n, f], w["out_w"][:, f, :], start=(f == 0),
                                                stop=(f == KT - 1))
                    last.then_inc(sig("out").sem, 1)
                in_lanes(pe, [(1, turn_x), (1, project), (2, transform_back), (1, transform), (2, turn_z), (2, output)])

            @block.scalar
            def _(act):
                halves = lambda bank: bank[:, 0:D].rearrange("p (t n) -> p t n", t=KT)

                def keep_xT(n, t):
                    act.wait_ge(sig("turned").sem, sig("turned").nth(t))
                    nc.scalar.copy(padded[:, n, :, 1:S + 1], halves(x_ps[n])).then_inc(sig("xT").sem, 1)

                def keep_v(n, t):
                    act.wait_ge(sig("proj").sem, sig("proj").nth(t))
                    nc.scalar.copy(v[:, n], a_ps[n][:, 0:D]).then_inc(sig("v1").sem, 1)

                def keep_zT(n, t):
                    act.wait_ge(sig("oT_ps").sem, sig("oT_ps").nth(t))
                    nc.scalar.copy(zT[:, n], halves(b_ps[n])).then_inc(sig("oT").sem, 1)
                in_lanes(act, [(1, keep_xT), (1, keep_v), (2, keep_zT)])
        for name in NORM_SIGNALS + ["scores", "rotated", "pv", "o", "out", "kept", "qk", "turned", "xT", "proj", "v1",
                                    "branch", "oT_ps", "oT"]:
            sig(name).advance(TILES)


def mixture(nc, k):
    E = 8
    r = k.region_a
    expert_w = r[:, 0:4096].rearrange("p (e t n) -> p e t n", e=E, t=KT)
    gate_w = r[:, 4096:4112].rearrange("p (t n) -> p t n", t=KT)
    gate_b, expert_b = r[:, 4112:4120], r[0:E, 4120:4376]
    C, sig = k.const, k.sig
    with ExitStack() as ctx:
        sb, ps = scratch(nc, ctx, "mixture")
        pieces = norm_pieces(ctx, nc, "mixture")
        x, xT = sb("x", [P, LANES, D]), sb("xT", [P, LANES, KT, P])
        gate, kept = sb("gate", [P, LANES, E]), sb("kept", [P, LANES, E])
        share, shareT = sb("share", [P, LANES, P]), sb("shareT", [P, LANES, P])
        bias_rows = sb("bias_rows", [P, D])
        top, den, inv, none = (sb(name, [P, LANES, 1]) for name in ("top", "den", "inv", "none"))
        a_ps = [ps(f"a_ps{n}", [P, KT, P]) for n in range(LANES)]
        bias_ps = [ps(f"bias_ps{n}", [P, 2, D]) for n in range(LANES)]
        pair_ps = [ps(f"pair_ps{q}", [P, 2, D]) for q in range(E // 2)]

        with nc.Block() as block:
            @block.vector
            def _(dve):
                def moments(n, t):
                    norm_moments(nc, k, dve, n, t, pieces)

                def norm(n, t):
                    norm_rows(nc, k, dve, n, t, pieces, x[:, n], "turned")

                def shifted_logits(n, t):
                    dve.wait_ge(sig("logits").sem, sig("logits").nth(t))
                    nc.vector.tensor_tensor(gate[:, n], a_ps[n][:, 0, 0:E], gate_b, ALU.add).then_inc(sig("xn").sem, 1)
                    dve.wait_ge(sig("xn").sem, sig("xn").nth(t))
                    nc.vector.tensor_reduce(top[:, n], gate[:, n], AX_X, ALU.max).then_inc(sig("top").sem, 1)
                    dve.wait_ge(sig("top").sem, sig("top").nth(t))
                    nc.vector.tensor_scalar(gate[:, n], gate[:, n], top[:, n], None, ALU.subtract
                                            ).then_inc(sig("shifted").sem, 1)

                def softmax(n, t):
                    dve.wait_ge(sig("probs").sem, sig("probs").nth(t))
                    nc.vector.tensor_reduce(den[:, n], gate[:, n], AX_X, ALU.add).then_inc(sig("den").sem, 1)
                    dve.wait_ge(sig("den").sem, sig("den").nth(t))
                    nc.vector.reciprocal(inv[:, n], den[:, n]).then_inc(sig("recip").sem, 1)
                    dve.wait_ge(sig("recip").sem, sig("recip").nth(t))
                    nc.vector.tensor_scalar(gate[:, n], gate[:, n], inv[:, n], None, ALU.mult
                                            ).then_inc(sig("normed").sem, 1)

                def threshold(n, t):
                    dve.wait_ge(sig("normed").sem, sig("normed").nth(t))
                    nc.vector.scalar_tensor_tensor(kept[:, n], gate[:, n], 0.1, gate[:, n], ALU.is_ge, ALU.mult
                                                   ).then_inc(sig("picked").sem, 1)
                    dve.wait_ge(sig("picked").sem, sig("picked").nth(t))
                    nc.vector.tensor_reduce(den[:, n], kept[:, n], AX_X, ALU.add).then_inc(sig("clipped").sem, 1)

                def norm_gates(n, t):
                    dve.wait_ge(sig("clipped").sem, sig("clipped").nth(t))
                    nc.vector.scalar_tensor_tensor(none[:, n], den[:, n], 0.0, den[:, n], ALU.is_equal, ALU.add
                                                   ).then_inc(sig("unit").sem, 1)
                    dve.wait_ge(sig("unit").sem, sig("unit").nth(t))
                    nc.vector.reciprocal(inv[:, n], none[:, n]).then_inc(sig("rounded").sem, 1)
                    dve.wait_ge(sig("rounded").sem, sig("rounded").nth(t))
                    nc.vector.tensor_scalar(share[:, n, 0:E], kept[:, n], inv[:, n], None, ALU.mult
                                            ).then_inc(sig("weighed").sem, 1)

                def add_biases(n, t):
                    dve.wait_ge(sig("combined").sem, sig("combined").nth(t * E + (E - 1)))
                    dve.wait_ge(sig("out").sem, sig("out").nth(t))
                    nc.vector.tensor_tensor(k.h[:, t, :], bias_ps[n][:, 1], k.h[:, t, :], ALU.add
                                            ).then_inc(sig("kept").sem, 1)

                def combine(q):
                    def op(n, t):
                        for e in (2 * q, 2 * q + 1):
                            if e % 2 == 0:
                                dve.wait_ge(sig("y_ps").sem, sig("y_ps").nth(t * (E // 2) + q))
                            if e:
                                dve.wait_ge(sig("combined").sem, sig("combined").nth(t * E + (e - 1)))
                            else:
                                dve.wait_ge(sig("weighed").sem, sig("weighed").nth(t))
                            nc.vector.scalar_tensor_tensor(k.h[:, t, :], pair_ps[q][:, e % 2], share[:, n, e:e + 1],
                                                           k.h[:, t, :], ALU.mult, ALU.add
                                                           ).then_inc(sig("combined").sem, 1)
                    return op
                nc.vector.memset(share[:], 0.0)
                nc.vector.memset(bias_rows[:], 0.0).then_inc(sig("ones_set").sem, 1)
                dve.wait_ge(sig("ones_set").sem, sig("ones_set").nth(0))
                dve.wait_ge(k.load_a.sem, k.load_a.all())
                nc.vector.tensor_copy(bias_rows[0:E], expert_b)
                in_lanes(dve, [(2, combine(0)), (1, shifted_logits), (2, combine(1)), (1, softmax), (0, moments),
                          (2, combine(2)), (1, threshold), (0, norm), (1, norm_gates), (2, combine(3)),
                          (2, add_biases)])

            @block.gpsimd
            def _(pool):
                in_lanes(pool, [(0, lambda n, t: norm_root(nc, k, pool, n, t, pieces))])

            @block.tensor
            def _(pe):
                def turn_x(n, t):
                    pe.wait_ge(sig("x").sem, sig("x").nth(t))
                    pe.wait_ge(sig("xn").sem, sig("xn").before(t))
                    for f in range(KT):
                        last = nc.tensor.transpose(a_ps[n][:, f], x[:, n, P * f:P * (f + 1)], C("ident"))
                    last.then_inc(sig("turned").sem, 1)

                def logits(n, t):
                    pe.wait_ge(sig("xT").sem, sig("xT").nth(t))
                    for f in range(KT):
                        last = nc.tensor.matmul(a_ps[n][:, 0, 0:E], xT[:, n, f], gate_w[:, f, :], start=(f == 0),
                                                stop=(f == KT - 1))
                    last.then_inc(sig("logits").sem, 1)

                def products(q):
                    def op(n, t):
                        pe.wait_ge(sig("combined").sem, sig("combined").nth(t * E + (2 * q + 1)) - E)
                        for f in range(KT):
                            last = nc.tensor.matmul(pair_ps[q][:], xT[:, n, f], expert_w[:, 2 * q:2 * q + 2, f, :],
                                                    start=(f == 0), stop=(f == KT - 1))
                        last.then_inc(sig("y_ps").sem, 1)
                    return op

                def turn_shares(n, t):
                    pe.wait_ge(sig("kept").sem, sig("kept").before(t))
                    pe.wait_ge(sig("weighed").sem, sig("weighed").nth(t))
                    nc.tensor.transpose(bias_ps[n][:, 0, 0:P], share[:, n], C("ident")).then_inc(
                        sig("share_ps").sem, 1)

                def weigh_biases(n, t):
                    pe.wait_ge(sig("share_T").sem, sig("share_T").nth(t))
                    nc.tensor.matmul(bias_ps[n][:, 1], shareT[:, n], bias_rows[:], start=True, stop=True
                                     ).then_inc(sig("out").sem, 1)
                pe.wait_ge(k.load_a.sem, k.load_a.all())
                in_lanes(pe, [(1, turn_x), (2, products(0)), (1, logits), (2, products(1)), (2, turn_shares),
                         (2, products(2)), (2, weigh_biases), (2, products(3))])

            @block.scalar
            def _(act):
                def keep_xT(n, t):
                    act.wait_ge(sig("turned").sem, sig("turned").nth(t))
                    nc.scalar.copy(xT[:, n], a_ps[n][:]).then_inc(sig("xT").sem, 1)

                def exponents(n, t):
                    act.wait_ge(sig("shifted").sem, sig("shifted").nth(t))
                    nc.scalar.activation(gate[:, n], gate[:, n], ACT.Exp).then_inc(sig("probs").sem, 1)

                def keep_shares(n, t):
                    act.wait_ge(sig("share_ps").sem, sig("share_ps").nth(t))
                    nc.scalar.copy(shareT[:, n], bias_ps[n][:, 0, 0:P]).then_inc(sig("share_T").sem, 1)
                in_lanes(act, [(1, keep_xT), (2, keep_shares), (1, exponents)])
        for name in NORM_SIGNALS + ["logits", "xn", "top", "shifted", "probs", "den", "recip", "normed", "picked",
                                    "clipped", "unit", "rounded", "weighed", "turned", "xT", "share_ps", "share_T",
                                    "out", "kept"]:
            sig(name).advance(TILES)
        sig("combined").advance(TILES * E)
        sig("y_ps").advance(TILES * E // 2)
        sig("ones_set").advance(1)


class Context:
    pass


def tower(nc, dram, out):
    k = Context()
    k.dram = dram
    with ExitStack() as ctx:
        sb = lambda name, shape, dt=F32: ctx.enter_context(nc.sbuf_tensor(name, shape, dt))
        k.const_sb = sb("const_sb", [P, CONST_COLS])
        k.h = sb("h", [P, TILES, D])
        k.rows = sb("rows", [P, TILES, D])
        k.xT = sb("xT", [P, KT, TILES * S])
        k.region_a = sb("region_a", [P, 10240])
        k.region_b = sb("region_b", [P, 5376])
        k.logits = sb("logits", [P, TILES, 32])
        k.gates = sb("gates", [P, TILES, 33])
        k.minus_half, k.eps_ln, k.eps_rms = (sb(name, [P, 1]) for name in ("minus_half", "eps_ln", "eps_rms"))
        k.ident16 = sb("ident16", [P, P], BF16)
        k.conv_w, k.conv_b = sb("conv_w", [P, 8, 3]), sb("conv_b", [P, 8])
        k.shared = sb("shared", [P, 6 * P])
        k.v_bias = sb("v_bias", [4, D])
        k.idle = sb("idle", [P, LANES])
        k.emb_rows = sb("emb_rows", [LEVELS, D])
        k.level_cols = sb("level_cols", [P, B])
        k.score_rows = sb("score_rows", [LEVELS, 512])
        k.value_rows = sb("value_rows", [P, 4, D])
        k.const = lambda name: k.const_sb[:, CONST_AT[name][0]:CONST_AT[name][0] + CONST_AT[name][1]]
        signals = {}

        def sig(name):
            if name not in signals:
                signals[name] = Signal(ctx.enter_context(nc.semaphore("s_" + name)))
            return signals[name]
        k.sig = sig
        k.load_small, k.load_a, k.load_b, k.store = (
            Loads(ctx.enter_context(nc.semaphore(name))) for name in ("load_small", "load_a", "load_b", "store"))
        chain_sem = ctx.enter_context(nc.semaphore("vector_step"))
        steps = [0]

        def chain(dve):
            def link(ins):
                steps[0] += 1
                ins.then_inc(chain_sem, 1)
                dve.wait_ge(chain_sem, steps[0])
            return link
        k.chain = chain
        k.load_lane = [Loads(ctx.enter_context(nc.semaphore(f"load_lane{n}"))) for n in range(LANES)]
        for name in SIGNALS:
            sig(name)
        with nc.Block() as block:
            @block.sync
            def _(sp):
                for name in SIGNALS:
                    sp.sem_inc(sig(name).sem, HEADSTART)
        level_tables(nc, k)
        level_attention(nc, k)
        repeat_heads(nc, k)
        self_attention(nc, k, rope=False)
        route(nc, k, 8, 2, int(1.25 * B * S * 2 / 8), biased=False)
        experts(nc, k, 8, dram["L0_ffn_w1"].rearrange("e (t p) f -> p e t f", p=P),
                dram["L0_ffn_w2"].rearrange("e (t p) n -> p e t n", p=P), gated=True, target=k.rows[:],
                hidden_bias=None, prefetch=load_mha)
        close_gqa(nc, k)
        self_attention(nc, k, rope=True)
        experts(nc, k, 2, dram["L1_attn_W1"].rearrange("(t p) (e f) -> p e t f", p=P, e=2),
                dram["L1_attn_W2"].rearrange("(e t p) n -> p e t n", p=P, e=2), gated=False, target=k.h[:],
                hidden_bias=attention_weights(k.region_a)["b1"], prefetch=load_bitlinear)
        bitlinear(nc, k)
        decay_attention(nc, k)
        with ExitStack() as layer:
            parts = [layer.enter_context(nc.sbuf_tensor(name, [P, KT, TILES * S], F32R)) for name in
                     ("x_high", "x_low")]
            swiglu_gates(nc, k, k.shared[:], *(x[:] for x in parts))
            route(nc, k, 32, 4, 2 * 2 * 512 * 4 // 32, biased=True)
            swiglu_experts(nc, k, *(x[:] for x in parts), k.shared[:])
        hyena(nc, k)
        mixture(nc, k)
        store(nc, k, out)


def store(nc, k, out):
    with nc.Block() as block:
        @block.sync
        def _(sp):
            sp.dma_start(out.rearrange("b s d -> s b d"), k.h[:]).then_inc(k.store.sem, 16)
            k.store.more()
            for loads in (k.load_a, k.load_b, k.load_small, *k.load_lane):
                if loads.count:
                    sp.wait_ge(loads.sem, loads.all())
            sp.wait_ge(k.store.sem, k.store.all())


_INS = [
    "x", "L0_tok_level_emb", "L0_attn_query_mat", "L0_attn_key_mat", "L0_attn_value_mat", "L0_attn_linear_m1",
    "L0_ffn_qw", "L0_ffn_qb", "L0_ffn_kw", "L0_ffn_kb", "L0_ffn_vw", "L0_ffn_vb", "L0_ffn_ow", "L0_ffn_ob",
    "L0_ffn_gate_w", "L0_ffn_w1", "L0_ffn_w2", "L0_ffn_norm1_w", "L0_ffn_norm2_w",
    "L1_attn_Wq", "L1_attn_bq", "L1_attn_Wk", "L1_attn_bk", "L1_attn_Wv", "L1_attn_bv", "L1_attn_Wo",
    "L1_attn_bo", "L1_attn_W1", "L1_attn_b1", "L1_attn_W2", "L1_attn_b2", "L1_attn_g1", "L1_attn_beta1",
    "L1_attn_g2", "L1_attn_beta2", "L1_ffn_w1", "L1_ffn_conv_w", "L1_ffn_conv_b", "L1_ffn_w2",
    "L2_attn_q", "L2_attn_k", "L2_attn_log_decay", "L2_attn_norm_weight", "L2_attn_o_w",
    "L2_ffn_gate_w", "L2_ffn_bias", "L2_ffn_W1", "L2_ffn_W3", "L2_ffn_W2", "L2_ffn_sw1", "L2_ffn_sw3",
    "L2_ffn_sw2", "L3_attn_in_proj_w", "L3_attn_in_proj_b", "L3_attn_short_w", "L3_attn_short_b",
    "L3_attn_fw1", "L3_attn_fb1", "L3_attn_fw2", "L3_attn_fb2", "L3_attn_fw3", "L3_attn_fb3",
    "L3_attn_out_w", "L3_attn_out_b", "L3_ffn_gate_w", "L3_ffn_gate_b", "L3_ffn_expert_w", "L3_ffn_expert_b",
]


def kernel(**inputs):
    from concourse import bacc
    from concourse.bass_utils import run_bass_kernel_spmd

    nc = bacc.Bacc("TRN2", target_bir_lowering=False, num_devices=1)
    arrays, dram = {}, {}
    for name in _INS:
        a = np.ascontiguousarray(inputs[name])
        arrays[f"in_{name}"] = a
        dram[name] = nc.dram_tensor(f"in_{name}", a.shape, mybir.dt.from_np(a.dtype), kind="ExternalInput").ap()
    arrays["in_constants"] = shape_constants()
    dram["constants"] = nc.dram_tensor("in_constants", [P, CONST_COLS], F32, kind="ExternalInput").ap()
    out = nc.dram_tensor("out_h", [B, S, D], F32, kind="ExternalOutput").ap()
    tower(nc, dram, out)
    return run_bass_kernel_spmd(nc, [arrays], core_ids=[0]).results[0]["out_h"]
```
